# Optimizing a Trainium2 kernel written in Bass

```python
import numpy as np
import jax
import jax.numpy as jnp

def _softmax(x, axis=-1):
    return jax.nn.softmax(x, axis=axis)

def _gelu(x):
    return jax.nn.gelu(x, approximate=True)

def _silu(x):
    return jax.nn.silu(x)

def _sigmoid(x):
    return jax.nn.sigmoid(x)

def _layernorm(x, axis=-1, eps=1e-05):
    m = jnp.mean(x, axis=axis, keepdims=True)
    v = jnp.var(x, axis=axis, keepdims=True)
    return (x - m) / jnp.sqrt(v + eps)

def _scatter_add(tgt, idx, src, axis=0):
    return tgt.at[idx].add(src)

def _segment_sum(src, seg, n):
    return jax.ops.segment_sum(src, seg, n)
kernel_name = 'mk_perceiver_d4_seqx_r8_4cad73'

def setup_inputs(seed: int=0):
    np.random.seed(seed)
    _w = jnp.asarray

    def _rec_inputs():
        import jax
        import jax.numpy as jnp
        _rk = jax.random.key(seed)
        x = -0.0005207 + 1.001 * jax.random.normal(jax.random.fold_in(_rk, 1), (4, 128, 128), jnp.float32)
        _lenS = 128 - jax.random.randint(jax.random.fold_in(_rk, 7), (4,), 0, max(1, 128 // 4) + 1, jnp.int32)
        _lenS2 = 2048 - jax.random.randint(jax.random.fold_in(_rk, 8), (4,), 0, max(1, 2048 // 4) + 1, jnp.int32)
        _ctx_1024P = jax.random.normal(jax.random.fold_in(_rk, 11), (4, 16, 128), jnp.float32)
        _ctx_1024c = jax.random.dirichlet(jax.random.fold_in(_rk, 511), 0.3 * jnp.ones((16,), jnp.float32), (4, 2048))
        _ctx_1024t = jnp.einsum('bsk,bkd->bsd', _ctx_1024c, _ctx_1024P)
        _ctx_1024t = _ctx_1024t * jax.lax.rsqrt(jnp.mean(jnp.square(_ctx_1024t)) + 1e-12) * 0.953939
        ctx_1024 = 2.81802e-05 + 1.00001 * (_ctx_1024t + 0.3 * jax.random.normal(jax.random.fold_in(_rk, 611), (4, 2048, 128), jnp.float32))
        _validS = jnp.arange(128)[None, :] < _lenS[:, None]
        _validS2 = jnp.arange(2048)[None, :] < _lenS2[:, None]
        _causal = jnp.tril(jnp.ones((128, 128), dtype=bool))
        mask_SxS2_bk1 = jnp.broadcast_to(_validS2[0:1, :], (128, 2048))
        return (x, ctx_1024, mask_SxS2_bk1)
    x, ctx_1024, mask_SxS2_bk1 = _rec_inputs()

    def _L0_xattn_setup():
        import jax, jax.numpy as jnp
        import numpy as np
        E = 128
        H = 16
        D = E // H
        key = jax.random.key(seed)
        ks = jax.random.split(key, 12)
        B, Tq, Tk = (2, 128, 1024)
        s = 0.02
        return {'hidden_states': jax.random.normal(ks[0], (B, Tq, E), jnp.float32), 'key_value_states': jax.random.normal(ks[1], (B, Tk, E), jnp.float32), 'Wq': jax.random.normal(ks[2], (E, E), jnp.float32) * s, 'bq': jnp.zeros((E,), jnp.float32), 'Wk': jax.random.normal(ks[3], (E, E), jnp.float32) * s, 'bk': jnp.zeros((E,), jnp.float32), 'Wv': jax.random.normal(ks[4], (E, E), jnp.float32) * s, 'bv': jnp.zeros((E,), jnp.float32), 'Wo': jax.random.normal(ks[5], (E, E), jnp.float32) * s, 'bo': jnp.zeros((E,), jnp.float32), 'stride': 16}
    _L0_xattn_all = _L0_xattn_setup()
    _L0_xattn_in = {k: v for k, v in _L0_xattn_all.items() if k in ('Wq', 'bq', 'Wk', 'bk', 'Wv', 'bv', 'Wo', 'bo')}
    del _L0_xattn_all

    def _L0_attn_setup():
        import jax, jax.numpy as jnp
        import numpy as np
        B, L, D, N = (4, 256, 128, 16)

        def _layernorm(x, g, b, eps=1e-05):
            mu = jnp.mean(x, axis=-1, keepdims=True)
            var = jnp.mean(jnp.square(x - mu), axis=-1, keepdims=True)
            return (x - mu) * jax.lax.rsqrt(var + eps) * g + b

        def _silu(x):
            return x * jax.nn.sigmoid(x)

        def _depthwise_conv(x, w):
            xc = x.transpose(0, 2, 1)
            y = jax.lax.conv_general_dilated(xc, w, window_strides=(1,), padding=[(1, 1)], feature_group_count=xc.shape[1], dimension_numbers=('NCH', 'OIH', 'NCH'))
            return y.transpose(0, 2, 1)

        def _selective_scan(u, A_log, D_skip, W_dt, b_dt, W_B, W_C):
            A = -jnp.exp(A_log)
            dt = jax.nn.softplus(u @ W_dt + b_dt)
            Bt = u @ W_B
            Ct = u @ W_C

            def step(h, inp):
                dt_t, B_t, C_t, u_t = inp
                dA = jnp.exp(dt_t[..., None] * A)
                h = dA * h + (dt_t * u_t)[..., None] * B_t[:, None, :]
                y = jnp.einsum('bdn,bn->bd', h, C_t)
                return (h, y)
            h0 = jnp.zeros((u.shape[0], u.shape[2], A.shape[1]), u.dtype)
            xs = (dt.transpose(1, 0, 2), Bt.transpose(1, 0, 2), Ct.transpose(1, 0, 2), u.transpose(1, 0, 2))
            _, ys = jax.lax.scan(step, h0, xs)
            return ys.transpose(1, 0, 2) + u * D_skip
        key = jax.random.key(seed)
        ks = jax.random.split(key, 12)
        s = 1.0 / np.sqrt(D)
        inp = {'x': jax.random.normal(ks[0], (B, L, D), jnp.float32), 'ln_g': jnp.ones((D,), jnp.float32), 'ln_b': jnp.zeros((D,), jnp.float32), 'w1_w': jax.random.normal(ks[1], (D, D), jnp.float32) * s, 'w1_b': jnp.zeros((D,), jnp.float32), 'v1_w': jax.random.normal(ks[2], (D, D), jnp.float32) * s, 'v1_b': jnp.zeros((D,), jnp.float32), 'w2_w': jax.random.normal(ks[3], (D, D), jnp.float32) * s, 'w2_b': jnp.zeros((D,), jnp.float32), 'conv_w': jax.random.normal(ks[4], (D, 1, 3), jnp.float32) * (1.0 / np.sqrt(3.0)), 'A_log': jnp.log(jnp.broadcast_to(jnp.arange(1, N + 1, dtype=jnp.float32), (D, N))), 'D_skip': jnp.ones((D,), jnp.float32), 'W_dt': jax.random.normal(ks[5], (D, D), jnp.float32) * (s * 0.1), 'b_dt': jnp.full((D,), -4.0, jnp.float32), 'W_B': jax.random.normal(ks[6], (D, N), jnp.float32) * s, 'W_C': jax.random.normal(ks[7], (D, N), jnp.float32) * s}
        return inp
    _L0_attn_all = _L0_attn_setup()
    _L0_attn_in = {k: v for k, v in _L0_attn_all.items() if k in ('ln_g', 'ln_b', 'w1_w', 'w1_b', 'v1_w', 'v1_b', 'w2_w', 'w2_b', 'conv_w', 'A_log', 'D_skip', 'W_dt', 'b_dt', 'W_B', 'W_C')}
    del _L0_attn_all

    def _L0_ffn_setup():
        import jax, jax.numpy as jnp
        import numpy as np
        D_MODEL, D_FF, N_EXPERTS, TOP_K = (128, 512, 8, 2)
        key = jax.random.key(seed)
        k0, k1, k2, k3 = jax.random.split(key, 4)
        x = jax.random.normal(k0, (2, 256, D_MODEL), dtype=jnp.float32)
        Wg = jax.random.normal(k1, (D_MODEL, N_EXPERTS), dtype=jnp.float32) * 0.02
        W1 = jax.random.normal(k2, (N_EXPERTS, D_MODEL, D_FF), dtype=jnp.float32) * 0.02
        b1 = jnp.zeros((N_EXPERTS, D_FF), dtype=jnp.float32)
        W2 = jax.random.normal(k3, (N_EXPERTS, D_FF, D_MODEL), dtype=jnp.float32) * 0.02
        b2 = jnp.zeros((N_EXPERTS, D_MODEL), dtype=jnp.float32)
        return {'x': x, 'Wg': Wg, 'W1': W1, 'b1': b1, 'W2': W2, 'b2': b2}
    _L0_ffn_all = _L0_ffn_setup()
    _L0_ffn_in = {k: v for k, v in _L0_ffn_all.items() if k in ('Wg', 'W1', 'b1', 'W2', 'b2')}
    del _L0_ffn_all

    def _L1_xattn_setup():
        import jax, jax.numpy as jnp
        import numpy as np
        B, S, D, H = (4, 256, 128, 16)
        HD = D // H
        key = jax.random.key(seed)
        ks = jax.random.split(key, 16)
        inv = 1.0 / np.sqrt(D)
        inv_hd = 1.0 / np.sqrt(D)
        inp = {'query': jax.random.normal(ks[0], (B, S, D), jnp.float32), 'key': jax.random.normal(ks[1], (B, S, D), jnp.float32), 'value': jax.random.normal(ks[2], (B, S, D), jnp.float32), 'mask': jnp.triu(jnp.ones((S, S), jnp.bool_), k=1), 'Wq': jax.random.normal(ks[3], (D, D), jnp.float32) * inv, 'Wk': jax.random.normal(ks[4], (D, D), jnp.float32) * inv, 'Wv': jax.random.normal(ks[5], (D, D), jnp.float32) * inv, 'wq_h': jax.random.normal(ks[6], (D, HD), jnp.float32) * inv_hd, 'bq_h': jax.random.normal(ks[7], (HD,), jnp.float32) * inv_hd, 'wk_h': jax.random.normal(ks[8], (D, HD), jnp.float32) * inv_hd, 'bk_h': jax.random.normal(ks[9], (HD,), jnp.float32) * inv_hd, 'wv_h': jax.random.normal(ks[10], (D, HD), jnp.float32) * inv_hd, 'bv_h': jax.random.normal(ks[11], (HD,), jnp.float32) * inv_hd, 'Wo': jax.random.normal(ks[12], (D, D), jnp.float32) * inv}
        return inp
    _L1_xattn_all = _L1_xattn_setup()
    _L1_xattn_in = {k: v for k, v in _L1_xattn_all.items() if k in ('Wq', 'Wk', 'Wv', 'wq_h', 'bq_h', 'wk_h', 'bk_h', 'wv_h', 'bv_h', 'Wo')}
    del _L1_xattn_all

    def _L1_attn_setup():
        import jax, jax.numpy as jnp
        import numpy as np
        key = jax.random.key(seed)
        ks = jax.random.split(key, 5)
        B, T, C = (2, 256, 128)
        x = jax.random.normal(ks[0], (B, T, C), dtype=jnp.float32)
        Wqkv = jax.random.normal(ks[1], (C, 3 * C), dtype=jnp.float32) * C ** (-0.5)
        bqkv = jax.random.normal(ks[2], (3 * C,), dtype=jnp.float32) * 0.02
        Wproj = jax.random.normal(ks[3], (C, C), dtype=jnp.float32) * C ** (-0.5)
        bproj = jax.random.normal(ks[4], (C,), dtype=jnp.float32) * 0.02
        return {'x': x, 'Wqkv': Wqkv, 'bqkv': bqkv, 'Wproj': Wproj, 'bproj': bproj}
    _L1_attn_all = _L1_attn_setup()
    _L1_attn_in = {k: v for k, v in _L1_attn_all.items() if k in ('Wqkv', 'bqkv', 'Wproj', 'bproj')}
    del _L1_attn_all

    def _L1_ffn_setup():
        import jax, jax.numpy as jnp
        import numpy as np
        B, T, D, H, R, N = (16, 128, 128, 32, 64, 8)
        key = jax.random.key(seed)
        ks = jax.random.split(key, 8)
        s = lambda k, shape, fan: jax.random.normal(k, shape, jnp.float32) / np.sqrt(fan)
        return {'x': jax.random.normal(ks[0], (B, T, D), jnp.float32), 'W_base': s(ks[1], (D, D), D), 'b_base': jnp.zeros((D,), jnp.float32), 'W_enc': s(ks[2], (N, D, H), D), 'b_enc': jnp.zeros((N, H), jnp.float32), 'W_dec': s(ks[3], (N, H, D), H), 'b_dec': jnp.zeros((N, D), jnp.float32), 'W_down': s(ks[4], (N, D, R), D), 'b_down': jnp.zeros((N, R), jnp.float32), 'W_up': s(ks[5], (N, R, D), R), 'b_up': jnp.zeros((N, D), jnp.float32), 'connected_idx': jnp.arange(N, dtype=jnp.int32)}
    _L1_ffn_all = _L1_ffn_setup()
    _L1_ffn_in = {k: v for k, v in _L1_ffn_all.items() if k in ('W_base', 'b_base', 'W_enc', 'b_enc', 'W_dec', 'b_dec', 'W_down', 'b_down', 'W_up', 'b_up', 'connected_idx')}
    del _L1_ffn_all

    def _L2_xattn_setup():
        import jax, jax.numpy as jnp
        import numpy as np
        import math
        B, SQ, SK, D = (4, 256, 256, 128)
        key = jax.random.key(seed)
        ks = jax.random.split(key, 9)
        s = 1.0 / math.sqrt(D)
        return {'q': jax.random.normal(ks[0], (B, SQ, D), jnp.float32), 'k': jax.random.normal(ks[1], (B, SK, D), jnp.float32), 'v': jax.random.normal(ks[2], (B, SK, D), jnp.float32), 'Wq': jax.random.normal(ks[3], (D, D), jnp.float32) * s, 'bq': jax.random.normal(ks[4], (D,), jnp.float32) * s, 'Wk': jax.random.normal(ks[5], (D, D), jnp.float32) * s, 'bk': jax.random.normal(ks[6], (D,), jnp.float32) * s, 'Wv': jax.random.normal(ks[7], (D, D), jnp.float32) * s, 'bv': jax.random.normal(ks[8], (D,), jnp.float32) * s}
    _L2_xattn_all = _L2_xattn_setup()
    _L2_xattn_in = {k: v for k, v in _L2_xattn_all.items() if k in ('Wq', 'bq', 'Wk', 'bk', 'Wv', 'bv')}
    del _L2_xattn_all

    def _L2_attn_setup():
        import jax, jax.numpy as jnp
        import numpy as np
        B, T, H, S = (8, 512, 128, 16)
        LN_EPS = 1e-05

        def _forward(x, W_in, b_in, B_mat, C_mat, W_B, b_B, W_D, b_D, W_out, b_out, W_ig, b_ig, W_fg, b_fg, gamma, beta):
            xp = x @ W_in + b_in
            Bx = (xp @ W_B + b_B) @ B_mat
            ig = jax.nn.sigmoid(xp @ W_ig + b_ig)
            fg = jax.nn.sigmoid(xp @ W_fg + b_fg)

            def step(h, inp):
                fg_t, ig_t, bx_t = inp
                h = fg_t * h + ig_t * bx_t
                return (h, h)
            h0 = jnp.zeros((xp.shape[0], B_mat.shape[1]), xp.dtype)
            xs = (jnp.swapaxes(fg, 0, 1), jnp.swapaxes(ig, 0, 1), jnp.swapaxes(Bx, 0, 1))
            _, hs = jax.lax.scan(step, h0, xs)
            hs = jnp.swapaxes(hs, 0, 1)
            y = jnp.tanh(hs @ C_mat + (xp @ W_D + b_D))
            y = y @ W_out + b_out + xp
            mu = jnp.mean(y, axis=-1, keepdims=True)
            var = jnp.var(y, axis=-1, keepdims=True)
            y = (y - mu) * jax.lax.rsqrt(var + LN_EPS) * gamma + beta
            return y
        key = jax.random.key(seed)
        ks = jax.random.split(key, 16)
        inv_h = 1.0 / np.sqrt(H)
        d = {'x': jax.random.normal(ks[0], (B, T, H), jnp.float32), 'W_in': jax.random.normal(ks[1], (H, H), jnp.float32) * inv_h, 'b_in': jnp.zeros((H,), jnp.float32), 'B_mat': jax.random.normal(ks[2], (H, S), jnp.float32) * 0.1, 'C_mat': jax.random.normal(ks[3], (S, H), jnp.float32) * 0.1, 'W_B': jax.random.normal(ks[4], (H, H), jnp.float32) * inv_h, 'b_B': jnp.zeros((H,), jnp.float32), 'W_D': jax.random.normal(ks[5], (H, H), jnp.float32) * inv_h, 'b_D': jnp.zeros((H,), jnp.float32), 'W_out': jax.random.normal(ks[6], (H, H), jnp.float32) * inv_h, 'b_out': jnp.zeros((H,), jnp.float32), 'W_ig': jax.random.normal(ks[7], (H, S), jnp.float32) * inv_h, 'b_ig': jnp.zeros((S,), jnp.float32), 'W_fg': jax.random.normal(ks[8], (H, S), jnp.float32) * inv_h, 'b_fg': jnp.zeros((S,), jnp.float32), 'gamma': jnp.ones((H,), jnp.float32), 'beta': jnp.zeros((H,), jnp.float32)}
        return d
    _L2_attn_all = _L2_attn_setup()
    _L2_attn_in = {k: v for k, v in _L2_attn_all.items() if k in ('W_in', 'b_in', 'B_mat', 'C_mat', 'W_B', 'b_B', 'W_D', 'b_D', 'W_out', 'b_out', 'W_ig', 'b_ig', 'W_fg', 'b_fg', 'gamma', 'beta')}
    del _L2_attn_all

    def _L2_ffn_setup():
        import jax, jax.numpy as jnp
        import numpy as np
        CAPACITY_FACTOR = 1.25
        key = jax.random.key(seed)
        k1, k2, k3, k4 = jax.random.split(key, 4)
        B, S, D, E, H = (2, 256, 128, 16, 512)
        inputs = jax.random.normal(k1, (B, S, D), dtype=jnp.float32)
        gate_w = jax.random.normal(k2, (E, D), dtype=jnp.float32) / np.float32(np.sqrt(D))
        w1 = jax.random.normal(k3, (E, D, H), dtype=jnp.float32) / np.float32(np.sqrt(D))
        w2 = jax.random.normal(k4, (E, H, D), dtype=jnp.float32) / np.float32(np.sqrt(H))
        return {'inputs': inputs, 'gate_w': gate_w, 'w1': w1, 'w2': w2}
    _L2_ffn_all = _L2_ffn_setup()
    _L2_ffn_in = {k: v for k, v in _L2_ffn_all.items() if k in ('gate_w', 'w1', 'w2')}
    del _L2_ffn_all

    def _L3_xattn_setup():
        import jax, jax.numpy as jnp
        import numpy as np
        B, N, M = (4, 256, 256)
        DIM = 128
        HEADS = 16
        DIM_HEAD = 64
        INNER = HEADS * DIM_HEAD
        SCALE = 8.0

        def layer_norm(x, g, eps=1e-05):
            mean = jnp.mean(x, axis=-1, keepdims=True)
            var = jnp.mean((x - mean) ** 2, axis=-1, keepdims=True)
            return (x - mean) * jax.lax.rsqrt(var + eps) * g

        def l2norm(t, eps=1e-12):
            n = jnp.maximum(jnp.linalg.norm(t, axis=-1, keepdims=True), eps)
            return t / n
        key = jax.random.key(seed)
        ks = jax.random.split(key, 8)
        x = jax.random.normal(ks[0], (B, N, DIM), dtype=jnp.float32)
        context = jax.random.normal(ks[1], (B, M, DIM), dtype=jnp.float32)
        g_norm = jnp.ones((DIM,), dtype=jnp.float32)
        null_kv = jax.random.normal(ks[2], (2, DIM_HEAD), dtype=jnp.float32)
        Wq = jax.random.normal(ks[3], (DIM, INNER), dtype=jnp.float32) / np.sqrt(DIM)
        Wkv = jax.random.normal(ks[4], (DIM, 2 * INNER), dtype=jnp.float32) / np.sqrt(DIM)
        q_scale = jnp.ones((DIM_HEAD,), dtype=jnp.float32)
        k_scale = jnp.ones((DIM_HEAD,), dtype=jnp.float32)
        Wout = jax.random.normal(ks[5], (INNER, DIM), dtype=jnp.float32) / np.sqrt(INNER)
        g_out = jnp.ones((DIM,), dtype=jnp.float32)
        return {'x': x, 'context': context, 'g_norm': g_norm, 'null_kv': null_kv, 'Wq': Wq, 'Wkv': Wkv, 'q_scale': q_scale, 'k_scale': k_scale, 'Wout': Wout, 'g_out': g_out}
    _L3_xattn_all = _L3_xattn_setup()
    _L3_xattn_in = {k: v for k, v in _L3_xattn_all.items() if k in ('g_norm', 'null_kv', 'Wq', 'Wkv', 'q_scale', 'k_scale', 'Wout', 'g_out')}
    del _L3_xattn_all

    def _L3_attn_setup():
        import jax, jax.numpy as jnp
        import numpy as np
        DIM_Q = 128
        DIM_K = 128
        DIM_V = 128
        OUT_DIM = 128
        B, N = (4, 256)

        def _layer_norm(h, gamma, beta, eps=1e-05):
            mu = jnp.mean(h, axis=-1, keepdims=True)
            var = jnp.mean(jnp.square(h - mu), axis=-1, keepdims=True)
            return (h - mu) * jax.lax.rsqrt(var + eps) * gamma + beta
        key = jax.random.key(seed)
        ks = jax.random.split(key, 8)
        s_in = 1.0 / np.sqrt(DIM_Q)
        s_v = 1.0 / np.sqrt(DIM_V)
        return {'x': jax.random.normal(ks[0], (B, N, DIM_Q), dtype=jnp.float32), 'Wq': jax.random.normal(ks[1], (DIM_Q, DIM_K), dtype=jnp.float32) * s_in, 'Wk': jax.random.normal(ks[2], (DIM_Q, DIM_K), dtype=jnp.float32) * s_in, 'Wv': jax.random.normal(ks[3], (DIM_Q, DIM_V), dtype=jnp.float32) * s_in, 'Wfc': jax.random.normal(ks[4], (DIM_V, OUT_DIM), dtype=jnp.float32) * s_v, 'bfc': jax.random.normal(ks[5], (OUT_DIM,), dtype=jnp.float32) * 0.02, 'gamma': jnp.ones((DIM_V,), dtype=jnp.float32), 'beta': jnp.zeros((DIM_V,), dtype=jnp.float32)}
    _L3_attn_all = _L3_attn_setup()
    _L3_attn_in = {k: v for k, v in _L3_attn_all.items() if k in ('Wq', 'Wk', 'Wv', 'Wfc', 'bfc', 'gamma', 'beta')}
    del _L3_attn_all

    def _L3_ffn_setup():
        import jax, jax.numpy as jnp
        import numpy as np
        from jax import lax
        DIM = 128
        INTER = 64
        N_EXPERTS = 16
        TOPK = 4
        ROUTE_SCALE = 2.5
        VOCAB = 4000

        def _silu_and_mul(gu):
            gate, up = jnp.split(gu, 2, axis=-1)
            return jax.nn.silu(gate) * up
        key = jax.random.key(seed)
        ks = jax.random.split(key, 8)
        x = jax.random.normal(ks[0], (2, 64, DIM), dtype=jnp.float32)
        input_ids = jax.random.randint(ks[1], (2, 64), 0, VOCAB)
        s = 0.02
        gate_w = jax.random.normal(ks[2], (N_EXPERTS, DIM), dtype=jnp.float32) * s
        gate_b = jax.random.normal(ks[3], (N_EXPERTS,), dtype=jnp.float32) * s
        w13 = jax.random.normal(ks[4], (N_EXPERTS, 2 * INTER, DIM), dtype=jnp.float32) * s
        w2 = jax.random.normal(ks[5], (N_EXPERTS, DIM, INTER), dtype=jnp.float32) * s
        w13_s = jax.random.normal(ks[6], (2 * INTER, DIM), dtype=jnp.float32) * s
        w2_s = jax.random.normal(ks[7], (DIM, INTER), dtype=jnp.float32) * s
        return {'x': x, 'input_ids': input_ids, 'gate_w': gate_w, 'gate_b': gate_b, 'w13': w13, 'w2': w2, 'w13_s': w13_s, 'w2_s': w2_s}
    _L3_ffn_all = _L3_ffn_setup()
    _L3_ffn_in = {k: v for k, v in _L3_ffn_all.items() if k in ('input_ids', 'gate_w', 'gate_b', 'w13', 'w2', 'w13_s', 'w2_s')}
    del _L3_ffn_all
    return {'x': x, 'ctx_1024': ctx_1024, 'mask_SxS2_bk1': mask_SxS2_bk1, 'L0_xattn_Wq': _L0_xattn_in['Wq'], 'L0_xattn_bq': _L0_xattn_in['bq'], 'L0_xattn_Wk': _L0_xattn_in['Wk'], 'L0_xattn_bk': _L0_xattn_in['bk'], 'L0_xattn_Wv': _L0_xattn_in['Wv'], 'L0_xattn_bv': _L0_xattn_in['bv'], 'L0_xattn_Wo': _L0_xattn_in['Wo'], 'L0_xattn_bo': _L0_xattn_in['bo'], 'L0_attn_ln_g': _L0_attn_in['ln_g'], 'L0_attn_ln_b': _L0_attn_in['ln_b'], 'L0_attn_w1_w': _L0_attn_in['w1_w'], 'L0_attn_w1_b': _L0_attn_in['w1_b'], 'L0_attn_v1_w': _L0_attn_in['v1_w'], 'L0_attn_v1_b': _L0_attn_in['v1_b'], 'L0_attn_w2_w': _L0_attn_in['w2_w'], 'L0_attn_w2_b': _L0_attn_in['w2_b'], 'L0_attn_conv_w': _L0_attn_in['conv_w'], 'L0_attn_A_log': _L0_attn_in['A_log'], 'L0_attn_D_skip': _L0_attn_in['D_skip'], 'L0_attn_W_dt': _L0_attn_in['W_dt'], 'L0_attn_b_dt': _L0_attn_in['b_dt'], 'L0_attn_W_B': _L0_attn_in['W_B'], 'L0_attn_W_C': _L0_attn_in['W_C'], 'L0_ffn_Wg': _L0_ffn_in['Wg'], 'L0_ffn_W1': _L0_ffn_in['W1'], 'L0_ffn_b1': _L0_ffn_in['b1'], 'L0_ffn_W2': _L0_ffn_in['W2'], 'L0_ffn_b2': _L0_ffn_in['b2'], 'L1_xattn_Wq': _L1_xattn_in['Wq'], 'L1_xattn_Wk': _L1_xattn_in['Wk'], 'L1_xattn_Wv': _L1_xattn_in['Wv'], 'L1_xattn_wq_h': _L1_xattn_in['wq_h'], 'L1_xattn_bq_h': _L1_xattn_in['bq_h'], 'L1_xattn_wk_h': _L1_xattn_in['wk_h'], 'L1_xattn_bk_h': _L1_xattn_in['bk_h'], 'L1_xattn_wv_h': _L1_xattn_in['wv_h'], 'L1_xattn_bv_h': _L1_xattn_in['bv_h'], 'L1_xattn_Wo': _L1_xattn_in['Wo'], 'L1_attn_Wqkv': _L1_attn_in['Wqkv'], 'L1_attn_bqkv': _L1_attn_in['bqkv'], 'L1_attn_Wproj': _L1_attn_in['Wproj'], 'L1_attn_bproj': _L1_attn_in['bproj'], 'L1_ffn_W_base': _L1_ffn_in['W_base'], 'L1_ffn_b_base': _L1_ffn_in['b_base'], 'L1_ffn_W_enc': _L1_ffn_in['W_enc'], 'L1_ffn_b_enc': _L1_ffn_in['b_enc'], 'L1_ffn_W_dec': _L1_ffn_in['W_dec'], 'L1_ffn_b_dec': _L1_ffn_in['b_dec'], 'L1_ffn_W_down': _L1_ffn_in['W_down'], 'L1_ffn_b_down': _L1_ffn_in['b_down'], 'L1_ffn_W_up': _L1_ffn_in['W_up'], 'L1_ffn_b_up': _L1_ffn_in['b_up'], 'L1_ffn_connected_idx': _L1_ffn_in['connected_idx'], 'L2_xattn_Wq': _L2_xattn_in['Wq'], 'L2_xattn_bq': _L2_xattn_in['bq'], 'L2_xattn_Wk': _L2_xattn_in['Wk'], 'L2_xattn_bk': _L2_xattn_in['bk'], 'L2_xattn_Wv': _L2_xattn_in['Wv'], 'L2_xattn_bv': _L2_xattn_in['bv'], 'L2_attn_W_in': _L2_attn_in['W_in'], 'L2_attn_b_in': _L2_attn_in['b_in'], 'L2_attn_B_mat': _L2_attn_in['B_mat'], 'L2_attn_C_mat': _L2_attn_in['C_mat'], 'L2_attn_W_B': _L2_attn_in['W_B'], 'L2_attn_b_B': _L2_attn_in['b_B'], 'L2_attn_W_D': _L2_attn_in['W_D'], 'L2_attn_b_D': _L2_attn_in['b_D'], 'L2_attn_W_out': _L2_attn_in['W_out'], 'L2_attn_b_out': _L2_attn_in['b_out'], 'L2_attn_W_ig': _L2_attn_in['W_ig'], 'L2_attn_b_ig': _L2_attn_in['b_ig'], 'L2_attn_W_fg': _L2_attn_in['W_fg'], 'L2_attn_b_fg': _L2_attn_in['b_fg'], 'L2_attn_gamma': _L2_attn_in['gamma'], 'L2_attn_beta': _L2_attn_in['beta'], 'L2_ffn_gate_w': _L2_ffn_in['gate_w'], 'L2_ffn_w1': _L2_ffn_in['w1'], 'L2_ffn_w2': _L2_ffn_in['w2'], 'L3_xattn_g_norm': _L3_xattn_in['g_norm'], 'L3_xattn_null_kv': _L3_xattn_in['null_kv'], 'L3_xattn_Wq': _L3_xattn_in['Wq'], 'L3_xattn_Wkv': _L3_xattn_in['Wkv'], 'L3_xattn_q_scale': _L3_xattn_in['q_scale'], 'L3_xattn_k_scale': _L3_xattn_in['k_scale'], 'L3_xattn_Wout': _L3_xattn_in['Wout'], 'L3_xattn_g_out': _L3_xattn_in['g_out'], 'L3_attn_Wq': _L3_attn_in['Wq'], 'L3_attn_Wk': _L3_attn_in['Wk'], 'L3_attn_Wv': _L3_attn_in['Wv'], 'L3_attn_Wfc': _L3_attn_in['Wfc'], 'L3_attn_bfc': _L3_attn_in['bfc'], 'L3_attn_gamma': _L3_attn_in['gamma'], 'L3_attn_beta': _L3_attn_in['beta'], 'L3_ffn_input_ids': _L3_ffn_in['input_ids'], 'L3_ffn_gate_w': _L3_ffn_in['gate_w'], 'L3_ffn_gate_b': _L3_ffn_in['gate_b'], 'L3_ffn_w13': _L3_ffn_in['w13'], 'L3_ffn_w2': _L3_ffn_in['w2'], 'L3_ffn_w13_s': _L3_ffn_in['w13_s'], 'L3_ffn_w2_s': _L3_ffn_in['w2_s']}

def reference(x, ctx_1024, mask_SxS2_bk1, L0_xattn_Wq, L0_xattn_bq, L0_xattn_Wk, L0_xattn_bk, L0_xattn_Wv, L0_xattn_bv, L0_xattn_Wo, L0_xattn_bo, L0_attn_ln_g, L0_attn_ln_b, L0_attn_w1_w, L0_attn_w1_b, L0_attn_v1_w, L0_attn_v1_b, L0_attn_w2_w, L0_attn_w2_b, L0_attn_conv_w, L0_attn_A_log, L0_attn_D_skip, L0_attn_W_dt, L0_attn_b_dt, L0_attn_W_B, L0_attn_W_C, L0_ffn_Wg, L0_ffn_W1, L0_ffn_b1, L0_ffn_W2, L0_ffn_b2, L1_xattn_Wq, L1_xattn_Wk, L1_xattn_Wv, L1_xattn_wq_h, L1_xattn_bq_h, L1_xattn_wk_h, L1_xattn_bk_h, L1_xattn_wv_h, L1_xattn_bv_h, L1_xattn_Wo, L1_attn_Wqkv, L1_attn_bqkv, L1_attn_Wproj, L1_attn_bproj, L1_ffn_W_base, L1_ffn_b_base, L1_ffn_W_enc, L1_ffn_b_enc, L1_ffn_W_dec, L1_ffn_b_dec, L1_ffn_W_down, L1_ffn_b_down, L1_ffn_W_up, L1_ffn_b_up, L1_ffn_connected_idx, L2_xattn_Wq, L2_xattn_bq, L2_xattn_Wk, L2_xattn_bk, L2_xattn_Wv, L2_xattn_bv, L2_attn_W_in, L2_attn_b_in, L2_attn_B_mat, L2_attn_C_mat, L2_attn_W_B, L2_attn_b_B, L2_attn_W_D, L2_attn_b_D, L2_attn_W_out, L2_attn_b_out, L2_attn_W_ig, L2_attn_b_ig, L2_attn_W_fg, L2_attn_b_fg, L2_attn_gamma, L2_attn_beta, L2_ffn_gate_w, L2_ffn_w1, L2_ffn_w2, L3_xattn_g_norm, L3_xattn_null_kv, L3_xattn_Wq, L3_xattn_Wkv, L3_xattn_q_scale, L3_xattn_k_scale, L3_xattn_Wout, L3_xattn_g_out, L3_attn_Wq, L3_attn_Wk, L3_attn_Wv, L3_attn_Wfc, L3_attn_bfc, L3_attn_gamma, L3_attn_beta, L3_ffn_input_ids, L3_ffn_gate_w, L3_ffn_gate_b, L3_ffn_w13, L3_ffn_w2, L3_ffn_w13_s, L3_ffn_w2_s):
    import jax
    import jax.numpy as jnp

    def _L0_xattn_ref(hidden_states, key_value_states, Wq, bq, Wk, bk, Wv, bv, Wo, bo, stride):
        import jax, jax.numpy as jnp
        import numpy as np
        E = 128
        H = 16
        D = E // H
        B, Tq, _ = hidden_states.shape
        Tk = key_value_states.shape[1]
        scaling = D ** (-0.5)
        Q = (hidden_states @ Wq.T + bq).reshape(B, Tq, H, D).transpose(0, 2, 1, 3)
        K = (key_value_states @ Wk.T + bk).reshape(B, Tk, H, D).transpose(0, 2, 1, 3)
        V = (key_value_states @ Wv.T + bv).reshape(B, Tk, H, D).transpose(0, 2, 1, 3)
        m = Tk // stride
        idx = jnp.arange(H)[:, None] + stride * jnp.arange(m)[None, :]
        gather = idx[None, :, :, None]
        Kg = jnp.take_along_axis(K, gather, axis=2)
        Vg = jnp.take_along_axis(V, gather, axis=2)
        scores = jnp.einsum('bhqd,bhkd->bhqk', Q, Kg) * scaling
        attn = jax.nn.softmax(scores, axis=-1)
        out = jnp.einsum('bhqk,bhkd->bhqd', attn, Vg)
        out = out.transpose(0, 2, 1, 3).reshape(B, Tq, E)
        return out @ Wo.T + bo

    def _L0_attn_ref(x, ln_g, ln_b, w1_w, w1_b, v1_w, v1_b, w2_w, w2_b, conv_w, A_log, D_skip, W_dt, b_dt, W_B, W_C):
        import jax, jax.numpy as jnp
        import numpy as np
        B, L, D, N = (4, 256, 128, 16)

        def _layernorm(x, g, b, eps=1e-05):
            mu = jnp.mean(x, axis=-1, keepdims=True)
            var = jnp.mean(jnp.square(x - mu), axis=-1, keepdims=True)
            return (x - mu) * jax.lax.rsqrt(var + eps) * g + b

        def _silu(x):
            return x * jax.nn.sigmoid(x)

        def _depthwise_conv(x, w):
            xc = x.transpose(0, 2, 1)
            y = jax.lax.conv_general_dilated(xc, w, window_strides=(1,), padding=[(1, 1)], feature_group_count=xc.shape[1], dimension_numbers=('NCH', 'OIH', 'NCH'))
            return y.transpose(0, 2, 1)

        def _selective_scan(u, A_log, D_skip, W_dt, b_dt, W_B, W_C):
            A = -jnp.exp(A_log)
            dt = jax.nn.softplus(u @ W_dt + b_dt)
            Bt = u @ W_B
            Ct = u @ W_C

            def step(h, inp):
                dt_t, B_t, C_t, u_t = inp
                dA = jnp.exp(dt_t[..., None] * A)
                h = dA * h + (dt_t * u_t)[..., None] * B_t[:, None, :]
                y = jnp.einsum('bdn,bn->bd', h, C_t)
                return (h, y)
            h0 = jnp.zeros((u.shape[0], u.shape[2], A.shape[1]), u.dtype)
            xs = (dt.transpose(1, 0, 2), Bt.transpose(1, 0, 2), Ct.transpose(1, 0, 2), u.transpose(1, 0, 2))
            _, ys = jax.lax.scan(step, h0, xs)
            return ys.transpose(1, 0, 2) + u * D_skip
        x_norm = _layernorm(x, ln_g, ln_b)
        x1 = x_norm @ w1_w + w1_b
        x_conv = _silu(_depthwise_conv(x1, conv_w))
        x_ssm = _selective_scan(x_conv, A_log, D_skip, W_dt, b_dt, W_B, W_C)
        v = _silu(x_norm @ v1_w + v1_b)
        return x_ssm * v @ w2_w + w2_b

    def _L0_ffn_ref(x, Wg, W1, b1, W2, b2):
        import jax, jax.numpy as jnp
        import numpy as np
        D_MODEL, D_FF, N_EXPERTS, TOP_K = (128, 512, 8, 2)
        B = x.shape[:-1]
        xs = x.reshape(-1, x.shape[-1])
        T = xs.shape[0]
        gate_logits = xs @ Wg
        weights, sel = jax.lax.top_k(gate_logits, TOP_K)
        weights = jax.nn.softmax(weights.astype(jnp.float32), axis=1).astype(x.dtype)
        h = jax.nn.relu(jnp.einsum('td,edf->etf', xs, W1) + b1[:, None, :])
        out_e = jnp.einsum('etf,efd->etd', h, W2) + b2[:, None, :]
        tok = jnp.arange(T)
        picked = out_e[sel, tok[:, None]]
        out = jnp.einsum('tk,tkd->td', weights, picked)
        return out.reshape(*B, x.shape[-1])

    def _L1_xattn_ref(query, key, value, mask, Wq, Wk, Wv, wq_h, bq_h, wk_h, bk_h, wv_h, bv_h, Wo):
        import jax, jax.numpy as jnp
        import numpy as np
        B, S, D, H = (4, 256, 128, 16)
        HD = D // H
        q = jnp.einsum('bsd,de->bse', query, Wq)
        k = jnp.einsum('bsd,de->bse', key, Wk)
        v = jnp.einsum('bsd,de->bse', value, Wv)
        qh = jnp.einsum('bsd,dh->bsh', q, wq_h) + bq_h
        kh = jnp.einsum('bsd,dh->bsh', k, wk_h) + bk_h
        vh = jnp.einsum('bsd,dh->bsh', v, wv_h) + bv_h
        scores = jnp.einsum('bsh,bth->bst', qh, kh) / jnp.sqrt(jnp.float32(HD))
        scores = jnp.where(mask, jnp.float32(-1000000000.0), scores)
        attn = jax.nn.softmax(scores, axis=-1)
        out_h = jnp.einsum('bst,bth->bsh', attn, vh)
        out = jnp.tile(out_h, (1, 1, H))
        return jnp.einsum('bsd,de->bse', out, Wo)

    def _L1_attn_ref(x, Wqkv, bqkv, Wproj, bproj):
        import jax, jax.numpy as jnp
        import numpy as np
        B, T, C = x.shape
        n_head = 16
        hd = C // n_head
        x_proj = x @ Wqkv + bqkv
        q = x_proj[:, :, :C].reshape(B, n_head, T, hd)
        k = x_proj[:, :, C:2 * C].reshape(B, n_head, T, hd)
        v = x_proj[:, :, 2 * C:].reshape(B, n_head, T, hd)
        att = jnp.einsum('bhtd,bhsd->bhts', q, k) * (1.0 / jnp.sqrt(jnp.float32(hd)))
        causal = jnp.tril(jnp.ones((T, T), dtype=bool))
        att = jnp.where(causal, att, jnp.float32(-jnp.inf))
        att = jax.nn.softmax(att, axis=-1)
        y = att @ v
        y = jnp.transpose(y, (0, 2, 1, 3)).reshape(B, T, C)
        return y @ Wproj + bproj

    def _L1_ffn_ref(x, W_base, b_base, W_enc, b_enc, W_dec, b_dec, W_down, b_down, W_up, b_up, connected_idx):
        import jax, jax.numpy as jnp
        import numpy as np
        B, T, D, H, R, N = (16, 128, 128, 32, 64, 8)
        base = jnp.einsum('btd,de->bte', x, W_base) + b_base
        h = jax.nn.relu(jnp.einsum('btd,ndh->nbth', x, W_enc) + b_enc[:, None, None, :])
        recon = jnp.einsum('nbth,nhd->nbtd', h, W_dec) + b_dec[:, None, None, :]
        losses = jnp.mean((recon - x[None]) ** 2, axis=(2, 3))
        top1 = jnp.argmin(losses, axis=0)
        adp = connected_idx[top1]
        Wd, bd = (W_down[adp], b_down[adp])
        Wu, bu = (W_up[adp], b_up[adp])
        mid = jax.nn.relu(jnp.einsum('btd,bdr->btr', x, Wd) + bd[:, None, :])
        adapter_out = jnp.einsum('btr,brd->btd', mid, Wu) + bu[:, None, :]
        return base + adapter_out

    def _L2_xattn_ref(q, k, v, Wq, bq, Wk, bk, Wv, bv):
        import jax, jax.numpy as jnp
        import numpy as np
        import math
        B, SQ, SK, D = (4, 256, 256, 128)
        qp = jnp.einsum('bsd,ed->bse', q, Wq) + bq
        kp = jnp.einsum('bsd,ed->bse', k, Wk) + bk
        vp = jnp.einsum('bsd,ed->bse', v, Wv) + bv
        scale = 1.0 / jnp.sqrt(jnp.asarray(kp.shape[-1], qp.dtype))
        scores = jnp.einsum('bqd,bkd->bqk', qp, kp) * scale
        attn = jax.nn.softmax(scores, axis=-1)
        return jnp.einsum('bqk,bkd->bqd', attn, vp)

    def _L2_attn_ref(x, W_in, b_in, B_mat, C_mat, W_B, b_B, W_D, b_D, W_out, b_out, W_ig, b_ig, W_fg, b_fg, gamma, beta):
        import jax, jax.numpy as jnp
        import numpy as np
        B, T, H, S = (8, 512, 128, 16)
        LN_EPS = 1e-05

        def _forward(x, W_in, b_in, B_mat, C_mat, W_B, b_B, W_D, b_D, W_out, b_out, W_ig, b_ig, W_fg, b_fg, gamma, beta):
            xp = x @ W_in + b_in
            Bx = (xp @ W_B + b_B) @ B_mat
            ig = jax.nn.sigmoid(xp @ W_ig + b_ig)
            fg = jax.nn.sigmoid(xp @ W_fg + b_fg)

            def step(h, inp):
                fg_t, ig_t, bx_t = inp
                h = fg_t * h + ig_t * bx_t
                return (h, h)
            h0 = jnp.zeros((xp.shape[0], B_mat.shape[1]), xp.dtype)
            xs = (jnp.swapaxes(fg, 0, 1), jnp.swapaxes(ig, 0, 1), jnp.swapaxes(Bx, 0, 1))
            _, hs = jax.lax.scan(step, h0, xs)
            hs = jnp.swapaxes(hs, 0, 1)
            y = jnp.tanh(hs @ C_mat + (xp @ W_D + b_D))
            y = y @ W_out + b_out + xp
            mu = jnp.mean(y, axis=-1, keepdims=True)
            var = jnp.var(y, axis=-1, keepdims=True)
            y = (y - mu) * jax.lax.rsqrt(var + LN_EPS) * gamma + beta
            return y
        return _forward(x, W_in, b_in, B_mat, C_mat, W_B, b_B, W_D, b_D, W_out, b_out, W_ig, b_ig, W_fg, b_fg, gamma, beta)

    def _L2_ffn_ref(inputs, gate_w, w1, w2):
        import jax, jax.numpy as jnp
        import numpy as np
        CAPACITY_FACTOR = 1.25
        orig_shape = inputs.shape
        D = orig_shape[-1]
        tokens = inputs.reshape(-1, D)
        T = tokens.shape[0]
        E = gate_w.shape[0]
        C = int(CAPACITY_FACTOR * T / E)
        logits = tokens @ gate_w.T
        probs = jax.nn.softmax(logits, axis=-1)
        expert_idx = jnp.argmax(probs, axis=-1)
        mask = jax.nn.one_hot(expert_idx, E, dtype=jnp.int32)
        locations = jnp.cumsum(mask, axis=0) - 1
        mask = mask * (locations < C)
        loc_oh = jax.nn.one_hot(locations, C, dtype=probs.dtype)
        sec_mask = mask[:, :, None].astype(probs.dtype) * loc_oh
        combine_weights = probs[:, :, None] * sec_mask
        dispatch = jnp.einsum('tec,td->ecd', sec_mask, tokens)
        h = jax.nn.relu(jnp.einsum('ecd,edh->ech', dispatch, w1))
        expert_out = jnp.einsum('ech,ehd->ecd', h, w2)
        ans = jnp.einsum('tec,ecd->td', combine_weights, expert_out)
        return ans.reshape(orig_shape)

    def _L3_xattn_ref(x, context, g_norm, null_kv, Wq, Wkv, q_scale, k_scale, Wout, g_out):
        import jax, jax.numpy as jnp
        import numpy as np
        B, N, M = (4, 256, 256)
        DIM = 128
        HEADS = 16
        DIM_HEAD = 64
        INNER = HEADS * DIM_HEAD
        SCALE = 8.0

        def layer_norm(x, g, eps=1e-05):
            mean = jnp.mean(x, axis=-1, keepdims=True)
            var = jnp.mean((x - mean) ** 2, axis=-1, keepdims=True)
            return (x - mean) * jax.lax.rsqrt(var + eps) * g

        def l2norm(t, eps=1e-12):
            n = jnp.maximum(jnp.linalg.norm(t, axis=-1, keepdims=True), eps)
            return t / n
        b = x.shape[0]
        xn = layer_norm(x, g_norm)
        ctx = context
        q = xn @ Wq
        kv = ctx @ Wkv
        k, v = jnp.split(kv, 2, axis=-1)
        split_heads = lambda t: t.reshape(b, t.shape[1], HEADS, DIM_HEAD).transpose(0, 2, 1, 3)
        q, k, v = map(split_heads, (q, k, v))
        nk = jnp.broadcast_to(null_kv[0], (b, HEADS, 1, DIM_HEAD))
        nv = jnp.broadcast_to(null_kv[1], (b, HEADS, 1, DIM_HEAD))
        k = jnp.concatenate([nk, k], axis=2)
        v = jnp.concatenate([nv, v], axis=2)
        q = l2norm(q) * q_scale
        k = l2norm(k) * k_scale
        sim = jnp.einsum('bhid,bhjd->bhij', q, k) * SCALE
        attn = jax.nn.softmax(sim.astype(jnp.float32), axis=-1).astype(sim.dtype)
        out = jnp.einsum('bhij,bhjd->bhid', attn, v)
        out = out.transpose(0, 2, 1, 3).reshape(b, -1, INNER)
        out = out @ Wout
        return layer_norm(out, g_out)

    def _L3_attn_ref(x, Wq, Wk, Wv, Wfc, bfc, gamma, beta):
        import jax, jax.numpy as jnp
        import numpy as np
        DIM_Q = 128
        DIM_K = 128
        DIM_V = 128
        OUT_DIM = 128
        B, N = (4, 256)

        def _layer_norm(h, gamma, beta, eps=1e-05):
            mu = jnp.mean(h, axis=-1, keepdims=True)
            var = jnp.mean(jnp.square(h - mu), axis=-1, keepdims=True)
            return (h - mu) * jax.lax.rsqrt(var + eps) * gamma + beta
        q = jnp.einsum('bnd,dk->bnk', x, Wq)
        k = jnp.einsum('bnd,dk->bnk', x, Wk)
        v = jnp.einsum('bnd,dv->bnv', x, Wv)
        scale = 1.0 / np.sqrt(DIM_K)
        scores = jnp.einsum('bnk,bmk->bnm', q, k) * scale
        n = x.shape[1]
        causal = jnp.tril(jnp.ones((n, n), dtype=bool))
        scores = jnp.where(causal, scores, -jnp.inf)
        att = jax.nn.softmax(scores, axis=-1)
        out = jnp.einsum('bnm,bmv->bnv', att, v)
        out = _layer_norm(out + v, gamma, beta)
        return jnp.einsum('bnv,vo->bno', out, Wfc) + bfc

    def _L3_ffn_ref(x, input_ids, gate_w, gate_b, w13, w2, w13_s, w2_s):
        import jax, jax.numpy as jnp
        import numpy as np
        from jax import lax
        DIM = 128
        INTER = 64
        N_EXPERTS = 16
        TOPK = 4
        ROUTE_SCALE = 2.5
        VOCAB = 4000

        def _silu_and_mul(gu):
            gate, up = jnp.split(gu, 2, axis=-1)
            return jax.nn.silu(gate) * up
        B, S, D = x.shape
        xt = x.reshape(-1, D)
        T = xt.shape[0]
        scores = jax.nn.sigmoid(xt.astype(jnp.float32) @ gate_w.T)
        biased = scores + gate_b
        _, idx = lax.top_k(biased, TOPK)
        w = jnp.take_along_axis(scores, idx, axis=-1)
        w = w / jnp.sum(w, axis=-1, keepdims=True)
        w = w * ROUTE_SCALE
        comb = jnp.zeros((T, N_EXPERTS), jnp.float32)
        comb = comb.at[jnp.arange(T)[:, None], idx].add(w)
        comb = comb.astype(x.dtype)

        def expert_body(y, args):
            w13_e, w2_e, c_e = args
            h = _silu_and_mul(xt @ w13_e.T)
            return (y + c_e[:, None] * (h @ w2_e.T), None)
        y, _ = lax.scan(expert_body, jnp.zeros_like(xt), (w13, w2, comb.T))
        y = y + _silu_and_mul(xt @ w13_s.T) @ w2_s.T
        return y.astype(x.dtype).reshape(B, S, D)
    x = x + _L0_xattn_ref(_layernorm(x, axis=-1), ctx_1024, L0_xattn_Wq, L0_xattn_bq, L0_xattn_Wk, L0_xattn_bk, L0_xattn_Wv, L0_xattn_bv, L0_xattn_Wo, L0_xattn_bo, 16)
    x = x + _L0_attn_ref(_layernorm(x, axis=-1), L0_attn_ln_g, L0_attn_ln_b, L0_attn_w1_w, L0_attn_w1_b, L0_attn_v1_w, L0_attn_v1_b, L0_attn_w2_w, L0_attn_w2_b, L0_attn_conv_w, L0_attn_A_log, L0_attn_D_skip, L0_attn_W_dt, L0_attn_b_dt, L0_attn_W_B, L0_attn_W_C)
    x = x + _L0_ffn_ref(_layernorm(x, axis=-1), L0_ffn_Wg, L0_ffn_W1, L0_ffn_b1, L0_ffn_W2, L0_ffn_b2)
    x = x + _L1_xattn_ref(_layernorm(x, axis=-1), ctx_1024, ctx_1024, mask_SxS2_bk1, L1_xattn_Wq, L1_xattn_Wk, L1_xattn_Wv, L1_xattn_wq_h, L1_xattn_bq_h, L1_xattn_wk_h, L1_xattn_bk_h, L1_xattn_wv_h, L1_xattn_bv_h, L1_xattn_Wo)
    x = x + _L1_attn_ref(_layernorm(x, axis=-1), L1_attn_Wqkv, L1_attn_bqkv, L1_attn_Wproj, L1_attn_bproj)
    x = x + _L1_ffn_ref(_layernorm(x, axis=-1), L1_ffn_W_base, L1_ffn_b_base, L1_ffn_W_enc, L1_ffn_b_enc, L1_ffn_W_dec, L1_ffn_b_dec, L1_ffn_W_down, L1_ffn_b_down, L1_ffn_W_up, L1_ffn_b_up, L1_ffn_connected_idx)
    x = x + _L2_xattn_ref(_layernorm(x, axis=-1), ctx_1024, ctx_1024, L2_xattn_Wq, L2_xattn_bq, L2_xattn_Wk, L2_xattn_bk, L2_xattn_Wv, L2_xattn_bv)
    x = x + _L2_attn_ref(_layernorm(x, axis=-1), L2_attn_W_in, L2_attn_b_in, L2_attn_B_mat, L2_attn_C_mat, L2_attn_W_B, L2_attn_b_B, L2_attn_W_D, L2_attn_b_D, L2_attn_W_out, L2_attn_b_out, L2_attn_W_ig, L2_attn_b_ig, L2_attn_W_fg, L2_attn_b_fg, L2_attn_gamma, L2_attn_beta)
    x = x + _L2_ffn_ref(_layernorm(x, axis=-1), L2_ffn_gate_w, L2_ffn_w1, L2_ffn_w2)
    x = x + _L3_xattn_ref(_layernorm(x, axis=-1), ctx_1024, L3_xattn_g_norm, L3_xattn_null_kv, L3_xattn_Wq, L3_xattn_Wkv, L3_xattn_q_scale, L3_xattn_k_scale, L3_xattn_Wout, L3_xattn_g_out)
    x = x + _L3_attn_ref(_layernorm(x, axis=-1), L3_attn_Wq, L3_attn_Wk, L3_attn_Wv, L3_attn_Wfc, L3_attn_bfc, L3_attn_gamma, L3_attn_beta)
    x = x + _L3_ffn_ref(_layernorm(x, axis=-1), L3_ffn_input_ids, L3_ffn_gate_w, L3_ffn_gate_b, L3_ffn_w13, L3_ffn_w2, L3_ffn_w13_s, L3_ffn_w2_s)
    return x

_drawn_inputs = setup_inputs


def setup_inputs(seed=0):
    import zlib

    import numpy as np

    out = dict(_drawn_inputs(seed))
    spreads = {'L0_xattn_bq': (0.0, 0.8),
     'L0_xattn_bk': (0.0, 0.8),
     'L0_xattn_bv': (0.0, 0.272),
     'L0_xattn_bo': (0.0, 0.1),
     'L0_attn_ln_g': (1.0, 0.2),
     'L0_attn_ln_b': (0.0, 0.1),
     'L0_attn_w1_b': (0.0, 0.1),
     'L0_attn_v1_b': (0.0, 0.1),
     'L0_attn_w2_b': (0.0, 0.1),
     'L0_attn_D_skip': (1.0, 0.2),
     'L0_attn_b_dt': (-4.0, 0.6),
     'L0_ffn_b1': (0.0, 0.402),
     'L0_ffn_b2': (0.0, 0.1),
     'L1_ffn_b_base': (0.0, 0.1),
     'L1_ffn_b_enc': (0.0, 0.1),
     'L1_ffn_b_dec': (0.0, 0.1),
     'L1_ffn_b_down': (0.0, 0.1),
     'L1_ffn_b_up': (0.0, 0.1),
     'L2_attn_b_in': (0.0, 0.1),
     'L2_attn_b_B': (0.0, 0.462),
     'L2_attn_b_D': (0.0, 0.303),
     'L2_attn_b_out': (0.0, 0.1),
     'L2_attn_b_ig': (0.0, 0.8),
     'L2_attn_b_fg': (0.0, 0.8),
     'L2_attn_gamma': (1.0, 0.2),
     'L2_attn_beta': (0.0, 0.1),
     'L3_xattn_g_norm': (1.0, 0.558),
     'L3_xattn_q_scale': (1.0, 0.547),
     'L3_xattn_k_scale': (1.0, 0.2),
     'L3_xattn_g_out': (1.0, 0.2),
     'L3_attn_gamma': (1.0, 0.2),
     'L3_attn_beta': (0.0, 0.1)}
    factors = {'L0_xattn_Wq': 8.0,
     'L0_xattn_Wk': 8.0,
     'L0_attn_W_dt': 8.0,
     'L1_xattn_bq_h': 3.918,
     'L1_xattn_bk_h': 8.0,
     'L1_attn_bqkv': 5.867,
     'L1_attn_bproj': 3.323,
     'L2_xattn_bq': 4.399,
     'L2_xattn_bk': 8.0,
     'L3_xattn_null_kv': 8.0,
     'L3_attn_bfc': 6.837,
     'L3_ffn_gate_w': 8.0,
     'L3_ffn_gate_b': 8.0,
     'L3_ffn_w13': 8.0,
     'L3_ffn_w2': 8.0,
     'L3_ffn_w13_s': 8.0,
     'L3_ffn_w2_s': 8.0}
    for name, (base, spread) in spreads.items():
        noise = np.random.default_rng([zlib.crc32(name.encode()), seed]).standard_normal(out[name].shape)
        drawn = base * np.exp(spread * noise) if base else spread * noise
        out[name] = jnp.asarray(drawn.astype(out[name].dtype))
    for name, factor in factors.items():
        out[name] = (out[name] * factor).astype(out[name].dtype)
    return out
```

```python
from contextlib import ExitStack

import concourse.bass as bass
import concourse.mybir as mybir
import numpy as np

F32 = mybir.dt.float32
BF16 = mybir.dt.bfloat16
I32 = mybir.dt.int32
U8 = mybir.dt.uint8
ALU = mybir.AluOpType
ACT = mybir.ActivationFunctionType
AX = mybir.AxisListType

P = 128
B = 4
T = B * P
S = 2048
NK = B * S
H = 16
HD = P // H
DH = 64
FF = 512
FC = FF // P
EPS = 1e-5
KEY_TILES = S // P
CAPACITY = int(1.25 * T / 16)
MASKED = -1.0e9
FAR = -1.0e30


class Engine:

    def __init__(self, engine):
        self.i, self.made, self.seen = engine, {}, {}

    def sends(self, signal):
        self.made[signal] = self.made.get(signal, 0) + 1
        return 1

    def sent(self, signal):
        return self.made[signal]

    def due(self, signal, n=1, lag=0):
        self.seen[signal] = self.seen.get(signal, 0) + n
        value = self.seen[signal] - lag
        if isinstance(value, int):
            value = max(value, 0)
        return value * 16 if signal.startswith("dma_") else value

    def loop(self, trips, made=(), seen=()):
        return _Loop(self, trips, dict(made), dict(seen))


class _Loop:

    def __init__(self, e, trips, made, seen):
        self.e, self.trips, self.per = e, trips, (made, seen)

    def __enter__(self):
        self.cm = self.e.i.Fori(0, self.trips)
        i = self.cm.__enter__()
        self.base = [{k: c.get(k, 0) for k in per} for c, per in zip((self.e.made, self.e.seen), self.per)]
        for c, per in zip((self.e.made, self.e.seen), self.per):
            for k, n in per.items():
                c[k] = c.get(k, 0) + i * n
        self.start = [dict(self.e.made), dict(self.e.seen)]
        self.i = i
        return i

    def __exit__(self, *a):
        self.cm.__exit__(*a)
        for c, per, base in zip((self.e.made, self.e.seen), self.per, self.base):
            for k, n in per.items():
                c[k] = base[k] + self.trips * n


def build(nc, d, cols, rows):
    with ExitStack() as ctx:
        def sb(name, shape, dt=F32):
            return ctx.enter_context(nc.sbuf_tensor(name, shape, dt))

        made = {}

        def sem(name):
            if name not in made:
                made[name] = ctx.enter_context(nc.semaphore(name))
            return made[name]

        n_a, n_b, n_c = (d[k].shape[1] for k in ("wa", "wb", "wc"))
        WA = sb("WA", [P, n_a])
        WB = sb("WB", [P, n_b])
        ROWS = sb("ROWS", [P, d["rows"].shape[1]])
        X = sb("X", [P, B, P])
        CT = sb("CT", [P, NK])
        CK = sb("CK", [P, B * KEY_TILES, P])
        ARENA = sb("ARENA", [P, 18432])
        EB = sb("EB", [P, 2, 2 * FF + FC])
        HN = sb("HN", [P, B, P])
        HT = sb("HT", [P, T])
        OT = sb("OT", [P, T])
        QT = sb("QT", [P, T])
        TMP = sb("TMP", [P, T])
        ACC = sb("ACC", [P, B, P])
        ST = sb("ST", [P, B, 6])
        MV = sb("MV", [P, B, 2])
        VE = sb("VE", [P, B])
        RSTD = sb("RSTD", [P, B])
        MHALF = sb("MHALF", [P, B])
        SM = sb("SM", [P, 1024])
        MASK8 = sb("MASK8", [P, S], U8)
        IDX = sb("IDX", [P, 8], I32)
        ONESB = sb("ONESB", [P, P], BF16)
        PSUM = ctx.enter_context(nc.psum_tensor("PSUM", [P, 8, 512], F32))

        WC = CK[:, :, :].rearrange("p a b -> p (a b)")[:, 0:n_c]
        SPARE = CK[:, :, :].rearrange("p a b -> p (a b)")[:, n_c:]

        def w(name, rows_=P):
            part, at, n = cols[name]
            return {"a": WA, "b": WB, "c": WC}[part][0:rows_, at:at + n]

        def row(name, off=0, n=None):
            at, m = rows[name]
            return ROWS[:, at + off:at + off + (n or m)]

        def bank(k, rows_=P):
            return PSUM[0:rows_, k, :]

        def bank4(k):
            return PSUM[:, k, :].rearrange("p (b f) -> p b f", b=B)

        def over(ap, n):
            return ap.unsqueeze(1).broadcast_to([ap.shape[0], n, ap.shape[1]])

        def each(ap, n):
            return ap.unsqueeze(2).broadcast_to([ap.shape[0], ap.shape[1], n])

        ident = w("ident")
        SP = Engine(nc.sync)
        PE = Engine(nc.tensor)
        AC = Engine(nc.scalar)
        DV = Engine(nc.vector)
        PO = Engine(nc.gpsimd)
        mm, tp = nc.tensor.matmul, nc.tensor.transpose
        act, ve = nc.scalar.activation, nc.vector

        def hT(b):
            return HT[:, b * P:(b + 1) * P]

        QS = ARENA[:, 0:8192]
        KS = ARENA[:, 8192:16384]
        SX = ARENA[:, 16384:17408].rearrange("p (k n) -> p k n", k=2)
        PT = ARENA[:, 17408:18432].rearrange("p (k n) -> p k n", k=2)
        L_SUM = SM[:, 0:B * H]
        L_INV = SM[:, 64:64 + B * H]
        MX = SM[:, 128:136].rearrange("p (k n) -> p k n", k=2)
        VS = SM[:, 512:1024]

        KT = ARENA[:, 0:NK]
        SL = ARENA[:, 8192:12288].rearrange("p (k n) -> p k n", k=2)
        PTL = ARENA[:, 12288:14336].rearrange("p (t n) -> p t n", t=KEY_TILES)
        KEEP = ARENA[:, 14336:16384]
        NEG = ARENA[:, 16384:18432]
        LMX, LNM, LSUM, LINV = (SM[:, k:k + B] for k in (160, 164, 168, 172))
        ZT = OT

        HB = ARENA[:, 0:4096].rearrange("p (k c n) -> p k c n", k=2, c=FC)
        GATE = SM[:, 192:192 + B * H]
        EACC = ACC

        CTB = CT[:, :].rearrange("p (b m s) -> p b s m", b=B, s=H)
        KSB = KS.rearrange("p (b m s) -> p b s m", b=B, s=H)
        QM = QS.rearrange("p (h n) -> p h n", h=H)

        N = 16
        CB = ARENA[:, 0:520].rearrange("p (b t) -> p b t", b=B)
        CONV, U, VG, DT, DTU, ZB, EB1 = (ARENA[:, 640 + k * 512:1152 + k * 512] for k in range(7))
        Y0, Y1 = (ARENA[:, 4224 + k * 512:4736 + k * 512] for k in range(2))
        DA = ARENA[:, 5376:5376 + 4096]
        DBU = ARENA[:, 9472:9472 + 4096]
        HS = ARENA[:, 13568:13568 + 4096]
        ANEG = SM[:, 176:192]

        LG = SM[:, 256:256 + B * H]
        M8 = SM[:, 320:320 + B * 8].rearrange("p (b e) -> p b e", b=B)
        GX = SM[:, 352:352 + B * H]
        GS = SM[:, 416:416 + B]
        GT = QT

        WKK, WVV = SM[:, 448:456], SM[:, 456:464]
        OH8 = SM[:, 464:496].rearrange("p (b e) -> p b e", b=B)

        def piece(x, a):
            return x[0:HD, a * P:(a + 1) * P]

        NA, NR, NH = 8, 64, 32
        ENC = ARENA[:, 0:1024].rearrange("p (k n) -> p k n", k=2)
        DIFF = ARENA[:, 1024:2048].rearrange("p (k n) -> p k n", k=2)
        MID = ARENA[:, 2048:4096].rearrange("p (k n) -> p k n", k=4)
        LOSS = SM[:, 0:32].rearrange("p (b n) -> p b n", b=B)
        LMIN = SM[:, 32:36]
        SEL = SM[:, 40:72].rearrange("p (b n) -> p b n", b=B)
        IDXF = SM[:, 72:80]
        EQ = SM[:, 192:256].rearrange("p (a n) -> p a n", a=NA)
        PICK = SM[:, 256:512].rearrange("p (b a n) -> p b a n", b=B, a=NA)
        OH = SM[:, 80:112].rearrange("p (b a) -> p b a", b=B)
        SHALF = SM[:, 112:128].rearrange("p (b j) -> p b j", b=B)
        BUP = SM[:, 136:140]

        OHT = SM[:, 512:1024]

        def PICKT_(b):
            return OHT[0:NA, b * P:(b + 1) * P]

        XP, XB, BX, IG, FG, HR, YT, YV = (ARENA[:, k * 512:(k + 1) * 512] for k in range(8))

        QP = ARENA[:, 0:8192]
        QSC = ARENA[:, 8192:12288].rearrange("p (c n) -> p c n", c=8)
        BB = ARENA[:, 8192:10240]
        ZS = ARENA[:, 10240:12288]
        PR = ARENA[:, 12288:16384].rearrange("p (k n) -> p k n", k=2)
        LS = ARENA[:, 16384:18432]
        RK = SM[:, 0:1024]
        QN = CT[:, 0:4096].rearrange("p (b n) -> p b n", b=B)
        T1 = CT[:, 4096:5120]
        OTK = CT[:, 5120:6144]
        OT8 = CT[:, 6144:7168]
        ZK = CT[:, 0:2048]
        DB = CT[:, 7168:8192].bitcast(BF16)
        CTT = SPARE[:, 0:256].rearrange("p (k n) -> p k n", k=2)
        CKT = SPARE[:, 256:512].rearrange("p (k n) -> p k n", k=2)
        SQ = ARENA[:, 12288:13312]
        SCR = SPARE[:, 512:576]
        NKH = SPARE[:, 576:640]
        NV = SPARE[:, 640:704]
        BN, PN, QSS, LT = (SPARE[:, k:k + 64] for k in (704, 768, 832, 896))
        BNB = SPARE[:, 960:992].bitcast(BF16)
        NSS = SPARE[:, 992:993]
        HAlf = SPARE[:, 1000:1064]
        OAT = ACC

        KT3 = KS[:, 0:512]
        V3 = ARENA[:, 0:512].rearrange("p (b f) -> p b f", b=B)

        HP = ARENA[:, 0:1024].rearrange("p (k n) -> p k n", k=2)
        TG = ARENA[:, 1024:2048].rearrange("p (k n) -> p k n", k=2)
        PAIRS = 9
        G18 = SM[:, 512:512 + B * 18].rearrange("p (b e) -> p b e", b=B)

        block = ctx.enter_context(nc.Block())

        @block.sync
        def _(sync):
            def experts_sp(src, n, first_gate=None):
                width = src.shape[1]
                for k in range(2):
                    nc.sync.wait_ge(sem("expert_out"), SP.due("expert_out", lag=2))
                    nc.sync.dma_start(EB[:, k, 0:width], src[k * P:(k + 1) * P, :]).then_inc(sem("dma_expert%d" % k), 16)
                with SP.loop(n // 2 - 1, seen=[("expert_out", 2)]) as i:
                    for k in range(2):
                        nc.sync.wait_ge(sem("expert_out"), SP.due("expert_out", lag=2))
                        nc.sync.dma_start(EB[:, k, 0:width], src[bass.ds((2 * i + 2 + k) * P, P), :])\
                            .then_inc(sem("dma_expert%d" % k), 16)
            def load(dst, src, signal):
                sync.dma_start(dst, src).then_inc(sem(signal), 16)

            load(X[:, :, :], d["x"], "dma_x")
            load(WA[:, :], d["wa"], "dma_wa")
            for c in range(B):
                load(CT[:, c * S:(c + 1) * S], d["ctxT"][:, c * S:(c + 1) * S], "dma_ctx%d" % c)
            load(ROWS[:, :], d["rows"].broadcast_to([P, d["rows"].shape[1]]), "dma_rows")
            load(WB[:, :], d["wb"], "dma_wb")
            load(MASK8[:, :], d["mask"], "dma_mask")
            load(IDX[:, :], d["idx"].broadcast_to([P, 8]), "dma_idx")
            experts_sp(d["l0f_experts"], 8)
            load(CK[:, :, :], d["ctxk"], "dma_ck")
            experts_sp(d["l2f_experts"], 16)
            nc.sync.wait_ge(sem("x_ready"), SP.due("x_ready", n=7))
            load(WC, d["wc"], "dma_wc")
            for b in range(B):
                for k in range(2):
                    n0 = (b * KEY_TILES + k) * P
                    nc.sync.wait_ge(sem("l3x_gathered"), SP.due("l3x_gathered", lag=2))
                    sync.dma_start(CTT[:, k, :], d["ctxT"][:, n0:n0 + P]).then_inc(sem("dma_ktile%d" % k), 16)
                    sync.dma_start(CKT[:, k, :], d["ctxr"][n0:n0 + P, :]).then_inc(sem("dma_ktile%d" % k), 16)
                with SP.loop(KEY_TILES // 2 - 1, seen=[("l3x_gathered", 2)]) as i:
                    for k in range(2):
                        n0 = i * 2 * P + ((b * KEY_TILES + 2 + k) * P)
                        nc.sync.wait_ge(sem("l3x_gathered"), SP.due("l3x_gathered", lag=2))
                        sync.dma_start(CTT[:, k, :], d["ctxT"][:, bass.ds(n0, P)]).then_inc(sem("dma_ktile%d" % k), 16)
                        sync.dma_start(CKT[:, k, :], d["ctxr"][bass.ds(n0, P), :]).then_inc(sem("dma_ktile%d" % k), 16)
            src = d["l3f_experts"]
            for p in range(PAIRS):
                k = p % 2
                nc.sync.wait_ge(sem("expert_out"), SP.due("expert_out", lag=2))
                load(EB[:, k, 0:3 * P], src[p * P:(p + 1) * P, :], "dma_expert%d" % k)
            sync.wait_ge(sem("x_ready"), 12)
            sync.dma_start(d["out"], X[:, :, :]).then_inc(sem("out_written"), 16)
            sync.wait_ge(sem("out_written"), 16)

        @block.gpsimd
        def _(gpsimd):
            def norm_pool():
                nc.gpsimd.wait_ge(sem("variance"), PO.due("variance"))
                nc.gpsimd.tensor_tensor(RSTD[:, :], VE[:, :], MHALF[:, :], ALU.pow).then_inc(sem("rstd"), PO.sends("rstd"))

            
            nc.gpsimd.memset(MHALF[:, :], -0.5).then_inc(sem("halves"), PO.sends("halves"))
            nc.gpsimd.wait_ge(sem("halves"), 1)
            norm_pool()

            
            nc.gpsimd.wait_ge(sem("x_ready"), PO.due("x_ready"))
            nc.gpsimd.memset(CB[:, :, 0:P + 2:P + 1], 0.0).then_inc(sem("l0a_pads"), PO.sends("l0a_pads"))
            norm_pool()
            norm_pool()
            for half in range(2):
                nc.gpsimd.wait_ge(sem("l0a_decay"), PO.due("l0a_decay"))
                cut = DA.rearrange("p (n t) -> p n t", t=P)[:, :, 0:1]
                nc.gpsimd.memset(cut, 0.0).then_inc(sem("l0a_decay_cut"), PO.sends("l0a_decay_cut"))

            
            norm_pool()

            
            norm_pool()

            
            norm_pool()

            
            norm_pool()

            norm_pool()

            
            norm_pool()
            norm_pool()

            norm_pool()

            
            nc.gpsimd.memset(ONESB[:, :], 1.0).then_inc(sem("ones16"), PO.sends("ones16"))
            norm_pool()
            norm_pool()
            nc.gpsimd.wait_ge(sem("l3x_null_square"), PO.due("l3x_null_square"))
            nc.gpsimd.tensor_tensor(NSS, NSS, MHALF[:, 0:1], ALU.pow).then_inc(sem("l3x_null_rnorm"), PO.sends("l3x_null_rnorm"))
            for b in range(B):
                if b:
                    nc.gpsimd.wait_ge(sem("l3x_o"), PO.due("l3x_o"))

                def add(k):
                    nc.gpsimd.wait_ge(sem("l3x_probs"), PO.due("l3x_probs"))
                    if k is None:
                        return
                    nc.gpsimd.tensor_tensor(LS, LS, PR[:, k, :], ALU.add).then_inc(sem("l3x_summed"), PO.sends("l3x_summed"))
                    nc.gpsimd.wait_ge(sem("l3x_summed"), PO.sent("l3x_summed"))

                nc.gpsimd.memset(LS, 0.0).then_inc(sem("pool_step"), PO.sends("pool_step"))
                nc.gpsimd.wait_ge(sem("pool_step"), PO.sent("pool_step"))
                with PO.loop(KEY_TILES // 2, made=[("l3x_summed", 2)], seen=[("l3x_probs", 2)]):
                    add(0)
                    add(1)
                nc.gpsimd.memset(HAlf[:, 0:1], 0.0).then_inc(sem("l3x_sums"), PO.sends("l3x_sums"))
            norm_pool()

            
            norm_pool()
            norm_pool()

            
            norm_pool()

        @block.scalar
        def _(scalar):
            def turn_act(dst, scale=1.0, bias=0.0):
                nc.scalar.wait_ge(sem("turned"), AC.due("turned"))
                act(dst[:, :], bank(0), ACT.Identity, scale=scale, bias=bias).then_inc(sem("turned_kept"), AC.sends("turned_kept"))

            def core_act(groups, scale):
                for g in range(groups):
                    nc.scalar.wait_ge(sem("scores_shifted"), AC.due("scores_shifted"))
                    act(SX[:, g % 2, :], SX[:, g % 2, :], ACT.Exp, scale=scale).then_inc(sem("probs"), AC.sends("probs"))
                    nc.scalar.wait_ge(sem("probs_turned"), AC.due("probs_turned"))
                    nc.scalar.wait_ge(sem("values_summed"), AC.due("values_summed", lag=2))
                    act(PT[:, g % 2, :], bank(3 + g % 2), ACT.Copy).then_inc(sem("pt_ready"), AC.sends("pt_ready"))

            def long_act(scale, masked):
                for b in range(B):
                    nc.scalar.wait_ge(sem("long_shift"), AC.due("long_shift"))
                    src = SL[:, b % 2, :] if masked else PSUM[:, 0:4, :].rearrange("p c n -> p (c n)")
                    act(SL[:, b % 2, :], src, ACT.Exp, scale=scale, bias=LNM[:, b:b + 1],
                        accum_out=LSUM[:, b:b + 1]).then_inc(sem("long_probs"), AC.sends("long_probs"))
                    for c in range(4):
                        nc.scalar.wait_ge(sem("long_turned"), AC.due("long_turned"))
                        act(PTL[:, 4 * c:4 * c + 4, :], bank4(4 + c % 2), ACT.Copy).then_inc(sem("long_pt"), AC.sends("long_pt"))
                    nc.scalar.wait_ge(sem("long_z"), AC.due("long_z"))
                    act(ZT[:, b * P:(b + 1) * P], PSUM[:, 6, 0:P], ACT.Copy).then_inc(sem("long_z_kept"), AC.sends("long_z_kept"))

            def experts_act(n, bias):
                def keep(k):
                    nc.scalar.wait_ge(sem("expert_out"), AC.due("expert_out", lag=2))
                    for c in range(FC):
                        nc.scalar.wait_ge(sem("hidden"), AC.due("hidden"))
                        b1 = EB[:, k, 2 * FF + c:2 * FF + c + 1] if bias else 0.0
                        act(HB[:, k, c, :], bank(1 + c % 2), ACT.Relu, bias=b1).then_inc(sem("hidden_kept"), AC.sends("hidden_kept"))

                keep(0)
                keep(1)
                with AC.loop(n // 2 - 1, made=[("hidden_kept", 2 * FC)], seen=[("hidden", 2 * FC), ("expert_out", 2)]):
                    keep(0)
                    keep(1)

            def context_keys_act(dst, bias, m=P):
                for c in range(NK // 512):
                    nc.scalar.wait_ge(sem("context_keys"), AC.due("context_keys"))
                    act(dst[0:m, c * 512:(c + 1) * 512], bank(1 + c % 2, m), ACT.Identity, bias=bias)\
                        .then_inc(sem("context_keys_kept"), AC.sends("context_keys_kept"))

            
            nc.scalar.wait_ge(sem("dma_wa"), AC.due("dma_wa"))
            context_keys_act(KS, w("l0x_bk"))
            turn_act(HT)
            nc.scalar.wait_ge(sem("l0x_q"), AC.due("l0x_q"))
            act(QT[:, :], bank(5), ACT.Identity, bias=w("l0x_bq")).then_inc(sem("l0x_q_kept"), AC.sends("l0x_q_kept"))
            core_act(16, HD ** -0.5)
            turn_act(OT)

            
            nc.scalar.wait_ge(sem("dma_wb"), AC.due("dma_wb"))
            turn_act(HT, scale=w("l0a_g"), bias=w("l0a_b"))
            act(ANEG, w("l0a_Alog"), ACT.Exp).then_inc(sem("l0a_expA"), AC.sends("l0a_expA"))
            nc.scalar.wait_ge(sem("l0a_x1"), AC.due("l0a_x1"))
            act(CB[:, :, 1:P + 1], bank4(1), ACT.Identity, bias=w("l0a_w1b"))\
                .then_inc(sem("l0a_x1_kept"), AC.sends("l0a_x1_kept"))
            nc.scalar.wait_ge(sem("l0a_conv"), AC.due("l0a_conv"))
            act(OT[:, :], CONV, ACT.Tanh, scale=0.5).then_inc(sem("l0a_conv_tanh"), AC.sends("l0a_conv_tanh"))
            nc.scalar.wait_ge(sem("l0a_vb"), AC.due("l0a_vb"))
            act(TMP[:, :], VG, ACT.Tanh, scale=0.5).then_inc(sem("l0a_v_tanh"), AC.sends("l0a_v_tanh"))
            nc.scalar.wait_ge(sem("l0a_z"), AC.due("l0a_z"))
            act(EB1, ZB, ACT.Abs).then_inc(sem("act_step"), AC.sends("act_step"))
            nc.scalar.wait_ge(sem("act_step"), AC.sent("act_step"))
            act(EB1, EB1, ACT.Exp, scale=-1.0).then_inc(sem("act_step"), AC.sends("act_step"))
            nc.scalar.wait_ge(sem("act_step"), AC.sent("act_step"))
            act(EB1, EB1, ACT.Ln, bias=1.0).then_inc(sem("l0a_log"), AC.sends("l0a_log"))
            nc.scalar.wait_ge(sem("l0a_dt_ready"), AC.due("l0a_dt_ready"))
            for half in range(2):
                if half:
                    nc.scalar.wait_ge(sem("l0a_scan"), AC.due("l0a_scan"))
                for n in range(8):
                    last = act(DA[:, n * 512:(n + 1) * 512], DT, ACT.Exp, scale=ANEG[:, half * 8 + n:half * 8 + n + 1])
                last.then_inc(sem("l0a_decay"), AC.sends("l0a_decay"))

            
            turn_act(HT)
            nc.scalar.wait_ge(sem("gate_shifted"), AC.due("gate_shifted"))
            act(GX[:, 0:32], GX[:, 0:32], ACT.Exp).then_inc(sem("gate_exp"), AC.sends("gate_exp"))
            experts_act(8, True)
            nc.scalar.wait_ge(sem("l0f_gates_turned"), AC.due("l0f_gates_turned"))
            act(GT[0:8, :], bank(6, 8), ACT.Copy).then_inc(sem("l0f_gates_kept"), AC.sends("l0f_gates_kept"))

            
            nc.scalar.wait_ge(sem("x_ready"), AC.due("x_ready", n=3))
            context_keys_act(KT, w("l1x_bkh", HD), HD)
            turn_act(HT)
            nc.scalar.wait_ge(sem("l1x_q"), AC.due("l1x_q"))
            act(TMP[:, :], bank(5), ACT.Copy).then_inc(sem("l1x_q_kept"), AC.sends("l1x_q_kept"))
            long_act(1.0, True)
            turn_act(OT)

            def pieces_act(part, dst):
                for j in range(H):
                    nc.scalar.wait_ge(sem("pieces"), AC.due("pieces"))
                    act(dst[0:HD, :].rearrange("p (t j) -> p t j", j=H)[:, :, j], bank(3 + j % 4, HD), ACT.Identity,
                        bias=w("l1a_bqkv", HD)[:, part * H + j:part * H + j + 1])\
                        .then_inc(sem("pieces_kept"), AC.sends("pieces_kept"))

            
            turn_act(HT)
            pieces_act(2, KS)
            pieces_act(0, QS)
            nc.scalar.wait_ge(sem("l1a_v"), AC.due("l1a_v"))
            pieces_act(1, KS)
            core_act(16, HD ** -0.5)
            turn_act(OT)

            
            turn_act(HT)
            for k in range(2):
                nc.scalar.wait_ge(sem("l1f_enc"), AC.due("l1f_enc"))
                act(ENC[:, k, :], bank(1 + k), ACT.Relu, bias=w("l1f_benc")[:, k:k + 1])\
                    .then_inc(sem("l1f_enc_kept"), AC.sends("l1f_enc_kept"))
            for k in range(4):
                nc.scalar.wait_ge(sem("l1f_mid"), AC.due("l1f_mid"))
                act(MID[:, k, :], bank(1 + k % 2), ACT.Relu, bias=w("l1f_bdown")[:, k:k + 1])\
                    .then_inc(sem("l1f_mid_kept"), AC.sends("l1f_mid_kept"))

            nc.scalar.wait_ge(sem("x_ready"), AC.due("x_ready", n=3))
            context_keys_act(KT, w("l2x_bk"))
            turn_act(HT)
            nc.scalar.wait_ge(sem("l2x_q"), AC.due("l2x_q"))
            act(QT[:, :], bank(5), ACT.Identity, bias=w("l2x_bq")).then_inc(sem("l2x_q_kept"), AC.sends("l2x_q_kept"))
            long_act(P ** -0.5, False)

            
            turn_act(HT)
            nc.scalar.wait_ge(sem("l2a_mm"), AC.due("l2a_mm"))
            act(XP, bank(1), ACT.Identity, bias=w("l2a_bin")).then_inc(sem("l2a_xp"), AC.sends("l2a_xp"))
            nc.scalar.wait_ge(sem("l2a_mm"), AC.due("l2a_mm"))
            act(XB, bank(2), ACT.Identity, bias=w("l2a_bB")).then_inc(sem("l2a_xb"), AC.sends("l2a_xb"))
            nc.scalar.wait_ge(sem("l2a_mm"), AC.due("l2a_mm", n=2))
            nc.scalar.wait_ge(sem("l2a_halves"), AC.due("l2a_halves"))
            act(IG[0:16, :], bank(3, 16), ACT.Tanh, scale=0.5, bias=SM[0:16, 0:1])
            act(FG[0:16, :], bank(4, 16), ACT.Tanh, scale=0.5, bias=SM[0:16, 1:2])\
                .then_inc(sem("l2a_gates"), AC.sends("l2a_gates"))
            nc.scalar.wait_ge(sem("l2a_mm"), AC.due("l2a_mm", n=2))
            act(YT, bank(6), ACT.Tanh, bias=w("l2a_bD")).then_inc(sem("l2a_y"), AC.sends("l2a_y"))

            turn_act(HT)
            nc.scalar.wait_ge(sem("gate_shifted"), AC.due("gate_shifted"))
            act(GX, GX, ACT.Exp).then_inc(sem("gate_exp"), AC.sends("gate_exp"))
            experts_act(16, False)

            
            for t in range(B * KEY_TILES):
                nc.scalar.wait_ge(sem("l3x_k"), AC.due("l3x_k"))
                nc.scalar.wait_ge(sem("l3x_k_summed"), AC.due("l3x_k_summed", lag=2))
                src = PSUM[:, 2 * (t % 2) + 1:2 * (t % 2) + 3, :].rearrange("p c n -> p (c n)")
                act(ARENA[:, 12288 + (t % 2) * 1024:13312 + (t % 2) * 1024], src, ACT.Square)\
                    .then_inc(sem("l3x_k_kept"), AC.sends("l3x_k_kept"))
            nc.scalar.wait_ge(sem("l3x_k_squares"), AC.due("l3x_k_squares"))
            act(RK, RK, ACT.Sqrt).then_inc(sem("l3x_k_norms"), AC.sends("l3x_k_norms"))
            turn_act(HT, scale=w("l3x_gn"))
            for b in range(B):
                nc.scalar.wait_ge(sem("l3x_q"), AC.due("l3x_q"))
                src = PSUM[:, 2 * (b % 2) + 1:2 * (b % 2) + 3, :].rearrange("p c n -> p (c n)")
                act(QN[:, b, :], src, ACT.Copy).then_inc(sem("l3x_q_kept"), AC.sends("l3x_q_kept"))
            nc.scalar.wait_ge(sem("l3x_q_squares"), AC.due("l3x_q_squares"))
            act(QSS, QSS, ACT.Sqrt).then_inc(sem("l3x_q_norms"), AC.sends("l3x_q_norms"))
            nc.scalar.wait_ge(sem("l3x_b_squares"), AC.due("l3x_b_squares"))
            act(BN, BN, ACT.Sqrt).then_inc(sem("l3x_b_norms"), AC.sends("l3x_b_norms"))
            for c in range(8):
                nc.scalar.wait_ge(sem("l3x_qT"), AC.due("l3x_qT"))
                act(QSC[:, c, :], bank(1 + c % 2), ACT.Copy).then_inc(sem("l3x_qT_kept"), AC.sends("l3x_qT_kept"))
            nc.scalar.wait_ge(sem("l3x_null_shifted"), AC.due("l3x_null_shifted"))
            act(PN, PN, ACT.Exp).then_inc(sem("l3x_null"), AC.sends("l3x_null"))
            qph = QP.rearrange("p (b h n) -> p h b n", b=B, h=H)
            for h in range(H):
                nc.scalar.wait_ge(sem("l3x_qp"), AC.due("l3x_qp"))
                act(qph[:, h, :, :], bank4(1 + h % 2), ACT.Copy).then_inc(sem("l3x_qp_kept"), AC.sends("l3x_qp_kept"))
            for b in range(B):
                nc.scalar.wait_ge(sem("l3x_bound"), AC.due("l3x_bound"))
                act(BB, PSUM[:, 0:4, :].rearrange("p c n -> p (c n)"), ACT.Copy)\
                    .then_inc(sem("l3x_bound_kept"), AC.sends("l3x_bound_kept"))

                def probs(k):
                    nc.scalar.wait_ge(sem("l3x_scores_taken"), AC.due("l3x_scores_taken", n=4))
                    act(PR[:, k, :], PR[:, k, :], ACT.Exp).then_inc(sem("l3x_probs"), AC.sends("l3x_probs"))

                with AC.loop(KEY_TILES // 2, made=[("l3x_probs", 2)], seen=[("l3x_scores_taken", 8)]):
                    probs(0)
                    probs(1)
                nc.scalar.wait_ge(sem("l3x_gathered"), AC.due("l3x_gathered", n=KEY_TILES))
                act(ZS, PSUM[:, 4:8, :].rearrange("p c n -> p (c n)"), ACT.Copy).then_inc(sem("l3x_z_kept"), AC.sends("l3x_z_kept"))
                nc.scalar.wait_ge(sem("l3x_oT"), AC.due("l3x_oT"))
                act(OT8, PSUM[:, 4:6, :].rearrange("p c n -> p (c n)"), ACT.Copy)\
                    .then_inc(sem("l3x_oT_kept"), AC.sends("l3x_oT_kept"))

            
            turn_act(HT)
            nc.scalar.wait_ge(sem("l3a_qk"), AC.due("l3a_qk"))
            act(QT[:, :], bank(5), ACT.Copy).then_inc(sem("l3a_qk_kept"), AC.sends("l3a_qk_kept"))
            nc.scalar.wait_ge(sem("l3a_qk"), AC.due("l3a_qk"))
            act(KT3, bank(6), ACT.Copy).then_inc(sem("l3a_qk_kept"), AC.sends("l3a_qk_kept"))
            core_act(1, P ** -0.5)
            turn_act(OT, scale=w("l3a_gamma"), bias=w("l3a_beta"))

            
            turn_act(HT)
            nc.scalar.wait_ge(sem("logits"), AC.due("logits", n=3))
            act(LG, PSUM[:, 5, 0:64], ACT.Tanh, scale=0.5).then_inc(sem("l3f_scores"), AC.sends("l3f_scores"))
            for p in range(PAIRS):
                k = p % 2
                nc.scalar.wait_ge(sem("l3f_up"), AC.due("l3f_up"))
                nc.scalar.wait_ge(sem("l3f_h"), AC.due("l3f_h", lag=2))
                act(TG[:, k, :], bank(1 + 2 * k), ACT.Tanh, scale=0.5).then_inc(sem("l3f_tanh"), AC.sends("l3f_tanh"))

        @block.vector
        def _(vector):
            def norm_dve(src, turned=True):
                for b in range(B):
                    last = ve.bn_stats(ST[:, b, :], src[:, b, :])
                last.then_inc(sem("dve_step"), DV.sends("dve_step"))
                nc.vector.wait_ge(sem("dve_step"), DV.sent("dve_step"))
                for b in range(B):
                    last = ve.bn_aggr(MV[:, b, :], ST[:, b, :])
                last.then_inc(sem("dve_step"), DV.sends("dve_step"))
                nc.vector.wait_ge(sem("dve_step"), DV.sent("dve_step"))
                ve.tensor_scalar(VE[:, :], MV[:, :, 1], EPS, None, ALU.add).then_inc(sem("variance"), DV.sends("variance"))
                nc.vector.wait_ge(sem("rstd"), DV.due("rstd"))
                for b in range(B):
                    last = ve.tensor_scalar(HN[:, b, :], src[:, b, :], MV[:, b, 0:1], RSTD[:, b:b + 1],
                                            ALU.subtract, ALU.mult)
                signal = "tokens_ready" if turned else "dve_step"
                last.then_inc(sem(signal), DV.sends(signal))
                nc.vector.wait_ge(sem(signal), DV.sent(signal))

            def tail_dve(bias_row=None):
                nc.vector.wait_ge(sem("block_out"), DV.due("block_out"))
                if bias_row is not None:
                    ve.tensor_tensor(ACC[:, :, :], bank4(7), over(bias_row, B), ALU.add).then_inc(sem("dve_step"), DV.sends("dve_step"))
                    nc.vector.wait_ge(sem("dve_step"), DV.sent("dve_step"))
                    ve.tensor_tensor(X[:, :, :], X[:, :, :], ACC[:, :, :], ALU.add).then_inc(sem("x_ready"), DV.sends("x_ready"))
                    nc.vector.wait_ge(sem("x_ready"), DV.sent("x_ready"))
                else:
                    ve.tensor_tensor(X[:, :, :], X[:, :, :], bank4(7), ALU.add).then_inc(sem("x_ready"), DV.sends("x_ready"))
                    nc.vector.wait_ge(sem("x_ready"), DV.sent("x_ready"))

            def core_dve(groups, causal=None):
                def shift(g):
                    nc.vector.wait_ge(sem("scores"), DV.due("scores"))
                    s = PSUM[:, 1 + g % 2, :].rearrange("p (j n) -> p j n", j=4)
                    sx = SX[:, g % 2, :].rearrange("p (j n) -> p j n", j=4)
                    nc.vector.wait_ge(sem("probs_turned"), DV.due("probs_turned", lag=2))
                    if g >= 2:
                        nc.vector.wait_ge(sem("probs_totalled"), DV.sent("probs_totalled"))
                    if causal is not None:
                        ve.tensor_tensor(sx, s, over(causal, 4), ALU.add).then_inc(sem("dve_step"), DV.sends("dve_step"))
                        nc.vector.wait_ge(sem("dve_step"), DV.sent("dve_step"))
                        ve.tensor_reduce(MX[:, g % 2, :], sx, AX.X, ALU.max).then_inc(sem("dve_step"), DV.sends("dve_step"))
                        nc.vector.wait_ge(sem("dve_step"), DV.sent("dve_step"))
                        ve.tensor_tensor(sx, sx, each(MX[:, g % 2, :], P), ALU.subtract)\
                            .then_inc(sem("scores_shifted"), DV.sends("scores_shifted"))
                    else:
                        ve.tensor_reduce(MX[:, g % 2, :], s, AX.X, ALU.max).then_inc(sem("dve_step"), DV.sends("dve_step"))
                        nc.vector.wait_ge(sem("dve_step"), DV.sent("dve_step"))
                        ve.tensor_tensor(sx, s, each(MX[:, g % 2, :], P), ALU.subtract)\
                            .then_inc(sem("scores_shifted"), DV.sends("scores_shifted"))

                def total(g):
                    nc.vector.wait_ge(sem("probs"), DV.due("probs"))
                    sx = SX[:, g % 2, :].rearrange("p (j n) -> p j n", j=4)
                    ve.tensor_reduce(L_SUM[:, 4 * g:4 * g + 4], sx, AX.X, ALU.add)\
                        .then_inc(sem("probs_totalled"), DV.sends("probs_totalled"))

                shift(0)
                for g in range(groups):
                    if g + 1 < groups:
                        shift(g + 1)
                    total(g)
                nc.vector.wait_ge(sem("probs_totalled"), DV.sent("probs_totalled"))
                ve.reciprocal(L_INV[:, 0:4 * groups], L_SUM[:, 0:4 * groups]).then_inc(sem("dve_step"), DV.sends("dve_step"))
                nc.vector.wait_ge(sem("dve_step"), DV.sent("dve_step"))

            def experts_dve(n, width):
                ve.memset(EACC[:, :, :], 0.0).then_inc(sem("dve_step"), DV.sends("dve_step"))
                nc.vector.wait_ge(sem("dve_step"), DV.sent("dve_step"))
                base = DV.made.get("dve_step", 0)
                with DV.loop(n // 2, made=[("expert_added", 2)], seen=[("expert_out", 2)]) as i:
                    for k in range(2):
                        nc.vector.wait_ge(sem("expert_out"), DV.due("expert_out"))
                        for b in range(B):
                            g = GATE[:, bass.ds(2 * i + (k + b * width), 1)]
                            last = ve.scalar_tensor_tensor(out=EACC[:, b, :], in0=PSUM[:, 3 + k, b * P:(b + 1) * P],
                                                           scalar=g, in1=EACC[:, b, :], op0=ALU.mult, op1=ALU.add)
                        last.then_inc(sem("expert_added"), DV.sends("expert_added"))
                        nc.vector.wait_ge(sem("expert_added"), DV.sent("expert_added"))

            
            nc.vector.wait_ge(sem("dma_x"), DV.due("dma_x"))
            nc.vector.wait_ge(sem("dma_wa"), DV.due("dma_wa"))
            nc.vector.wait_ge(sem("dma_rows"), DV.due("dma_rows"))
            norm_dve(X)
            nc.vector.wait_ge(sem("l0x_v"), DV.due("l0x_v"))
            ve.tensor_tensor(VS.rearrange("p (b f) -> p b f", b=B), bank4(3), over(row("l0x_bv"), B), ALU.add)\
                .then_inc(sem("dve_step"), DV.sends("dve_step"))
            nc.vector.wait_ge(sem("dve_step"), DV.sent("dve_step"))
            nc.vector.wait_ge(sem("l0x_q_kept"), DV.due("l0x_q_kept"))
            for h in range(H):
                last = ve.tensor_scalar(QM[:, h, :], QT[:, :], w("headmask")[:, h:h + 1], None, ALU.mult)
            last.then_inc(sem("l0x_q_heads"), DV.sends("l0x_q_heads"))
            nc.vector.wait_ge(sem("l0x_q_heads"), DV.sent("l0x_q_heads"))
            core_dve(16)
            nc.vector.wait_ge(sem("values_summed"), DV.due("values_summed", n=16))
            o = ACC[:, :, :].rearrange("p b (h e) -> p (b h) e", h=H)
            ve.tensor_tensor(o, PSUM[:, 6, :].rearrange("p (a e) -> p a e", e=HD), each(L_INV, HD), ALU.mult)\
                .then_inc(sem("tokens_ready"), DV.sends("tokens_ready"))
            nc.vector.wait_ge(sem("tokens_ready"), DV.sent("tokens_ready"))
            tail_dve(row("l0x_bo"))

            
            nc.vector.wait_ge(sem("dma_wb"), DV.due("dma_wb"))
            norm_dve(X, turned=False)
            norm_dve(HN)
            nc.vector.wait_ge(sem("l0a_expA"), DV.due("l0a_expA"))
            ve.tensor_scalar(ANEG, ANEG, -1.0, None, ALU.mult).then_inc(sem("l0a_A"), DV.sends("l0a_A"))
            nc.vector.wait_ge(sem("l0a_A"), DV.sent("l0a_A"))
            nc.vector.wait_ge(sem("l0a_x1_kept"), DV.due("l0a_x1_kept"))
            nc.vector.wait_ge(sem("l0a_pads"), DV.due("l0a_pads"))
            conv = CONV.rearrange("p (b t) -> p b t", b=B)
            ve.tensor_scalar(conv, CB[:, :, 0:P], w("l0a_conv")[:, 0:1], None, ALU.mult)\
                .then_inc(sem("dve_step"), DV.sends("dve_step"))
            nc.vector.wait_ge(sem("dve_step"), DV.sent("dve_step"))
            ve.scalar_tensor_tensor(out=conv, in0=CB[:, :, 1:P + 1], scalar=w("l0a_conv")[:, 1:2], in1=conv,
                                    op0=ALU.mult, op1=ALU.add).then_inc(sem("dve_step"), DV.sends("dve_step"))
            nc.vector.wait_ge(sem("dve_step"), DV.sent("dve_step"))
            ve.scalar_tensor_tensor(out=conv, in0=CB[:, :, 2:P + 2], scalar=w("l0a_conv")[:, 2:3], in1=conv,
                                    op0=ALU.mult, op1=ALU.add).then_inc(sem("l0a_conv"), DV.sends("l0a_conv"))
            nc.vector.wait_ge(sem("l0a_conv"), DV.sent("l0a_conv"))
            nc.vector.wait_ge(sem("l0a_v"), DV.due("l0a_v"))
            ve.tensor_scalar(VG, bank(2), w("l0a_v1b"), None, ALU.add).then_inc(sem("l0a_vb"), DV.sends("l0a_vb"))
            nc.vector.wait_ge(sem("l0a_vb"), DV.sent("l0a_vb"))
            nc.vector.wait_ge(sem("l0a_conv_tanh"), DV.due("l0a_conv_tanh"))
            ve.scalar_tensor_tensor(out=U, in0=OT[:, :], scalar=1.0, in1=CONV, op0=ALU.add, op1=ALU.mult)\
                .then_inc(sem("dve_step"), DV.sends("dve_step"))
            nc.vector.wait_ge(sem("dve_step"), DV.sent("dve_step"))
            ve.tensor_scalar(U, U, 0.5, None, ALU.mult).then_inc(sem("l0a_u"), DV.sends("l0a_u"))
            nc.vector.wait_ge(sem("l0a_u"), DV.sent("l0a_u"))
            nc.vector.wait_ge(sem("l0a_v_tanh"), DV.due("l0a_v_tanh"))
            ve.scalar_tensor_tensor(out=VG, in0=TMP[:, :], scalar=1.0, in1=VG, op0=ALU.add, op1=ALU.mult)\
                .then_inc(sem("dve_step"), DV.sends("dve_step"))
            nc.vector.wait_ge(sem("dve_step"), DV.sent("dve_step"))
            nc.vector.wait_ge(sem("l0a_dt"), DV.due("l0a_dt"))
            ve.tensor_scalar(ZB, bank(3), w("l0a_bdt"), None, ALU.add).then_inc(sem("l0a_z"), DV.sends("l0a_z"))
            nc.vector.wait_ge(sem("l0a_z"), DV.sent("l0a_z"))
            nc.vector.wait_ge(sem("l0a_log"), DV.due("l0a_log"))
            ve.scalar_tensor_tensor(out=DT, in0=ZB, scalar=0.0, in1=EB1, op0=ALU.max, op1=ALU.add)\
                .then_inc(sem("l0a_dt_ready"), DV.sends("l0a_dt_ready"))
            nc.vector.wait_ge(sem("l0a_dt_ready"), DV.sent("l0a_dt_ready"))
            ve.tensor_tensor(DTU, DT, U, ALU.mult).then_inc(sem("dve_step"), DV.sends("dve_step"))
            nc.vector.wait_ge(sem("dve_step"), DV.sent("dve_step"))
            for half, y in enumerate((Y0, Y1)):
                for n in range(8):
                    nc.vector.wait_ge(sem("l0a_bc"), DV.due("l0a_bc"))
                    ve.tensor_tensor(DBU[:, n * 512:(n + 1) * 512], bank(4 + (n + half * 16) % 3), DTU, ALU.mult)\
                        .then_inc(sem("l0a_bc_taken"), DV.sends("l0a_bc_taken"))
                nc.vector.wait_ge(sem("l0a_bc_taken"), DV.sent("l0a_bc_taken"))
                nc.vector.wait_ge(sem("l0a_decay_cut"), DV.due("l0a_decay_cut"))
                ve.tensor_tensor_scan(HS, DA, DBU, 0.0, ALU.mult, ALU.add).then_inc(sem("l0a_scan"), DV.sends("l0a_scan"))
                nc.vector.wait_ge(sem("l0a_scan"), DV.sent("l0a_scan"))
                for n in range(8):
                    nc.vector.wait_ge(sem("l0a_bc"), DV.due("l0a_bc"))
                    ve.tensor_tensor(DBU[:, n * 512:(n + 1) * 512], HS[:, n * 512:(n + 1) * 512],
                                     bank(4 + (n + 8 + half * 16) % 3), ALU.mult)\
                        .then_inc(sem("l0a_bc_taken"), DV.sends("l0a_bc_taken"))
                nc.vector.wait_ge(sem("l0a_bc_taken"), DV.sent("l0a_bc_taken"))
                ve.tensor_reduce(y, DBU.rearrange("p (n t) -> p t n", n=8), AX.X, ALU.add)\
                    .then_inc(sem("dve_step"), DV.sends("dve_step"))
                nc.vector.wait_ge(sem("dve_step"), DV.sent("dve_step"))
            ve.tensor_tensor(Y0, Y0, Y1, ALU.add).then_inc(sem("dve_step"), DV.sends("dve_step"))
            nc.vector.wait_ge(sem("dve_step"), DV.sent("dve_step"))
            ve.scalar_tensor_tensor(out=Y0, in0=U, scalar=w("l0a_D"), in1=Y0, op0=ALU.mult, op1=ALU.add)\
                .then_inc(sem("dve_step"), DV.sends("dve_step"))
            nc.vector.wait_ge(sem("dve_step"), DV.sent("dve_step"))
            ve.scalar_tensor_tensor(out=OT[:, :], in0=Y0, scalar=0.5, in1=VG, op0=ALU.mult, op1=ALU.mult)\
                .then_inc(sem("l0a_y"), DV.sends("l0a_y"))
            nc.vector.wait_ge(sem("l0a_y"), DV.sent("l0a_y"))
            tail_dve(row("l0a_w2b"))

            
            norm_dve(X)
            nc.vector.wait_ge(sem("logits"), DV.due("logits"))
            ve.tensor_copy(LG[:, 0:32], PSUM[:, 5, 0:32]).then_inc(sem("dve_step"), DV.sends("dve_step"))
            nc.vector.wait_ge(sem("dve_step"), DV.sent("dve_step"))
            lg = LG[:, 0:32].rearrange("p (b e) -> p b e", b=B)
            gx = GX[:, 0:32].rearrange("p (b e) -> p b e", b=B)
            for b in range(B):
                last = ve.max(M8[:, b, :], lg[:, b, :])
            last.then_inc(sem("dve_step"), DV.sends("dve_step"))
            nc.vector.wait_ge(sem("dve_step"), DV.sent("dve_step"))
            ve.tensor_tensor(gx, lg, M8[:, :, 0:1].broadcast_to([P, B, 8]), ALU.subtract)\
                .then_inc(sem("gate_shifted"), DV.sends("gate_shifted"))
            nc.vector.wait_ge(sem("gate_shifted"), DV.sent("gate_shifted"))
            ve.tensor_tensor(lg, lg, M8[:, :, 1:2].broadcast_to([P, B, 8]), ALU.is_ge)\
                .then_inc(sem("dve_step"), DV.sends("dve_step"))
            nc.vector.wait_ge(sem("dve_step"), DV.sent("dve_step"))
            nc.vector.wait_ge(sem("gate_exp"), DV.due("gate_exp"))
            ve.tensor_tensor(gx, gx, lg, ALU.mult).then_inc(sem("dve_step"), DV.sends("dve_step"))
            nc.vector.wait_ge(sem("dve_step"), DV.sent("dve_step"))
            ve.tensor_reduce(GS, gx, AX.X, ALU.add).then_inc(sem("dve_step"), DV.sends("dve_step"))
            nc.vector.wait_ge(sem("dve_step"), DV.sent("dve_step"))
            ve.reciprocal(GS, GS).then_inc(sem("dve_step"), DV.sends("dve_step"))
            nc.vector.wait_ge(sem("dve_step"), DV.sent("dve_step"))
            ve.tensor_tensor(GATE[:, 0:32].rearrange("p (b e) -> p b e", b=B), gx, each(GS, 8), ALU.mult)\
                .then_inc(sem("l0f_gates"), DV.sends("l0f_gates"))
            nc.vector.wait_ge(sem("l0f_gates"), DV.sent("l0f_gates"))
            experts_dve(8, 8)
            nc.vector.wait_ge(sem("block_out"), DV.due("block_out"))
            ve.tensor_tensor(EACC[:, :, :], EACC[:, :, :], bank4(7), ALU.add).then_inc(sem("dve_step"), DV.sends("dve_step"))
            nc.vector.wait_ge(sem("dve_step"), DV.sent("dve_step"))
            ve.tensor_tensor(X[:, :, :], X[:, :, :], EACC[:, :, :], ALU.add).then_inc(sem("x_ready"), DV.sends("x_ready"))
            nc.vector.wait_ge(sem("x_ready"), DV.sent("x_ready"))

            
            nc.vector.wait_ge(sem("dma_mask"), DV.due("dma_mask"))
            ve.tensor_copy(NEG, MASK8[:, :]).then_inc(sem("dve_step"), DV.sends("dve_step"))
            nc.vector.wait_ge(sem("dve_step"), DV.sent("dve_step"))
            ve.tensor_scalar(KEEP, NEG, -1.0, 1.0, ALU.mult, ALU.add).then_inc(sem("dve_step"), DV.sends("dve_step"))
            nc.vector.wait_ge(sem("dve_step"), DV.sent("dve_step"))
            ve.tensor_scalar(NEG, NEG, MASKED, None, ALU.mult).then_inc(sem("dve_step"), DV.sends("dve_step"))
            nc.vector.wait_ge(sem("dve_step"), DV.sent("dve_step"))
            nc.vector.wait_ge(sem("l1x_fold"), DV.due("l1x_fold", n=2))
            ve.tensor_copy(SM[:, 448:464], PSUM[:, 3, 0:2 * HD]).then_inc(sem("l1x_folded"), DV.sends("l1x_folded"))
            nc.vector.wait_ge(sem("l1x_folded"), DV.sent("l1x_folded"))
            norm_dve(X)
            nc.vector.wait_ge(sem("l1x_qh"), DV.due("l1x_qh"))
            ve.tensor_scalar(QT[0:HD, :], bank(6, HD), w("l1x_bqh", HD), HD ** -0.5, ALU.add, ALU.mult)\
                .then_inc(sem("l1x_qh_kept"), DV.sends("l1x_qh_kept"))
            nc.vector.wait_ge(sem("l1x_qh_kept"), DV.sent("l1x_qh_kept"))
            for b in range(B):
                nc.vector.wait_ge(sem("long_scores"), DV.due("long_scores"))
                s = SL[:, b % 2, :]
                ve.tensor_tensor(s, PSUM[:, 0:4, :].rearrange("p c n -> p (c n)"), KEEP, ALU.mult)\
                    .then_inc(sem("dve_step"), DV.sends("dve_step"))
                nc.vector.wait_ge(sem("dve_step"), DV.sent("dve_step"))
                ve.tensor_tensor(s, s, NEG, ALU.add).then_inc(sem("dve_step"), DV.sends("dve_step"))
                nc.vector.wait_ge(sem("dve_step"), DV.sent("dve_step"))
                ve.tensor_reduce(LMX[:, b:b + 1], s, AX.X, ALU.max).then_inc(sem("dve_step"), DV.sends("dve_step"))
                nc.vector.wait_ge(sem("dve_step"), DV.sent("dve_step"))
                ve.tensor_scalar(LNM[:, b:b + 1], LMX[:, b:b + 1], -1.0, None, ALU.mult)\
                    .then_inc(sem("long_shift"), DV.sends("long_shift"))
                nc.vector.wait_ge(sem("long_shift"), DV.sent("long_shift"))
            nc.vector.wait_ge(sem("l1x_o"), DV.due("l1x_o"))
            ve.reciprocal(LINV, LSUM).then_inc(sem("dve_step"), DV.sends("dve_step"))
            nc.vector.wait_ge(sem("dve_step"), DV.sent("dve_step"))
            ve.tensor_tensor(OH8, PSUM[:, 5, 0:B * HD].rearrange("p (b e) -> p b e", b=B), each(LINV, HD), ALU.mult)\
                .then_inc(sem("dve_step"), DV.sends("dve_step"))
            nc.vector.wait_ge(sem("dve_step"), DV.sent("dve_step"))
            ve.tensor_tensor(OH8, OH8, over(row("l1x_bvh"), B), ALU.add).then_inc(sem("dve_step"), DV.sends("dve_step"))
            nc.vector.wait_ge(sem("dve_step"), DV.sent("dve_step"))
            for b in range(B):
                last = ve.tensor_copy(ACC[:, b, :].rearrange("p (h e) -> p h e", h=H), over(OH8[:, b, :], H))
            last.then_inc(sem("tokens_ready"), DV.sends("tokens_ready"))
            nc.vector.wait_ge(sem("tokens_ready"), DV.sent("tokens_ready"))
            tail_dve()

            
            norm_dve(X)
            nc.vector.wait_ge(sem("l1a_v"), DV.due("l1a_v"))
            ve.tensor_copy(VS, bank(1)).then_inc(sem("l1a_v_kept"), DV.sends("l1a_v_kept"))
            nc.vector.wait_ge(sem("l1a_v_kept"), DV.sent("l1a_v_kept"))
            core_dve(16, w("causal"))
            nc.vector.wait_ge(sem("values_summed"), DV.due("values_summed", n=16))
            o = ACC[:, :, :].rearrange("p b (h e) -> p (b h) e", h=H)
            ve.tensor_tensor(o, PSUM[:, 6, :].rearrange("p (a e) -> p a e", e=HD), each(L_INV, HD), ALU.mult)\
                .then_inc(sem("tokens_ready"), DV.sends("tokens_ready"))
            nc.vector.wait_ge(sem("tokens_ready"), DV.sent("tokens_ready"))
            tail_dve(row("l1a_bproj"))

            
            norm_dve(X)
            nc.vector.wait_ge(sem("dma_idx"), DV.due("dma_idx"))
            ve.tensor_copy(IDXF, IDX[:, :]).then_inc(sem("dve_step"), DV.sends("dve_step"))
            nc.vector.wait_ge(sem("dve_step"), DV.sent("dve_step"))
            iota = row("iota")[:, 0:NA]
            ve.tensor_tensor(EQ, each(iota, NA), over(IDXF, NA), ALU.is_equal).then_inc(sem("dve_step"), DV.sends("dve_step"))
            nc.vector.wait_ge(sem("dve_step"), DV.sent("dve_step"))
            for n in range(NA):
                nc.vector.wait_ge(sem("l1f_recon"), DV.due("l1f_recon"))
                ve.scalar_tensor_tensor(out=DIFF[:, n % 2, :], in0=bank(3 + n % 2), scalar=w("l1f_bdec")[:, n:n + 1],
                                        in1=HT[:, :], op0=ALU.add, op1=ALU.subtract)\
                    .then_inc(sem("l1f_recon_taken"), DV.sends("l1f_recon_taken"))
                nc.vector.wait_ge(sem("l1f_recon_taken"), DV.sent("l1f_recon_taken"))
                ve.tensor_tensor(DIFF[:, n % 2, :], DIFF[:, n % 2, :], DIFF[:, n % 2, :], ALU.mult)\
                    .then_inc(sem("dve_step"), DV.sends("dve_step"))
                nc.vector.wait_ge(sem("dve_step"), DV.sent("dve_step"))
                last = ve.tensor_reduce(LOSS[:, :, n], DIFF[:, n % 2, :].rearrange("p (b t) -> p b t", b=B), AX.X, ALU.add)
            last.then_inc(sem("l1f_losses"), DV.sends("l1f_losses"))
            nc.vector.wait_ge(sem("l1f_losses"), DV.sent("l1f_losses"))
            nc.vector.wait_ge(sem("l1f_loss"), DV.due("l1f_loss"))
            loss = PSUM[:, 5, 0:32].rearrange("p (b n) -> p b n", b=B)
            ve.tensor_reduce(LMIN, loss, AX.X, ALU.min).then_inc(sem("dve_step"), DV.sends("dve_step"))
            nc.vector.wait_ge(sem("dve_step"), DV.sent("dve_step"))
            ve.tensor_tensor(SEL, loss, each(LMIN, NA), ALU.is_equal).then_inc(sem("dve_step"), DV.sends("dve_step"))
            nc.vector.wait_ge(sem("dve_step"), DV.sent("dve_step"))
            for b in range(B):
                last = ve.tensor_tensor(PICK[:, b, :, :], EQ, over(SEL[:, b, :], NA), ALU.mult)
            last.then_inc(sem("dve_step"), DV.sends("dve_step"))
            nc.vector.wait_ge(sem("dve_step"), DV.sent("dve_step"))
            ve.tensor_reduce(OH, PICK, AX.X, ALU.add).then_inc(sem("dve_step"), DV.sends("dve_step"))
            nc.vector.wait_ge(sem("dve_step"), DV.sent("dve_step"))
            oh2 = OH.rearrange("p b (j i) -> p b j i", i=2)
            ve.tensor_copy(SHALF[0:NR, :, :], oh2[0:NR, :, :, 0])
            ve.tensor_copy(SHALF[NR:P, :, :], oh2[NR:P, :, :, 1]).then_inc(sem("dve_step"), DV.sends("dve_step"))
            nc.vector.wait_ge(sem("dve_step"), DV.sent("dve_step"))
            ohd = PICK[:, :, :, 0]
            ve.tensor_tensor(ohd[0:NA, :, :], OH[0:NA, :, :], over(ident[0:NA, 0:NA], B), ALU.mult)\
                .then_inc(sem("dve_step"), DV.sends("dve_step"))
            nc.vector.wait_ge(sem("dve_step"), DV.sent("dve_step"))
            ve.tensor_reduce(BUP[0:NA, :], ohd[0:NA, :, :], AX.X, ALU.add).then_inc(sem("dve_step"), DV.sends("dve_step"))
            nc.vector.wait_ge(sem("dve_step"), DV.sent("dve_step"))
            ve.tensor_copy(OHT[0:NA, :].rearrange("p (b t) -> p b t", b=B), each(BUP[0:NA, :], P))\
                .then_inc(sem("dve_step"), DV.sends("dve_step"))
            nc.vector.wait_ge(sem("dve_step"), DV.sent("dve_step"))
            nc.vector.wait_ge(sem("l1f_mid_kept"), DV.due("l1f_mid_kept", n=4))
            for k in range(4):
                m = MID[:, k, :].rearrange("p (b t) -> p b t", b=B)
                last = ve.tensor_tensor(m, m, each(SHALF[:, :, k], P), ALU.mult)
            last.then_inc(sem("l1f_masked"), DV.sends("l1f_masked"))
            nc.vector.wait_ge(sem("l1f_masked"), DV.sent("l1f_masked"))
            nc.vector.wait_ge(sem("block_out"), DV.due("block_out"))
            ve.tensor_tensor(ACC[:, :, :], bank4(6), over(row("l1f_bbase"), B), ALU.add)\
                .then_inc(sem("dve_step"), DV.sends("dve_step"))
            nc.vector.wait_ge(sem("dve_step"), DV.sent("dve_step"))
            ve.tensor_tensor(X[:, :, :], X[:, :, :], ACC[:, :, :], ALU.add).then_inc(sem("x_ready"), DV.sends("x_ready"))
            nc.vector.wait_ge(sem("x_ready"), DV.sent("x_ready"))

            norm_dve(X)
            for b in range(B):
                nc.vector.wait_ge(sem("long_scores"), DV.due("long_scores"))
                ve.tensor_reduce(LMX[:, b:b + 1], PSUM[:, 0:4, :].rearrange("p c n -> p (c n)"), AX.X, ALU.max)\
                    .then_inc(sem("dve_step"), DV.sends("dve_step"))
                nc.vector.wait_ge(sem("dve_step"), DV.sent("dve_step"))
                ve.tensor_scalar(LNM[:, b:b + 1], LMX[:, b:b + 1], -(P ** -0.5), None, ALU.mult)\
                    .then_inc(sem("long_shift"), DV.sends("long_shift"))
                nc.vector.wait_ge(sem("long_shift"), DV.sent("long_shift"))
            nc.vector.wait_ge(sem("block_out"), DV.due("block_out"))
            ve.reciprocal(LINV, LSUM).then_inc(sem("dve_step"), DV.sends("dve_step"))
            nc.vector.wait_ge(sem("dve_step"), DV.sent("dve_step"))
            ve.tensor_tensor(ACC[:, :, :], bank4(7), each(LINV, P), ALU.mult).then_inc(sem("dve_step"), DV.sends("dve_step"))
            nc.vector.wait_ge(sem("dve_step"), DV.sent("dve_step"))
            ve.tensor_tensor(ACC[:, :, :], ACC[:, :, :], over(row("l2x_bv"), B), ALU.add)\
                .then_inc(sem("dve_step"), DV.sends("dve_step"))
            nc.vector.wait_ge(sem("dve_step"), DV.sent("dve_step"))
            ve.tensor_tensor(X[:, :, :], X[:, :, :], ACC[:, :, :], ALU.add).then_inc(sem("x_ready"), DV.sends("x_ready"))
            nc.vector.wait_ge(sem("x_ready"), DV.sent("x_ready"))

            
            ve.tensor_scalar(SM[0:16, 0:1], w("l2a_big", 16), 0.5, None, ALU.mult).then_inc(sem("dve_step"), DV.sends("dve_step"))
            nc.vector.wait_ge(sem("dve_step"), DV.sent("dve_step"))
            ve.tensor_scalar(SM[0:16, 1:2], w("l2a_bfg", 16), 0.5, None, ALU.mult)\
                .then_inc(sem("l2a_halves"), DV.sends("l2a_halves"))
            nc.vector.wait_ge(sem("l2a_halves"), DV.sent("l2a_halves"))
            norm_dve(X)
            nc.vector.wait_ge(sem("l2a_gates"), DV.due("l2a_gates"))
            ve.tensor_scalar(IG[0:16, :], IG[0:16, :], 0.5, 0.5, ALU.mult, ALU.add)\
                .then_inc(sem("dve_step"), DV.sends("dve_step"))
            nc.vector.wait_ge(sem("dve_step"), DV.sent("dve_step"))
            ve.tensor_scalar(FG[0:16, :], FG[0:16, :], 0.5, 0.5, ALU.mult, ALU.add)\
                .then_inc(sem("dve_step"), DV.sends("dve_step"))
            nc.vector.wait_ge(sem("dve_step"), DV.sent("dve_step"))
            ve.memset(FG[0:16, :].rearrange("p (b t) -> p b t", b=B)[:, :, 0:1], 0.0)\
                .then_inc(sem("dve_step"), DV.sends("dve_step"))
            nc.vector.wait_ge(sem("dve_step"), DV.sent("dve_step"))
            nc.vector.wait_ge(sem("l2a_mm"), DV.due("l2a_mm", n=5))
            ve.tensor_tensor(BX[0:16, :], bank(5, 16), IG[0:16, :], ALU.mult).then_inc(sem("dve_step"), DV.sends("dve_step"))
            nc.vector.wait_ge(sem("dve_step"), DV.sent("dve_step"))
            ve.tensor_tensor_scan(HR[0:16, :], FG[0:16, :], BX[0:16, :], 0.0, ALU.mult, ALU.add)\
                .then_inc(sem("l2a_h"), DV.sends("l2a_h"))
            nc.vector.wait_ge(sem("l2a_h"), DV.sent("l2a_h"))
            nc.vector.wait_ge(sem("l2a_out"), DV.due("l2a_out"))
            ve.tensor_tensor(ACC[:, :, :], bank4(7), over(row("l2a_bout"), B), ALU.add)\
                .then_inc(sem("dve_step"), DV.sends("dve_step"))
            nc.vector.wait_ge(sem("dve_step"), DV.sent("dve_step"))
            norm_dve(ACC, turned=False)
            ve.tensor_tensor(ACC[:, :, :], HN[:, :, :], over(row("l2a_gamma"), B), ALU.mult)\
                .then_inc(sem("dve_step"), DV.sends("dve_step"))
            nc.vector.wait_ge(sem("dve_step"), DV.sent("dve_step"))
            ve.tensor_tensor(ACC[:, :, :], ACC[:, :, :], over(row("l2a_beta"), B), ALU.add)\
                .then_inc(sem("dve_step"), DV.sends("dve_step"))
            nc.vector.wait_ge(sem("dve_step"), DV.sent("dve_step"))
            ve.tensor_tensor(X[:, :, :], X[:, :, :], ACC[:, :, :], ALU.add).then_inc(sem("x_ready"), DV.sends("x_ready"))
            nc.vector.wait_ge(sem("x_ready"), DV.sent("x_ready"))

            norm_dve(X)
            nc.vector.wait_ge(sem("logits"), DV.due("logits"))
            lp = PSUM[:, 5, 0:B * 16].rearrange("p (b e) -> p b e", b=B)
            lg = LG.rearrange("p (b e) -> p b e", b=B)
            gx = GX.rearrange("p (b e) -> p b e", b=B)
            ve.tensor_reduce(GS, lp, AX.X, ALU.max).then_inc(sem("dve_step"), DV.sends("dve_step"))
            nc.vector.wait_ge(sem("dve_step"), DV.sent("dve_step"))
            ve.tensor_tensor(lg, lp, each(GS, 16), ALU.is_equal).then_inc(sem("l2f_onehot"), DV.sends("l2f_onehot"))
            nc.vector.wait_ge(sem("l2f_onehot"), DV.sent("l2f_onehot"))
            ve.tensor_tensor(gx, lp, each(GS, 16), ALU.subtract).then_inc(sem("gate_shifted"), DV.sends("gate_shifted"))
            nc.vector.wait_ge(sem("gate_shifted"), DV.sent("gate_shifted"))
            nc.vector.wait_ge(sem("gate_exp"), DV.due("gate_exp"))
            ve.tensor_reduce(GS, gx, AX.X, ALU.add).then_inc(sem("dve_step"), DV.sends("dve_step"))
            nc.vector.wait_ge(sem("dve_step"), DV.sent("dve_step"))
            ve.reciprocal(GS, GS).then_inc(sem("dve_step"), DV.sends("dve_step"))
            nc.vector.wait_ge(sem("dve_step"), DV.sent("dve_step"))
            nc.vector.wait_ge(sem("l2f_places"), DV.due("l2f_places"))
            ve.scalar_tensor_tensor(out=GX, in0=PSUM[:, 6, 0:B * 16], scalar=float(CAPACITY), in1=LG,
                                    op0=ALU.is_le, op1=ALU.mult)\
                .then_inc(sem("dve_step"), DV.sends("dve_step"))
            nc.vector.wait_ge(sem("dve_step"), DV.sent("dve_step"))
            ve.tensor_tensor(GATE.rearrange("p (b e) -> p b e", b=B), gx, each(GS, 16), ALU.mult)\
                .then_inc(sem("dve_step"), DV.sends("dve_step"))
            nc.vector.wait_ge(sem("dve_step"), DV.sent("dve_step"))
            experts_dve(16, 16)
            ve.tensor_tensor(X[:, :, :], X[:, :, :], EACC[:, :, :], ALU.add).then_inc(sem("x_ready"), DV.sends("x_ready"))
            nc.vector.wait_ge(sem("x_ready"), DV.sent("x_ready"))

            
            for t in range(B * KEY_TILES):
                nc.vector.wait_ge(sem("l3x_k_kept"), DV.due("l3x_k_kept"))
                sq = ARENA[:, 12288 + (t % 2) * 1024:13312 + (t % 2) * 1024].rearrange("p (h e) -> p h e", h=H)
                ve.tensor_reduce(RK[:, t * H:(t + 1) * H], sq, AX.X, ALU.add).then_inc(sem("l3x_k_summed"), DV.sends("l3x_k_summed"))
            nc.vector.wait_ge(sem("l3x_k_summed"), DV.sent("l3x_k_summed"))
            ve.tensor_scalar(RK, RK, 1e-24, None, ALU.max).then_inc(sem("l3x_k_squares"), DV.sends("l3x_k_squares"))
            norm_dve(X, turned=False)
            norm_dve(HN)
            nc.vector.wait_ge(sem("l3x_k_norms"), DV.due("l3x_k_norms"))
            ve.reciprocal(RK, RK).then_inc(sem("dve_step"), DV.sends("dve_step"))
            nc.vector.wait_ge(sem("dve_step"), DV.sent("dve_step"))
            nc.vector.wait_ge(sem("dma_wc"), DV.due("dma_wc"))
            ve.tensor_tensor(SCR, row("l3x_qs"), row("l3x_ks"), ALU.mult).then_inc(sem("dve_step"), DV.sends("dve_step"))
            nc.vector.wait_ge(sem("dve_step"), DV.sent("dve_step"))
            ve.tensor_scalar(SCR, SCR, 8.0, None, ALU.mult).then_inc(sem("dve_step"), DV.sends("dve_step"))
            nc.vector.wait_ge(sem("dve_step"), DV.sent("dve_step"))
            ve.tensor_tensor(NKH, row("l3x_nk"), row("l3x_nk"), ALU.mult).then_inc(sem("dve_step"), DV.sends("dve_step"))
            nc.vector.wait_ge(sem("dve_step"), DV.sent("dve_step"))
            ve.tensor_reduce(NSS, NKH, AX.X, ALU.add).then_inc(sem("dve_step"), DV.sends("dve_step"))
            nc.vector.wait_ge(sem("dve_step"), DV.sent("dve_step"))
            ve.tensor_scalar(NSS, NSS, 1e-24, None, ALU.max).then_inc(sem("l3x_null_square"), DV.sends("l3x_null_square"))
            nc.vector.wait_ge(sem("l3x_null_square"), DV.sent("l3x_null_square"))
            nc.vector.wait_ge(sem("l3x_null_rnorm"), DV.due("l3x_null_rnorm"))
            ve.tensor_scalar(NKH, row("l3x_nk"), NSS, None, ALU.mult).then_inc(sem("dve_step"), DV.sends("dve_step"))
            nc.vector.wait_ge(sem("dve_step"), DV.sent("dve_step"))
            q4 = QN.rearrange("p b (h e) -> p b h e", h=H)
            t1 = T1.rearrange("p (h e) -> p h e", h=H)
            for b in range(B):
                nc.vector.wait_ge(sem("l3x_q_kept"), DV.due("l3x_q_kept"))
                ve.tensor_tensor(T1, QN[:, b, :], QN[:, b, :], ALU.mult).then_inc(sem("dve_step"), DV.sends("dve_step"))
                nc.vector.wait_ge(sem("dve_step"), DV.sent("dve_step"))
                ve.tensor_reduce(QSS[:, b * H:(b + 1) * H], t1, AX.X, ALU.add).then_inc(sem("dve_step"), DV.sends("dve_step"))
                nc.vector.wait_ge(sem("dve_step"), DV.sent("dve_step"))
            ve.tensor_scalar(QSS, QSS, 1e-24, None, ALU.max).then_inc(sem("l3x_q_squares"), DV.sends("l3x_q_squares"))
            nc.vector.wait_ge(sem("l3x_q_squares"), DV.sent("l3x_q_squares"))
            nc.vector.wait_ge(sem("l3x_q_norms"), DV.due("l3x_q_norms"))
            ve.reciprocal(QSS, QSS).then_inc(sem("dve_step"), DV.sends("dve_step"))
            nc.vector.wait_ge(sem("dve_step"), DV.sent("dve_step"))
            for b in range(B):
                ve.tensor_tensor(q4[:, b, :, :], q4[:, b, :, :], each(QSS[:, b * H:(b + 1) * H], DH), ALU.mult)\
                    .then_inc(sem("dve_step"), DV.sends("dve_step"))
                nc.vector.wait_ge(sem("dve_step"), DV.sent("dve_step"))
                ve.tensor_tensor(q4[:, b, :, :], q4[:, b, :, :], over(SCR, H), ALU.mult)\
                    .then_inc(sem("dve_step"), DV.sends("dve_step"))
                nc.vector.wait_ge(sem("dve_step"), DV.sent("dve_step"))
                ve.tensor_tensor(T1, QN[:, b, :], QN[:, b, :], ALU.mult).then_inc(sem("dve_step"), DV.sends("dve_step"))
                nc.vector.wait_ge(sem("dve_step"), DV.sent("dve_step"))
                ve.tensor_reduce(BN[:, b * H:(b + 1) * H], t1, AX.X, ALU.add).then_inc(sem("dve_step"), DV.sends("dve_step"))
                nc.vector.wait_ge(sem("dve_step"), DV.sent("dve_step"))
                ve.tensor_tensor(t1, q4[:, b, :, :], over(NKH, H), ALU.mult).then_inc(sem("dve_step"), DV.sends("dve_step"))
                nc.vector.wait_ge(sem("dve_step"), DV.sent("dve_step"))
                ve.tensor_reduce(PN[:, b * H:(b + 1) * H], t1, AX.X, ALU.add).then_inc(sem("dve_step"), DV.sends("dve_step"))
                nc.vector.wait_ge(sem("dve_step"), DV.sent("dve_step"))
            ve.tensor_scalar(BN, BN, 1.0, None, ALU.mult).then_inc(sem("l3x_b_squares"), DV.sends("l3x_b_squares"))
            nc.vector.wait_ge(sem("l3x_b_squares"), DV.sent("l3x_b_squares"))
            nc.vector.wait_ge(sem("l3x_b_norms"), DV.due("l3x_b_norms"))
            ve.tensor_copy(BNB, BN).then_inc(sem("dve_step"), DV.sends("dve_step"))
            nc.vector.wait_ge(sem("dve_step"), DV.sent("dve_step"))
            ve.tensor_tensor(PN, PN, BNB, ALU.subtract).then_inc(sem("l3x_null_shifted"), DV.sends("l3x_null_shifted"))
            nc.vector.wait_ge(sem("l3x_null_shifted"), DV.sent("l3x_null_shifted"))
            nc.vector.wait_ge(sem("l3x_null"), DV.due("l3x_null"))
            for b in range(B):
                db = DB.rearrange("p (h q) -> p h q", h=H)
                ve.tensor_tensor(db, over(ident, H), each(BNB[:, b * H:(b + 1) * H], P), ALU.mult)\
                    .then_inc(sem("l3x_diag"), DV.sends("l3x_diag"))
                nc.vector.wait_ge(sem("l3x_diag"), DV.sent("l3x_diag"))
                nc.vector.wait_ge(sem("l3x_bound_kept"), DV.due("l3x_bound_kept"))

                def shift(k, t, first=False):
                    for c in range(4):
                        nc.vector.wait_ge(sem("l3x_scores"), DV.due("l3x_scores"))
                        if c == 0:
                            nc.vector.wait_ge(sem("l3x_gathered"), DV.due("l3x_gathered", lag=2))
                            nc.vector.wait_ge(sem("l3x_summed"), DV.due("l3x_summed", lag=2))
                        for j in range(4):
                            h = 4 * c + j
                            rk = RK[:, bass.ds(t * H + (b * KEY_TILES * H + h), 1)] if not isinstance(t, int) else \
                                RK[:, t * H + b * KEY_TILES * H + h:t * H + b * KEY_TILES * H + h + 1]
                            last = ve.scalar_tensor_tensor(out=PR[:, k, h * P:(h + 1) * P],
                                                           in0=PSUM[:, c, j * P:(j + 1) * P], scalar=rk,
                                                           in1=BB[:, h * P:(h + 1) * P], op0=ALU.mult, op1=ALU.subtract)
                        last.then_inc(sem("l3x_scores_taken"), DV.sends("l3x_scores_taken"))

                shift(0, 0)
                shift(1, 1)
                with DV.loop(KEY_TILES // 2 - 1, made=[("l3x_scores_taken", 8)],
                             seen=[("l3x_scores", 8), ("l3x_gathered", 2), ("l3x_summed", 2)]) as i:
                    shift(0, 2 * i + 2)
                    shift(1, 2 * i + 3)
                nc.vector.wait_ge(sem("l3x_o"), DV.due("l3x_o"))
                ln = LT[:, 0:H]
                ve.tensor_tensor(ln, PSUM[:, 6, 0:H], PN[:, b * H:(b + 1) * H], ALU.add)\
                    .then_inc(sem("dve_step"), DV.sends("dve_step"))
                nc.vector.wait_ge(sem("dve_step"), DV.sent("dve_step"))
                ve.reciprocal(ln, ln).then_inc(sem("dve_step"), DV.sends("dve_step"))
                nc.vector.wait_ge(sem("dve_step"), DV.sent("dve_step"))
                o = OTK.rearrange("p (h e) -> p h e", h=H)
                ve.tensor_tensor(t1, over(row("l3x_nv"), H), each(PN[:, b * H:(b + 1) * H], DH), ALU.mult)\
                    .then_inc(sem("dve_step"), DV.sends("dve_step"))
                nc.vector.wait_ge(sem("dve_step"), DV.sent("dve_step"))
                ve.tensor_tensor(o, PSUM[:, 4:6, :].rearrange("p c (h e) -> p (c h) e", h=8), t1, ALU.add)\
                    .then_inc(sem("dve_step"), DV.sends("dve_step"))
                nc.vector.wait_ge(sem("dve_step"), DV.sent("dve_step"))
                ve.tensor_tensor(o, o, each(ln, DH), ALU.mult).then_inc(sem("l3x_o_kept"), DV.sends("l3x_o_kept"))
                nc.vector.wait_ge(sem("l3x_o_kept"), DV.sent("l3x_o_kept"))
                nc.vector.wait_ge(sem("l3x_out"), DV.due("l3x_out"))
                ve.tensor_copy(OAT[:, b, :], PSUM[:, 7, 0:P]).then_inc(sem("dve_step"), DV.sends("dve_step"))
                nc.vector.wait_ge(sem("dve_step"), DV.sent("dve_step"))
            norm_dve(OAT, turned=False)
            ve.tensor_tensor(ACC[:, :, :], HN[:, :, :], over(row("l3x_go"), B), ALU.mult)\
                .then_inc(sem("dve_step"), DV.sends("dve_step"))
            nc.vector.wait_ge(sem("dve_step"), DV.sent("dve_step"))
            ve.tensor_tensor(X[:, :, :], X[:, :, :], ACC[:, :, :], ALU.add).then_inc(sem("x_ready"), DV.sends("x_ready"))
            nc.vector.wait_ge(sem("x_ready"), DV.sent("x_ready"))

            
            norm_dve(X)
            nc.vector.wait_ge(sem("l3a_v"), DV.due("l3a_v"))
            ve.tensor_copy(V3, bank4(7)).then_inc(sem("l3a_v_kept"), DV.sends("l3a_v_kept"))
            nc.vector.wait_ge(sem("l3a_v_kept"), DV.sent("l3a_v_kept"))
            core_dve(1, w("causal"))
            nc.vector.wait_ge(sem("values_summed"), DV.due("values_summed"))
            ve.tensor_tensor(ACC[:, :, :], bank4(6), each(L_INV[:, 0:B], P), ALU.mult)\
                .then_inc(sem("dve_step"), DV.sends("dve_step"))
            nc.vector.wait_ge(sem("dve_step"), DV.sent("dve_step"))
            ve.tensor_tensor(ACC[:, :, :], ACC[:, :, :], V3, ALU.add).then_inc(sem("dve_step"), DV.sends("dve_step"))
            nc.vector.wait_ge(sem("dve_step"), DV.sent("dve_step"))
            norm_dve(ACC)
            tail_dve(row("l3a_bfc"))

            
            norm_dve(X)
            nc.vector.wait_ge(sem("l3f_scores"), DV.due("l3f_scores"))
            lg = LG.rearrange("p (b e) -> p b e", b=B)
            gx = GX.rearrange("p (b e) -> p b e", b=B)
            ve.tensor_scalar(LG, LG, 0.5, 0.5, ALU.mult, ALU.add).then_inc(sem("dve_step"), DV.sends("dve_step"))
            nc.vector.wait_ge(sem("dve_step"), DV.sent("dve_step"))
            ve.tensor_tensor(gx, lg, over(row("l3f_gb"), B), ALU.add).then_inc(sem("dve_step"), DV.sends("dve_step"))
            nc.vector.wait_ge(sem("dve_step"), DV.sent("dve_step"))
            for b in range(B):
                last = ve.max(M8[:, b, :], gx[:, b, :])
            last.then_inc(sem("dve_step"), DV.sends("dve_step"))
            nc.vector.wait_ge(sem("dve_step"), DV.sent("dve_step"))
            ve.tensor_tensor(gx, gx, M8[:, :, 3:4].broadcast_to([P, B, 16]), ALU.is_ge)\
                .then_inc(sem("dve_step"), DV.sends("dve_step"))
            nc.vector.wait_ge(sem("dve_step"), DV.sent("dve_step"))
            ve.tensor_tensor(lg, lg, gx, ALU.mult).then_inc(sem("dve_step"), DV.sends("dve_step"))
            nc.vector.wait_ge(sem("dve_step"), DV.sent("dve_step"))
            ve.tensor_reduce(GS, lg, AX.X, ALU.add).then_inc(sem("dve_step"), DV.sends("dve_step"))
            nc.vector.wait_ge(sem("dve_step"), DV.sent("dve_step"))
            ve.reciprocal(GS, GS).then_inc(sem("dve_step"), DV.sends("dve_step"))
            nc.vector.wait_ge(sem("dve_step"), DV.sent("dve_step"))
            ve.tensor_scalar(GS, GS, 2.5 * 0.5, None, ALU.mult).then_inc(sem("dve_step"), DV.sends("dve_step"))
            nc.vector.wait_ge(sem("dve_step"), DV.sent("dve_step"))
            ve.memset(G18, 0.5).then_inc(sem("dve_step"), DV.sends("dve_step"))
            nc.vector.wait_ge(sem("dve_step"), DV.sent("dve_step"))
            ve.tensor_tensor(G18[:, :, 0:16], lg, each(GS, 16), ALU.mult).then_inc(sem("dve_step"), DV.sends("dve_step"))
            nc.vector.wait_ge(sem("dve_step"), DV.sent("dve_step"))
            ve.memset(EACC[:, :, :], 0.0).then_inc(sem("dve_step"), DV.sends("dve_step"))
            nc.vector.wait_ge(sem("dve_step"), DV.sent("dve_step"))

            def hidden(p):
                k = p % 2
                nc.vector.wait_ge(sem("l3f_tanh"), DV.due("l3f_tanh"))
                nc.vector.wait_ge(sem("expert_out"), DV.due("expert_out", lag=2))
                ve.scalar_tensor_tensor(out=HP[:, k, :], in0=TG[:, k, :], scalar=1.0, in1=bank(1 + 2 * k),
                                        op0=ALU.add, op1=ALU.mult)\
                    .then_inc(sem("dve_step"), DV.sends("dve_step"))
                nc.vector.wait_ge(sem("dve_step"), DV.sent("dve_step"))
                ve.tensor_tensor(HP[:, k, :], HP[:, k, :], bank(2 + 2 * k), ALU.mult).then_inc(sem("l3f_h"), DV.sends("l3f_h"))
                nc.vector.wait_ge(sem("l3f_h"), DV.sent("l3f_h"))

            def add(p):
                nc.vector.wait_ge(sem("expert_out"), out0 + p + 1)
                for i in range(2 if p < PAIRS - 1 else 1):
                    for b in range(B):
                        last = ve.scalar_tensor_tensor(out=EACC[:, b, :], in0=PSUM[:, 6 + i, b * P:(b + 1) * P],
                                                       scalar=G18[:, b, 2 * p + i:2 * p + i + 1], in1=EACC[:, b, :],
                                                       op0=ALU.mult, op1=ALU.add)
                    if i == 0 and p < PAIRS - 1:
                        last.then_inc(sem("dve_step"), DV.sends("dve_step"))
                        nc.vector.wait_ge(sem("dve_step"), DV.sent("dve_step"))
                last.then_inc(sem("l3f_added"), DV.sends("l3f_added"))
                nc.vector.wait_ge(sem("l3f_added"), DV.sent("l3f_added"))

            out0 = DV.seen["expert_out"]
            hidden(0)
            for p in range(PAIRS):
                if p + 1 < PAIRS:
                    hidden(p + 1)
                add(p)
            ve.tensor_tensor(X[:, :, :], X[:, :, :], EACC[:, :, :], ALU.add).then_inc(sem("x_ready"), DV.sends("x_ready"))
            nc.vector.wait_ge(sem("x_ready"), DV.sent("x_ready"))

        @block.tensor
        def _(tensor):
            def turn_pe(src=HN):
                nc.tensor.wait_ge(sem("tokens_ready"), PE.due("tokens_ready"))
                for b in range(B):
                    last = tp(PSUM[:, 0, b * P:(b + 1) * P], src[:, b, :], ident)
                last.then_inc(sem("turned"), PE.sends("turned"))

            def tail_pe(weight, src=OT):
                for b in range(B):
                    last = mm(PSUM[:, 7, b * P:(b + 1) * P], src[:, b * P:(b + 1) * P], weight, start=True, stop=True)
                last.then_inc(sem("block_out"), PE.sends("block_out"))

            def core_pe(groups, q_of, k_of, v_of, out_of):
                def scores(g):
                    nc.tensor.wait_ge(sem("scores_shifted"), PE.due("scores_shifted", lag=2))
                    for j in range(4):
                        last = mm(PSUM[:, 1 + g % 2, j * P:(j + 1) * P], q_of(g, j), k_of(g, j), start=True, stop=True)
                    last.then_inc(sem("scores"), PE.sends("scores"))

                scores(0)
                for g in range(groups):
                    if g + 1 < groups:
                        scores(g + 1)
                    nc.tensor.wait_ge(sem("probs"), PE.due("probs"))
                    for j in range(4):
                        last = tp(PSUM[:, 3 + g % 2, j * P:(j + 1) * P], SX[:, g % 2, j * P:(j + 1) * P], ident)
                    last.then_inc(sem("probs_turned"), PE.sends("probs_turned"))
                    nc.tensor.wait_ge(sem("pt_ready"), PE.due("pt_ready"))
                    for j in range(4):
                        last = mm(out_of(g, j), PT[:, g % 2, j * P:(j + 1) * P], v_of(g, j), start=True, stop=True)
                    last.then_inc(sem("values_summed"), PE.sends("values_summed"))

            def long_pe(rows_):
                def scores(b):
                    for c in range(4):
                        last = mm(PSUM[:, c, :], QT[0:rows_, b * P:(b + 1) * P],
                                  KT[0:rows_, b * S + c * 512:b * S + (c + 1) * 512], start=True, stop=True)
                    last.then_inc(sem("long_scores"), PE.sends("long_scores"))

                scores(0)
                for b in range(B):
                    nc.tensor.wait_ge(sem("long_probs"), PE.due("long_probs"))
                    for c in range(4):
                        nc.tensor.wait_ge(sem("long_pt"), PE.due("long_pt", lag=2))
                        for j in range(4):
                            t = 4 * c + j
                            last = tp(PSUM[:, 4 + c % 2, j * P:(j + 1) * P], SL[:, b % 2, t * P:(t + 1) * P], ident)
                        last.then_inc(sem("long_turned"), PE.sends("long_turned"))
                    if b + 1 < B:
                        scores(b + 1)
                    nc.tensor.wait_ge(sem("long_pt"), PE.seen["long_pt"])
                    nc.tensor.wait_ge(sem("long_z_kept"), PE.due("long_z_kept", lag=1))
                    for t in range(KEY_TILES):
                        last = mm(PSUM[:, 6, 0:P], CK[:, b * KEY_TILES + t, :], PTL[:, t, :],
                                  start=t == 0, stop=t == KEY_TILES - 1)
                    last.then_inc(sem("long_z"), PE.sends("long_z"))

            def experts_pe(n):
                def first(k):
                    nc.tensor.wait_ge(sem("dma_expert%d" % k), PE.due("dma_expert%d" % k))
                    for c in range(FC):
                        nc.tensor.wait_ge(sem("hidden_kept"), PE.due("hidden_kept", lag=2))
                        mm(bank(1 + c % 2), EB[:, k, c * P:(c + 1) * P], HT[:, :], start=True, stop=True)\
                            .then_inc(sem("hidden"), PE.sends("hidden"))

                def second(k):
                    nc.tensor.wait_ge(sem("hidden_kept"), PE.need_hidden)
                    nc.tensor.wait_ge(sem("expert_added"), PE.due("expert_added", lag=2))
                    for b in range(B):
                        for c in range(FC):
                            last = mm(PSUM[:, 3 + k, b * P:(b + 1) * P], HB[:, k, c, b * P:(b + 1) * P],
                                      EB[:, k, FF + c * P:FF + (c + 1) * P], start=c == 0, stop=c == FC - 1)
                    last.then_inc(sem("expert_out"), PE.sends("expert_out"))
                    PE.need_hidden = PE.need_hidden + FC

                PE.need_hidden = PE.seen.get("hidden_kept", 0) + FC
                first(0)
                first(1)
                second(0)
                first(0)
                second(1)
                h0 = PE.need_hidden
                with PE.loop(n // 2 - 2, made=[("hidden", 2 * FC), ("expert_out", 2)],
                             seen=[("dma_expert0", 1), ("dma_expert1", 1), ("hidden_kept", 2 * FC), ("expert_added", 2)]) as i:
                    PE.need_hidden = h0 + i * 2 * FC
                    first(1)
                    second(0)
                    first(0)
                    second(1)
                PE.need_hidden = h0 + (n // 2 - 2) * 2 * FC
                first(1)
                second(0)
                second(1)

            def context_keys_pe(weight, m=P):
                for c in range(NK // 512):
                    nc.tensor.wait_ge(sem("context_keys_kept"), PE.due("context_keys_kept", lag=2))
                    mm(bank(1 + c % 2, m), weight, CT[:, c * 512:(c + 1) * 512], start=True, stop=True)\
                        .then_inc(sem("context_keys"), PE.sends("context_keys"))

            
            nc.tensor.wait_ge(sem("dma_wa"), PE.due("dma_wa"))
            for c in range(B):
                nc.tensor.wait_ge(sem("dma_ctx%d" % c), PE.due("dma_ctx%d" % c))
            context_keys_pe(w("l0x_WkT"))
            for b in range(B):
                for h in range(H):
                    at = (b * H + h) * HD
                    last = mm(PSUM[:, 3, at:at + HD], CTB[:, b, h, :], w("l0x_WvT")[:, h * HD:(h + 1) * HD],
                              start=True, stop=True)
            last.then_inc(sem("l0x_v"), PE.sends("l0x_v"))
            turn_pe()
            nc.tensor.wait_ge(sem("turned_kept"), PE.due("turned_kept"))
            mm(bank(5), w("l0x_WqT"), HT[:, :], start=True, stop=True).then_inc(sem("l0x_q"), PE.sends("l0x_q"))
            nc.tensor.wait_ge(sem("l0x_q_heads"), PE.due("l0x_q_heads"))
            nc.tensor.wait_ge(sem("context_keys_kept"), 16)
            core_pe(16, lambda g, j: QM[:, 4 * (g % 4) + j, (g // 4) * P:(g // 4 + 1) * P],
                    lambda g, j: KSB[:, g // 4, 4 * (g % 4) + j, :],
                    lambda g, j: VS[:, (4 * g + j) * HD:(4 * g + j + 1) * HD],
                    lambda g, j: PSUM[:, 6, (4 * g + j) * HD:(4 * g + j + 1) * HD])
            turn_pe(ACC)
            nc.tensor.wait_ge(sem("turned_kept"), PE.due("turned_kept"))
            tail_pe(w("l0x_WoT"))

            
            nc.tensor.wait_ge(sem("dma_wb"), PE.due("dma_wb"))
            turn_pe()
            nc.tensor.wait_ge(sem("turned_kept"), PE.due("turned_kept"))
            mm(bank(1), w("l0a_w1"), HT[:, :], start=True, stop=True).then_inc(sem("l0a_x1"), PE.sends("l0a_x1"))
            mm(bank(2), w("l0a_v1"), HT[:, :], start=True, stop=True).then_inc(sem("l0a_v"), PE.sends("l0a_v"))
            nc.tensor.wait_ge(sem("l0a_u"), PE.due("l0a_u"))
            mm(bank(3), w("l0a_Wdt"), U, start=True, stop=True).then_inc(sem("l0a_dt"), PE.sends("l0a_dt"))
            for half in range(2):
                for name in ("l0a_WB", "l0a_WC"):
                    for n in range(8):
                        col = w(name)[:, half * 8 + n:half * 8 + n + 1].broadcast_to([P, P])
                        nc.tensor.wait_ge(sem("l0a_bc_taken"), PE.due("l0a_bc_taken", lag=3))
                        mm(bank(4 + (n + half * 16 + (8 if name == "l0a_WC" else 0)) % 3), col, U,
                            start=True, stop=True).then_inc(sem("l0a_bc"), PE.sends("l0a_bc"))
            nc.tensor.wait_ge(sem("l0a_y"), PE.due("l0a_y"))
            tail_pe(w("l0a_w2"))

            def logits_pe(weight, e):
                for b in range(B):
                    last = mm(PSUM[:, 5, b * e:(b + 1) * e], hT(b), weight, start=True, stop=True)
                last.then_inc(sem("logits"), PE.sends("logits"))

            
            turn_pe()
            nc.tensor.wait_ge(sem("turned_kept"), PE.due("turned_kept"))
            logits_pe(w("l0f_Wg"), 8)
            experts_pe(8)
            nc.tensor.wait_ge(sem("l0f_gates"), PE.due("l0f_gates"))
            for b in range(B):
                last = tp(PSUM[0:8, 6, b * P:(b + 1) * P], GATE[:, b * 8:(b + 1) * 8], ident)
            last.then_inc(sem("l0f_gates_turned"), PE.sends("l0f_gates_turned"))
            nc.tensor.wait_ge(sem("l0f_gates_kept"), PE.due("l0f_gates_kept"))
            for b in range(B):
                last = mm(PSUM[:, 7, b * P:(b + 1) * P], GT[0:8, b * P:(b + 1) * P], w("l0f_b2", 8), start=True, stop=True)
            last.then_inc(sem("block_out"), PE.sends("block_out"))

            
            nc.tensor.wait_ge(sem("dma_ck"), PE.due("dma_ck"))
            nc.tensor.wait_ge(sem("x_ready"), PE.due("x_ready", n=3))
            mm(PSUM[:, 3, 0:HD], w("l1x_WkT"), w("l1x_wkh"), start=True, stop=True)\
                .then_inc(sem("l1x_fold"), PE.sends("l1x_fold"))
            mm(PSUM[:, 3, HD:2 * HD], w("l1x_WvT"), w("l1x_wvh"), start=True, stop=True)\
                .then_inc(sem("l1x_fold"), PE.sends("l1x_fold"))
            nc.tensor.wait_ge(sem("l1x_folded"), PE.due("l1x_folded"))
            context_keys_pe(WKK, HD)
            turn_pe()
            nc.tensor.wait_ge(sem("turned_kept"), PE.due("turned_kept"))
            mm(bank(5), w("l1x_Wq"), HT[:, :], start=True, stop=True).then_inc(sem("l1x_q"), PE.sends("l1x_q"))
            nc.tensor.wait_ge(sem("l1x_q_kept"), PE.due("l1x_q_kept"))
            mm(bank(6, HD), w("l1x_wqh"), TMP[:, :], start=True, stop=True).then_inc(sem("l1x_qh"), PE.sends("l1x_qh"))
            nc.tensor.wait_ge(sem("l1x_qh_kept"), PE.due("l1x_qh_kept"))
            nc.tensor.wait_ge(sem("context_keys_kept"), 32)
            long_pe(HD)
            nc.tensor.wait_ge(sem("long_z_kept"), 4)
            for b in range(B):
                last = mm(PSUM[:, 5, b * HD:(b + 1) * HD], ZT[:, b * P:(b + 1) * P], WVV, start=True, stop=True)
            last.then_inc(sem("l1x_o"), PE.sends("l1x_o"))
            turn_pe(ACC)
            nc.tensor.wait_ge(sem("turned_kept"), PE.due("turned_kept"))
            tail_pe(w("l1x_Wo"))

            def pieces_pe(part):
                for j in range(H):
                    at = part * P + j * HD
                    nc.tensor.wait_ge(sem("pieces_kept"), PE.due("pieces_kept", lag=4))
                    mm(bank(3 + j % 4, HD), w("l1a_Wqkv")[:, at:at + HD], HT[:, :], start=True, stop=True)\
                        .then_inc(sem("pieces"), PE.sends("pieces"))

            
            turn_pe()
            nc.tensor.wait_ge(sem("turned_kept"), PE.due("turned_kept"))
            pieces_pe(2)
            nc.tensor.wait_ge(sem("pieces_kept"), 16)
            for a in range(B * H):
                last = tp(PSUM[:, 1, a * HD:(a + 1) * HD], piece(KS, a), ident[0:HD, 0:HD])
            last.then_inc(sem("l1a_v"), PE.sends("l1a_v"))
            pieces_pe(0)
            pieces_pe(1)
            nc.tensor.wait_ge(sem("pieces_kept"), 48)
            nc.tensor.wait_ge(sem("l1a_v_kept"), PE.due("l1a_v_kept"))
            core_pe(16, lambda g, j: piece(QS, 4 * g + j), lambda g, j: piece(KS, 4 * g + j),
                    lambda g, j: VS[:, (4 * g + j) * HD:(4 * g + j + 1) * HD],
                    lambda g, j: PSUM[:, 6, (4 * g + j) * HD:(4 * g + j + 1) * HD])
            turn_pe(ACC)
            nc.tensor.wait_ge(sem("turned_kept"), PE.due("turned_kept"))
            tail_pe(w("l1a_Wproj"))

            
            turn_pe()
            nc.tensor.wait_ge(sem("turned_kept"), PE.due("turned_kept"))
            for k in range(2):
                mm(bank(1 + k), w("l1f_Wenc")[:, k * P:(k + 1) * P], HT[:, :], start=True, stop=True)\
                    .then_inc(sem("l1f_enc"), PE.sends("l1f_enc"))
            nc.tensor.wait_ge(sem("l1f_enc_kept"), PE.due("l1f_enc_kept", n=2))
            for n in range(NA):
                r = NH * (n % 4)
                nc.tensor.wait_ge(sem("l1f_recon_taken"), PE.due("l1f_recon_taken", lag=2))
                mm(bank(3 + n % 2), w("l1f_Wdec")[r:r + NH, (n // 4) * P:(n // 4 + 1) * P],
                    ENC[r:r + NH, n // 4, :], start=True, stop=True)\
                    .then_inc(sem("l1f_recon"), PE.sends("l1f_recon"))
            for k in range(4):
                if k >= 2:
                    nc.tensor.wait_ge(sem("l1f_mid_kept"), PE.due("l1f_mid_kept"))
                mm(bank(1 + k % 2), w("l1f_Wdown")[:, k * P:(k + 1) * P], HT[:, :], start=True, stop=True)\
                    .then_inc(sem("l1f_mid"), PE.sends("l1f_mid"))
            nc.tensor.wait_ge(sem("l1f_losses"), PE.due("l1f_losses"))
            mm(PSUM[:, 5, 0:32], w("ones"), SM[:, 0:32], start=True, stop=True).then_inc(sem("l1f_loss"), PE.sends("l1f_loss"))
            nc.tensor.wait_ge(sem("l1f_masked"), PE.due("l1f_masked"))
            for b in range(B):
                sl = slice(b * P, (b + 1) * P)
                mm(PSUM[:, 6, sl], HT[:, sl], w("l1f_Wbase"), start=True, stop=False)
                for k in range(4):
                    last = mm(PSUM[:, 6, sl], MID[:, k, sl], w("l1f_Wup")[:, k * P:(k + 1) * P],
                              start=False, stop=False)
                last = mm(PSUM[:, 6, sl], PICKT_(b), w("l1f_bup", NA), start=False, stop=True)
            last.then_inc(sem("block_out"), PE.sends("block_out"))

            nc.tensor.wait_ge(sem("x_ready"), PE.due("x_ready", n=3))
            context_keys_pe(w("l2x_WkT"))
            turn_pe()
            nc.tensor.wait_ge(sem("turned_kept"), PE.due("turned_kept"))
            mm(bank(5), w("l2x_WqT"), HT[:, :], start=True, stop=True).then_inc(sem("l2x_q"), PE.sends("l2x_q"))
            nc.tensor.wait_ge(sem("l2x_q_kept"), PE.due("l2x_q_kept"))
            nc.tensor.wait_ge(sem("context_keys_kept"), 48)
            long_pe(P)
            nc.tensor.wait_ge(sem("long_z_kept"), 8)
            tail_pe(w("l2x_WvT"))

            
            turn_pe()
            nc.tensor.wait_ge(sem("turned_kept"), PE.due("turned_kept"))
            mm(bank(1), w("l2a_Win"), HT[:, :], start=True, stop=True).then_inc(sem("l2a_mm"), PE.sends("l2a_mm"))
            nc.tensor.wait_ge(sem("l2a_xp"), PE.due("l2a_xp"))
            mm(bank(2), w("l2a_WB"), XP, start=True, stop=True).then_inc(sem("l2a_mm"), PE.sends("l2a_mm"))
            mm(bank(3, 16), w("l2a_Wig"), XP, start=True, stop=True).then_inc(sem("l2a_mm"), PE.sends("l2a_mm"))
            mm(bank(4, 16), w("l2a_Wfg"), XP, start=True, stop=True).then_inc(sem("l2a_mm"), PE.sends("l2a_mm"))
            nc.tensor.wait_ge(sem("l2a_xb"), PE.due("l2a_xb"))
            mm(bank(5, 16), w("l2a_Bmat"), XB, start=True, stop=True).then_inc(sem("l2a_mm"), PE.sends("l2a_mm"))
            nc.tensor.wait_ge(sem("l2a_h"), PE.due("l2a_h"))
            mm(bank(6), w("l2a_WD"), XP, start=True, stop=False)
            mm(bank(6), w("l2a_Cmat", 16), HR[0:16, :], start=False, stop=True).then_inc(sem("l2a_mm"), PE.sends("l2a_mm"))
            nc.tensor.wait_ge(sem("l2a_y"), PE.due("l2a_y"))
            for b in range(B):
                sl = slice(b * P, (b + 1) * P)
                mm(PSUM[:, 7, sl], YT[:, sl], w("l2a_Wout"), start=True, stop=False)
                last = mm(PSUM[:, 7, sl], XP[:, sl], ident, start=False, stop=True)
            last.then_inc(sem("l2a_out"), PE.sends("l2a_out"))

            turn_pe()
            nc.tensor.wait_ge(sem("turned_kept"), PE.due("turned_kept"))
            logits_pe(w("l2f_WgT"), 16)
            nc.tensor.wait_ge(sem("l2f_onehot"), PE.due("l2f_onehot"))
            for b in range(B):
                for c in range(b + 1):
                    last = mm(PSUM[:, 6, b * 16:(b + 1) * 16], w("upto") if c == b else w("ones"),
                              LG[:, c * 16:(c + 1) * 16], start=c == 0, stop=c == b)
            last.then_inc(sem("l2f_places"), PE.sends("l2f_places"))
            experts_pe(16)

            
            nc.tensor.wait_ge(sem("dma_wc"), PE.due("dma_wc"))
            nc.tensor.wait_ge(sem("x_ready"), PE.due("x_ready", n=3))
            for t in range(B * KEY_TILES):
                nc.tensor.wait_ge(sem("l3x_k_kept"), PE.due("l3x_k_kept", lag=2))
                for c in range(2):
                    last = mm(bank(2 * (t % 2) + 1 + c), CT[:, t * P:(t + 1) * P], w("l3x_Wk")[:, c * 512:(c + 1) * 512],
                              start=True, stop=True)
                last.then_inc(sem("l3x_k"), PE.sends("l3x_k"))
            turn_pe()
            nc.tensor.wait_ge(sem("turned_kept"), PE.due("turned_kept"))
            for b in range(B):
                nc.tensor.wait_ge(sem("l3x_q_kept"), PE.due("l3x_q_kept", lag=2))
                for c in range(2):
                    last = mm(bank(2 * (b % 2) + 1 + c), hT(b), w("l3x_Wq")[:, c * 512:(c + 1) * 512], start=True, stop=True)
                last.then_inc(sem("l3x_q"), PE.sends("l3x_q"))
            nc.tensor.wait_ge(sem("l3x_b_squares"), PE.due("l3x_b_squares"))
            for c in range(8):
                nc.tensor.wait_ge(sem("l3x_qT_kept"), PE.due("l3x_qT_kept", lag=2))
                for b in range(B):
                    last = tp(PSUM[:, 1 + c % 2, b * P:(b + 1) * P], QN[:, b, c * P:(c + 1) * P], ident)
                last.then_inc(sem("l3x_qT"), PE.sends("l3x_qT"))
            nc.tensor.wait_ge(sem("l3x_qT_kept"), 8)
            for h in range(H):
                r = DH * (h % 2)
                nc.tensor.wait_ge(sem("l3x_qp_kept"), PE.due("l3x_qp_kept", lag=2))
                mm(bank(1 + h % 2), w("l3x_WkT")[r:r + DH, (h // 2) * P:(h // 2 + 1) * P],
                    QSC[r:r + DH, h // 2, :], start=True, stop=True).then_inc(sem("l3x_qp"), PE.sends("l3x_qp"))
            nc.tensor.wait_ge(sem("l3x_qp_kept"), 16)
            qpb = QP.rearrange("p (b n) -> p b n", b=B)
            for b in range(B):
                nc.tensor.wait_ge(sem("l3x_diag"), PE.due("l3x_diag"))
                for c in range(4):
                    last = mm(bank(c), ONESB[:, :], DB[:, c * 512:(c + 1) * 512], start=True, stop=True)
                last.then_inc(sem("l3x_bound"), PE.sends("l3x_bound"))
                nc.tensor.wait_ge(sem("l3x_bound_kept"), PE.due("l3x_bound_kept"))

                def scores(k, more=True):
                    nc.tensor.wait_ge(sem("dma_ktile%d" % k), PE.due("dma_ktile%d" % k, n=2))
                    for c in range(4):
                        nc.tensor.wait_ge(sem("l3x_scores_taken"), PE.due("l3x_scores_taken", lag=4))
                        mm(bank(c), CTT[:, k, :], qpb[:, b, c * 512:(c + 1) * 512], start=True, stop=True)\
                            .then_inc(sem("l3x_scores"), PE.sends("l3x_scores"))

                def gather(k, first, last_):
                    nc.tensor.wait_ge(sem("l3x_probs"), PE.due("l3x_probs"))
                    for c in range(4):
                        last = mm(bank(4 + c), CKT[:, k, :], PR[:, k, c * 512:(c + 1) * 512], start=first, stop=last_,
                                  skip_group_check=True)
                    last.then_inc(sem("l3x_gathered"), PE.sends("l3x_gathered"))

                scores(0)
                scores(1)
                gather(0, True, False)
                scores(0)
                gather(1, False, False)
                with PE.loop(KEY_TILES // 2 - 2, made=[("l3x_scores", 8), ("l3x_gathered", 2)],
                             seen=[("dma_ktile0", 2), ("dma_ktile1", 2), ("l3x_scores_taken", 8), ("l3x_probs", 2)]):
                    scores(1)
                    gather(0, False, False)
                    scores(0)
                    gather(1, False, False)
                scores(1)
                gather(0, False, False)
                gather(1, False, True)
                nc.tensor.wait_ge(sem("l3x_sums"), PE.due("l3x_sums"))
                nc.tensor.wait_ge(sem("l3x_z_kept"), PE.due("l3x_z_kept"))
                for h in range(H):
                    last = mm(PSUM[:, 6, h:h + 1], LS[:, h * P:(h + 1) * P], w("ones")[:, 0:1], start=True, stop=True)
                for h in range(H):
                    last = mm(PSUM[:, 4 + h // 8, (h % 8) * DH:(h % 8 + 1) * DH], ZS[:, h * P:(h + 1) * P],
                              w("l3x_Wv")[:, h * DH:(h + 1) * DH], start=True, stop=True)
                last.then_inc(sem("l3x_o"), PE.sends("l3x_o"))
                nc.tensor.wait_ge(sem("l3x_o_kept"), PE.due("l3x_o_kept"))
                for c in range(8):
                    last = tp(PSUM[:, 4 + c // 4, (c % 4) * P:(c % 4 + 1) * P], OTK[:, c * P:(c + 1) * P], ident)
                last.then_inc(sem("l3x_oT"), PE.sends("l3x_oT"))
                nc.tensor.wait_ge(sem("l3x_oT_kept"), PE.due("l3x_oT_kept"))
                for c in range(8):
                    last = mm(PSUM[:, 7, 0:P], OT8[:, c * P:(c + 1) * P], w("l3x_Wout")[:, c * P:(c + 1) * P],
                              start=c == 0, stop=c == 7)
                last.then_inc(sem("l3x_out"), PE.sends("l3x_out"))

            
            turn_pe()
            nc.tensor.wait_ge(sem("turned_kept"), PE.due("turned_kept"))
            mm(bank(5), w("l3a_Wq"), HT[:, :], start=True, stop=True).then_inc(sem("l3a_qk"), PE.sends("l3a_qk"))
            mm(bank(6), w("l3a_Wk"), HT[:, :], start=True, stop=True).then_inc(sem("l3a_qk"), PE.sends("l3a_qk"))
            for b in range(B):
                last = mm(PSUM[:, 7, b * P:(b + 1) * P], hT(b), w("l3a_Wv"), start=True, stop=True)
            last.then_inc(sem("l3a_v"), PE.sends("l3a_v"))
            nc.tensor.wait_ge(sem("l3a_qk_kept"), PE.due("l3a_qk_kept", n=2))
            nc.tensor.wait_ge(sem("l3a_v_kept"), PE.due("l3a_v_kept"))
            core_pe(1, lambda g, j: QT[:, j * P:(j + 1) * P], lambda g, j: KT3[:, j * P:(j + 1) * P],
                    lambda g, j: V3[:, j, :], lambda g, j: PSUM[:, 6, j * P:(j + 1) * P])
            turn_pe()
            nc.tensor.wait_ge(sem("turned_kept"), PE.due("turned_kept"))
            tail_pe(w("l3a_Wfc"))

            
            turn_pe()
            nc.tensor.wait_ge(sem("turned_kept"), PE.due("turned_kept"))
            logits_pe(w("l3f_WgT"), 16)

            def up(p):
                k = p % 2
                nc.tensor.wait_ge(sem("dma_expert%d" % k), PE.due("dma_expert%d" % k))
                nc.tensor.wait_ge(sem("l3f_h"), PE.due("l3f_h", lag=2))
                for c in range(2):
                    last = mm(bank(1 + 2 * k + c), EB[:, k, c * P:(c + 1) * P], HT[:, :], start=True, stop=True)
                last.then_inc(sem("l3f_up"), PE.sends("l3f_up"))

            def down(p):
                k = p % 2
                nc.tensor.wait_ge(sem("l3f_h"), p + 1)
                nc.tensor.wait_ge(sem("l3f_added"), PE.due("l3f_added", lag=1))
                for i in range(2 if p < PAIRS - 1 else 1):
                    r = DH * i
                    for b in range(B):
                        last = mm(PSUM[:, 6 + i, b * P:(b + 1) * P], HP[r:r + DH, k, b * P:(b + 1) * P],
                                  EB[r:r + DH, k, 2 * P:3 * P], start=True, stop=True)
                last.then_inc(sem("expert_out"), PE.sends("expert_out"))

            up(0)
            for p in range(PAIRS):
                if p + 1 < PAIRS:
                    up(p + 1)
                down(p)


def pack(parts):
    where, out, at = {}, [], 0
    for name, a in parts:
        full = np.zeros((P, a.shape[1]), a.dtype)
        full[:a.shape[0]] = a
        where[name] = (at, a.shape[1])
        out.append(full)
        at += a.shape[1]
    return where, np.concatenate(out, axis=1)


def lay_out(i):
    c = lambda v: np.ascontiguousarray(v)
    col = lambda v: v.reshape(-1, 1)
    eye = np.eye(P, dtype=np.float32)
    k = np.arange(P)
    a = [("ident", eye), ("ones", np.ones((P, P), np.float32)),
         ("headmask", (k[:, None] // HD == np.arange(H)[None]).astype(np.float32)),
         ("l0x_WqT", i["L0_xattn_Wq"].T), ("l0x_WkT", i["L0_xattn_Wk"].T), ("l0x_WvT", i["L0_xattn_Wv"].T),
         ("l0x_WoT", i["L0_xattn_Wo"].T), ("l0x_bq", col(i["L0_xattn_bq"])), ("l0x_bk", col(i["L0_xattn_bk"]))]
    enc, dec = i["L1_ffn_W_enc"], i["L1_ffn_W_dec"]
    down, up = i["L1_ffn_W_down"], i["L1_ffn_W_up"]
    bqkv = i["L1_attn_bqkv"]
    b = [("causal", np.where(k[:, None] >= k[None], 0.0, FAR).astype(np.float32)),
         ("upto", (k[:, None] <= k[None]).astype(np.float32)),
         ("l0a_w1", i["L0_attn_w1_w"]), ("l0a_v1", i["L0_attn_v1_w"]), ("l0a_w2", i["L0_attn_w2_w"]),
         ("l0a_Wdt", i["L0_attn_W_dt"]), ("l0a_WB", i["L0_attn_W_B"]), ("l0a_WC", i["L0_attn_W_C"]),
         ("l0a_Alog", i["L0_attn_A_log"]), ("l0a_conv", i["L0_attn_conv_w"].reshape(P, 3)),
         ("l0a_g", col(i["L0_attn_ln_g"])), ("l0a_b", col(i["L0_attn_ln_b"])), ("l0a_w1b", col(i["L0_attn_w1_b"])),
         ("l0a_v1b", col(i["L0_attn_v1_b"])), ("l0a_bdt", col(i["L0_attn_b_dt"])), ("l0a_D", col(i["L0_attn_D_skip"])),
         ("l0f_Wg", i["L0_ffn_Wg"]), ("l0f_b2", i["L0_ffn_b2"]),
         ("l1x_WkT", i["L1_xattn_Wk"].T), ("l1x_WvT", i["L1_xattn_Wv"].T), ("l1x_wkh", i["L1_xattn_wk_h"]),
         ("l1x_wvh", i["L1_xattn_wv_h"]), ("l1x_Wq", i["L1_xattn_Wq"]), ("l1x_wqh", i["L1_xattn_wq_h"]),
         ("l1x_bqh", col(i["L1_xattn_bq_h"])), ("l1x_bkh", col(i["L1_xattn_bk_h"])), ("l1x_Wo", i["L1_xattn_Wo"]),
         ("l1a_Wqkv", i["L1_attn_Wqkv"]), ("l1a_bqkv", bqkv.reshape(3 * H, HD).T), ("l1a_Wproj", i["L1_attn_Wproj"]),
         ("l1f_Wenc", enc.transpose(1, 0, 2).reshape(P, 256)),
         ("l1f_benc", i["L1_ffn_b_enc"].reshape(2, P).T),
         ("l1f_Wdec", dec.reshape(2, P, P).transpose(1, 0, 2).reshape(P, 256)),
         ("l1f_bdec", i["L1_ffn_b_dec"].T),
         ("l1f_Wdown", down.transpose(1, 0, 2).reshape(P, 512)),
         ("l1f_bdown", i["L1_ffn_b_down"].reshape(4, P).T),
         ("l1f_Wup", up.reshape(4, P, P).transpose(1, 0, 2).reshape(P, 512)),
         ("l1f_bup", i["L1_ffn_b_up"]), ("l1f_Wbase", i["L1_ffn_W_base"]),
         ("l2x_WqT", i["L2_xattn_Wq"].T), ("l2x_WkT", i["L2_xattn_Wk"].T), ("l2x_WvT", i["L2_xattn_Wv"].T),
         ("l2x_bq", col(i["L2_xattn_bq"])), ("l2x_bk", col(i["L2_xattn_bk"])),
         ("l2a_Win", i["L2_attn_W_in"]), ("l2a_bin", col(i["L2_attn_b_in"])), ("l2a_WB", i["L2_attn_W_B"]),
         ("l2a_bB", col(i["L2_attn_b_B"])), ("l2a_Bmat", i["L2_attn_B_mat"]), ("l2a_Cmat", i["L2_attn_C_mat"]),
         ("l2a_Wig", i["L2_attn_W_ig"]), ("l2a_Wfg", i["L2_attn_W_fg"]), ("l2a_big", col(i["L2_attn_b_ig"])),
         ("l2a_bfg", col(i["L2_attn_b_fg"])), ("l2a_WD", i["L2_attn_W_D"]), ("l2a_bD", col(i["L2_attn_b_D"])),
         ("l2a_Wout", i["L2_attn_W_out"]), ("l2f_WgT", i["L2_ffn_gate_w"].T),
         ("l3a_Wq", i["L3_attn_Wq"]), ("l3a_Wk", i["L3_attn_Wk"]), ("l3a_Wv", i["L3_attn_Wv"]),
         ("l3a_Wfc", i["L3_attn_Wfc"]), ("l3a_gamma", col(i["L3_attn_gamma"])), ("l3a_beta", col(i["L3_attn_beta"])),
         ("l3f_WgT", i["L3_ffn_gate_w"].T), ("l3x_gn", col(i["L3_xattn_g_norm"]))]
    wkv = i["L3_xattn_Wkv"]
    cc = [("l3x_Wq", i["L3_xattn_Wq"]), ("l3x_Wk", wkv[:, :H * DH]),
          ("l3x_WkT", wkv[:, :H * DH].T.reshape(8, P, P).transpose(1, 0, 2).reshape(P, 1024)),
          ("l3x_Wv", wkv[:, H * DH:]),
          ("l3x_Wout", i["L3_xattn_Wout"].reshape(8, P, P).transpose(1, 0, 2).reshape(P, 1024))]
    r = [("iota", np.arange(16, dtype=np.float32)), ("l0x_bv", i["L0_xattn_bv"]), ("l0x_bo", i["L0_xattn_bo"]),
         ("l0a_w2b", i["L0_attn_w2_b"]), ("l1x_bvh", i["L1_xattn_bv_h"]), ("l1a_bproj", i["L1_attn_bproj"]),
         ("l1f_bbase", i["L1_ffn_b_base"]), ("l2x_bv", i["L2_xattn_bv"]), ("l2a_bout", i["L2_attn_b_out"]),
         ("l2a_gamma", i["L2_attn_gamma"]), ("l2a_beta", i["L2_attn_beta"]), ("l3x_qs", i["L3_xattn_q_scale"]),
         ("l3x_ks", i["L3_xattn_k_scale"]), ("l3x_nk", i["L3_xattn_null_kv"][0]), ("l3x_nv", i["L3_xattn_null_kv"][1]),
         ("l3x_go", i["L3_xattn_g_out"]), ("l3a_bfc", i["L3_attn_bfc"]), ("l3f_gb", i["L3_ffn_gate_b"])]
    cols, arrays = {}, {}
    for part, parts in (("a", a), ("b", b), ("c", cc)):
        where, arrays["w" + part] = pack(parts)
        cols.update({n: (part, *v) for n, v in where.items()})
    rows, at = {}, 0
    for name, v in r:
        rows[name] = (at, v.shape[0])
        at += v.shape[0]
    arrays["rows"] = np.concatenate([v for _, v in r])[None]
    ctx = i["ctx_1024"].reshape(NK, P)
    arrays["x"] = c(i["x"].transpose(1, 0, 2))
    arrays["ctxT"] = c(ctx.T)
    arrays["ctxr"] = c(ctx)
    arrays["ctxk"] = c(ctx.reshape(NK // P, P, P).transpose(1, 0, 2))
    arrays["mask"] = c(i["mask_SxS2_bk1"])
    arrays["idx"] = c(i["L1_ffn_connected_idx"])[None]

    def expert_rows(w1, w2, b1=None):
        e = w1.shape[0]
        parts = [w1, w2.reshape(e, FC, P, P).transpose(0, 2, 1, 3).reshape(e, P, FF)]
        if b1 is not None:
            parts.append(b1.reshape(e, FC, P).transpose(0, 2, 1))
        return c(np.concatenate(parts, axis=2).reshape(e * P, -1))

    arrays["l0f_experts"] = expert_rows(i["L0_ffn_W1"], i["L0_ffn_W2"], i["L0_ffn_b1"])
    arrays["l2f_experts"] = expert_rows(i["L2_ffn_w1"], i["L2_ffn_w2"])
    w13, w2 = i["L3_ffn_w13"], i["L3_ffn_w2"]
    pairs = np.zeros((9, P, 3 * P), np.float32)
    for p in range(9):
        for q in range(2):
            if p == 8 and q == 1:
                continue
            w13e, w2e = (w13[2 * p + q], w2[2 * p + q]) if p < 8 else (i["L3_ffn_w13_s"], i["L3_ffn_w2_s"])
            pairs[p, :, q * DH:(q + 1) * DH] = w13e[:DH].T
            pairs[p, :, P + q * DH:P + (q + 1) * DH] = w13e[DH:].T
            pairs[p, q * DH:(q + 1) * DH, 2 * P:] = w2e.T
    arrays["l3f_experts"] = pairs.reshape(9 * P, 3 * P)
    return arrays, cols, rows



def kernel(**inputs):
    import concourse.bacc as bacc
    from concourse.bass_utils import run_bass_kernel_spmd

    arrays, cols, rows = lay_out({k: np.asarray(v) for k, v in inputs.items()})
    nc = bacc.Bacc("TRN2", target_bir_lowering=False, num_devices=1)
    d = {n: nc.dram_tensor("in_" + n, a.shape, mybir.dt.from_np(a.dtype), kind="ExternalInput").ap()
         for n, a in arrays.items()}
    d["out"] = nc.dram_tensor("out_x", (P, B, P), F32, kind="ExternalOutput").ap()
    build(nc, d, cols, rows)
    r = run_bass_kernel_spmd(nc, [{"in_" + n: a for n, a in arrays.items()}], core_ids=[0])
    return np.ascontiguousarray(r.results[0]["out_x"].transpose(1, 0, 2))
```

```python
from contextlib import ExitStack

import concourse.bass as bass
import concourse.mybir as mybir
import numpy as np

F32 = mybir.dt.float32
BF16 = mybir.dt.bfloat16
I32 = mybir.dt.int32
U8 = mybir.dt.uint8
ALU = mybir.AluOpType
ACT = mybir.ActivationFunctionType
AX = mybir.AxisListType

P = 128
B = 4
T = B * P
S = 2048
NK = B * S
H = 16
HD = P // H
DH = 64
FF = 512
FC = FF // P
EPS = 1e-5
KEY_TILES = S // P
CAPACITY = int(1.25 * T / 16)
MASKED = -1.0e9
FAR = -1.0e30
SAFE_EXPONENT = 60.0


class Engine:

    def __init__(self, engine):
        self.i, self.made, self.seen = engine, {}, {}

    def sends(self, signal):
        self.made[signal] = self.made.get(signal, 0) + 1
        return 1

    def sent(self, signal):
        return self.made[signal]

    def due(self, signal, n=1, lag=0):
        self.seen[signal] = self.seen.get(signal, 0) + n
        value = self.seen[signal] - lag
        if isinstance(value, int):
            value = max(value, 0)
        return value * 16 if signal.startswith("dma_") else value

    def loop(self, trips, made=(), seen=()):
        return _Loop(self, trips, dict(made), dict(seen))


class _Loop:

    def __init__(self, e, trips, made, seen):
        self.e, self.trips, self.per = e, trips, (made, seen)

    def __enter__(self):
        self.cm = self.e.i.Fori(0, self.trips)
        i = self.cm.__enter__()
        self.base = [{k: c.get(k, 0) for k in per} for c, per in zip((self.e.made, self.e.seen), self.per)]
        for c, per in zip((self.e.made, self.e.seen), self.per):
            for k, n in per.items():
                c[k] = c.get(k, 0) + i * n
        self.start = [dict(self.e.made), dict(self.e.seen)]
        self.i = i
        return i

    def __exit__(self, *a):
        self.cm.__exit__(*a)
        for c, per, base in zip((self.e.made, self.e.seen), self.per, self.base):
            for k, n in per.items():
                c[k] = base[k] + self.trips * n


def build(nc, d, cols, rows):
    with ExitStack() as ctx:
        def sb(name, shape, dt=F32):
            return ctx.enter_context(nc.sbuf_tensor(name, shape, dt))

        made = {}

        def sem(name):
            if name not in made:
                made[name] = ctx.enter_context(nc.semaphore(name))
            return made[name]

        n_a, n_b, n_c = (d[k].shape[1] for k in ("wa", "wb", "wc"))
        WA = sb("WA", [P, n_a])
        WB = sb("WB", [P, n_b])
        ROWS = sb("ROWS", [P, d["rows"].shape[1]])
        X = sb("X", [P, B, P])
        CT = sb("CT", [P, NK])
        CK = sb("CK", [P, B * KEY_TILES, P])
        ARENA = sb("ARENA", [P, 18432])
        EB = sb("EB", [P, 2, 2 * FF + FC])
        HN = sb("HN", [P, B, P])
        HT = sb("HT", [P, T])
        OT = sb("OT", [P, T])
        QT = sb("QT", [P, T])
        TMP = sb("TMP", [P, T])
        ACC = sb("ACC", [P, B, P])
        ST = sb("ST", [P, B, 6])
        MV = sb("MV", [P, B, 2])
        VE = sb("VE", [P, B])
        RSTD = sb("RSTD", [P, B])
        MHALF = sb("MHALF", [P, B])
        SM = sb("SM", [P, 1024])
        RK = sb("RK", [P, B * KEY_TILES * H])
        WK = sb("WK", [P, H * DH])
        SQ = sb("SQ", [P, 2, 512])
        MASK8 = sb("MASK8", [P, S], U8)
        IDX = sb("IDX", [P, 8], I32)
        PSUM = ctx.enter_context(nc.psum_tensor("PSUM", [P, 8, 512], F32))

        WC = CK[:, :, :].rearrange("p a b -> p (a b)")[:, 0:n_c]
        SPARE = CK[:, :, :].rearrange("p a b -> p (a b)")[:, n_c:]

        def w(name, rows_=P):
            part, at, n = cols[name]
            return {"a": WA, "b": WB, "c": WC}[part][0:rows_, at:at + n]

        def row(name, off=0, n=None):
            at, m = rows[name]
            return ROWS[:, at + off:at + off + (n or m)]

        def bank(k, rows_=P):
            return PSUM[0:rows_, k, :]

        def bank4(k):
            return PSUM[:, k, :].rearrange("p (b f) -> p b f", b=B)

        def over(ap, n):
            return ap.unsqueeze(1).broadcast_to([ap.shape[0], n, ap.shape[1]])

        def each(ap, n):
            return ap.unsqueeze(2).broadcast_to([ap.shape[0], ap.shape[1], n])

        ident = w("ident")
        SP = Engine(nc.sync)
        PE = Engine(nc.tensor)
        AC = Engine(nc.scalar)
        DV = Engine(nc.vector)
        PO = Engine(nc.gpsimd)
        mm, tp = nc.tensor.matmul, nc.tensor.transpose
        act, ve = nc.scalar.activation, nc.vector

        def hT(b):
            return HT[:, b * P:(b + 1) * P]

        QS = ARENA[:, 0:8192]
        KS = ARENA[:, 8192:16384]
        SX = ARENA[:, 16384:17408].rearrange("p (k n) -> p k n", k=2)
        PT = ARENA[:, 17408:18432].rearrange("p (k n) -> p k n", k=2)
        L_SUM = SM[:, 0:B * H]
        L_INV = SM[:, 64:64 + B * H]
        MX = SM[:, 128:136].rearrange("p (k n) -> p k n", k=2)
        VS = SM[:, 512:1024]

        KT = ARENA[:, 0:NK]
        SL = ARENA[:, 8192:12288].rearrange("p (k n) -> p k n", k=2)
        PTL = ARENA[:, 12288:14336].rearrange("p (t n) -> p t n", t=KEY_TILES)
        KEEP = ARENA[:, 14336:16384]
        NEG = ARENA[:, 16384:18432]
        LMX, LNM, LSUM, LINV = (SM[:, k:k + B] for k in (160, 164, 168, 172))
        ZT = OT

        HB = ARENA[:, 0:4096].rearrange("p (k c n) -> p k c n", k=2, c=FC)
        GATE = SM[:, 192:192 + B * H]
        EACC = ACC

        CTB = CT[:, :].rearrange("p (b m s) -> p b s m", b=B, s=H)
        KSB = KS.rearrange("p (b m s) -> p b s m", b=B, s=H)
        QM = QS.rearrange("p (h n) -> p h n", h=H)

        N = 16
        CB = ARENA[:, 0:520].rearrange("p (b t) -> p b t", b=B)
        CONV, U, VG, DT, DTU, ZB, EB1 = (ARENA[:, 640 + k * 512:1152 + k * 512] for k in range(7))
        Y0, Y1 = (ARENA[:, 4224 + k * 512:4736 + k * 512] for k in range(2))
        DA = ARENA[:, 5376:5376 + 4096]
        DBU = ARENA[:, 9472:9472 + 4096]
        HS = ARENA[:, 13568:13568 + 4096]
        ANEG = SM[:, 176:192]

        LG = SM[:, 256:256 + B * H]
        M8 = SM[:, 320:320 + B * 8].rearrange("p (b e) -> p b e", b=B)
        GX = SM[:, 352:352 + B * H]
        GS = SM[:, 416:416 + B]
        GT = QT

        WKK, WVV = SM[:, 448:456], SM[:, 456:464]
        OH8 = SM[:, 464:496].rearrange("p (b e) -> p b e", b=B)

        def piece(x, a):
            return x[0:HD, a * P:(a + 1) * P]

        NA, NR, NH = 8, 64, 32
        ENC = ARENA[:, 0:1024].rearrange("p (k n) -> p k n", k=2)
        DIFF = ARENA[:, 1024:2048].rearrange("p (k n) -> p k n", k=2)
        MID = ARENA[:, 2048:4096].rearrange("p (k n) -> p k n", k=4)
        LOSS = SM[:, 0:32].rearrange("p (b n) -> p b n", b=B)
        LMIN = SM[:, 32:36]
        SEL = SM[:, 40:72].rearrange("p (b n) -> p b n", b=B)
        IDXF = SM[:, 72:80]
        EQ = SM[:, 192:256].rearrange("p (a n) -> p a n", a=NA)
        PICK = SM[:, 256:512].rearrange("p (b a n) -> p b a n", b=B, a=NA)
        OH = SM[:, 80:112].rearrange("p (b a) -> p b a", b=B)
        SHALF = SM[:, 112:128].rearrange("p (b j) -> p b j", b=B)
        BUP = SM[:, 136:140]

        OHT = SM[:, 512:1024]

        def PICKT_(b):
            return OHT[0:NA, b * P:(b + 1) * P]

        XP, XB, BX, IG, FG, HR, YT, YV = (ARENA[:, k * 512:(k + 1) * 512] for k in range(8))

        QP = ARENA[:, 0:8192]
        QSC = ARENA[:, 8192:12288].rearrange("p (c n) -> p c n", c=8)
        ZS = ARENA[:, 10240:12288]
        PR = ARENA[:, 12288:16384].rearrange("p (k n) -> p k n", k=2)
        LS = (ARENA[:, 8192:10240], ARENA[:, 16384:18432])
        QN = CT[:, 0:4096].rearrange("p (b n) -> p b n", b=B)
        T1 = CT[:, 4096:5120]
        OTK = CT[:, 5120:6144]
        OT8 = CT[:, 6144:7168]
        DEEP = 4
        CTT = SPARE[:, 0:512].rearrange("p (k n) -> p k n", k=DEEP)
        CKT = SPARE[:, 512:1024].rearrange("p (k n) -> p k n", k=DEEP)
        SCR = SPARE[:, 1024:1088]
        NKH = SPARE[:, 1088:1152]
        BN, PN, QSS, LT = (SPARE[:, k:k + 64] for k in (1152, 1216, 1280, 1344))
        NSS, BMAX, BTOP, NBTOP = (SPARE[:, k:k + 1] for k in range(1408, 1412))
        OAT = ACC
        TILE_GROUPS = KEY_TILES // DEEP

        KT3 = KS[:, 0:512]
        V3 = ARENA[:, 0:512].rearrange("p (b f) -> p b f", b=B)

        HP = ARENA[:, 0:1024].rearrange("p (k n) -> p k n", k=2)
        TG = ARENA[:, 1024:2048].rearrange("p (k n) -> p k n", k=2)
        PAIRS = 9
        G18 = SM[:, 512:512 + B * 18].rearrange("p (b e) -> p b e", b=B)

        block = ctx.enter_context(nc.Block())

        @block.sync
        def _(sync):
            def experts_sp(src, n, first_gate=None):
                width = src.shape[1]
                for k in range(2):
                    nc.sync.wait_ge(sem("expert_out"), SP.due("expert_out", lag=2))
                    nc.sync.dma_start(EB[:, k, 0:width], src[k * P:(k + 1) * P, :]).then_inc(sem("dma_expert%d" % k), 16)
                with SP.loop(n // 2 - 1, seen=[("expert_out", 2)]) as i:
                    for k in range(2):
                        nc.sync.wait_ge(sem("expert_out"), SP.due("expert_out", lag=2))
                        nc.sync.dma_start(EB[:, k, 0:width], src[bass.ds((2 * i + 2 + k) * P, P), :])\
                            .then_inc(sem("dma_expert%d" % k), 16)
            def load(dst, src, signal):
                sync.dma_start(dst, src).then_inc(sem(signal), 16)

            load(X[:, :, :], d["x"], "dma_x")
            load(WA[:, :], d["wa"], "dma_wa")
            for c in range(B):
                load(CT[:, c * S:(c + 1) * S], d["ctxT"][:, c * S:(c + 1) * S], "dma_ctx%d" % c)
            load(WK[:, :], d["wk"], "dma_wk")
            load(ROWS[:, :], d["rows"].broadcast_to([P, d["rows"].shape[1]]), "dma_rows")
            load(WB[:, :], d["wb"], "dma_wb")
            load(MASK8[:, :], d["mask"], "dma_mask")
            load(IDX[:, :], d["idx"].broadcast_to([P, 8]), "dma_idx")
            experts_sp(d["l0f_experts"], 8)
            load(CK[:, :, :], d["ctxk"], "dma_ck")
            experts_sp(d["l2f_experts"], 16)
            nc.sync.wait_ge(sem("x_ready"), SP.due("x_ready", n=7))
            load(WC, d["wc"], "dma_wc")
            for b in range(B):
                for k in range(DEEP):
                    n0 = (b * KEY_TILES + k) * P
                    nc.sync.wait_ge(sem("l3x_gathered"), SP.due("l3x_gathered", lag=DEEP))
                    sync.dma_start(CTT[:, k, :], d["ctxT"][:, n0:n0 + P]).then_inc(sem("dma_ktile%d" % k), 16)
                    sync.dma_start(CKT[:, k, :], d["ctxr"][n0:n0 + P, :]).then_inc(sem("dma_ktile%d" % k), 16)
                with SP.loop(TILE_GROUPS - 1, seen=[("l3x_gathered", DEEP)]) as i:
                    for k in range(DEEP):
                        n0 = i * DEEP * P + ((b * KEY_TILES + DEEP + k) * P)
                        nc.sync.wait_ge(sem("l3x_gathered"), SP.due("l3x_gathered", lag=DEEP))
                        sync.dma_start(CTT[:, k, :], d["ctxT"][:, bass.ds(n0, P)]).then_inc(sem("dma_ktile%d" % k), 16)
                        sync.dma_start(CKT[:, k, :], d["ctxr"][bass.ds(n0, P), :]).then_inc(sem("dma_ktile%d" % k), 16)
            src = d["l3f_experts"]
            for p in range(PAIRS):
                k = p % 2
                nc.sync.wait_ge(sem("expert_out"), SP.due("expert_out", lag=2))
                load(EB[:, k, 0:3 * P], src[p * P:(p + 1) * P, :], "dma_expert%d" % k)
            sync.wait_ge(sem("x_ready"), 12)
            sync.dma_start(d["out"], X[:, :, :]).then_inc(sem("out_written"), 16)
            sync.wait_ge(sem("out_written"), 16)

        @block.gpsimd
        def _(gpsimd):
            def norm_pool():
                nc.gpsimd.wait_ge(sem("variance"), PO.due("variance"))
                nc.gpsimd.tensor_tensor(RSTD[:, :], VE[:, :], MHALF[:, :], ALU.pow).then_inc(sem("rstd"), PO.sends("rstd"))

            
            nc.gpsimd.memset(MHALF[:, :], -0.5).then_inc(sem("halves"), PO.sends("halves"))
            nc.gpsimd.wait_ge(sem("halves"), 1)
            norm_pool()

            
            nc.gpsimd.wait_ge(sem("x_ready"), PO.due("x_ready"))
            nc.gpsimd.memset(CB[:, :, 0:P + 2:P + 1], 0.0).then_inc(sem("l0a_pads"), PO.sends("l0a_pads"))
            norm_pool()
            norm_pool()
            for half in range(2):
                nc.gpsimd.wait_ge(sem("l0a_decay"), PO.due("l0a_decay"))
                cut = DA.rearrange("p (n t) -> p n t", t=P)[:, :, 0:1]
                nc.gpsimd.memset(cut, 0.0).then_inc(sem("l0a_decay_cut"), PO.sends("l0a_decay_cut"))

            
            norm_pool()

            
            norm_pool()

            
            norm_pool()

            
            norm_pool()

            norm_pool()

            
            norm_pool()
            norm_pool()

            norm_pool()

            
            norm_pool()
            norm_pool()
            nc.gpsimd.wait_ge(sem("l3x_null_square"), PO.due("l3x_null_square"))
            nc.gpsimd.tensor_tensor(NSS, NSS, MHALF[:, 0:1], ALU.pow).then_inc(sem("l3x_null_rnorm"), PO.sends("l3x_null_rnorm"))
            for b in range(B):
                def add(k, first=False):
                    nc.gpsimd.wait_ge(sem("l3x_probs"), PO.due("l3x_probs"))
                    if first:
                        nc.gpsimd.wait_ge(sem("l3x_l"), PO.due("l3x_l", lag=2))
                        nc.gpsimd.tensor_copy(LS[b % 2], PR[:, k % 2, :]).then_inc(sem("l3x_summed"), PO.sends("l3x_summed"))
                        nc.gpsimd.wait_ge(sem("l3x_summed"), PO.sent("l3x_summed"))
                    else:
                        nc.gpsimd.tensor_tensor(LS[b % 2], LS[b % 2], PR[:, k % 2, :], ALU.add)\
                            .then_inc(sem("l3x_summed"), PO.sends("l3x_summed"))
                        nc.gpsimd.wait_ge(sem("l3x_summed"), PO.sent("l3x_summed"))

                for k in range(DEEP):
                    add(k, first=k == 0)
                with PO.loop(TILE_GROUPS - 1, made=[("l3x_summed", 4)], seen=[("l3x_probs", 4)]):
                    for k in range(DEEP):
                        add(k)
            norm_pool()

            
            norm_pool()
            norm_pool()

            
            norm_pool()

        @block.scalar
        def _(scalar):
            def turn_act(dst, scale=1.0, bias=0.0):
                nc.scalar.wait_ge(sem("turned"), AC.due("turned"))
                act(dst[:, :], bank(0), ACT.Identity, scale=scale, bias=bias).then_inc(sem("turned_kept"), AC.sends("turned_kept"))

            def key_norms_act(n0, n):
                for m in range(n0, n0 + n):
                    nc.scalar.wait_ge(sem("key_rows"), AC.due("key_rows"))
                    nc.scalar.wait_ge(sem("key_norm"), AC.due("key_norm", lag=2))
                    act(SQ[:, m % 2, :], bank(5 + 2 * (m % 2)), ACT.Square).then_inc(sem("key_squares"), AC.sends("key_squares"))

            def core_act(groups, scale, norms_from=None):
                for g in range(groups):
                    nc.scalar.wait_ge(sem("scores_shifted"), AC.due("scores_shifted"))
                    act(SX[:, g % 2, :], SX[:, g % 2, :], ACT.Exp, scale=scale).then_inc(sem("probs"), AC.sends("probs"))
                    if norms_from is not None:
                        key_norms_act(norms_from + 4 * g, 2)
                    nc.scalar.wait_ge(sem("probs_turned"), AC.due("probs_turned"))
                    nc.scalar.wait_ge(sem("values_summed"), AC.due("values_summed", lag=2))
                    act(PT[:, g % 2, :], bank(3 + g % 2), ACT.Copy).then_inc(sem("pt_ready"), AC.sends("pt_ready"))
                    if norms_from is not None:
                        key_norms_act(norms_from + 4 * g + 2, 2)

            def long_act(scale, masked):
                for b in range(B):
                    nc.scalar.wait_ge(sem("long_shift"), AC.due("long_shift"))
                    src = SL[:, b % 2, :] if masked else PSUM[:, 0:4, :].rearrange("p c n -> p (c n)")
                    act(SL[:, b % 2, :], src, ACT.Exp, scale=scale, bias=LNM[:, b:b + 1],
                        accum_out=LSUM[:, b:b + 1]).then_inc(sem("long_probs"), AC.sends("long_probs"))
                    for c in range(4):
                        nc.scalar.wait_ge(sem("long_turned"), AC.due("long_turned"))
                        act(PTL[:, 4 * c:4 * c + 4, :], bank4(4 + c % 2), ACT.Copy).then_inc(sem("long_pt"), AC.sends("long_pt"))
                    nc.scalar.wait_ge(sem("long_z"), AC.due("long_z"))
                    act(ZT[:, b * P:(b + 1) * P], PSUM[:, 6, 0:P], ACT.Copy).then_inc(sem("long_z_kept"), AC.sends("long_z_kept"))

            def experts_act(n, bias):
                def keep(k):
                    nc.scalar.wait_ge(sem("expert_out"), AC.due("expert_out", lag=2))
                    for c in range(FC):
                        nc.scalar.wait_ge(sem("hidden"), AC.due("hidden"))
                        b1 = EB[:, k, 2 * FF + c:2 * FF + c + 1] if bias else 0.0
                        act(HB[:, k, c, :], bank(1 + c % 2), ACT.Relu, bias=b1).then_inc(sem("hidden_kept"), AC.sends("hidden_kept"))

                keep(0)
                keep(1)
                with AC.loop(n // 2 - 1, made=[("hidden_kept", 2 * FC)], seen=[("hidden", 2 * FC), ("expert_out", 2)]):
                    keep(0)
                    keep(1)

            def context_keys_act(dst, bias, m=P):
                for c in range(NK // 512):
                    nc.scalar.wait_ge(sem("context_keys"), AC.due("context_keys"))
                    act(dst[0:m, c * 512:(c + 1) * 512], bank(1 + c % 2, m), ACT.Identity, bias=bias)\
                        .then_inc(sem("context_keys_kept"), AC.sends("context_keys_kept"))

            
            nc.scalar.wait_ge(sem("dma_wa"), AC.due("dma_wa"))
            context_keys_act(KS, w("l0x_bk"))
            turn_act(HT)
            nc.scalar.wait_ge(sem("q_rows"), AC.due("q_rows"))
            act(QT[:, :], bank(5), ACT.Identity, bias=w("l0x_bq")).then_inc(sem("l0x_q_kept"), AC.sends("l0x_q_kept"))
            core_act(16, HD ** -0.5, norms_from=0)
            turn_act(OT)

            
            nc.scalar.wait_ge(sem("dma_wb"), AC.due("dma_wb"))
            turn_act(HT, scale=w("l0a_g"), bias=w("l0a_b"))
            act(ANEG, w("l0a_Alog"), ACT.Exp).then_inc(sem("l0a_expA"), AC.sends("l0a_expA"))
            nc.scalar.wait_ge(sem("l0a_x1"), AC.due("l0a_x1"))
            act(CB[:, :, 1:P + 1], bank4(1), ACT.Identity, bias=w("l0a_w1b"))\
                .then_inc(sem("l0a_x1_kept"), AC.sends("l0a_x1_kept"))
            nc.scalar.wait_ge(sem("l0a_preact"), AC.due("l0a_preact"))
            act(OT[:, :], CONV, ACT.Tanh, scale=0.5).then_inc(sem("l0a_tanh"), AC.sends("l0a_tanh"))
            nc.scalar.wait_ge(sem("l0a_preact"), AC.due("l0a_preact"))
            act(TMP[:, :], VG, ACT.Tanh, scale=0.5).then_inc(sem("l0a_tanh"), AC.sends("l0a_tanh"))
            nc.scalar.wait_ge(sem("l0a_preact"), AC.due("l0a_preact"))
            act(EB1, ZB, ACT.Abs).then_inc(sem("act_step"), AC.sends("act_step"))
            nc.scalar.wait_ge(sem("act_step"), AC.sent("act_step"))
            act(EB1, EB1, ACT.Exp, scale=-1.0).then_inc(sem("act_step"), AC.sends("act_step"))
            nc.scalar.wait_ge(sem("act_step"), AC.sent("act_step"))
            act(EB1, EB1, ACT.Ln, bias=1.0).then_inc(sem("l0a_log"), AC.sends("l0a_log"))
            nc.scalar.wait_ge(sem("l0a_dt_ready"), AC.due("l0a_dt_ready"))
            for half in range(2):
                if half:
                    nc.scalar.wait_ge(sem("l0a_scan"), AC.due("l0a_scan"))
                for n in range(8):
                    last = act(DA[:, n * 512:(n + 1) * 512], DT, ACT.Exp, scale=ANEG[:, half * 8 + n:half * 8 + n + 1])
                last.then_inc(sem("l0a_decay"), AC.sends("l0a_decay"))

            
            turn_act(HT)
            nc.scalar.wait_ge(sem("gate_shifted"), AC.due("gate_shifted"))
            act(GX[:, 0:32], GX[:, 0:32], ACT.Exp).then_inc(sem("gate_exp"), AC.sends("gate_exp"))
            experts_act(8, True)
            nc.scalar.wait_ge(sem("l0f_gates_turned"), AC.due("l0f_gates_turned"))
            act(GT[0:8, :], bank(6, 8), ACT.Copy).then_inc(sem("l0f_gates_kept"), AC.sends("l0f_gates_kept"))

            
            nc.scalar.wait_ge(sem("x_ready"), AC.due("x_ready", n=3))
            context_keys_act(KT, w("l1x_bkh", HD), HD)
            turn_act(HT)
            nc.scalar.wait_ge(sem("q_rows"), AC.due("q_rows"))
            act(TMP[:, :], bank(5), ACT.Copy).then_inc(sem("q_rows_kept"), AC.sends("q_rows_kept"))
            long_act(1.0, True)
            turn_act(OT)

            def pieces_act(part, dst):
                for j in range(H):
                    nc.scalar.wait_ge(sem("pieces"), AC.due("pieces"))
                    act(dst[0:HD, :].rearrange("p (t j) -> p t j", j=H)[:, :, j], bank(3 + j % 4, HD), ACT.Identity,
                        bias=w("l1a_bqkv", HD)[:, part * H + j:part * H + j + 1])\
                        .then_inc(sem("pieces_kept"), AC.sends("pieces_kept"))

            
            turn_act(HT)
            pieces_act(2, KS)
            pieces_act(0, QS)
            nc.scalar.wait_ge(sem("l1a_v"), AC.due("l1a_v"))
            pieces_act(1, KS)
            core_act(16, HD ** -0.5, norms_from=64)
            turn_act(OT)

            
            turn_act(HT)
            for k in range(2):
                nc.scalar.wait_ge(sem("l1f_enc"), AC.due("l1f_enc"))
                act(ENC[:, k, :], bank(1 + k), ACT.Relu, bias=w("l1f_benc")[:, k:k + 1])\
                    .then_inc(sem("l1f_enc_kept"), AC.sends("l1f_enc_kept"))
            for k in range(4):
                nc.scalar.wait_ge(sem("l1f_mid"), AC.due("l1f_mid"))
                act(MID[:, k, :], bank(1 + k % 2), ACT.Relu, bias=w("l1f_bdown")[:, k:k + 1])\
                    .then_inc(sem("l1f_mid_kept"), AC.sends("l1f_mid_kept"))

            nc.scalar.wait_ge(sem("x_ready"), AC.due("x_ready", n=3))
            context_keys_act(KT, w("l2x_bk"))
            turn_act(HT)
            nc.scalar.wait_ge(sem("q_rows"), AC.due("q_rows"))
            act(QT[:, :], bank(5), ACT.Identity, bias=w("l2x_bq")).then_inc(sem("q_rows_kept"), AC.sends("q_rows_kept"))
            long_act(P ** -0.5, False)

            
            turn_act(HT)
            nc.scalar.wait_ge(sem("l2a_mm"), AC.due("l2a_mm"))
            act(XP, bank(1), ACT.Identity, bias=w("l2a_bin")).then_inc(sem("l2a_kept"), AC.sends("l2a_kept"))
            nc.scalar.wait_ge(sem("l2a_mm"), AC.due("l2a_mm"))
            act(XB, bank(2), ACT.Identity, bias=w("l2a_bB")).then_inc(sem("l2a_kept"), AC.sends("l2a_kept"))
            nc.scalar.wait_ge(sem("l2a_mm"), AC.due("l2a_mm", n=2))
            nc.scalar.wait_ge(sem("l2a_halves"), AC.due("l2a_halves"))
            act(IG[0:16, :], bank(3, 16), ACT.Tanh, scale=0.5, bias=SM[0:16, 0:1])
            act(FG[0:16, :], bank(4, 16), ACT.Tanh, scale=0.5, bias=SM[0:16, 1:2])\
                .then_inc(sem("l2a_gates"), AC.sends("l2a_gates"))
            nc.scalar.wait_ge(sem("l2a_mm"), AC.due("l2a_mm", n=2))
            act(YT, bank(6), ACT.Tanh, bias=w("l2a_bD")).then_inc(sem("l2a_kept"), AC.sends("l2a_kept"))

            turn_act(HT)
            nc.scalar.wait_ge(sem("gate_shifted"), AC.due("gate_shifted"))
            act(GX, GX, ACT.Exp).then_inc(sem("gate_exp"), AC.sends("gate_exp"))
            experts_act(16, False)

            
            turn_act(HT, scale=w("l3x_gn"))
            nc.scalar.wait_ge(sem("key_squares_all"), AC.due("key_squares_all"))
            act(RK[:, :], RK[:, :], ACT.Sqrt).then_inc(sem("l3x_norms"), AC.sends("l3x_norms"))
            for b in range(B):
                nc.scalar.wait_ge(sem("l3x_q"), AC.due("l3x_q"))
                src = PSUM[:, 2 * (b % 2) + 1:2 * (b % 2) + 3, :].rearrange("p c n -> p (c n)")
                act(QN[:, b, :], src, ACT.Copy).then_inc(sem("l3x_q_kept"), AC.sends("l3x_q_kept"))
            nc.scalar.wait_ge(sem("l3x_q_squares"), AC.due("l3x_q_squares"))
            act(QSS, QSS, ACT.Sqrt).then_inc(sem("l3x_norms"), AC.sends("l3x_norms"))
            nc.scalar.wait_ge(sem("l3x_b_squares"), AC.due("l3x_b_squares"))
            act(BN, BN, ACT.Sqrt).then_inc(sem("l3x_norms"), AC.sends("l3x_norms"))
            for c in range(8):
                nc.scalar.wait_ge(sem("l3x_qT"), AC.due("l3x_qT"))
                act(QSC[:, c, :], bank(1 + c % 2), ACT.Copy).then_inc(sem("l3x_qT_kept"), AC.sends("l3x_qT_kept"))
            nc.scalar.wait_ge(sem("l3x_shift_ready"), AC.due("l3x_shift_ready"))
            act(PN, PN, ACT.Exp, bias=NBTOP).then_inc(sem("l3x_null"), AC.sends("l3x_null"))
            qph = QP.rearrange("p (b h n) -> p h b n", b=B, h=H)
            for h in range(H):
                nc.scalar.wait_ge(sem("l3x_qp"), AC.due("l3x_qp"))
                act(qph[:, h, :, :], bank4(1 + h % 2), ACT.Copy).then_inc(sem("l3x_qp_kept"), AC.sends("l3x_qp_kept"))

            def probs(k):
                nc.scalar.wait_ge(sem("l3x_scores_taken"), AC.due("l3x_scores_taken", n=4))
                act(PR[:, k % 2, :], PR[:, k % 2, :], ACT.Exp, bias=NBTOP).then_inc(sem("l3x_probs"), AC.sends("l3x_probs"))

            def finish_turn():
                nc.scalar.wait_ge(sem("l3x_oT"), AC.due("l3x_oT"))
                act(OT8, PSUM[:, 2:4, :].rearrange("p c n -> p (c n)"), ACT.Copy)\
                    .then_inc(sem("l3x_oT_kept"), AC.sends("l3x_oT_kept"))

            for b in range(B):
                for k in range(DEEP):
                    probs(k)
                if b:
                    finish_turn()
                with AC.loop(TILE_GROUPS - 1, made=[("l3x_probs", 4)], seen=[("l3x_scores_taken", 16)]):
                    for k in range(DEEP):
                        probs(k)
                nc.scalar.wait_ge(sem("l3x_gathered"), AC.due("l3x_gathered", n=KEY_TILES))
                act(ZS, PSUM[:, 4:8, :].rearrange("p c n -> p (c n)"), ACT.Copy).then_inc(sem("l3x_z_kept"), AC.sends("l3x_z_kept"))
            finish_turn()

            
            turn_act(HT)
            nc.scalar.wait_ge(sem("l3a_qk"), AC.due("l3a_qk"))
            act(QT[:, :], bank(5), ACT.Copy).then_inc(sem("l3a_qk_kept"), AC.sends("l3a_qk_kept"))
            nc.scalar.wait_ge(sem("l3a_qk"), AC.due("l3a_qk"))
            act(KT3, bank(6), ACT.Copy).then_inc(sem("l3a_qk_kept"), AC.sends("l3a_qk_kept"))
            core_act(1, P ** -0.5)
            turn_act(OT, scale=w("l3a_gamma"), bias=w("l3a_beta"))

            
            turn_act(HT)
            nc.scalar.wait_ge(sem("logits"), AC.due("logits", n=3))
            act(LG, PSUM[:, 5, 0:64], ACT.Tanh, scale=0.5).then_inc(sem("l3f_scores"), AC.sends("l3f_scores"))
            for p in range(PAIRS):
                k = p % 2
                nc.scalar.wait_ge(sem("l3f_up"), AC.due("l3f_up"))
                nc.scalar.wait_ge(sem("l3f_h"), AC.due("l3f_h", lag=2))
                act(TG[:, k, :], bank(1 + 2 * k), ACT.Tanh, scale=0.5).then_inc(sem("l3f_tanh"), AC.sends("l3f_tanh"))

        @block.vector
        def _(vector):
            def norm_dve(src, turned=True):
                for b in range(B):
                    last = ve.bn_stats(ST[:, b, :], src[:, b, :])
                last.then_inc(sem("dve_step"), DV.sends("dve_step"))
                nc.vector.wait_ge(sem("dve_step"), DV.sent("dve_step"))
                for b in range(B):
                    last = ve.bn_aggr(MV[:, b, :], ST[:, b, :])
                last.then_inc(sem("dve_step"), DV.sends("dve_step"))
                nc.vector.wait_ge(sem("dve_step"), DV.sent("dve_step"))
                ve.tensor_scalar(VE[:, :], MV[:, :, 1], EPS, None, ALU.add).then_inc(sem("variance"), DV.sends("variance"))
                nc.vector.wait_ge(sem("rstd"), DV.due("rstd"))
                for b in range(B):
                    last = ve.tensor_scalar(HN[:, b, :], src[:, b, :], MV[:, b, 0:1], RSTD[:, b:b + 1],
                                            ALU.subtract, ALU.mult)
                signal = "tokens_ready" if turned else "dve_step"
                last.then_inc(sem(signal), DV.sends(signal))
                nc.vector.wait_ge(sem(signal), DV.sent(signal))

            def tail_dve(bias_row=None):
                nc.vector.wait_ge(sem("block_out"), DV.due("block_out"))
                if bias_row is not None:
                    ve.tensor_tensor(ACC[:, :, :], bank4(7), over(bias_row, B), ALU.add).then_inc(sem("dve_step"), DV.sends("dve_step"))
                    nc.vector.wait_ge(sem("dve_step"), DV.sent("dve_step"))
                    ve.tensor_tensor(X[:, :, :], X[:, :, :], ACC[:, :, :], ALU.add).then_inc(sem("x_ready"), DV.sends("x_ready"))
                    nc.vector.wait_ge(sem("x_ready"), DV.sent("x_ready"))
                else:
                    ve.tensor_tensor(X[:, :, :], X[:, :, :], bank4(7), ALU.add).then_inc(sem("x_ready"), DV.sends("x_ready"))
                    nc.vector.wait_ge(sem("x_ready"), DV.sent("x_ready"))

            def key_norms_dve(n0, n):
                for m in range(n0, n0 + n):
                    nc.vector.wait_ge(sem("key_squares"), DV.due("key_squares"))
                    ve.tensor_reduce(RK[:, m * 8:(m + 1) * 8], SQ[:, m % 2, :].rearrange("p (h e) -> p h e", e=DH),
                                     AX.X, ALU.add).then_inc(sem("key_norm"), DV.sends("key_norm"))

            def core_dve(groups, causal=None, norms_from=None):
                def shift(g):
                    nc.vector.wait_ge(sem("scores"), DV.due("scores"))
                    s = PSUM[:, 1 + g % 2, :].rearrange("p (j n) -> p j n", j=4)
                    sx = SX[:, g % 2, :].rearrange("p (j n) -> p j n", j=4)
                    nc.vector.wait_ge(sem("probs_turned"), DV.due("probs_turned", lag=2))
                    if g >= 2:
                        nc.vector.wait_ge(sem("probs_totalled"), DV.sent("probs_totalled"))
                    if causal is not None:
                        ve.tensor_tensor(sx, s, over(causal, 4), ALU.add).then_inc(sem("dve_step"), DV.sends("dve_step"))
                        nc.vector.wait_ge(sem("dve_step"), DV.sent("dve_step"))
                        ve.tensor_reduce(MX[:, g % 2, :], sx, AX.X, ALU.max).then_inc(sem("dve_step"), DV.sends("dve_step"))
                        nc.vector.wait_ge(sem("dve_step"), DV.sent("dve_step"))
                        ve.tensor_tensor(sx, sx, each(MX[:, g % 2, :], P), ALU.subtract)\
                            .then_inc(sem("scores_shifted"), DV.sends("scores_shifted"))
                    else:
                        ve.tensor_reduce(MX[:, g % 2, :], s, AX.X, ALU.max).then_inc(sem("dve_step"), DV.sends("dve_step"))
                        nc.vector.wait_ge(sem("dve_step"), DV.sent("dve_step"))
                        ve.tensor_tensor(sx, s, each(MX[:, g % 2, :], P), ALU.subtract)\
                            .then_inc(sem("scores_shifted"), DV.sends("scores_shifted"))

                def total(g):
                    nc.vector.wait_ge(sem("probs"), DV.due("probs"))
                    sx = SX[:, g % 2, :].rearrange("p (j n) -> p j n", j=4)
                    ve.tensor_reduce(L_SUM[:, 4 * g:4 * g + 4], sx, AX.X, ALU.add)\
                        .then_inc(sem("probs_totalled"), DV.sends("probs_totalled"))

                shift(0)
                for g in range(groups):
                    if g + 1 < groups:
                        shift(g + 1)
                    total(g)
                    if norms_from is not None:
                        key_norms_dve(norms_from + 4 * g, 4)
                nc.vector.wait_ge(sem("probs_totalled"), DV.sent("probs_totalled"))
                ve.reciprocal(L_INV[:, 0:4 * groups], L_SUM[:, 0:4 * groups]).then_inc(sem("dve_step"), DV.sends("dve_step"))
                nc.vector.wait_ge(sem("dve_step"), DV.sent("dve_step"))

            def experts_dve(n, width):
                ve.memset(EACC[:, :, :], 0.0).then_inc(sem("dve_step"), DV.sends("dve_step"))
                nc.vector.wait_ge(sem("dve_step"), DV.sent("dve_step"))
                base = DV.made.get("dve_step", 0)
                with DV.loop(n // 2, made=[("expert_added", 2)], seen=[("expert_out", 2)]) as i:
                    for k in range(2):
                        nc.vector.wait_ge(sem("expert_out"), DV.due("expert_out"))
                        for b in range(B):
                            g = GATE[:, bass.ds(2 * i + (k + b * width), 1)]
                            last = ve.scalar_tensor_tensor(out=EACC[:, b, :], in0=PSUM[:, 3 + k, b * P:(b + 1) * P],
                                                           scalar=g, in1=EACC[:, b, :], op0=ALU.mult, op1=ALU.add)
                        last.then_inc(sem("expert_added"), DV.sends("expert_added"))
                        nc.vector.wait_ge(sem("expert_added"), DV.sent("expert_added"))

            
            nc.vector.wait_ge(sem("dma_x"), DV.due("dma_x"))
            nc.vector.wait_ge(sem("dma_wa"), DV.due("dma_wa"))
            nc.vector.wait_ge(sem("dma_rows"), DV.due("dma_rows"))
            norm_dve(X)
            nc.vector.wait_ge(sem("l0x_v"), DV.due("l0x_v"))
            ve.tensor_tensor(VS.rearrange("p (b f) -> p b f", b=B), bank4(3), over(row("l0x_bv"), B), ALU.add)\
                .then_inc(sem("dve_step"), DV.sends("dve_step"))
            nc.vector.wait_ge(sem("dve_step"), DV.sent("dve_step"))
            nc.vector.wait_ge(sem("l0x_q_kept"), DV.due("l0x_q_kept"))
            for h in range(H):
                last = ve.tensor_scalar(QM[:, h, :], QT[:, :], w("headmask")[:, h:h + 1], None, ALU.mult)
            last.then_inc(sem("l0x_q_heads"), DV.sends("l0x_q_heads"))
            nc.vector.wait_ge(sem("l0x_q_heads"), DV.sent("l0x_q_heads"))
            core_dve(16, norms_from=0)
            nc.vector.wait_ge(sem("values_summed"), DV.due("values_summed", n=16))
            o = ACC[:, :, :].rearrange("p b (h e) -> p (b h) e", h=H)
            ve.tensor_tensor(o, PSUM[:, 6, :].rearrange("p (a e) -> p a e", e=HD), each(L_INV, HD), ALU.mult)\
                .then_inc(sem("tokens_ready"), DV.sends("tokens_ready"))
            nc.vector.wait_ge(sem("tokens_ready"), DV.sent("tokens_ready"))
            tail_dve(row("l0x_bo"))

            
            nc.vector.wait_ge(sem("dma_wb"), DV.due("dma_wb"))
            norm_dve(X, turned=False)
            norm_dve(HN)
            nc.vector.wait_ge(sem("l0a_expA"), DV.due("l0a_expA"))
            ve.tensor_scalar(ANEG, ANEG, -1.0, None, ALU.mult).then_inc(sem("l0a_A"), DV.sends("l0a_A"))
            nc.vector.wait_ge(sem("l0a_A"), DV.sent("l0a_A"))
            nc.vector.wait_ge(sem("l0a_x1_kept"), DV.due("l0a_x1_kept"))
            nc.vector.wait_ge(sem("l0a_pads"), DV.due("l0a_pads"))
            conv = CONV.rearrange("p (b t) -> p b t", b=B)
            ve.tensor_scalar(conv, CB[:, :, 0:P], w("l0a_conv")[:, 0:1], None, ALU.mult)\
                .then_inc(sem("dve_step"), DV.sends("dve_step"))
            nc.vector.wait_ge(sem("dve_step"), DV.sent("dve_step"))
            ve.scalar_tensor_tensor(out=conv, in0=CB[:, :, 1:P + 1], scalar=w("l0a_conv")[:, 1:2], in1=conv,
                                    op0=ALU.mult, op1=ALU.add).then_inc(sem("dve_step"), DV.sends("dve_step"))
            nc.vector.wait_ge(sem("dve_step"), DV.sent("dve_step"))
            ve.scalar_tensor_tensor(out=conv, in0=CB[:, :, 2:P + 2], scalar=w("l0a_conv")[:, 2:3], in1=conv,
                                    op0=ALU.mult, op1=ALU.add)\
                .then_inc(sem("l0a_preact"), DV.sends("l0a_preact"))
            nc.vector.wait_ge(sem("l0a_preact"), DV.sent("l0a_preact"))
            nc.vector.wait_ge(sem("l0a_v"), DV.due("l0a_v"))
            ve.tensor_scalar(VG, bank(2), w("l0a_v1b"), None, ALU.add).then_inc(sem("l0a_preact"), DV.sends("l0a_preact"))
            nc.vector.wait_ge(sem("l0a_preact"), DV.sent("l0a_preact"))
            nc.vector.wait_ge(sem("l0a_tanh"), DV.due("l0a_tanh"))
            ve.scalar_tensor_tensor(out=U, in0=OT[:, :], scalar=1.0, in1=CONV, op0=ALU.add, op1=ALU.mult)\
                .then_inc(sem("dve_step"), DV.sends("dve_step"))
            nc.vector.wait_ge(sem("dve_step"), DV.sent("dve_step"))
            ve.tensor_scalar(U, U, 0.5, None, ALU.mult).then_inc(sem("l0a_u"), DV.sends("l0a_u"))
            nc.vector.wait_ge(sem("l0a_u"), DV.sent("l0a_u"))
            nc.vector.wait_ge(sem("l0a_tanh"), DV.due("l0a_tanh"))
            ve.scalar_tensor_tensor(out=VG, in0=TMP[:, :], scalar=1.0, in1=VG, op0=ALU.add, op1=ALU.mult)\
                .then_inc(sem("dve_step"), DV.sends("dve_step"))
            nc.vector.wait_ge(sem("dve_step"), DV.sent("dve_step"))
            nc.vector.wait_ge(sem("l0a_dt"), DV.due("l0a_dt"))
            ve.tensor_scalar(ZB, bank(3), w("l0a_bdt"), None, ALU.add).then_inc(sem("l0a_preact"), DV.sends("l0a_preact"))
            nc.vector.wait_ge(sem("l0a_preact"), DV.sent("l0a_preact"))
            nc.vector.wait_ge(sem("l0a_log"), DV.due("l0a_log"))
            ve.scalar_tensor_tensor(out=DT, in0=ZB, scalar=0.0, in1=EB1, op0=ALU.max, op1=ALU.add)\
                .then_inc(sem("l0a_dt_ready"), DV.sends("l0a_dt_ready"))
            nc.vector.wait_ge(sem("l0a_dt_ready"), DV.sent("l0a_dt_ready"))
            ve.tensor_tensor(DTU, DT, U, ALU.mult).then_inc(sem("dve_step"), DV.sends("dve_step"))
            nc.vector.wait_ge(sem("dve_step"), DV.sent("dve_step"))
            for half, y in enumerate((Y0, Y1)):
                for n in range(8):
                    nc.vector.wait_ge(sem("l0a_bc"), DV.due("l0a_bc"))
                    ve.tensor_tensor(DBU[:, n * 512:(n + 1) * 512], bank(4 + (n + half * 16) % 3), DTU, ALU.mult)\
                        .then_inc(sem("l0a_bc_taken"), DV.sends("l0a_bc_taken"))
                nc.vector.wait_ge(sem("l0a_bc_taken"), DV.sent("l0a_bc_taken"))
                nc.vector.wait_ge(sem("l0a_decay_cut"), DV.due("l0a_decay_cut"))
                ve.tensor_tensor_scan(HS, DA, DBU, 0.0, ALU.mult, ALU.add).then_inc(sem("l0a_scan"), DV.sends("l0a_scan"))
                nc.vector.wait_ge(sem("l0a_scan"), DV.sent("l0a_scan"))
                for n in range(8):
                    nc.vector.wait_ge(sem("l0a_bc"), DV.due("l0a_bc"))
                    ve.tensor_tensor(DBU[:, n * 512:(n + 1) * 512], HS[:, n * 512:(n + 1) * 512],
                                     bank(4 + (n + 8 + half * 16) % 3), ALU.mult)\
                        .then_inc(sem("l0a_bc_taken"), DV.sends("l0a_bc_taken"))
                nc.vector.wait_ge(sem("l0a_bc_taken"), DV.sent("l0a_bc_taken"))
                ve.tensor_reduce(y, DBU.rearrange("p (n t) -> p t n", n=8), AX.X, ALU.add)\
                    .then_inc(sem("dve_step"), DV.sends("dve_step"))
                nc.vector.wait_ge(sem("dve_step"), DV.sent("dve_step"))
            ve.tensor_tensor(Y0, Y0, Y1, ALU.add).then_inc(sem("dve_step"), DV.sends("dve_step"))
            nc.vector.wait_ge(sem("dve_step"), DV.sent("dve_step"))
            ve.scalar_tensor_tensor(out=Y0, in0=U, scalar=w("l0a_D"), in1=Y0, op0=ALU.mult, op1=ALU.add)\
                .then_inc(sem("dve_step"), DV.sends("dve_step"))
            nc.vector.wait_ge(sem("dve_step"), DV.sent("dve_step"))
            ve.scalar_tensor_tensor(out=OT[:, :], in0=Y0, scalar=0.5, in1=VG, op0=ALU.mult, op1=ALU.mult)\
                .then_inc(sem("l0a_y"), DV.sends("l0a_y"))
            nc.vector.wait_ge(sem("l0a_y"), DV.sent("l0a_y"))
            tail_dve(row("l0a_w2b"))

            
            norm_dve(X)
            nc.vector.wait_ge(sem("logits"), DV.due("logits"))
            ve.tensor_copy(LG[:, 0:32], PSUM[:, 5, 0:32]).then_inc(sem("dve_step"), DV.sends("dve_step"))
            nc.vector.wait_ge(sem("dve_step"), DV.sent("dve_step"))
            lg = LG[:, 0:32].rearrange("p (b e) -> p b e", b=B)
            gx = GX[:, 0:32].rearrange("p (b e) -> p b e", b=B)
            for b in range(B):
                last = ve.max(M8[:, b, :], lg[:, b, :])
            last.then_inc(sem("dve_step"), DV.sends("dve_step"))
            nc.vector.wait_ge(sem("dve_step"), DV.sent("dve_step"))
            ve.tensor_tensor(gx, lg, M8[:, :, 0:1].broadcast_to([P, B, 8]), ALU.subtract)\
                .then_inc(sem("gate_shifted"), DV.sends("gate_shifted"))
            nc.vector.wait_ge(sem("gate_shifted"), DV.sent("gate_shifted"))
            ve.tensor_tensor(lg, lg, M8[:, :, 1:2].broadcast_to([P, B, 8]), ALU.is_ge)\
                .then_inc(sem("dve_step"), DV.sends("dve_step"))
            nc.vector.wait_ge(sem("dve_step"), DV.sent("dve_step"))
            nc.vector.wait_ge(sem("gate_exp"), DV.due("gate_exp"))
            ve.tensor_tensor(gx, gx, lg, ALU.mult).then_inc(sem("dve_step"), DV.sends("dve_step"))
            nc.vector.wait_ge(sem("dve_step"), DV.sent("dve_step"))
            ve.tensor_reduce(GS, gx, AX.X, ALU.add).then_inc(sem("dve_step"), DV.sends("dve_step"))
            nc.vector.wait_ge(sem("dve_step"), DV.sent("dve_step"))
            ve.reciprocal(GS, GS).then_inc(sem("dve_step"), DV.sends("dve_step"))
            nc.vector.wait_ge(sem("dve_step"), DV.sent("dve_step"))
            ve.tensor_tensor(GATE[:, 0:32].rearrange("p (b e) -> p b e", b=B), gx, each(GS, 8), ALU.mult)\
                .then_inc(sem("l0f_gates"), DV.sends("l0f_gates"))
            nc.vector.wait_ge(sem("l0f_gates"), DV.sent("l0f_gates"))
            experts_dve(8, 8)
            nc.vector.wait_ge(sem("block_out"), DV.due("block_out"))
            ve.tensor_tensor(EACC[:, :, :], EACC[:, :, :], bank4(7), ALU.add).then_inc(sem("dve_step"), DV.sends("dve_step"))
            nc.vector.wait_ge(sem("dve_step"), DV.sent("dve_step"))
            ve.tensor_tensor(X[:, :, :], X[:, :, :], EACC[:, :, :], ALU.add).then_inc(sem("x_ready"), DV.sends("x_ready"))
            nc.vector.wait_ge(sem("x_ready"), DV.sent("x_ready"))

            
            nc.vector.wait_ge(sem("dma_mask"), DV.due("dma_mask"))
            ve.tensor_copy(NEG, MASK8[:, :]).then_inc(sem("dve_step"), DV.sends("dve_step"))
            nc.vector.wait_ge(sem("dve_step"), DV.sent("dve_step"))
            ve.tensor_scalar(KEEP, NEG, -1.0, 1.0, ALU.mult, ALU.add).then_inc(sem("dve_step"), DV.sends("dve_step"))
            nc.vector.wait_ge(sem("dve_step"), DV.sent("dve_step"))
            ve.tensor_scalar(NEG, NEG, MASKED, None, ALU.mult).then_inc(sem("dve_step"), DV.sends("dve_step"))
            nc.vector.wait_ge(sem("dve_step"), DV.sent("dve_step"))
            nc.vector.wait_ge(sem("l1x_fold"), DV.due("l1x_fold", n=2))
            ve.tensor_copy(SM[:, 448:464], PSUM[:, 3, 0:2 * HD]).then_inc(sem("l1x_folded"), DV.sends("l1x_folded"))
            nc.vector.wait_ge(sem("l1x_folded"), DV.sent("l1x_folded"))
            norm_dve(X)
            nc.vector.wait_ge(sem("l1x_qh"), DV.due("l1x_qh"))
            ve.tensor_scalar(QT[0:HD, :], bank(6, HD), w("l1x_bqh", HD), HD ** -0.5, ALU.add, ALU.mult)\
                .then_inc(sem("l1x_qh_kept"), DV.sends("l1x_qh_kept"))
            nc.vector.wait_ge(sem("l1x_qh_kept"), DV.sent("l1x_qh_kept"))
            for b in range(B):
                nc.vector.wait_ge(sem("long_scores"), DV.due("long_scores"))
                s = SL[:, b % 2, :]
                ve.tensor_tensor(s, PSUM[:, 0:4, :].rearrange("p c n -> p (c n)"), KEEP, ALU.mult)\
                    .then_inc(sem("dve_step"), DV.sends("dve_step"))
                nc.vector.wait_ge(sem("dve_step"), DV.sent("dve_step"))
                ve.tensor_tensor(s, s, NEG, ALU.add).then_inc(sem("dve_step"), DV.sends("dve_step"))
                nc.vector.wait_ge(sem("dve_step"), DV.sent("dve_step"))
                ve.tensor_reduce(LMX[:, b:b + 1], s, AX.X, ALU.max).then_inc(sem("dve_step"), DV.sends("dve_step"))
                nc.vector.wait_ge(sem("dve_step"), DV.sent("dve_step"))
                ve.tensor_scalar(LNM[:, b:b + 1], LMX[:, b:b + 1], -1.0, None, ALU.mult)\
                    .then_inc(sem("long_shift"), DV.sends("long_shift"))
                nc.vector.wait_ge(sem("long_shift"), DV.sent("long_shift"))
            nc.vector.wait_ge(sem("l1x_o"), DV.due("l1x_o"))
            ve.reciprocal(LINV, LSUM).then_inc(sem("dve_step"), DV.sends("dve_step"))
            nc.vector.wait_ge(sem("dve_step"), DV.sent("dve_step"))
            ve.tensor_tensor(OH8, PSUM[:, 5, 0:B * HD].rearrange("p (b e) -> p b e", b=B), each(LINV, HD), ALU.mult)\
                .then_inc(sem("dve_step"), DV.sends("dve_step"))
            nc.vector.wait_ge(sem("dve_step"), DV.sent("dve_step"))
            ve.tensor_tensor(OH8, OH8, over(row("l1x_bvh"), B), ALU.add).then_inc(sem("dve_step"), DV.sends("dve_step"))
            nc.vector.wait_ge(sem("dve_step"), DV.sent("dve_step"))
            for b in range(B):
                last = ve.tensor_copy(ACC[:, b, :].rearrange("p (h e) -> p h e", h=H), over(OH8[:, b, :], H))
            last.then_inc(sem("tokens_ready"), DV.sends("tokens_ready"))
            nc.vector.wait_ge(sem("tokens_ready"), DV.sent("tokens_ready"))
            tail_dve()

            
            norm_dve(X)
            nc.vector.wait_ge(sem("l1a_v"), DV.due("l1a_v"))
            ve.tensor_copy(VS, bank(1)).then_inc(sem("l1a_v_kept"), DV.sends("l1a_v_kept"))
            nc.vector.wait_ge(sem("l1a_v_kept"), DV.sent("l1a_v_kept"))
            core_dve(16, w("causal"), norms_from=64)
            nc.vector.wait_ge(sem("values_summed"), DV.due("values_summed", n=16))
            o = ACC[:, :, :].rearrange("p b (h e) -> p (b h) e", h=H)
            ve.tensor_tensor(o, PSUM[:, 6, :].rearrange("p (a e) -> p a e", e=HD), each(L_INV, HD), ALU.mult)\
                .then_inc(sem("tokens_ready"), DV.sends("tokens_ready"))
            nc.vector.wait_ge(sem("tokens_ready"), DV.sent("tokens_ready"))
            tail_dve(row("l1a_bproj"))

            
            norm_dve(X)
            nc.vector.wait_ge(sem("dma_idx"), DV.due("dma_idx"))
            ve.tensor_copy(IDXF, IDX[:, :]).then_inc(sem("dve_step"), DV.sends("dve_step"))
            nc.vector.wait_ge(sem("dve_step"), DV.sent("dve_step"))
            iota = row("iota")[:, 0:NA]
            ve.tensor_tensor(EQ, each(iota, NA), over(IDXF, NA), ALU.is_equal).then_inc(sem("dve_step"), DV.sends("dve_step"))
            nc.vector.wait_ge(sem("dve_step"), DV.sent("dve_step"))
            for n in range(NA):
                nc.vector.wait_ge(sem("l1f_recon"), DV.due("l1f_recon"))
                ve.scalar_tensor_tensor(out=DIFF[:, n % 2, :], in0=bank(3 + n % 2), scalar=w("l1f_bdec")[:, n:n + 1],
                                        in1=HT[:, :], op0=ALU.add, op1=ALU.subtract)\
                    .then_inc(sem("l1f_recon_taken"), DV.sends("l1f_recon_taken"))
                nc.vector.wait_ge(sem("l1f_recon_taken"), DV.sent("l1f_recon_taken"))
                ve.tensor_tensor(DIFF[:, n % 2, :], DIFF[:, n % 2, :], DIFF[:, n % 2, :], ALU.mult)\
                    .then_inc(sem("dve_step"), DV.sends("dve_step"))
                nc.vector.wait_ge(sem("dve_step"), DV.sent("dve_step"))
                last = ve.tensor_reduce(LOSS[:, :, n], DIFF[:, n % 2, :].rearrange("p (b t) -> p b t", b=B), AX.X, ALU.add)
            last.then_inc(sem("l1f_losses"), DV.sends("l1f_losses"))
            nc.vector.wait_ge(sem("l1f_losses"), DV.sent("l1f_losses"))
            nc.vector.wait_ge(sem("l1f_loss"), DV.due("l1f_loss"))
            loss = PSUM[:, 5, 0:32].rearrange("p (b n) -> p b n", b=B)
            ve.tensor_reduce(LMIN, loss, AX.X, ALU.min).then_inc(sem("dve_step"), DV.sends("dve_step"))
            nc.vector.wait_ge(sem("dve_step"), DV.sent("dve_step"))
            ve.tensor_tensor(SEL, loss, each(LMIN, NA), ALU.is_equal).then_inc(sem("dve_step"), DV.sends("dve_step"))
            nc.vector.wait_ge(sem("dve_step"), DV.sent("dve_step"))
            for b in range(B):
                last = ve.tensor_tensor(PICK[:, b, :, :], EQ, over(SEL[:, b, :], NA), ALU.mult)
            last.then_inc(sem("dve_step"), DV.sends("dve_step"))
            nc.vector.wait_ge(sem("dve_step"), DV.sent("dve_step"))
            ve.tensor_reduce(OH, PICK, AX.X, ALU.add).then_inc(sem("dve_step"), DV.sends("dve_step"))
            nc.vector.wait_ge(sem("dve_step"), DV.sent("dve_step"))
            oh2 = OH.rearrange("p b (j i) -> p b j i", i=2)
            ve.tensor_copy(SHALF[0:NR, :, :], oh2[0:NR, :, :, 0])
            ve.tensor_copy(SHALF[NR:P, :, :], oh2[NR:P, :, :, 1]).then_inc(sem("dve_step"), DV.sends("dve_step"))
            nc.vector.wait_ge(sem("dve_step"), DV.sent("dve_step"))
            ohd = PICK[:, :, :, 0]
            ve.tensor_tensor(ohd[0:NA, :, :], OH[0:NA, :, :], over(ident[0:NA, 0:NA], B), ALU.mult)\
                .then_inc(sem("dve_step"), DV.sends("dve_step"))
            nc.vector.wait_ge(sem("dve_step"), DV.sent("dve_step"))
            ve.tensor_reduce(BUP[0:NA, :], ohd[0:NA, :, :], AX.X, ALU.add).then_inc(sem("dve_step"), DV.sends("dve_step"))
            nc.vector.wait_ge(sem("dve_step"), DV.sent("dve_step"))
            ve.tensor_copy(OHT[0:NA, :].rearrange("p (b t) -> p b t", b=B), each(BUP[0:NA, :], P))\
                .then_inc(sem("dve_step"), DV.sends("dve_step"))
            nc.vector.wait_ge(sem("dve_step"), DV.sent("dve_step"))
            nc.vector.wait_ge(sem("l1f_mid_kept"), DV.due("l1f_mid_kept", n=4))
            for k in range(4):
                m = MID[:, k, :].rearrange("p (b t) -> p b t", b=B)
                last = ve.tensor_tensor(m, m, each(SHALF[:, :, k], P), ALU.mult)
            last.then_inc(sem("l1f_masked"), DV.sends("l1f_masked"))
            nc.vector.wait_ge(sem("l1f_masked"), DV.sent("l1f_masked"))
            nc.vector.wait_ge(sem("block_out"), DV.due("block_out"))
            ve.tensor_tensor(ACC[:, :, :], bank4(6), over(row("l1f_bbase"), B), ALU.add)\
                .then_inc(sem("dve_step"), DV.sends("dve_step"))
            nc.vector.wait_ge(sem("dve_step"), DV.sent("dve_step"))
            ve.tensor_tensor(X[:, :, :], X[:, :, :], ACC[:, :, :], ALU.add).then_inc(sem("x_ready"), DV.sends("x_ready"))
            nc.vector.wait_ge(sem("x_ready"), DV.sent("x_ready"))

            norm_dve(X)
            for b in range(B):
                nc.vector.wait_ge(sem("long_scores"), DV.due("long_scores"))
                ve.tensor_reduce(LMX[:, b:b + 1], PSUM[:, 0:4, :].rearrange("p c n -> p (c n)"), AX.X, ALU.max)\
                    .then_inc(sem("dve_step"), DV.sends("dve_step"))
                nc.vector.wait_ge(sem("dve_step"), DV.sent("dve_step"))
                ve.tensor_scalar(LNM[:, b:b + 1], LMX[:, b:b + 1], -(P ** -0.5), None, ALU.mult)\
                    .then_inc(sem("long_shift"), DV.sends("long_shift"))
                nc.vector.wait_ge(sem("long_shift"), DV.sent("long_shift"))
            nc.vector.wait_ge(sem("block_out"), DV.due("block_out"))
            ve.reciprocal(LINV, LSUM).then_inc(sem("dve_step"), DV.sends("dve_step"))
            nc.vector.wait_ge(sem("dve_step"), DV.sent("dve_step"))
            ve.tensor_tensor(ACC[:, :, :], bank4(7), each(LINV, P), ALU.mult).then_inc(sem("dve_step"), DV.sends("dve_step"))
            nc.vector.wait_ge(sem("dve_step"), DV.sent("dve_step"))
            ve.tensor_tensor(ACC[:, :, :], ACC[:, :, :], over(row("l2x_bv"), B), ALU.add)\
                .then_inc(sem("dve_step"), DV.sends("dve_step"))
            nc.vector.wait_ge(sem("dve_step"), DV.sent("dve_step"))
            ve.tensor_tensor(X[:, :, :], X[:, :, :], ACC[:, :, :], ALU.add).then_inc(sem("x_ready"), DV.sends("x_ready"))
            nc.vector.wait_ge(sem("x_ready"), DV.sent("x_ready"))

            
            ve.tensor_scalar(SM[0:16, 0:1], w("l2a_big", 16), 0.5, None, ALU.mult).then_inc(sem("dve_step"), DV.sends("dve_step"))
            nc.vector.wait_ge(sem("dve_step"), DV.sent("dve_step"))
            ve.tensor_scalar(SM[0:16, 1:2], w("l2a_bfg", 16), 0.5, None, ALU.mult)\
                .then_inc(sem("l2a_halves"), DV.sends("l2a_halves"))
            nc.vector.wait_ge(sem("l2a_halves"), DV.sent("l2a_halves"))
            norm_dve(X)
            nc.vector.wait_ge(sem("l2a_gates"), DV.due("l2a_gates"))
            ve.tensor_scalar(IG[0:16, :], IG[0:16, :], 0.5, 0.5, ALU.mult, ALU.add)\
                .then_inc(sem("dve_step"), DV.sends("dve_step"))
            nc.vector.wait_ge(sem("dve_step"), DV.sent("dve_step"))
            ve.tensor_scalar(FG[0:16, :], FG[0:16, :], 0.5, 0.5, ALU.mult, ALU.add)\
                .then_inc(sem("dve_step"), DV.sends("dve_step"))
            nc.vector.wait_ge(sem("dve_step"), DV.sent("dve_step"))
            ve.memset(FG[0:16, :].rearrange("p (b t) -> p b t", b=B)[:, :, 0:1], 0.0)\
                .then_inc(sem("dve_step"), DV.sends("dve_step"))
            nc.vector.wait_ge(sem("dve_step"), DV.sent("dve_step"))
            nc.vector.wait_ge(sem("l2a_mm"), DV.due("l2a_mm", n=5))
            ve.tensor_tensor(BX[0:16, :], bank(5, 16), IG[0:16, :], ALU.mult).then_inc(sem("dve_step"), DV.sends("dve_step"))
            nc.vector.wait_ge(sem("dve_step"), DV.sent("dve_step"))
            ve.tensor_tensor_scan(HR[0:16, :], FG[0:16, :], BX[0:16, :], 0.0, ALU.mult, ALU.add)\
                .then_inc(sem("l2a_h"), DV.sends("l2a_h"))
            nc.vector.wait_ge(sem("l2a_h"), DV.sent("l2a_h"))
            nc.vector.wait_ge(sem("l2a_out"), DV.due("l2a_out"))
            ve.tensor_tensor(ACC[:, :, :], bank4(7), over(row("l2a_bout"), B), ALU.add)\
                .then_inc(sem("dve_step"), DV.sends("dve_step"))
            nc.vector.wait_ge(sem("dve_step"), DV.sent("dve_step"))
            norm_dve(ACC, turned=False)
            ve.tensor_tensor(ACC[:, :, :], HN[:, :, :], over(row("l2a_gamma"), B), ALU.mult)\
                .then_inc(sem("dve_step"), DV.sends("dve_step"))
            nc.vector.wait_ge(sem("dve_step"), DV.sent("dve_step"))
            ve.tensor_tensor(ACC[:, :, :], ACC[:, :, :], over(row("l2a_beta"), B), ALU.add)\
                .then_inc(sem("dve_step"), DV.sends("dve_step"))
            nc.vector.wait_ge(sem("dve_step"), DV.sent("dve_step"))
            ve.tensor_tensor(X[:, :, :], X[:, :, :], ACC[:, :, :], ALU.add).then_inc(sem("x_ready"), DV.sends("x_ready"))
            nc.vector.wait_ge(sem("x_ready"), DV.sent("x_ready"))

            norm_dve(X)
            nc.vector.wait_ge(sem("logits"), DV.due("logits"))
            lp = PSUM[:, 5, 0:B * 16].rearrange("p (b e) -> p b e", b=B)
            lg = LG.rearrange("p (b e) -> p b e", b=B)
            gx = GX.rearrange("p (b e) -> p b e", b=B)
            ve.tensor_reduce(GS, lp, AX.X, ALU.max).then_inc(sem("dve_step"), DV.sends("dve_step"))
            nc.vector.wait_ge(sem("dve_step"), DV.sent("dve_step"))
            ve.tensor_tensor(lg, lp, each(GS, 16), ALU.is_equal).then_inc(sem("l2f_onehot"), DV.sends("l2f_onehot"))
            nc.vector.wait_ge(sem("l2f_onehot"), DV.sent("l2f_onehot"))
            ve.tensor_tensor(gx, lp, each(GS, 16), ALU.subtract).then_inc(sem("gate_shifted"), DV.sends("gate_shifted"))
            nc.vector.wait_ge(sem("gate_shifted"), DV.sent("gate_shifted"))
            nc.vector.wait_ge(sem("gate_exp"), DV.due("gate_exp"))
            ve.tensor_reduce(GS, gx, AX.X, ALU.add).then_inc(sem("dve_step"), DV.sends("dve_step"))
            nc.vector.wait_ge(sem("dve_step"), DV.sent("dve_step"))
            ve.reciprocal(GS, GS).then_inc(sem("dve_step"), DV.sends("dve_step"))
            nc.vector.wait_ge(sem("dve_step"), DV.sent("dve_step"))
            nc.vector.wait_ge(sem("l2f_places"), DV.due("l2f_places"))
            ve.scalar_tensor_tensor(out=GX, in0=PSUM[:, 6, 0:B * 16], scalar=float(CAPACITY), in1=LG,
                                    op0=ALU.is_le, op1=ALU.mult)\
                .then_inc(sem("dve_step"), DV.sends("dve_step"))
            nc.vector.wait_ge(sem("dve_step"), DV.sent("dve_step"))
            ve.tensor_tensor(GATE.rearrange("p (b e) -> p b e", b=B), gx, each(GS, 16), ALU.mult)\
                .then_inc(sem("dve_step"), DV.sends("dve_step"))
            nc.vector.wait_ge(sem("dve_step"), DV.sent("dve_step"))
            experts_dve(16, 16)
            ve.tensor_tensor(X[:, :, :], X[:, :, :], EACC[:, :, :], ALU.add).then_inc(sem("x_ready"), DV.sends("x_ready"))
            nc.vector.wait_ge(sem("x_ready"), DV.sent("x_ready"))

            
            nc.vector.wait_ge(sem("key_norm"), DV.sent("key_norm"))
            ve.tensor_scalar(RK[:, :], RK[:, :], 1e-24, None, ALU.max)\
                .then_inc(sem("key_squares_all"), DV.sends("key_squares_all"))
            norm_dve(X, turned=False)
            norm_dve(HN)
            nc.vector.wait_ge(sem("dma_wc"), DV.due("dma_wc"))
            ve.tensor_tensor(SCR, row("l3x_qs"), row("l3x_ks"), ALU.mult).then_inc(sem("dve_step"), DV.sends("dve_step"))
            nc.vector.wait_ge(sem("dve_step"), DV.sent("dve_step"))
            ve.tensor_scalar(SCR, SCR, 8.0, None, ALU.mult).then_inc(sem("dve_step"), DV.sends("dve_step"))
            nc.vector.wait_ge(sem("dve_step"), DV.sent("dve_step"))
            ve.tensor_tensor(NKH, row("l3x_nk"), row("l3x_nk"), ALU.mult).then_inc(sem("dve_step"), DV.sends("dve_step"))
            nc.vector.wait_ge(sem("dve_step"), DV.sent("dve_step"))
            ve.tensor_reduce(NSS, NKH, AX.X, ALU.add).then_inc(sem("dve_step"), DV.sends("dve_step"))
            nc.vector.wait_ge(sem("dve_step"), DV.sent("dve_step"))
            ve.tensor_scalar(NSS, NSS, 1e-24, None, ALU.max).then_inc(sem("l3x_null_square"), DV.sends("l3x_null_square"))
            nc.vector.wait_ge(sem("l3x_null_square"), DV.sent("l3x_null_square"))
            nc.vector.wait_ge(sem("l3x_null_rnorm"), DV.due("l3x_null_rnorm"))
            ve.tensor_scalar(NKH, row("l3x_nk"), NSS, None, ALU.mult).then_inc(sem("dve_step"), DV.sends("dve_step"))
            nc.vector.wait_ge(sem("dve_step"), DV.sent("dve_step"))
            nc.vector.wait_ge(sem("l3x_norms"), DV.due("l3x_norms"))
            ve.reciprocal(RK[:, :], RK[:, :]).then_inc(sem("dve_step"), DV.sends("dve_step"))
            nc.vector.wait_ge(sem("dve_step"), DV.sent("dve_step"))
            q4 = QN.rearrange("p b (h e) -> p b h e", h=H)
            t1 = T1.rearrange("p (h e) -> p h e", h=H)
            for b in range(B):
                nc.vector.wait_ge(sem("l3x_q_kept"), DV.due("l3x_q_kept"))
                ve.tensor_tensor(T1, QN[:, b, :], QN[:, b, :], ALU.mult).then_inc(sem("dve_step"), DV.sends("dve_step"))
                nc.vector.wait_ge(sem("dve_step"), DV.sent("dve_step"))
                ve.tensor_reduce(QSS[:, b * H:(b + 1) * H], t1, AX.X, ALU.add).then_inc(sem("dve_step"), DV.sends("dve_step"))
                nc.vector.wait_ge(sem("dve_step"), DV.sent("dve_step"))
            ve.tensor_scalar(QSS, QSS, 1e-24, None, ALU.max).then_inc(sem("l3x_q_squares"), DV.sends("l3x_q_squares"))
            nc.vector.wait_ge(sem("l3x_q_squares"), DV.sent("l3x_q_squares"))
            nc.vector.wait_ge(sem("l3x_norms"), DV.due("l3x_norms"))
            ve.reciprocal(QSS, QSS).then_inc(sem("dve_step"), DV.sends("dve_step"))
            nc.vector.wait_ge(sem("dve_step"), DV.sent("dve_step"))
            for b in range(B):
                ve.tensor_tensor(q4[:, b, :, :], q4[:, b, :, :], each(QSS[:, b * H:(b + 1) * H], DH), ALU.mult)\
                    .then_inc(sem("dve_step"), DV.sends("dve_step"))
                nc.vector.wait_ge(sem("dve_step"), DV.sent("dve_step"))
                ve.tensor_tensor(q4[:, b, :, :], q4[:, b, :, :], over(SCR, H), ALU.mult)\
                    .then_inc(sem("dve_step"), DV.sends("dve_step"))
                nc.vector.wait_ge(sem("dve_step"), DV.sent("dve_step"))
                ve.tensor_tensor(T1, QN[:, b, :], QN[:, b, :], ALU.mult).then_inc(sem("dve_step"), DV.sends("dve_step"))
                nc.vector.wait_ge(sem("dve_step"), DV.sent("dve_step"))
                ve.tensor_reduce(BN[:, b * H:(b + 1) * H], t1, AX.X, ALU.add).then_inc(sem("dve_step"), DV.sends("dve_step"))
                nc.vector.wait_ge(sem("dve_step"), DV.sent("dve_step"))
                ve.tensor_tensor(t1, q4[:, b, :, :], over(NKH, H), ALU.mult).then_inc(sem("dve_step"), DV.sends("dve_step"))
                nc.vector.wait_ge(sem("dve_step"), DV.sent("dve_step"))
                last = ve.tensor_reduce(PN[:, b * H:(b + 1) * H], t1, AX.X, ALU.add)
            last.then_inc(sem("l3x_b_squares"), DV.sends("l3x_b_squares"))
            nc.vector.wait_ge(sem("l3x_b_squares"), DV.sent("l3x_b_squares"))
            nc.vector.wait_ge(sem("l3x_norms"), DV.due("l3x_norms"))
            ve.tensor_reduce(BMAX, BN, AX.X, ALU.max).then_inc(sem("l3x_bound_rows"), DV.sends("l3x_bound_rows"))
            nc.vector.wait_ge(sem("l3x_bound_rows"), DV.sent("l3x_bound_rows"))
            nc.vector.wait_ge(sem("l3x_bound_row"), DV.due("l3x_bound_row"))
            ve.tensor_reduce(BTOP[0:1, :], PSUM[0:1, 3, 0:P], AX.X, ALU.max)\
                .then_inc(sem("l3x_bound_top"), DV.sends("l3x_bound_top"))
            nc.vector.wait_ge(sem("l3x_bound_top"), DV.sent("l3x_bound_top"))
            nc.vector.wait_ge(sem("l3x_bound_all"), DV.due("l3x_bound_all"))
            ve.tensor_scalar(NBTOP, PSUM[:, 3, 0:1], -1.0, SAFE_EXPONENT, ALU.mult, ALU.add)\
                .then_inc(sem("dve_step"), DV.sends("dve_step"))
            nc.vector.wait_ge(sem("dve_step"), DV.sent("dve_step"))
            ve.tensor_scalar(NBTOP, NBTOP, 0.0, None, ALU.min).then_inc(sem("l3x_shift_ready"), DV.sends("l3x_shift_ready"))
            nc.vector.wait_ge(sem("l3x_shift_ready"), DV.sent("l3x_shift_ready"))

            def scale(b, k, t):
                for c in range(4):
                    nc.vector.wait_ge(sem("l3x_scores"), DV.due("l3x_scores"))
                    if c == 0:
                        nc.vector.wait_ge(sem("l3x_gathered"), DV.due("l3x_gathered", lag=2))
                        nc.vector.wait_ge(sem("l3x_summed"), DV.due("l3x_summed", lag=2))
                    at = t * H + (b * KEY_TILES * H + 4 * c)
                    rk = RK[:, at:at + 4] if isinstance(t, int) else RK[:, bass.ds(at, 4)]
                    ve.tensor_tensor(PR[:, k % 2, c * 512:(c + 1) * 512].rearrange("p (j n) -> p j n", j=4),
                                     PSUM[:, c % 2, :].rearrange("p (j n) -> p j n", j=4), each(rk, P), ALU.mult)\
                        .then_inc(sem("l3x_scores_taken"), DV.sends("l3x_scores_taken"))

            ln = LT[:, 0:H]
            o = OTK.rearrange("p (h e) -> p h e", h=H)

            def finish_sums(b):
                nc.vector.wait_ge(sem("l3x_l"), DV.due("l3x_l"))
                ve.tensor_tensor(ln, PSUM[:, 2, 0:H], PN[:, b * H:(b + 1) * H], ALU.add)\
                    .then_inc(sem("l3x_l_kept"), DV.sends("l3x_l_kept"))
                nc.vector.wait_ge(sem("l3x_l_kept"), DV.sent("l3x_l_kept"))
                ve.reciprocal(ln, ln).then_inc(sem("dve_step"), DV.sends("dve_step"))
                nc.vector.wait_ge(sem("dve_step"), DV.sent("dve_step"))
                ve.tensor_tensor(t1, over(row("l3x_nv"), H), each(PN[:, b * H:(b + 1) * H], DH), ALU.mult)\
                    .then_inc(sem("dve_step"), DV.sends("dve_step"))
                nc.vector.wait_ge(sem("dve_step"), DV.sent("dve_step"))

            def finish_values():
                nc.vector.wait_ge(sem("l3x_o"), DV.due("l3x_o"))
                ve.tensor_tensor(o, PSUM[:, 2:4, :].rearrange("p c (h e) -> p (c h) e", h=8), t1, ALU.add)\
                    .then_inc(sem("dve_step"), DV.sends("dve_step"))
                nc.vector.wait_ge(sem("dve_step"), DV.sent("dve_step"))
                ve.tensor_tensor(o, o, each(ln, DH), ALU.mult).then_inc(sem("l3x_o_kept"), DV.sends("l3x_o_kept"))
                nc.vector.wait_ge(sem("l3x_o_kept"), DV.sent("l3x_o_kept"))

            def finish_out(b):
                nc.vector.wait_ge(sem("l3x_out"), DV.due("l3x_out"))
                ve.tensor_copy(OAT[:, b, :], PSUM[:, 2, 0:P]).then_inc(sem("l3x_out_kept"), DV.sends("l3x_out_kept"))
                nc.vector.wait_ge(sem("l3x_out_kept"), DV.sent("l3x_out_kept"))

            nc.vector.wait_ge(sem("l3x_null"), DV.due("l3x_null"))
            for b in range(B):
                for k in range(DEEP):
                    scale(b, k, k)
                    if b and k == 1:
                        finish_sums(b - 1)
                    if b and k == 2:
                        finish_values()
                with DV.loop(TILE_GROUPS - 1, made=[("l3x_scores_taken", 16)],
                             seen=[("l3x_scores", 16), ("l3x_gathered", 4), ("l3x_summed", 4)]) as i:
                    for k in range(DEEP):
                        scale(b, k, DEEP * i + (DEEP + k))
                if b:
                    finish_out(b - 1)
            finish_sums(B - 1)
            finish_values()
            finish_out(B - 1)
            norm_dve(OAT, turned=False)
            ve.tensor_tensor(ACC[:, :, :], HN[:, :, :], over(row("l3x_go"), B), ALU.mult)\
                .then_inc(sem("dve_step"), DV.sends("dve_step"))
            nc.vector.wait_ge(sem("dve_step"), DV.sent("dve_step"))
            ve.tensor_tensor(X[:, :, :], X[:, :, :], ACC[:, :, :], ALU.add).then_inc(sem("x_ready"), DV.sends("x_ready"))
            nc.vector.wait_ge(sem("x_ready"), DV.sent("x_ready"))

            
            norm_dve(X)
            nc.vector.wait_ge(sem("l3a_v"), DV.due("l3a_v"))
            ve.tensor_copy(V3, bank4(7)).then_inc(sem("l3a_v_kept"), DV.sends("l3a_v_kept"))
            nc.vector.wait_ge(sem("l3a_v_kept"), DV.sent("l3a_v_kept"))
            core_dve(1, w("causal"))
            nc.vector.wait_ge(sem("values_summed"), DV.due("values_summed"))
            ve.tensor_tensor(ACC[:, :, :], bank4(6), each(L_INV[:, 0:B], P), ALU.mult)\
                .then_inc(sem("dve_step"), DV.sends("dve_step"))
            nc.vector.wait_ge(sem("dve_step"), DV.sent("dve_step"))
            ve.tensor_tensor(ACC[:, :, :], ACC[:, :, :], V3, ALU.add).then_inc(sem("dve_step"), DV.sends("dve_step"))
            nc.vector.wait_ge(sem("dve_step"), DV.sent("dve_step"))
            norm_dve(ACC)
            tail_dve(row("l3a_bfc"))

            
            norm_dve(X)
            nc.vector.wait_ge(sem("l3f_scores"), DV.due("l3f_scores"))
            lg = LG.rearrange("p (b e) -> p b e", b=B)
            gx = GX.rearrange("p (b e) -> p b e", b=B)
            ve.tensor_scalar(LG, LG, 0.5, 0.5, ALU.mult, ALU.add).then_inc(sem("dve_step"), DV.sends("dve_step"))
            nc.vector.wait_ge(sem("dve_step"), DV.sent("dve_step"))
            ve.tensor_tensor(gx, lg, over(row("l3f_gb"), B), ALU.add).then_inc(sem("dve_step"), DV.sends("dve_step"))
            nc.vector.wait_ge(sem("dve_step"), DV.sent("dve_step"))
            for b in range(B):
                last = ve.max(M8[:, b, :], gx[:, b, :])
            last.then_inc(sem("dve_step"), DV.sends("dve_step"))
            nc.vector.wait_ge(sem("dve_step"), DV.sent("dve_step"))
            ve.tensor_tensor(gx, gx, M8[:, :, 3:4].broadcast_to([P, B, 16]), ALU.is_ge)\
                .then_inc(sem("dve_step"), DV.sends("dve_step"))
            nc.vector.wait_ge(sem("dve_step"), DV.sent("dve_step"))
            ve.tensor_tensor(lg, lg, gx, ALU.mult).then_inc(sem("dve_step"), DV.sends("dve_step"))
            nc.vector.wait_ge(sem("dve_step"), DV.sent("dve_step"))
            ve.tensor_reduce(GS, lg, AX.X, ALU.add).then_inc(sem("dve_step"), DV.sends("dve_step"))
            nc.vector.wait_ge(sem("dve_step"), DV.sent("dve_step"))
            ve.reciprocal(GS, GS).then_inc(sem("dve_step"), DV.sends("dve_step"))
            nc.vector.wait_ge(sem("dve_step"), DV.sent("dve_step"))
            ve.tensor_scalar(GS, GS, 2.5 * 0.5, None, ALU.mult).then_inc(sem("dve_step"), DV.sends("dve_step"))
            nc.vector.wait_ge(sem("dve_step"), DV.sent("dve_step"))
            ve.memset(G18, 0.5).then_inc(sem("dve_step"), DV.sends("dve_step"))
            nc.vector.wait_ge(sem("dve_step"), DV.sent("dve_step"))
            ve.tensor_tensor(G18[:, :, 0:16], lg, each(GS, 16), ALU.mult).then_inc(sem("dve_step"), DV.sends("dve_step"))
            nc.vector.wait_ge(sem("dve_step"), DV.sent("dve_step"))
            ve.memset(EACC[:, :, :], 0.0).then_inc(sem("dve_step"), DV.sends("dve_step"))
            nc.vector.wait_ge(sem("dve_step"), DV.sent("dve_step"))

            def hidden(p):
                k = p % 2
                nc.vector.wait_ge(sem("l3f_tanh"), DV.due("l3f_tanh"))
                nc.vector.wait_ge(sem("expert_out"), DV.due("expert_out", lag=2))
                ve.scalar_tensor_tensor(out=HP[:, k, :], in0=TG[:, k, :], scalar=1.0, in1=bank(1 + 2 * k),
                                        op0=ALU.add, op1=ALU.mult)\
                    .then_inc(sem("dve_step"), DV.sends("dve_step"))
                nc.vector.wait_ge(sem("dve_step"), DV.sent("dve_step"))
                ve.tensor_tensor(HP[:, k, :], HP[:, k, :], bank(2 + 2 * k), ALU.mult).then_inc(sem("l3f_h"), DV.sends("l3f_h"))
                nc.vector.wait_ge(sem("l3f_h"), DV.sent("l3f_h"))

            def add(p):
                nc.vector.wait_ge(sem("expert_out"), out0 + p + 1)
                for i in range(2 if p < PAIRS - 1 else 1):
                    for b in range(B):
                        last = ve.scalar_tensor_tensor(out=EACC[:, b, :], in0=PSUM[:, 6 + i, b * P:(b + 1) * P],
                                                       scalar=G18[:, b, 2 * p + i:2 * p + i + 1], in1=EACC[:, b, :],
                                                       op0=ALU.mult, op1=ALU.add)
                    if i == 0 and p < PAIRS - 1:
                        last.then_inc(sem("dve_step"), DV.sends("dve_step"))
                        nc.vector.wait_ge(sem("dve_step"), DV.sent("dve_step"))
                last.then_inc(sem("l3f_added"), DV.sends("l3f_added"))
                nc.vector.wait_ge(sem("l3f_added"), DV.sent("l3f_added"))

            out0 = DV.seen["expert_out"]
            hidden(0)
            for p in range(PAIRS):
                if p + 1 < PAIRS:
                    hidden(p + 1)
                add(p)
            ve.tensor_tensor(X[:, :, :], X[:, :, :], EACC[:, :, :], ALU.add).then_inc(sem("x_ready"), DV.sends("x_ready"))
            nc.vector.wait_ge(sem("x_ready"), DV.sent("x_ready"))

        @block.tensor
        def _(tensor):
            def turn_pe(src=HN):
                nc.tensor.wait_ge(sem("tokens_ready"), PE.due("tokens_ready"))
                for b in range(B):
                    last = tp(PSUM[:, 0, b * P:(b + 1) * P], src[:, b, :], ident)
                last.then_inc(sem("turned"), PE.sends("turned"))

            def tail_pe(weight, src=OT):
                for b in range(B):
                    last = mm(PSUM[:, 7, b * P:(b + 1) * P], src[:, b * P:(b + 1) * P], weight, start=True, stop=True)
                last.then_inc(sem("block_out"), PE.sends("block_out"))

            def key_norms_pe(n0, n):
                for m in range(n0, n0 + n):
                    t, c = m // 2, m % 2
                    nc.tensor.wait_ge(sem("key_squares"), PE.due("key_squares", lag=2))
                    mm(bank(5 + 2 * c), CT[:, t * P:(t + 1) * P], WK[:, c * 512:(c + 1) * 512],
                        start=True, stop=True).then_inc(sem("key_rows"), PE.sends("key_rows"))

            def core_pe(groups, q_of, k_of, v_of, out_of, norms_from=None):
                def scores(g):
                    nc.tensor.wait_ge(sem("scores_shifted"), PE.due("scores_shifted", lag=2))
                    for j in range(4):
                        last = mm(PSUM[:, 1 + g % 2, j * P:(j + 1) * P], q_of(g, j), k_of(g, j), start=True, stop=True)
                    last.then_inc(sem("scores"), PE.sends("scores"))

                scores(0)
                for g in range(groups):
                    if g + 1 < groups:
                        scores(g + 1)
                    if norms_from is not None:
                        key_norms_pe(norms_from + 4 * g, 2)
                    nc.tensor.wait_ge(sem("probs"), PE.due("probs"))
                    for j in range(4):
                        last = tp(PSUM[:, 3 + g % 2, j * P:(j + 1) * P], SX[:, g % 2, j * P:(j + 1) * P], ident)
                    last.then_inc(sem("probs_turned"), PE.sends("probs_turned"))
                    if norms_from is not None:
                        key_norms_pe(norms_from + 4 * g + 2, 2)
                    nc.tensor.wait_ge(sem("pt_ready"), PE.due("pt_ready"))
                    for j in range(4):
                        last = mm(out_of(g, j), PT[:, g % 2, j * P:(j + 1) * P], v_of(g, j), start=True, stop=True)
                    last.then_inc(sem("values_summed"), PE.sends("values_summed"))

            def long_pe(rows_):
                def scores(b):
                    for c in range(4):
                        last = mm(PSUM[:, c, :], QT[0:rows_, b * P:(b + 1) * P],
                                  KT[0:rows_, b * S + c * 512:b * S + (c + 1) * 512], start=True, stop=True)
                    last.then_inc(sem("long_scores"), PE.sends("long_scores"))

                scores(0)
                for b in range(B):
                    nc.tensor.wait_ge(sem("long_probs"), PE.due("long_probs"))
                    for c in range(4):
                        nc.tensor.wait_ge(sem("long_pt"), PE.due("long_pt", lag=2))
                        for j in range(4):
                            t = 4 * c + j
                            last = tp(PSUM[:, 4 + c % 2, j * P:(j + 1) * P], SL[:, b % 2, t * P:(t + 1) * P], ident)
                        last.then_inc(sem("long_turned"), PE.sends("long_turned"))
                    if b + 1 < B:
                        scores(b + 1)
                    nc.tensor.wait_ge(sem("long_pt"), PE.seen["long_pt"])
                    nc.tensor.wait_ge(sem("long_z_kept"), PE.due("long_z_kept", lag=1))
                    for t in range(KEY_TILES):
                        last = mm(PSUM[:, 6, 0:P], CK[:, b * KEY_TILES + t, :], PTL[:, t, :],
                                  start=t == 0, stop=t == KEY_TILES - 1)
                    last.then_inc(sem("long_z"), PE.sends("long_z"))

            def experts_pe(n):
                def first(k):
                    nc.tensor.wait_ge(sem("dma_expert%d" % k), PE.due("dma_expert%d" % k))
                    for c in range(FC):
                        nc.tensor.wait_ge(sem("hidden_kept"), PE.due("hidden_kept", lag=2))
                        mm(bank(1 + c % 2), EB[:, k, c * P:(c + 1) * P], HT[:, :], start=True, stop=True)\
                            .then_inc(sem("hidden"), PE.sends("hidden"))

                def second(k):
                    nc.tensor.wait_ge(sem("hidden_kept"), PE.need_hidden)
                    nc.tensor.wait_ge(sem("expert_added"), PE.due("expert_added", lag=2))
                    for b in range(B):
                        for c in range(FC):
                            last = mm(PSUM[:, 3 + k, b * P:(b + 1) * P], HB[:, k, c, b * P:(b + 1) * P],
                                      EB[:, k, FF + c * P:FF + (c + 1) * P], start=c == 0, stop=c == FC - 1)
                    last.then_inc(sem("expert_out"), PE.sends("expert_out"))
                    PE.need_hidden = PE.need_hidden + FC

                PE.need_hidden = PE.seen.get("hidden_kept", 0) + FC
                first(0)
                first(1)
                second(0)
                first(0)
                second(1)
                h0 = PE.need_hidden
                with PE.loop(n // 2 - 2, made=[("hidden", 2 * FC), ("expert_out", 2)],
                             seen=[("dma_expert0", 1), ("dma_expert1", 1), ("hidden_kept", 2 * FC), ("expert_added", 2)]) as i:
                    PE.need_hidden = h0 + i * 2 * FC
                    first(1)
                    second(0)
                    first(0)
                    second(1)
                PE.need_hidden = h0 + (n // 2 - 2) * 2 * FC
                first(1)
                second(0)
                second(1)

            def context_keys_pe(weight, m=P):
                for c in range(NK // 512):
                    nc.tensor.wait_ge(sem("context_keys_kept"), PE.due("context_keys_kept", lag=2))
                    mm(bank(1 + c % 2, m), weight, CT[:, c * 512:(c + 1) * 512], start=True, stop=True)\
                        .then_inc(sem("context_keys"), PE.sends("context_keys"))

            
            nc.tensor.wait_ge(sem("dma_wa"), PE.due("dma_wa"))
            for c in range(B):
                nc.tensor.wait_ge(sem("dma_ctx%d" % c), PE.due("dma_ctx%d" % c))
            context_keys_pe(w("l0x_WkT"))
            nc.tensor.wait_ge(sem("dma_wk"), PE.due("dma_wk"))
            for b in range(B):
                for h in range(H):
                    at = (b * H + h) * HD
                    last = mm(PSUM[:, 3, at:at + HD], CTB[:, b, h, :], w("l0x_WvT")[:, h * HD:(h + 1) * HD],
                              start=True, stop=True)
            last.then_inc(sem("l0x_v"), PE.sends("l0x_v"))
            turn_pe()
            nc.tensor.wait_ge(sem("turned_kept"), PE.due("turned_kept"))
            mm(bank(5), w("l0x_WqT"), HT[:, :], start=True, stop=True).then_inc(sem("q_rows"), PE.sends("q_rows"))
            nc.tensor.wait_ge(sem("l0x_q_heads"), PE.due("l0x_q_heads"))
            nc.tensor.wait_ge(sem("context_keys_kept"), 16)
            core_pe(16, lambda g, j: QM[:, 4 * (g % 4) + j, (g // 4) * P:(g // 4 + 1) * P],
                    lambda g, j: KSB[:, g // 4, 4 * (g % 4) + j, :],
                    lambda g, j: VS[:, (4 * g + j) * HD:(4 * g + j + 1) * HD],
                    lambda g, j: PSUM[:, 6, (4 * g + j) * HD:(4 * g + j + 1) * HD], norms_from=0)
            turn_pe(ACC)
            nc.tensor.wait_ge(sem("turned_kept"), PE.due("turned_kept"))
            tail_pe(w("l0x_WoT"))

            
            nc.tensor.wait_ge(sem("dma_wb"), PE.due("dma_wb"))
            turn_pe()
            nc.tensor.wait_ge(sem("turned_kept"), PE.due("turned_kept"))
            mm(bank(1), w("l0a_w1"), HT[:, :], start=True, stop=True).then_inc(sem("l0a_x1"), PE.sends("l0a_x1"))
            mm(bank(2), w("l0a_v1"), HT[:, :], start=True, stop=True).then_inc(sem("l0a_v"), PE.sends("l0a_v"))
            nc.tensor.wait_ge(sem("l0a_u"), PE.due("l0a_u"))
            mm(bank(3), w("l0a_Wdt"), U, start=True, stop=True).then_inc(sem("l0a_dt"), PE.sends("l0a_dt"))
            for half in range(2):
                for name in ("l0a_WB", "l0a_WC"):
                    for n in range(8):
                        col = w(name)[:, half * 8 + n:half * 8 + n + 1].broadcast_to([P, P])
                        nc.tensor.wait_ge(sem("l0a_bc_taken"), PE.due("l0a_bc_taken", lag=3))
                        mm(bank(4 + (n + half * 16 + (8 if name == "l0a_WC" else 0)) % 3), col, U,
                            start=True, stop=True).then_inc(sem("l0a_bc"), PE.sends("l0a_bc"))
            nc.tensor.wait_ge(sem("l0a_y"), PE.due("l0a_y"))
            tail_pe(w("l0a_w2"))

            def logits_pe(weight, e):
                for b in range(B):
                    last = mm(PSUM[:, 5, b * e:(b + 1) * e], hT(b), weight, start=True, stop=True)
                last.then_inc(sem("logits"), PE.sends("logits"))

            
            turn_pe()
            nc.tensor.wait_ge(sem("turned_kept"), PE.due("turned_kept"))
            logits_pe(w("l0f_Wg"), 8)
            experts_pe(8)
            nc.tensor.wait_ge(sem("l0f_gates"), PE.due("l0f_gates"))
            for b in range(B):
                last = tp(PSUM[0:8, 6, b * P:(b + 1) * P], GATE[:, b * 8:(b + 1) * 8], ident)
            last.then_inc(sem("l0f_gates_turned"), PE.sends("l0f_gates_turned"))
            nc.tensor.wait_ge(sem("l0f_gates_kept"), PE.due("l0f_gates_kept"))
            for b in range(B):
                last = mm(PSUM[:, 7, b * P:(b + 1) * P], GT[0:8, b * P:(b + 1) * P], w("l0f_b2", 8), start=True, stop=True)
            last.then_inc(sem("block_out"), PE.sends("block_out"))

            
            nc.tensor.wait_ge(sem("dma_ck"), PE.due("dma_ck"))
            nc.tensor.wait_ge(sem("x_ready"), PE.due("x_ready", n=3))
            mm(PSUM[:, 3, 0:HD], w("l1x_WkT"), w("l1x_wkh"), start=True, stop=True)\
                .then_inc(sem("l1x_fold"), PE.sends("l1x_fold"))
            mm(PSUM[:, 3, HD:2 * HD], w("l1x_WvT"), w("l1x_wvh"), start=True, stop=True)\
                .then_inc(sem("l1x_fold"), PE.sends("l1x_fold"))
            nc.tensor.wait_ge(sem("l1x_folded"), PE.due("l1x_folded"))
            context_keys_pe(WKK, HD)
            turn_pe()
            nc.tensor.wait_ge(sem("turned_kept"), PE.due("turned_kept"))
            mm(bank(5), w("l1x_Wq"), HT[:, :], start=True, stop=True).then_inc(sem("q_rows"), PE.sends("q_rows"))
            nc.tensor.wait_ge(sem("q_rows_kept"), PE.due("q_rows_kept"))
            mm(bank(6, HD), w("l1x_wqh"), TMP[:, :], start=True, stop=True).then_inc(sem("l1x_qh"), PE.sends("l1x_qh"))
            nc.tensor.wait_ge(sem("l1x_qh_kept"), PE.due("l1x_qh_kept"))
            nc.tensor.wait_ge(sem("context_keys_kept"), 32)
            long_pe(HD)
            nc.tensor.wait_ge(sem("long_z_kept"), 4)
            for b in range(B):
                last = mm(PSUM[:, 5, b * HD:(b + 1) * HD], ZT[:, b * P:(b + 1) * P], WVV, start=True, stop=True)
            last.then_inc(sem("l1x_o"), PE.sends("l1x_o"))
            turn_pe(ACC)
            nc.tensor.wait_ge(sem("turned_kept"), PE.due("turned_kept"))
            tail_pe(w("l1x_Wo"))

            def pieces_pe(part):
                for j in range(H):
                    at = part * P + j * HD
                    nc.tensor.wait_ge(sem("pieces_kept"), PE.due("pieces_kept", lag=4))
                    mm(bank(3 + j % 4, HD), w("l1a_Wqkv")[:, at:at + HD], HT[:, :], start=True, stop=True)\
                        .then_inc(sem("pieces"), PE.sends("pieces"))

            
            turn_pe()
            nc.tensor.wait_ge(sem("turned_kept"), PE.due("turned_kept"))
            pieces_pe(2)
            nc.tensor.wait_ge(sem("pieces_kept"), 16)
            for a in range(B * H):
                last = tp(PSUM[:, 1, a * HD:(a + 1) * HD], piece(KS, a), ident[0:HD, 0:HD])
            last.then_inc(sem("l1a_v"), PE.sends("l1a_v"))
            pieces_pe(0)
            pieces_pe(1)
            nc.tensor.wait_ge(sem("pieces_kept"), 48)
            nc.tensor.wait_ge(sem("l1a_v_kept"), PE.due("l1a_v_kept"))
            core_pe(16, lambda g, j: piece(QS, 4 * g + j), lambda g, j: piece(KS, 4 * g + j),
                    lambda g, j: VS[:, (4 * g + j) * HD:(4 * g + j + 1) * HD],
                    lambda g, j: PSUM[:, 6, (4 * g + j) * HD:(4 * g + j + 1) * HD], norms_from=64)
            turn_pe(ACC)
            nc.tensor.wait_ge(sem("turned_kept"), PE.due("turned_kept"))
            tail_pe(w("l1a_Wproj"))

            
            turn_pe()
            nc.tensor.wait_ge(sem("turned_kept"), PE.due("turned_kept"))
            for k in range(2):
                mm(bank(1 + k), w("l1f_Wenc")[:, k * P:(k + 1) * P], HT[:, :], start=True, stop=True)\
                    .then_inc(sem("l1f_enc"), PE.sends("l1f_enc"))
            nc.tensor.wait_ge(sem("l1f_enc_kept"), PE.due("l1f_enc_kept", n=2))
            for n in range(NA):
                r = NH * (n % 4)
                nc.tensor.wait_ge(sem("l1f_recon_taken"), PE.due("l1f_recon_taken", lag=2))
                mm(bank(3 + n % 2), w("l1f_Wdec")[r:r + NH, (n // 4) * P:(n // 4 + 1) * P],
                    ENC[r:r + NH, n // 4, :], start=True, stop=True)\
                    .then_inc(sem("l1f_recon"), PE.sends("l1f_recon"))
            for k in range(4):
                if k >= 2:
                    nc.tensor.wait_ge(sem("l1f_mid_kept"), PE.due("l1f_mid_kept"))
                mm(bank(1 + k % 2), w("l1f_Wdown")[:, k * P:(k + 1) * P], HT[:, :], start=True, stop=True)\
                    .then_inc(sem("l1f_mid"), PE.sends("l1f_mid"))
            nc.tensor.wait_ge(sem("l1f_losses"), PE.due("l1f_losses"))
            mm(PSUM[:, 5, 0:32], w("ones"), SM[:, 0:32], start=True, stop=True).then_inc(sem("l1f_loss"), PE.sends("l1f_loss"))
            nc.tensor.wait_ge(sem("l1f_masked"), PE.due("l1f_masked"))
            for b in range(B):
                sl = slice(b * P, (b + 1) * P)
                mm(PSUM[:, 6, sl], HT[:, sl], w("l1f_Wbase"), start=True, stop=False)
                for k in range(4):
                    last = mm(PSUM[:, 6, sl], MID[:, k, sl], w("l1f_Wup")[:, k * P:(k + 1) * P],
                              start=False, stop=False)
                last = mm(PSUM[:, 6, sl], PICKT_(b), w("l1f_bup", NA), start=False, stop=True)
            last.then_inc(sem("block_out"), PE.sends("block_out"))

            nc.tensor.wait_ge(sem("x_ready"), PE.due("x_ready", n=3))
            context_keys_pe(w("l2x_WkT"))
            turn_pe()
            nc.tensor.wait_ge(sem("turned_kept"), PE.due("turned_kept"))
            mm(bank(5), w("l2x_WqT"), HT[:, :], start=True, stop=True).then_inc(sem("q_rows"), PE.sends("q_rows"))
            nc.tensor.wait_ge(sem("q_rows_kept"), PE.due("q_rows_kept"))
            nc.tensor.wait_ge(sem("context_keys_kept"), 48)
            long_pe(P)
            nc.tensor.wait_ge(sem("long_z_kept"), 8)
            tail_pe(w("l2x_WvT"))

            
            turn_pe()
            nc.tensor.wait_ge(sem("turned_kept"), PE.due("turned_kept"))
            mm(bank(1), w("l2a_Win"), HT[:, :], start=True, stop=True).then_inc(sem("l2a_mm"), PE.sends("l2a_mm"))
            nc.tensor.wait_ge(sem("l2a_kept"), PE.due("l2a_kept"))
            mm(bank(2), w("l2a_WB"), XP, start=True, stop=True).then_inc(sem("l2a_mm"), PE.sends("l2a_mm"))
            mm(bank(3, 16), w("l2a_Wig"), XP, start=True, stop=True).then_inc(sem("l2a_mm"), PE.sends("l2a_mm"))
            mm(bank(4, 16), w("l2a_Wfg"), XP, start=True, stop=True).then_inc(sem("l2a_mm"), PE.sends("l2a_mm"))
            nc.tensor.wait_ge(sem("l2a_kept"), PE.due("l2a_kept"))
            mm(bank(5, 16), w("l2a_Bmat"), XB, start=True, stop=True).then_inc(sem("l2a_mm"), PE.sends("l2a_mm"))
            nc.tensor.wait_ge(sem("l2a_h"), PE.due("l2a_h"))
            mm(bank(6), w("l2a_WD"), XP, start=True, stop=False)
            mm(bank(6), w("l2a_Cmat", 16), HR[0:16, :], start=False, stop=True).then_inc(sem("l2a_mm"), PE.sends("l2a_mm"))
            nc.tensor.wait_ge(sem("l2a_kept"), PE.due("l2a_kept"))
            for b in range(B):
                sl = slice(b * P, (b + 1) * P)
                mm(PSUM[:, 7, sl], YT[:, sl], w("l2a_Wout"), start=True, stop=False)
                last = mm(PSUM[:, 7, sl], XP[:, sl], ident, start=False, stop=True)
            last.then_inc(sem("l2a_out"), PE.sends("l2a_out"))

            turn_pe()
            nc.tensor.wait_ge(sem("turned_kept"), PE.due("turned_kept"))
            logits_pe(w("l2f_WgT"), 16)
            nc.tensor.wait_ge(sem("l2f_onehot"), PE.due("l2f_onehot"))
            for b in range(B):
                for c in range(b + 1):
                    last = mm(PSUM[:, 6, b * 16:(b + 1) * 16], w("upto") if c == b else w("ones"),
                              LG[:, c * 16:(c + 1) * 16], start=c == 0, stop=c == b)
            last.then_inc(sem("l2f_places"), PE.sends("l2f_places"))
            experts_pe(16)

            
            nc.tensor.wait_ge(sem("dma_wc"), PE.due("dma_wc"))
            turn_pe()
            nc.tensor.wait_ge(sem("turned_kept"), PE.due("turned_kept"))
            for b in range(B):
                nc.tensor.wait_ge(sem("l3x_q_kept"), PE.due("l3x_q_kept", lag=2))
                for c in range(2):
                    last = mm(bank(2 * (b % 2) + 1 + c), hT(b), w("l3x_Wq")[:, c * 512:(c + 1) * 512], start=True, stop=True)
                last.then_inc(sem("l3x_q"), PE.sends("l3x_q"))
            nc.tensor.wait_ge(sem("l3x_b_squares"), PE.due("l3x_b_squares"))
            for c in range(8):
                nc.tensor.wait_ge(sem("l3x_qT_kept"), PE.due("l3x_qT_kept", lag=2))
                for b in range(B):
                    last = tp(PSUM[:, 1 + c % 2, b * P:(b + 1) * P], QN[:, b, c * P:(c + 1) * P], ident)
                last.then_inc(sem("l3x_qT"), PE.sends("l3x_qT"))
            nc.tensor.wait_ge(sem("l3x_bound_rows"), PE.due("l3x_bound_rows"))
            tp(PSUM[0:1, 3, 0:P], BMAX, ident).then_inc(sem("l3x_bound_row"), PE.sends("l3x_bound_row"))
            nc.tensor.wait_ge(sem("l3x_bound_top"), PE.due("l3x_bound_top"))
            mm(PSUM[:, 3, 0:1], w("ones", 1), BTOP[0:1, :], start=True, stop=True)\
                .then_inc(sem("l3x_bound_all"), PE.sends("l3x_bound_all"))
            nc.tensor.wait_ge(sem("l3x_qT_kept"), 8)
            for h in range(H):
                r = DH * (h % 2)
                nc.tensor.wait_ge(sem("l3x_qp_kept"), PE.due("l3x_qp_kept", lag=2))
                mm(bank(1 + h % 2), w("l3x_WkT")[r:r + DH, (h // 2) * P:(h // 2 + 1) * P],
                    QSC[r:r + DH, h // 2, :], start=True, stop=True).then_inc(sem("l3x_qp"), PE.sends("l3x_qp"))
            nc.tensor.wait_ge(sem("l3x_qp_kept"), 16)
            qpb = QP.rearrange("p (b n) -> p b n", b=B)

            def score(b, k, c):
                nc.tensor.wait_ge(sem("l3x_scores_taken"), PE.due("l3x_scores_taken", lag=2))
                mm(bank(c % 2), CTT[:, k, :], qpb[:, b, c * 512:(c + 1) * 512], start=True, stop=True)\
                    .then_inc(sem("l3x_scores"), PE.sends("l3x_scores"))

            def gather(k, c, first=False, final=False):
                return mm(bank(4 + c), CKT[:, k, :], PR[:, k % 2, c * 512:(c + 1) * 512], start=first, stop=final,
                          skip_group_check=True)

            def tile(b, k, first=False):
                nc.tensor.wait_ge(sem("dma_ktile%d" % ((k + 1) % DEEP)), PE.due("dma_ktile%d" % ((k + 1) % DEEP), n=2))
                score(b, (k + 1) % DEEP, 0)
                score(b, (k + 1) % DEEP, 1)
                nc.tensor.wait_ge(sem("l3x_probs"), PE.due("l3x_probs"))
                for c in range(4):
                    last = gather(k, c, first)
                    if c < 2:
                        score(b, (k + 1) % DEEP, c + 2)
                last.then_inc(sem("l3x_gathered"), PE.sends("l3x_gathered"))

            def finish_sums(b):
                nc.tensor.wait_ge(sem("l3x_summed"), PE.due("l3x_summed", n=KEY_TILES))
                nc.tensor.wait_ge(sem("l3x_out_kept"), PE.due("l3x_out_kept", lag=1))
                for h in range(H):
                    last = mm(PSUM[:, 2, h:h + 1], LS[b % 2][:, h * P:(h + 1) * P], w("ones")[:, 0:1], start=True, stop=True)
                last.then_inc(sem("l3x_l"), PE.sends("l3x_l"))

            def finish_values():
                nc.tensor.wait_ge(sem("l3x_l_kept"), PE.due("l3x_l_kept"))
                for h in range(H):
                    last = mm(PSUM[:, 2 + h // 8, (h % 8) * DH:(h % 8 + 1) * DH], ZS[:, h * P:(h + 1) * P],
                              w("l3x_Wv")[:, h * DH:(h + 1) * DH], start=True, stop=True)
                last.then_inc(sem("l3x_o"), PE.sends("l3x_o"))

            def finish_turn():
                nc.tensor.wait_ge(sem("l3x_o_kept"), PE.due("l3x_o_kept"))
                for c in range(8):
                    last = tp(PSUM[:, 2 + c // 4, (c % 4) * P:(c % 4 + 1) * P], OTK[:, c * P:(c + 1) * P], ident)
                last.then_inc(sem("l3x_oT"), PE.sends("l3x_oT"))

            def finish_out():
                nc.tensor.wait_ge(sem("l3x_oT_kept"), PE.due("l3x_oT_kept"))
                for c in range(8):
                    last = mm(PSUM[:, 2, 0:P], OT8[:, c * P:(c + 1) * P], w("l3x_Wout")[:, c * P:(c + 1) * P],
                              start=c == 0, stop=c == 7)
                last.then_inc(sem("l3x_out"), PE.sends("l3x_out"))

            for b in range(B):
                nc.tensor.wait_ge(sem("dma_ktile0"), PE.due("dma_ktile0", n=2))
                for c in range(4):
                    score(b, 0, c)
                if b:
                    nc.tensor.wait_ge(sem("l3x_z_kept"), PE.due("l3x_z_kept"))
                tile(b, 0, first=True)
                if b:
                    finish_sums(b - 1)
                tile(b, 1)
                if b:
                    finish_values()
                tile(b, 2)
                if b:
                    finish_turn()
                tile(b, 3)
                if b:
                    finish_out()
                with PE.loop(TILE_GROUPS - 2, made=[("l3x_scores", 16), ("l3x_gathered", 4)],
                             seen=[("dma_ktile%d" % k, 2) for k in range(DEEP)] + [("l3x_scores_taken", 16), ("l3x_probs", 4)]):
                    for k in range(DEEP):
                        tile(b, k)
                for k in range(DEEP - 1):
                    tile(b, k)
                nc.tensor.wait_ge(sem("l3x_probs"), PE.due("l3x_probs"))
                for c in range(4):
                    last = gather(DEEP - 1, c, final=True)
                last.then_inc(sem("l3x_gathered"), PE.sends("l3x_gathered"))
            nc.tensor.wait_ge(sem("l3x_z_kept"), PE.due("l3x_z_kept"))
            finish_sums(B - 1)
            finish_values()
            finish_turn()
            finish_out()

            
            turn_pe()
            nc.tensor.wait_ge(sem("turned_kept"), PE.due("turned_kept"))
            mm(bank(5), w("l3a_Wq"), HT[:, :], start=True, stop=True).then_inc(sem("l3a_qk"), PE.sends("l3a_qk"))
            mm(bank(6), w("l3a_Wk"), HT[:, :], start=True, stop=True).then_inc(sem("l3a_qk"), PE.sends("l3a_qk"))
            for b in range(B):
                last = mm(PSUM[:, 7, b * P:(b + 1) * P], hT(b), w("l3a_Wv"), start=True, stop=True)
            last.then_inc(sem("l3a_v"), PE.sends("l3a_v"))
            nc.tensor.wait_ge(sem("l3a_qk_kept"), PE.due("l3a_qk_kept", n=2))
            nc.tensor.wait_ge(sem("l3a_v_kept"), PE.due("l3a_v_kept"))
            core_pe(1, lambda g, j: QT[:, j * P:(j + 1) * P], lambda g, j: KT3[:, j * P:(j + 1) * P],
                    lambda g, j: V3[:, j, :], lambda g, j: PSUM[:, 6, j * P:(j + 1) * P])
            turn_pe()
            nc.tensor.wait_ge(sem("turned_kept"), PE.due("turned_kept"))
            tail_pe(w("l3a_Wfc"))

            
            turn_pe()
            nc.tensor.wait_ge(sem("turned_kept"), PE.due("turned_kept"))
            logits_pe(w("l3f_WgT"), 16)

            def up(p):
                k = p % 2
                nc.tensor.wait_ge(sem("dma_expert%d" % k), PE.due("dma_expert%d" % k))
                nc.tensor.wait_ge(sem("l3f_h"), PE.due("l3f_h", lag=2))
                for c in range(2):
                    last = mm(bank(1 + 2 * k + c), EB[:, k, c * P:(c + 1) * P], HT[:, :], start=True, stop=True)
                last.then_inc(sem("l3f_up"), PE.sends("l3f_up"))

            def down(p):
                k = p % 2
                nc.tensor.wait_ge(sem("l3f_h"), p + 1)
                nc.tensor.wait_ge(sem("l3f_added"), PE.due("l3f_added", lag=1))
                for i in range(2 if p < PAIRS - 1 else 1):
                    r = DH * i
                    for b in range(B):
                        last = mm(PSUM[:, 6 + i, b * P:(b + 1) * P], HP[r:r + DH, k, b * P:(b + 1) * P],
                                  EB[r:r + DH, k, 2 * P:3 * P], start=True, stop=True)
                last.then_inc(sem("expert_out"), PE.sends("expert_out"))

            up(0)
            for p in range(PAIRS):
                if p + 1 < PAIRS:
                    up(p + 1)
                down(p)


def pack(parts):
    where, out, at = {}, [], 0
    for name, a in parts:
        full = np.zeros((P, a.shape[1]), a.dtype)
        full[:a.shape[0]] = a
        where[name] = (at, a.shape[1])
        out.append(full)
        at += a.shape[1]
    return where, np.concatenate(out, axis=1)


def lay_out(i):
    c = lambda v: np.ascontiguousarray(v)
    col = lambda v: v.reshape(-1, 1)
    eye = np.eye(P, dtype=np.float32)
    k = np.arange(P)
    a = [("ident", eye), ("ones", np.ones((P, P), np.float32)),
         ("headmask", (k[:, None] // HD == np.arange(H)[None]).astype(np.float32)),
         ("l0x_WqT", i["L0_xattn_Wq"].T), ("l0x_WkT", i["L0_xattn_Wk"].T), ("l0x_WvT", i["L0_xattn_Wv"].T),
         ("l0x_WoT", i["L0_xattn_Wo"].T), ("l0x_bq", col(i["L0_xattn_bq"])), ("l0x_bk", col(i["L0_xattn_bk"]))]
    enc, dec = i["L1_ffn_W_enc"], i["L1_ffn_W_dec"]
    down, up = i["L1_ffn_W_down"], i["L1_ffn_W_up"]
    bqkv = i["L1_attn_bqkv"]
    b = [("causal", np.where(k[:, None] >= k[None], 0.0, FAR).astype(np.float32)),
         ("upto", (k[:, None] <= k[None]).astype(np.float32)),
         ("l0a_w1", i["L0_attn_w1_w"]), ("l0a_v1", i["L0_attn_v1_w"]), ("l0a_w2", i["L0_attn_w2_w"]),
         ("l0a_Wdt", i["L0_attn_W_dt"]), ("l0a_WB", i["L0_attn_W_B"]), ("l0a_WC", i["L0_attn_W_C"]),
         ("l0a_Alog", i["L0_attn_A_log"]), ("l0a_conv", i["L0_attn_conv_w"].reshape(P, 3)),
         ("l0a_g", col(i["L0_attn_ln_g"])), ("l0a_b", col(i["L0_attn_ln_b"])), ("l0a_w1b", col(i["L0_attn_w1_b"])),
         ("l0a_v1b", col(i["L0_attn_v1_b"])), ("l0a_bdt", col(i["L0_attn_b_dt"])), ("l0a_D", col(i["L0_attn_D_skip"])),
         ("l0f_Wg", i["L0_ffn_Wg"]), ("l0f_b2", i["L0_ffn_b2"]),
         ("l1x_WkT", i["L1_xattn_Wk"].T), ("l1x_WvT", i["L1_xattn_Wv"].T), ("l1x_wkh", i["L1_xattn_wk_h"]),
         ("l1x_wvh", i["L1_xattn_wv_h"]), ("l1x_Wq", i["L1_xattn_Wq"]), ("l1x_wqh", i["L1_xattn_wq_h"]),
         ("l1x_bqh", col(i["L1_xattn_bq_h"])), ("l1x_bkh", col(i["L1_xattn_bk_h"])), ("l1x_Wo", i["L1_xattn_Wo"]),
         ("l1a_Wqkv", i["L1_attn_Wqkv"]), ("l1a_bqkv", bqkv.reshape(3 * H, HD).T), ("l1a_Wproj", i["L1_attn_Wproj"]),
         ("l1f_Wenc", enc.transpose(1, 0, 2).reshape(P, 256)),
         ("l1f_benc", i["L1_ffn_b_enc"].reshape(2, P).T),
         ("l1f_Wdec", dec.reshape(2, P, P).transpose(1, 0, 2).reshape(P, 256)),
         ("l1f_bdec", i["L1_ffn_b_dec"].T),
         ("l1f_Wdown", down.transpose(1, 0, 2).reshape(P, 512)),
         ("l1f_bdown", i["L1_ffn_b_down"].reshape(4, P).T),
         ("l1f_Wup", up.reshape(4, P, P).transpose(1, 0, 2).reshape(P, 512)),
         ("l1f_bup", i["L1_ffn_b_up"]), ("l1f_Wbase", i["L1_ffn_W_base"]),
         ("l2x_WqT", i["L2_xattn_Wq"].T), ("l2x_WkT", i["L2_xattn_Wk"].T), ("l2x_WvT", i["L2_xattn_Wv"].T),
         ("l2x_bq", col(i["L2_xattn_bq"])), ("l2x_bk", col(i["L2_xattn_bk"])),
         ("l2a_Win", i["L2_attn_W_in"]), ("l2a_bin", col(i["L2_attn_b_in"])), ("l2a_WB", i["L2_attn_W_B"]),
         ("l2a_bB", col(i["L2_attn_b_B"])), ("l2a_Bmat", i["L2_attn_B_mat"]), ("l2a_Cmat", i["L2_attn_C_mat"]),
         ("l2a_Wig", i["L2_attn_W_ig"]), ("l2a_Wfg", i["L2_attn_W_fg"]), ("l2a_big", col(i["L2_attn_b_ig"])),
         ("l2a_bfg", col(i["L2_attn_b_fg"])), ("l2a_WD", i["L2_attn_W_D"]), ("l2a_bD", col(i["L2_attn_b_D"])),
         ("l2a_Wout", i["L2_attn_W_out"]), ("l2f_WgT", i["L2_ffn_gate_w"].T),
         ("l3a_Wq", i["L3_attn_Wq"]), ("l3a_Wk", i["L3_attn_Wk"]), ("l3a_Wv", i["L3_attn_Wv"]),
         ("l3a_Wfc", i["L3_attn_Wfc"]), ("l3a_gamma", col(i["L3_attn_gamma"])), ("l3a_beta", col(i["L3_attn_beta"])),
         ("l3f_WgT", i["L3_ffn_gate_w"].T), ("l3x_gn", col(i["L3_xattn_g_norm"]))]
    wkv = i["L3_xattn_Wkv"]
    cc = [("l3x_Wq", i["L3_xattn_Wq"]),
          ("l3x_WkT", wkv[:, :H * DH].T.reshape(8, P, P).transpose(1, 0, 2).reshape(P, 1024)),
          ("l3x_Wv", wkv[:, H * DH:]),
          ("l3x_Wout", i["L3_xattn_Wout"].reshape(8, P, P).transpose(1, 0, 2).reshape(P, 1024))]
    r = [("iota", np.arange(16, dtype=np.float32)), ("l0x_bv", i["L0_xattn_bv"]), ("l0x_bo", i["L0_xattn_bo"]),
         ("l0a_w2b", i["L0_attn_w2_b"]), ("l1x_bvh", i["L1_xattn_bv_h"]), ("l1a_bproj", i["L1_attn_bproj"]),
         ("l1f_bbase", i["L1_ffn_b_base"]), ("l2x_bv", i["L2_xattn_bv"]), ("l2a_bout", i["L2_attn_b_out"]),
         ("l2a_gamma", i["L2_attn_gamma"]), ("l2a_beta", i["L2_attn_beta"]), ("l3x_qs", i["L3_xattn_q_scale"]),
         ("l3x_ks", i["L3_xattn_k_scale"]), ("l3x_nk", i["L3_xattn_null_kv"][0]), ("l3x_nv", i["L3_xattn_null_kv"][1]),
         ("l3x_go", i["L3_xattn_g_out"]), ("l3a_bfc", i["L3_attn_bfc"]), ("l3f_gb", i["L3_ffn_gate_b"])]
    cols, arrays = {}, {}
    for part, parts in (("a", a), ("b", b), ("c", cc)):
        where, arrays["w" + part] = pack(parts)
        cols.update({n: (part, *v) for n, v in where.items()})
    rows, at = {}, 0
    for name, v in r:
        rows[name] = (at, v.shape[0])
        at += v.shape[0]
    arrays["rows"] = np.concatenate([v for _, v in r])[None]
    ctx = i["ctx_1024"].reshape(NK, P)
    arrays["wk"] = c(wkv[:, :H * DH])
    arrays["x"] = c(i["x"].transpose(1, 0, 2))
    arrays["ctxT"] = c(ctx.T)
    arrays["ctxr"] = c(ctx)
    arrays["ctxk"] = c(ctx.reshape(NK // P, P, P).transpose(1, 0, 2))
    arrays["mask"] = c(i["mask_SxS2_bk1"])
    arrays["idx"] = c(i["L1_ffn_connected_idx"])[None]

    def expert_rows(w1, w2, b1=None):
        e = w1.shape[0]
        parts = [w1, w2.reshape(e, FC, P, P).transpose(0, 2, 1, 3).reshape(e, P, FF)]
        if b1 is not None:
            parts.append(b1.reshape(e, FC, P).transpose(0, 2, 1))
        return c(np.concatenate(parts, axis=2).reshape(e * P, -1))

    arrays["l0f_experts"] = expert_rows(i["L0_ffn_W1"], i["L0_ffn_W2"], i["L0_ffn_b1"])
    arrays["l2f_experts"] = expert_rows(i["L2_ffn_w1"], i["L2_ffn_w2"])
    w13, w2 = i["L3_ffn_w13"], i["L3_ffn_w2"]
    pairs = np.zeros((9, P, 3 * P), np.float32)
    for p in range(9):
        for q in range(2):
            if p == 8 and q == 1:
                continue
            w13e, w2e = (w13[2 * p + q], w2[2 * p + q]) if p < 8 else (i["L3_ffn_w13_s"], i["L3_ffn_w2_s"])
            pairs[p, :, q * DH:(q + 1) * DH] = w13e[:DH].T
            pairs[p, :, P + q * DH:P + (q + 1) * DH] = w13e[DH:].T
            pairs[p, q * DH:(q + 1) * DH, 2 * P:] = w2e.T
    arrays["l3f_experts"] = pairs.reshape(9 * P, 3 * P)
    return arrays, cols, rows



def kernel(**inputs):
    import concourse.bacc as bacc
    from concourse.bass_utils import run_bass_kernel_spmd

    arrays, cols, rows = lay_out({k: np.asarray(v) for k, v in inputs.items()})
    nc = bacc.Bacc("TRN2", target_bir_lowering=False, num_devices=1)
    d = {n: nc.dram_tensor("in_" + n, a.shape, mybir.dt.from_np(a.dtype), kind="ExternalInput").ap()
         for n, a in arrays.items()}
    d["out"] = nc.dram_tensor("out_x", (P, B, P), F32, kind="ExternalOutput").ap()
    build(nc, d, cols, rows)
    r = run_bass_kernel_spmd(nc, [{"in_" + n: a for n, a in arrays.items()}], core_ids=[0])
    return np.ascontiguousarray(r.results[0]["out_x"].transpose(1, 0, 2))
```

```python
from contextlib import ExitStack

import concourse.bass as bass
import concourse.mybir as mybir
import numpy as np

F32 = mybir.dt.float32
I32 = mybir.dt.int32
U8 = mybir.dt.uint8
ALU = mybir.AluOpType
ACT = mybir.ActivationFunctionType
AX = mybir.AxisListType

P = 128
B = 4
T = B * P
S = 2048
NK = B * S
H = 16
HD = P // H
DH = 64
FF = 512
FC = FF // P
EPS = 1e-5
KEY_TILES = S // P
CAPACITY = int(1.25 * T / 16)
MASKED = -1.0e9
FAR = -1.0e30
SAFE_EXPONENT = 60.0


class Engine:

    def __init__(self, engine):
        self.i, self.made, self.seen = engine, {}, {}

    def sends(self, signal):
        self.made[signal] = self.made.get(signal, 0) + 1
        return 1

    def sent(self, signal):
        return self.made[signal]

    def due(self, signal, n=1, lag=0):
        self.seen[signal] = self.seen.get(signal, 0) + n
        value = self.seen[signal] - lag
        if isinstance(value, int) and value <= 0:
            return None
        return value * 16 if signal.startswith("dma_") else value

    def loop(self, trips, made=(), seen=()):
        return _Loop(self, trips, dict(made), dict(seen))


class _Loop:

    def __init__(self, e, trips, made, seen):
        self.e, self.trips, self.per = e, trips, (made, seen)

    def __enter__(self):
        self.cm = self.e.i.Fori(0, self.trips)
        i = self.cm.__enter__()
        self.base = [{k: c.get(k, 0) for k in per} for c, per in zip((self.e.made, self.e.seen), self.per)]
        for c, per in zip((self.e.made, self.e.seen), self.per):
            for k, n in per.items():
                c[k] = c.get(k, 0) + i * n
        return i

    def __exit__(self, *a):
        self.cm.__exit__(*a)
        for c, per, base in zip((self.e.made, self.e.seen), self.per, self.base):
            for k, n in per.items():
                c[k] = base[k] + self.trips * n


def build(nc, d, cols, rows):
    with ExitStack() as ctx:
        def sb(name, shape, dt=F32):
            return ctx.enter_context(nc.sbuf_tensor(name, shape, dt))

        made = {}

        def sem(name):
            if name not in made:
                made[name] = ctx.enter_context(nc.semaphore(name))
            return made[name]

        n_a, n_b, n_c = (d[k].shape[1] for k in ("wa", "wb", "wc"))
        WA = sb("WA", [P, n_a])
        WB = sb("WB", [P, n_b])
        ROWS = sb("ROWS", [P, d["rows"].shape[1]])
        X = sb("X", [P, B, P])
        CT = sb("CT", [P, NK])
        CK = sb("CK", [P, B * KEY_TILES, P])
        ARENA = sb("ARENA", [P, 18432])
        HN = sb("HN", [P, B, P])
        HT = sb("HT", [P, T])
        OT = sb("OT", [P, T])
        QT = sb("QT", [P, T])
        TMP = sb("TMP", [P, T])
        ACC = sb("ACC", [P, B, P])
        ST = sb("ST", [P, B, 6])
        MV = sb("MV", [P, B, 2])
        VE = sb("VE", [P, B])
        RSTD = sb("RSTD", [P, B])
        MHALF = sb("MHALF", [P, B])
        SM = sb("SM", [P, 1024])
        RK = sb("RK", [P, B * KEY_TILES * H])
        WK = sb("WK", [P, H * DH])
        SQ = sb("SQ", [P, 2, 512])
        W8 = sb("W8", [P, 4 * FF])
        MASK8 = W8[:, 0:S // 4].bitcast(U8)
        IDX = sb("IDX", [P, 8], I32)
        PSUM = ctx.enter_context(nc.psum_tensor("PSUM", [P, 8, 512], F32))

        WC = CK[:, :, :].rearrange("p a b -> p (a b)")[:, 0:n_c]
        SPARE = CK[:, :, :].rearrange("p a b -> p (a b)")[:, n_c:]

        def w(name, rows_=P):
            part, at, n = cols[name]
            return {"a": WA, "b": WB, "c": WC}[part][0:rows_, at:at + n]

        def row(name, off=0, n=None):
            at, m = rows[name]
            return ROWS[:, at + off:at + off + (n or m)]

        def bank(k, rows_=P):
            return PSUM[0:rows_, k, :]

        def bank4(k):
            return PSUM[:, k, :].rearrange("p (b f) -> p b f", b=B)

        def over(ap, n):
            return ap.unsqueeze(1).broadcast_to([ap.shape[0], n, ap.shape[1]])

        def each(ap, n):
            return ap.unsqueeze(2).broadcast_to([ap.shape[0], ap.shape[1], n])

        ident = w("ident")
        SP = Engine(nc.sync)
        PE = Engine(nc.tensor)
        AC = Engine(nc.scalar)
        DV = Engine(nc.vector)
        PO = Engine(nc.gpsimd)
        mm, tp = nc.tensor.matmul, nc.tensor.transpose
        act, ve = nc.scalar.activation, nc.vector

        def hT(b):
            return HT[:, b * P:(b + 1) * P]

        QS = ARENA[:, 0:8192]
        KS = ARENA[:, 8192:16384]
        SX = ARENA[:, 16384:17408].rearrange("p (k n) -> p k n", k=2)
        PT = ARENA[:, 17408:18432].rearrange("p (k n) -> p k n", k=2)
        L_SUM = SM[:, 0:B * H]
        L_INV = SM[:, 64:64 + B * H]
        MX = SM[:, 128:136].rearrange("p (k n) -> p k n", k=2)
        VS = SM[:, 512:1024]

        KT = ARENA[:, 0:NK]
        SL = ARENA[:, 8192:12288].rearrange("p (k n) -> p k n", k=2)
        PTL = ARENA[:, 12288:14336].rearrange("p (t n) -> p t n", t=KEY_TILES)
        KEEP = ARENA[:, 14336:16384]
        NEG = ARENA[:, 16384:18432]
        LMX, LNM, LSUM, LINV = (SM[:, k:k + B] for k in (160, 164, 168, 172))
        ZT = OT

        GATE = SM[:, 192:192 + B * H]
        EACC = ACC

        CTB = CT[:, :].rearrange("p (b m s) -> p b s m", b=B, s=H)
        KSB = KS.rearrange("p (b m s) -> p b s m", b=B, s=H)
        QM = QS.rearrange("p (h n) -> p h n", h=H)

        CHUNKS = NK // 512

        CB = ARENA[:, 0:520].rearrange("p (b t) -> p b t", b=B)
        CONV, U, VG, DT, DTU, ZB, EB1 = (ARENA[:, 640 + k * 512:1152 + k * 512] for k in range(7))
        Y0 = ARENA[:, 4224:4736]
        DA = ARENA[:, 5376:5376 + 4096]
        DBU = ARENA[:, 9472:9472 + 4096]
        HS = ARENA[:, 13568:13568 + 4096]
        SPREAD_BANKS = (4, 5, 6, 7, 0, 2)
        ANEG = SM[:, 176:192]
        FOLDED = SM[:, 448:448 + 2 * HD]
        WKK, WVV = FOLDED[:, 0:HD], FOLDED[:, HD:2 * HD]

        LG = SM[:, 256:256 + B * H]
        M8 = SM[:, 320:320 + B * 8].rearrange("p (b e) -> p b e", b=B)
        GX = SM[:, 352:352 + B * H]
        GS = SM[:, 416:416 + B]
        GT = QT
        N2, NW = 8, 2 * FF
        HB = ARENA[:, 8192:12288].rearrange("p (k c n) -> p k c n", k=2, c=FC)
        E2 = CK[:, :, :].rearrange("p a b -> p (a b)")

        OH8 = SM[:, 464:496].rearrange("p (b e) -> p b e", b=B)

        QKV = ARENA[:, 16384:17920].rearrange("p (b c) -> p b c", b=B)
        PIECES = ("pieces_even", "pieces_odd")
        PIECES_KEPT = ("pieces_kept_act", "pieces_kept_dve")

        def piece(x, a):
            return x[0:HD, a * P:(a + 1) * P]

        NA, NR, NH = 8, 64, 32
        ENC = ARENA[:, 8192:9216].rearrange("p (k n) -> p k n", k=2)
        DIFF = ARENA[:, 9216:10240].rearrange("p (k n) -> p k n", k=2)
        MID = ARENA[:, 10240:12288].rearrange("p (k n) -> p k n", k=4)
        LOSS = SM[:, 0:32].rearrange("p (b n) -> p b n", b=B)
        LMIN = SM[:, 32:36]
        SEL = SM[:, 40:72].rearrange("p (b n) -> p b n", b=B)
        IDXF = SM[:, 72:80]
        EQ = SM[:, 192:256].rearrange("p (a n) -> p a n", a=NA)
        PICK = SM[:, 256:512].rearrange("p (b a n) -> p b a n", b=B, a=NA)
        OH = SM[:, 80:112].rearrange("p (b a) -> p b a", b=B)
        SHALF = SM[:, 112:128].rearrange("p (b j) -> p b j", b=B)
        BUP = SM[:, 136:140]

        OHT = SM[:, 512:1024]

        def PICKT_(b):
            return OHT[0:NA, b * P:(b + 1) * P]

        XP, XB, BX, IG, FG, HR, YT = (ARENA[:, k * 512:(k + 1) * 512] for k in range(7))

        QP = ARENA[:, 0:8192]
        QSC = ARENA[:, 8192:12288].rearrange("p (c n) -> p c n", c=8)
        ZS = ARENA[:, 10240:12288]
        PR = ARENA[:, 12288:16384].rearrange("p (k n) -> p k n", k=2)
        LS = (ARENA[:, 8192:10240], ARENA[:, 16384:18432])
        QN = CT[:, 0:4096].rearrange("p (b n) -> p b n", b=B)
        T1 = CT[:, 4096:5120]
        Q2 = CT[:, 4096:6144].rearrange("p (k n) -> p k n", k=2)
        OTK = CT[:, 5120:6144]
        OT8 = CT[:, 6144:7168]
        DEEP = 4
        CTT = SPARE[:, 0:512].rearrange("p (k n) -> p k n", k=DEEP)
        CKT = SPARE[:, 512:1024].rearrange("p (k n) -> p k n", k=DEEP)
        SCR = SPARE[:, 1024:1088]
        NKH = SPARE[:, 1088:1152]
        SNK, PN, QSS, LT = (SPARE[:, k:k + 64] for k in (1152, 1216, 1280, 1344))
        NSS, TOP, LOW, SHIFT, SCRC = (SPARE[:, k:k + 1] for k in range(1408, 1413))
        OAT = ACC
        TILE_GROUPS = KEY_TILES // DEEP

        N8, SLOTS = 16, 16 * CAPACITY
        HALF = SLOTS // 2
        PAIRS8 = N8 // 2
        PW = 2 * FC * CAPACITY
        E8 = [ARENA[:, 14336 + e * NW:14336 + (e + 1) * NW] if e < 4 else
              ARENA[:, 4096 + (e - 4) * NW:4096 + (e - 3) * NW] if e < 14 else
              W8[:, (e - 14) * NW:(e - 13) * NW] for e in range(N8)]
        PLACED = CT[:, 0:B * SLOTS]
        PLACED_T = CT[0:CAPACITY, 2560:2560 + 4 * T].rearrange("p (k n) -> p k n", k=4)
        HID8 = CT[:, 5120:5120 + PAIRS8 * PW]
        XD = SPARE[:, 2048:2048 + SLOTS]
        OS = SPARE[0:CAPACITY, 2688:2688 + 4 * P].rearrange("p (k n) -> p k n", k=2)

        KT3 = KS[:, 0:512]
        V3 = ARENA[:, 0:512].rearrange("p (b f) -> p b f", b=B)

        HP = ARENA[:, 0:1024].rearrange("p (k n) -> p k n", k=2)
        TG = ARENA[:, 1024:2048].rearrange("p (k n) -> p k n", k=2)
        PAIRS = 9
        E11 = ARENA[:, 2048:2048 + PAIRS * 3 * P].rearrange("p (k n) -> p k n", k=PAIRS)
        PICK2 = ARENA[0:16, 2048 + PAIRS * 3 * P:2048 + PAIRS * 3 * P + 16 * DH]

        block = ctx.enter_context(nc.Block())

        @block.sync
        def _(sync):
            def load(dst, src, signal):
                sync.dma_start(dst, src).then_inc(sem(signal), 16)

            load(X[:, :, :], d["x"], "dma_x")
            load(WA[:, :], d["wa"], "dma_wa")
            for c in range(B):
                load(CT[:, c * S:(c + 1) * S], d["ctxT"][:, c * S:(c + 1) * S], "dma_ctx%d" % c)
            load(WK[:, :], d["wk"], "dma_wk")
            nc.sync.wait_ge(sem("dma_ctx3"), SP.due("dma_ctx3"))
            load(ROWS[:, :], d["rows"].broadcast_to([P, d["rows"].shape[1]]), "dma_rows")
            load(WB[:, :], d["wb"], "dma_wb")
            load(MASK8[:, :], d["mask"], "dma_mask")
            load(IDX[:, :], d["idx"].broadcast_to([P, 8]), "dma_idx")
            load(CK[:, :, :].rearrange("p a b -> p (a b)"), d["l0f_experts"], "dma_moe2")
            nc.sync.wait_ge(sem("x_ready"), SP.due("x_ready", n=3))
            load(CK[:, :, :], d["ctxk"], "dma_ck")
            nc.sync.wait_ge(sem("x_ready"), SP.due("x_ready", n=2))
            load(W8[:, :], d["l2f_experts"][:, 14 * NW:16 * NW], "dma_moe8_early")
            load(ARENA[:, 14336:14336 + 4 * NW], d["l2f_experts"][:, 0:4 * NW], "dma_moe8_early")
            nc.sync.wait_ge(sem("x_ready"), SP.due("x_ready", n=2))
            load(ARENA[:, 4096:4096 + 4 * NW], d["l2f_experts"][:, 4 * NW:8 * NW], "dma_moe8")
            load(ARENA[:, 4096 + 4 * NW:4096 + 10 * NW], d["l2f_experts"][:, 8 * NW:14 * NW], "dma_moe8_late")
            load(WC, d["wc"], "dma_wc")
            for b in range(B):
                for k in range(DEEP):
                    n0 = (b * KEY_TILES + k) * P
                    due = SP.due("l3x_gathered", lag=DEEP)
                    if due is not None:
                        nc.sync.wait_ge(sem("l3x_gathered"), due)
                    sync.dma_start(CTT[:, k, :], d["ctxT"][:, n0:n0 + P]).then_inc(sem("dma_ktile%d" % k), 16)
                    sync.dma_start(CKT[:, k, :], d["ctxr"][n0:n0 + P, :]).then_inc(sem("dma_ktile%d" % k), 16)
                with SP.loop(TILE_GROUPS - 1, seen=[("l3x_gathered", DEEP)]) as i:
                    for k in range(DEEP):
                        n0 = i * DEEP * P + ((b * KEY_TILES + DEEP + k) * P)
                        due = SP.due("l3x_gathered", lag=DEEP)
                        if due is not None:
                            nc.sync.wait_ge(sem("l3x_gathered"), due)
                        sync.dma_start(CTT[:, k, :], d["ctxT"][:, bass.ds(n0, P)]).then_inc(sem("dma_ktile%d" % k), 16)
                        sync.dma_start(CKT[:, k, :], d["ctxr"][bass.ds(n0, P), :]).then_inc(sem("dma_ktile%d" % k), 16)
            nc.sync.wait_ge(sem("x_ready"), SP.due("x_ready", n=3))
            load(ARENA[:, 2048:2048 + d["l3f_experts"].shape[1]], d["l3f_experts"], "dma_moe11")
            sync.wait_ge(sem("x_ready"), 12)
            sync.dma_start(d["out"], X[:, :, :]).then_inc(sem("out_written"), 16)
            sync.wait_ge(sem("out_written"), 16)

        @block.gpsimd
        def _(gpsimd):
            def norm_pool():
                nc.gpsimd.wait_ge(sem("variance"), PO.due("variance"))
                nc.gpsimd.tensor_tensor(RSTD[:, :], VE[:, :], MHALF[:, :], ALU.pow).then_inc(sem("rstd"), PO.sends("rstd"))

            nc.gpsimd.memset(MHALF[:, :], -0.5).then_inc(sem("halves"), PO.sends("halves"))
            nc.gpsimd.wait_ge(sem("halves"), 1)
            norm_pool()

            nc.gpsimd.wait_ge(sem("x_ready"), PO.due("x_ready"))
            nc.gpsimd.memset(CB[:, :, 0:P + 2:P + 1], 0.0).then_inc(sem("l0a_pads"), PO.sends("l0a_pads"))
            norm_pool()
            norm_pool()
            for half in range(2):
                nc.gpsimd.wait_ge(sem("l0a_decay"), PO.due("l0a_decay"))
                cut = DA.rearrange("p (n t) -> p n t", t=P)[:, :, 0:1]
                nc.gpsimd.memset(cut, 0.0).then_inc(sem("l0a_decay_cut"), PO.sends("l0a_decay_cut"))

            norm_pool()

            norm_pool()

            norm_pool()

            norm_pool()

            norm_pool()

            norm_pool()
            norm_pool()

            norm_pool()
            nc.gpsimd.wait_ge(sem("l3x_null_square"), PO.due("l3x_null_square"))
            nc.gpsimd.tensor_tensor(NSS, NSS, MHALF[:, 0:1], ALU.pow).then_inc(sem("l3x_null_rnorm"), PO.sends("l3x_null_rnorm"))

            norm_pool()
            norm_pool()
            for b in range(B):
                if b == 0:
                    nc.gpsimd.wait_ge(sem("l3x_qp_kept"), PO.due("l3x_qp_kept", n=4 * B))
                due = PO.due("l3x_l", lag=2)
                if due is not None:
                    nc.gpsimd.wait_ge(sem("l3x_l"), due)
                nc.gpsimd.memset(LS[b % 2], 0.0).then_inc(sem("pool_step"), PO.sends("pool_step"))
                nc.gpsimd.wait_ge(sem("pool_step"), PO.sent("pool_step"))

                def add(k):
                    nc.gpsimd.wait_ge(sem("l3x_probs"), PO.due("l3x_probs"))
                    nc.gpsimd.tensor_tensor(LS[b % 2], LS[b % 2], PR[:, k % 2, :], ALU.add)\
                        .then_inc(sem("l3x_summed"), PO.sends("l3x_summed"))
                    nc.gpsimd.wait_ge(sem("l3x_summed"), PO.sent("l3x_summed"))

                for k in range(DEEP):
                    add(k)
                with PO.loop(TILE_GROUPS - 1, made=[("l3x_summed", 4)], seen=[("l3x_probs", 4)]):
                    for k in range(DEEP):
                        add(k)
            norm_pool()

            norm_pool()
            norm_pool()

            norm_pool()

        @block.scalar
        def _(scalar):
            def turn_act(dst, scale=1.0, bias=0.0):
                nc.scalar.wait_ge(sem("turned"), AC.due("turned"))
                act(dst[:, :], bank(0), ACT.Identity, scale=scale, bias=bias).then_inc(sem("turned_kept"), AC.sends("turned_kept"))

            def key_norms_act(n0, n):
                for m in range(n0, n0 + n):
                    nc.scalar.wait_ge(sem("key_rows"), AC.due("key_rows"))
                    due = AC.due("key_norm", lag=2)
                    if due is not None:
                        nc.scalar.wait_ge(sem("key_norm"), due)
                    act(SQ[:, m % 2, :], bank(5 + 2 * (m % 2)), ACT.Square).then_inc(sem("key_squares"), AC.sends("key_squares"))

            def core_act(groups, scale, norms_from=None):
                for g in range(groups):
                    nc.scalar.wait_ge(sem("scores_shifted"), AC.due("scores_shifted"))
                    act(SX[:, g % 2, :], SX[:, g % 2, :], ACT.Exp, scale=scale).then_inc(sem("probs"), AC.sends("probs"))
                    if norms_from is not None:
                        key_norms_act(norms_from + 4 * g, 2)
                    nc.scalar.wait_ge(sem("probs_turned"), AC.due("probs_turned"))
                    due = AC.due("values_summed", lag=2)
                    if due is not None:
                        nc.scalar.wait_ge(sem("values_summed"), due)
                    act(PT[:, g % 2, :], bank(3 + g % 2), ACT.Copy).then_inc(sem("pt_ready"), AC.sends("pt_ready"))
                    if norms_from is not None:
                        key_norms_act(norms_from + 4 * g + 2, 2)

            def long_act(scale, masked):
                def probs(b):
                    nc.scalar.wait_ge(sem("long_shift"), AC.due("long_shift"))
                    src = SL[:, b % 2, :] if masked else PSUM[:, 0:4, :].rearrange("p c n -> p (c n)")
                    act(SL[:, b % 2, :], src, ACT.Exp, scale=scale, bias=LNM[:, b:b + 1],
                        accum_out=LSUM[:, b:b + 1]).then_inc(sem("long_probs"), AC.sends("long_probs"))

                probs(0)
                for b in range(B):
                    for c in range(4):
                        nc.scalar.wait_ge(sem("long_turned"), AC.due("long_turned"))
                        act(PTL[:, 4 * c:4 * c + 4, :], bank4(4 + c % 2), ACT.Copy).then_inc(sem("long_pt"), AC.sends("long_pt"))
                    if b + 1 < B:
                        probs(b + 1)
                    nc.scalar.wait_ge(sem("long_z"), AC.due("long_z"))
                    act(ZT[:, b * P:(b + 1) * P], PSUM[:, 6, 0:P], ACT.Copy).then_inc(sem("long_z_kept"), AC.sends("long_z_kept"))

            def context_keys_act(dst, bias, m=P, c0=0, c1=CHUNKS):
                for c in range(c0, c1):
                    nc.scalar.wait_ge(sem("context_keys"), AC.due("context_keys"))
                    act(dst[0:m, c * 512:(c + 1) * 512], bank(1 + c % 2, m), ACT.Identity, bias=bias)\
                        .then_inc(sem("context_keys_kept"), AC.sends("context_keys_kept"))

            nc.scalar.wait_ge(sem("dma_wa"), AC.due("dma_wa"))
            turn_act(HT)
            nc.scalar.wait_ge(sem("q_rows"), AC.due("q_rows"))
            act(QT[:, :], bank(5), ACT.Identity, bias=w("l0x_bq")).then_inc(sem("q_rows_kept"), AC.sends("q_rows_kept"))
            context_keys_act(KS, w("l0x_bk"))
            core_act(16, HD ** -0.5, norms_from=0)
            turn_act(OT, bias=w("l0x_bv"))

            nc.scalar.wait_ge(sem("dma_wb"), AC.due("dma_wb"))
            turn_act(HT, scale=w("l0a_g"), bias=w("l0a_b"))
            act(ANEG, w("l0a_Alog"), ACT.Exp).then_inc(sem("l0a_expA"), AC.sends("l0a_expA"))
            nc.scalar.wait_ge(sem("l0a_x1"), AC.due("l0a_x1"))
            act(CB[:, :, 1:P + 1], bank4(1), ACT.Identity, bias=w("l0a_w1b"))\
                .then_inc(sem("l0a_x1_kept"), AC.sends("l0a_x1_kept"))
            nc.scalar.wait_ge(sem("l0a_preact"), AC.due("l0a_preact"))
            act(OT[:, :], CONV, ACT.Tanh, scale=0.5).then_inc(sem("l0a_tanh"), AC.sends("l0a_tanh"))
            nc.scalar.wait_ge(sem("l0a_preact"), AC.due("l0a_preact"))
            act(TMP[:, :], VG, ACT.Tanh, scale=0.5).then_inc(sem("l0a_tanh"), AC.sends("l0a_tanh"))
            nc.scalar.wait_ge(sem("l0a_preact"), AC.due("l0a_preact"))
            act(EB1, ZB, ACT.Abs).then_inc(sem("act_step"), AC.sends("act_step"))
            nc.scalar.wait_ge(sem("act_step"), AC.sent("act_step"))
            act(EB1, EB1, ACT.Exp, scale=-1.0).then_inc(sem("act_step"), AC.sends("act_step"))
            nc.scalar.wait_ge(sem("act_step"), AC.sent("act_step"))
            act(EB1, EB1, ACT.Ln, bias=1.0).then_inc(sem("l0a_log"), AC.sends("l0a_log"))
            nc.scalar.wait_ge(sem("l0a_dt_ready"), AC.due("l0a_dt_ready"))
            for half in range(2):
                if half:
                    nc.scalar.wait_ge(sem("l0a_scan"), AC.due("l0a_scan"))
                for n in range(8):
                    last = act(DA[:, n * 512:(n + 1) * 512], DT, ACT.Exp, scale=ANEG[:, half * 8 + n:half * 8 + n + 1])
                last.then_inc(sem("l0a_decay"), AC.sends("l0a_decay"))

            nc.scalar.wait_ge(sem("x_ready"), AC.due("x_ready", n=2))
            context_keys_act(KT, w("l1x_bkh", HD), HD, 0, CHUNKS // 2)
            turn_act(HT)
            nc.scalar.wait_ge(sem("gate_shifted"), AC.due("gate_shifted"))
            act(GX[:, 0:32], GX[:, 0:32], ACT.Exp).then_inc(sem("gate_exp"), AC.sends("gate_exp"))
            for e in range(N2):
                if e == 2:
                    nc.scalar.wait_ge(sem("gates_turned"), AC.due("gates_turned"))
                    act(GT[0:8, :], bank(6, 8), ACT.Copy).then_inc(sem("gates_kept"), AC.sends("gates_kept"))
                due = AC.due("expert_out", lag=2)
                if due is not None:
                    nc.scalar.wait_ge(sem("expert_out"), due)
                for c in range(FC):
                    nc.scalar.wait_ge(sem("hidden"), AC.due("hidden"))
                    act(HB[:, e % 2, c, :], bank(1 + c % 2), ACT.Relu,
                        bias=w("l0f_b1")[:, e * FC + c:e * FC + c + 1])\
                        .then_inc(sem("hidden_kept"), AC.sends("hidden_kept"))

            context_keys_act(KT, w("l1x_bkh", HD), HD, CHUNKS // 2)
            turn_act(HT)
            nc.scalar.wait_ge(sem("q_rows"), AC.due("q_rows"))
            act(TMP[:, :], bank(5), ACT.Copy).then_inc(sem("q_rows_kept"), AC.sends("q_rows_kept"))
            long_act(1.0, True)
            turn_act(OT)

            def pieces_act(dst):
                for j in range(0, H, 2):
                    nc.scalar.wait_ge(sem("pieces_even"), AC.due("pieces_even"))
                    act(dst[0:HD, :].rearrange("p (t j) -> p t j", j=H)[:, :, j], bank(3 + j % 4, HD), ACT.Copy)\
                        .then_inc(sem("pieces_kept_act"), AC.sends("pieces_kept_act"))

            turn_act(HT)
            pieces_act(KS)
            pieces_act(QS)
            nc.scalar.wait_ge(sem("l1a_v"), AC.due("l1a_v"))
            pieces_act(KS)
            core_act(16, HD ** -0.5, norms_from=64)
            turn_act(OT)

            nc.scalar.wait_ge(sem("x_ready"), AC.due("x_ready", n=3))
            context_keys_act(KT, w("l2x_bk"), c1=CHUNKS // 2)
            turn_act(HT)
            for k in range(2):
                nc.scalar.wait_ge(sem("l1f_hidden"), AC.due("l1f_hidden"))
                act(ENC[:, k, :], bank(1 + k), ACT.Relu, bias=w("l1f_benc")[:, k:k + 1])\
                    .then_inc(sem("l1f_hidden_kept"), AC.sends("l1f_hidden_kept"))
            for k in range(4):
                nc.scalar.wait_ge(sem("l1f_hidden"), AC.due("l1f_hidden"))
                act(MID[:, k, :], bank(1 + k % 2), ACT.Relu, bias=w("l1f_bdown")[:, k:k + 1])\
                    .then_inc(sem("l1f_hidden_kept"), AC.sends("l1f_hidden_kept"))

            context_keys_act(KT, w("l2x_bk"), c0=CHUNKS // 2)
            turn_act(HT)
            nc.scalar.wait_ge(sem("q_rows"), AC.due("q_rows"))
            act(QT[:, :], bank(5), ACT.Identity, bias=w("l2x_bq")).then_inc(sem("q_rows_kept"), AC.sends("q_rows_kept"))
            long_act(P ** -0.5, False)

            turn_act(HT)
            nc.scalar.wait_ge(sem("l2a_mm"), AC.due("l2a_mm"))
            act(XP, bank(1), ACT.Identity, bias=w("l2a_bin")).then_inc(sem("l2a_kept"), AC.sends("l2a_kept"))
            nc.scalar.wait_ge(sem("l2a_mm"), AC.due("l2a_mm"))
            act(XB, bank(2), ACT.Identity, bias=w("l2a_bB")).then_inc(sem("l2a_kept"), AC.sends("l2a_kept"))
            nc.scalar.wait_ge(sem("l2a_mm"), AC.due("l2a_mm", n=2))
            nc.scalar.wait_ge(sem("l2a_halves"), AC.due("l2a_halves"))
            act(IG[0:16, :], bank(3, 16), ACT.Tanh, scale=0.5, bias=SM[0:16, 0:1])
            act(FG[0:16, :], bank(4, 16), ACT.Tanh, scale=0.5, bias=SM[0:16, 1:2])\
                .then_inc(sem("l2a_gates"), AC.sends("l2a_gates"))
            nc.scalar.wait_ge(sem("l2a_mm"), AC.due("l2a_mm", n=2))
            act(YT, bank(6), ACT.Tanh, bias=w("l2a_bD")).then_inc(sem("l2a_kept"), AC.sends("l2a_kept"))

            nc.scalar.wait_ge(sem("key_squares_all"), AC.due("key_squares_all"))
            act(RK[:, :], RK[:, :], ACT.Sqrt).then_inc(sem("key_norms"), AC.sends("key_norms"))
            turn_act(HT)
            nc.scalar.wait_ge(sem("gate_shifted"), AC.due("gate_shifted"))
            act(GX, GX, ACT.Exp).then_inc(sem("gate_exp"), AC.sends("gate_exp"))
            for s in range(2):
                nc.scalar.wait_ge(sem("l2f_part"), AC.due("l2f_part"))
                act(XD[:, s * HALF:(s + 1) * HALF], PSUM[:, 1 + s, 0:HALF], ACT.Copy)\
                    .then_inc(sem("l2f_part_kept"), AC.sends("l2f_part_kept"))

            def hidden(g):
                nc.scalar.wait_ge(sem("hidden"), AC.due("hidden"))
                act(HID8[:, g * PW:(g + 1) * PW], PSUM[:, 3 + g % 2, 0:PW], ACT.Relu)\
                    .then_inc(sem("hidden_kept"), AC.sends("hidden_kept"))

            hidden(0)
            hidden(1)
            for g in range(PAIRS8):
                nc.scalar.wait_ge(sem("l2f_part"), AC.due("l2f_part"))
                due = AC.due("l2f_combined", lag=2)
                if due is not None:
                    nc.scalar.wait_ge(sem("l2f_combined"), due)
                act(OS[:, g % 2, :], PSUM[0:CAPACITY, 5 + g % 2, 0:2 * P], ACT.Copy)\
                    .then_inc(sem("l2f_part_kept"), AC.sends("l2f_part_kept"))
                if g + 2 < PAIRS8:
                    hidden(g + 2)

            turn_act(HT, scale=w("l3x_gn"))
            for b in range(B):
                nc.scalar.wait_ge(sem("l3x_q"), AC.due("l3x_q"))
                due = AC.due("l3x_squares_summed", lag=2)
                if due is not None:
                    nc.scalar.wait_ge(sem("l3x_squares_summed"), due)
                src = PSUM[:, 2 * b:2 * b + 2, :].rearrange("p c n -> p (c n)")
                act(Q2[:, b % 2, :], src, ACT.Square).then_inc(sem("l3x_squares"), AC.sends("l3x_squares"))
            nc.scalar.wait_ge(sem("l3x_squares_ready"), AC.due("l3x_squares_ready"))
            act(QSS, QSS, ACT.Sqrt).then_inc(sem("l3x_norms"), AC.sends("l3x_norms"))
            nc.scalar.wait_ge(sem("l3x_scales"), AC.due("l3x_scales"))
            for b in range(B):
                nc.scalar.wait_ge(sem("l3x_q_turned"), AC.due("l3x_q_turned"))
                act(QSC[:, :, b * P:(b + 1) * P], PSUM[:, 2 * b:2 * b + 2, :].rearrange("p k (c n) -> p (k c) n", n=P),
                    ACT.Identity, scale=SCRC).then_inc(sem("l3x_q_scaled"), AC.sends("l3x_q_scaled"))
            qph = QP.rearrange("p (b k h n) -> p b k h n", b=B, k=2, n=P)
            for b in range(B):
                for j in range(4):
                    nc.scalar.wait_ge(sem("l3x_qp"), AC.due("l3x_qp"))
                    act(qph[:, b, j // 2, j % 2:8:2, :], bank4(j % 2), ACT.Copy).then_inc(sem("l3x_qp_kept"), AC.sends("l3x_qp_kept"))

            def probs(k):
                nc.scalar.wait_ge(sem("l3x_scores_taken"), AC.due("l3x_scores_taken", n=4))
                act(PR[:, k % 2, :], PR[:, k % 2, :], ACT.Exp, bias=SHIFT).then_inc(sem("l3x_probs"), AC.sends("l3x_probs"))

            def finish_turn():
                nc.scalar.wait_ge(sem("l3x_oT"), AC.due("l3x_oT"))
                act(OT8, PSUM[:, 2:4, :].rearrange("p c n -> p (c n)"), ACT.Copy)\
                    .then_inc(sem("l3x_oT_kept"), AC.sends("l3x_oT_kept"))

            probs(0)
            for b in range(B):
                for k in range(1, DEEP):
                    probs(k)
                if b:
                    finish_turn()
                nc.scalar.wait_ge(sem("l3x_null_scores"), AC.due("l3x_null_scores"))
                act(PN[:, b * H:(b + 1) * H], PN[:, b * H:(b + 1) * H], ACT.Exp, bias=SHIFT)\
                    .then_inc(sem("l3x_null"), AC.sends("l3x_null"))
                with AC.loop(TILE_GROUPS - 1, made=[("l3x_probs", 4)], seen=[("l3x_scores_taken", 16)]):
                    for k in range(DEEP):
                        probs(k)
                if b + 1 < B:
                    probs(0)
                nc.scalar.wait_ge(sem("l3x_gathered"), AC.due("l3x_gathered", n=KEY_TILES))
                act(ZS, PSUM[:, 4:8, :].rearrange("p c n -> p (c n)"), ACT.Copy).then_inc(sem("l3x_z_kept"), AC.sends("l3x_z_kept"))
            finish_turn()

            turn_act(HT)
            nc.scalar.wait_ge(sem("l3a_qk"), AC.due("l3a_qk"))
            act(QT[:, :], bank(5), ACT.Copy).then_inc(sem("l3a_qk_kept"), AC.sends("l3a_qk_kept"))
            nc.scalar.wait_ge(sem("l3a_qk"), AC.due("l3a_qk"))
            act(KT3, bank(6), ACT.Copy).then_inc(sem("l3a_qk_kept"), AC.sends("l3a_qk_kept"))
            core_act(1, P ** -0.5)
            turn_act(OT, scale=w("l3a_gamma"), bias=w("l3a_beta"))

            turn_act(HT)
            nc.scalar.wait_ge(sem("logits"), AC.due("logits", n=3))
            act(LG, PSUM[:, 5, 0:64], ACT.Tanh, scale=0.5).then_inc(sem("l3f_scores"), AC.sends("l3f_scores"))

            def tanh(p):
                k = p % 2
                nc.scalar.wait_ge(sem("l3f_up"), AC.due("l3f_up"))
                due = AC.due("l3f_h", lag=2)
                if due is not None:
                    nc.scalar.wait_ge(sem("l3f_h"), due)
                act(TG[:, k, :], bank(1 + 2 * k), ACT.Tanh, scale=0.5).then_inc(sem("l3f_tanh"), AC.sends("l3f_tanh"))

            tanh(0)
            tanh(1)
            nc.scalar.wait_ge(sem("gates_turned"), AC.due("gates_turned"))
            act(GT[0:16, :], bank(6, 16), ACT.Copy).then_inc(sem("gates_kept"), AC.sends("gates_kept"))
            for p in range(2, PAIRS):
                tanh(p)

        @block.vector
        def _(vector):
            def norm_dve(src, turned=True):
                for b in range(B):
                    last = ve.bn_stats(ST[:, b, :], src[:, b, :])
                last.then_inc(sem("dve_step"), DV.sends("dve_step"))
                nc.vector.wait_ge(sem("dve_step"), DV.sent("dve_step"))
                for b in range(B):
                    last = ve.bn_aggr(MV[:, b, :], ST[:, b, :])
                last.then_inc(sem("dve_step"), DV.sends("dve_step"))
                nc.vector.wait_ge(sem("dve_step"), DV.sent("dve_step"))
                ve.tensor_scalar(VE[:, :], MV[:, :, 1], EPS, None, ALU.add).then_inc(sem("variance"), DV.sends("variance"))
                nc.vector.wait_ge(sem("rstd"), DV.due("rstd"))
                for b in range(B):
                    last = ve.tensor_scalar(HN[:, b, :], src[:, b, :], MV[:, b, 0:1], RSTD[:, b:b + 1],
                                            ALU.subtract, ALU.mult)
                signal = "tokens_ready" if turned else "dve_step"
                last.then_inc(sem(signal), DV.sends(signal))
                nc.vector.wait_ge(sem(signal), DV.sent(signal))

            def lift_dve(bias_row):
                ve.tensor_tensor(X[:, :, :], X[:, :, :], over(bias_row, B), ALU.add).then_inc(sem("dve_step"), DV.sends("dve_step"))
                nc.vector.wait_ge(sem("dve_step"), DV.sent("dve_step"))

            def tail_dve():
                nc.vector.wait_ge(sem("block_out"), DV.due("block_out"))
                ve.tensor_tensor(X[:, :, :], X[:, :, :], bank4(7), ALU.add).then_inc(sem("x_ready"), DV.sends("x_ready"))
                nc.vector.wait_ge(sem("x_ready"), DV.sent("x_ready"))

            def key_norms_dve(n0, n):
                for m in range(n0, n0 + n):
                    nc.vector.wait_ge(sem("key_squares"), DV.due("key_squares"))
                    ve.tensor_reduce(RK[:, m * 8:(m + 1) * 8], SQ[:, m % 2, :].rearrange("p (h e) -> p h e", e=DH),
                                     AX.X, ALU.add).then_inc(sem("key_norm"), DV.sends("key_norm"))

            def core_dve(groups, causal=None, norms_from=None):
                def shift(g):
                    nc.vector.wait_ge(sem("scores"), DV.due("scores"))
                    s = PSUM[:, 1 + g % 2, :].rearrange("p (j n) -> p j n", j=4)
                    sx = SX[:, g % 2, :].rearrange("p (j n) -> p j n", j=4)
                    due = DV.due("probs_turned", lag=2)
                    if due is not None:
                        nc.vector.wait_ge(sem("probs_turned"), due)
                    if g >= 2:
                        nc.vector.wait_ge(sem("probs_totalled"), DV.sent("probs_totalled"))
                    if causal is not None:
                        ve.tensor_tensor(sx, s, over(causal, 4), ALU.add).then_inc(sem("dve_step"), DV.sends("dve_step"))
                        nc.vector.wait_ge(sem("dve_step"), DV.sent("dve_step"))
                        ve.tensor_reduce(MX[:, g % 2, :], sx, AX.X, ALU.max).then_inc(sem("dve_step"), DV.sends("dve_step"))
                        nc.vector.wait_ge(sem("dve_step"), DV.sent("dve_step"))
                        ve.tensor_tensor(sx, sx, each(MX[:, g % 2, :], P), ALU.subtract)\
                            .then_inc(sem("scores_shifted"), DV.sends("scores_shifted"))
                    else:
                        ve.tensor_reduce(MX[:, g % 2, :], s, AX.X, ALU.max).then_inc(sem("dve_step"), DV.sends("dve_step"))
                        nc.vector.wait_ge(sem("dve_step"), DV.sent("dve_step"))
                        ve.tensor_tensor(sx, s, each(MX[:, g % 2, :], P), ALU.subtract)\
                            .then_inc(sem("scores_shifted"), DV.sends("scores_shifted"))

                def total(g):
                    nc.vector.wait_ge(sem("probs"), DV.due("probs"))
                    sx = SX[:, g % 2, :].rearrange("p (j n) -> p j n", j=4)
                    ve.tensor_reduce(L_SUM[:, 4 * g:4 * g + 4], sx, AX.X, ALU.add)\
                        .then_inc(sem("probs_totalled"), DV.sends("probs_totalled"))

                shift(0)
                for g in range(groups):
                    if g + 1 < groups:
                        shift(g + 1)
                    total(g)
                    if norms_from is not None:
                        key_norms_dve(norms_from + 4 * g, 4)
                nc.vector.wait_ge(sem("probs_totalled"), DV.sent("probs_totalled"))
                ve.reciprocal(L_INV[:, 0:4 * groups], L_SUM[:, 0:4 * groups]).then_inc(sem("dve_step"), DV.sends("dve_step"))
                nc.vector.wait_ge(sem("dve_step"), DV.sent("dve_step"))

            nc.vector.wait_ge(sem("dma_x"), DV.due("dma_x"))
            norm_dve(X)
            nc.vector.wait_ge(sem("dma_wa"), DV.due("dma_wa"))
            nc.vector.wait_ge(sem("q_rows_kept"), DV.due("q_rows_kept"))
            for h in range(H):
                last = ve.tensor_scalar(QM[:, h, :], QT[:, :], w("headmask")[:, h:h + 1], None, ALU.mult)
            last.then_inc(sem("l0x_q_heads"), DV.sends("l0x_q_heads"))
            nc.vector.wait_ge(sem("l0x_q_heads"), DV.sent("l0x_q_heads"))
            nc.vector.wait_ge(sem("l0x_v"), DV.due("l0x_v"))
            ve.tensor_copy(VS, bank(3)).then_inc(sem("v_kept"), DV.sends("v_kept"))
            nc.vector.wait_ge(sem("v_kept"), DV.sent("v_kept"))
            core_dve(16, norms_from=0)
            nc.vector.wait_ge(sem("dma_rows"), DV.due("dma_rows"))
            lift_dve(row("l0x_bo"))
            nc.vector.wait_ge(sem("values_summed"), DV.due("values_summed", n=16))
            o = ACC[:, :, :].rearrange("p b (h e) -> p (b h) e", h=H)
            ve.tensor_tensor(o, PSUM[:, 6, :].rearrange("p (a e) -> p a e", e=HD), each(L_INV, HD), ALU.mult)\
                .then_inc(sem("tokens_ready"), DV.sends("tokens_ready"))
            nc.vector.wait_ge(sem("tokens_ready"), DV.sent("tokens_ready"))
            tail_dve()

            nc.vector.wait_ge(sem("dma_wb"), DV.due("dma_wb"))
            norm_dve(X, turned=False)
            norm_dve(HN)
            lift_dve(row("l0a_w2b"))
            nc.vector.wait_ge(sem("l0a_expA"), DV.due("l0a_expA"))
            ve.tensor_scalar(ANEG, ANEG, -1.0, None, ALU.mult).then_inc(sem("l0a_A"), DV.sends("l0a_A"))
            nc.vector.wait_ge(sem("l0a_A"), DV.sent("l0a_A"))
            nc.vector.wait_ge(sem("l0a_x1_kept"), DV.due("l0a_x1_kept"))
            nc.vector.wait_ge(sem("l0a_pads"), DV.due("l0a_pads"))
            conv = CONV.rearrange("p (b t) -> p b t", b=B)
            ve.tensor_scalar(conv, CB[:, :, 0:P], w("l0a_conv")[:, 0:1], None, ALU.mult)\
                .then_inc(sem("dve_step"), DV.sends("dve_step"))
            nc.vector.wait_ge(sem("dve_step"), DV.sent("dve_step"))
            ve.scalar_tensor_tensor(out=conv, in0=CB[:, :, 1:P + 1], scalar=w("l0a_conv")[:, 1:2], in1=conv,
                                    op0=ALU.mult, op1=ALU.add).then_inc(sem("dve_step"), DV.sends("dve_step"))
            nc.vector.wait_ge(sem("dve_step"), DV.sent("dve_step"))
            ve.scalar_tensor_tensor(out=conv, in0=CB[:, :, 2:P + 2], scalar=w("l0a_conv")[:, 2:3], in1=conv,
                                    op0=ALU.mult, op1=ALU.add)\
                .then_inc(sem("l0a_preact"), DV.sends("l0a_preact"))
            nc.vector.wait_ge(sem("l0a_preact"), DV.sent("l0a_preact"))
            nc.vector.wait_ge(sem("l0a_product"), DV.due("l0a_product"))
            ve.tensor_scalar(VG, bank(2), w("l0a_v1b"), None, ALU.add).then_inc(sem("l0a_preact"), DV.sends("l0a_preact"))
            nc.vector.wait_ge(sem("l0a_preact"), DV.sent("l0a_preact"))
            nc.vector.wait_ge(sem("l1x_product"), DV.due("l1x_product", n=2))
            ve.tensor_copy(FOLDED, PSUM[:, 7, 0:2 * HD]).then_inc(sem("l1x_product_kept"), DV.sends("l1x_product_kept"))
            nc.vector.wait_ge(sem("l0a_tanh"), DV.due("l0a_tanh"))
            ve.scalar_tensor_tensor(out=U, in0=OT[:, :], scalar=1.0, in1=CONV, op0=ALU.add, op1=ALU.mult)\
                .then_inc(sem("dve_step"), DV.sends("dve_step"))
            nc.vector.wait_ge(sem("dve_step"), DV.sent("dve_step"))
            ve.tensor_scalar(U, U, 0.5, None, ALU.mult).then_inc(sem("l0a_u"), DV.sends("l0a_u"))
            nc.vector.wait_ge(sem("l0a_u"), DV.sent("l0a_u"))
            nc.vector.wait_ge(sem("l0a_tanh"), DV.due("l0a_tanh"))
            ve.scalar_tensor_tensor(out=VG, in0=TMP[:, :], scalar=1.0, in1=VG, op0=ALU.add, op1=ALU.mult)\
                .then_inc(sem("dve_step"), DV.sends("dve_step"))
            nc.vector.wait_ge(sem("dve_step"), DV.sent("dve_step"))
            nc.vector.wait_ge(sem("l0a_product"), DV.due("l0a_product"))
            ve.tensor_scalar(ZB, bank(3), w("l0a_bdt"), None, ALU.add).then_inc(sem("l0a_preact"), DV.sends("l0a_preact"))
            nc.vector.wait_ge(sem("l0a_preact"), DV.sent("l0a_preact"))
            nc.vector.wait_ge(sem("l0a_log"), DV.due("l0a_log"))
            ve.scalar_tensor_tensor(out=DT, in0=ZB, scalar=0.0, in1=EB1, op0=ALU.max, op1=ALU.add)\
                .then_inc(sem("l0a_dt_ready"), DV.sends("l0a_dt_ready"))
            nc.vector.wait_ge(sem("l0a_dt_ready"), DV.sent("l0a_dt_ready"))
            ve.tensor_tensor(DTU, DT, U, ALU.mult).then_inc(sem("dve_step"), DV.sends("dve_step"))
            nc.vector.wait_ge(sem("dve_step"), DV.sent("dve_step"))
            for half in range(2):
                for n in range(8):
                    nc.vector.wait_ge(sem("l0a_bc"), DV.due("l0a_bc"))
                    if half:
                        nc.vector.wait_ge(sem("l0a_added"), DV.due("l0a_added"))
                    ve.tensor_tensor(DBU[:, n * 512:(n + 1) * 512], bank(SPREAD_BANKS[(n + half * 16) % 6]), DTU, ALU.mult)\
                        .then_inc(sem("l0a_bc_taken"), DV.sends("l0a_bc_taken"))
                nc.vector.wait_ge(sem("l0a_bc_taken"), DV.sent("l0a_bc_taken"))
                nc.vector.wait_ge(sem("l0a_decay_cut"), DV.due("l0a_decay_cut"))
                ve.tensor_tensor_scan(HS, DA, DBU, 0.0, ALU.mult, ALU.add).then_inc(sem("l0a_scan"), DV.sends("l0a_scan"))
                nc.vector.wait_ge(sem("l0a_scan"), DV.sent("l0a_scan"))
                for n in range(8):
                    nc.vector.wait_ge(sem("l0a_bc"), DV.due("l0a_bc"))
                    ve.tensor_tensor(DBU[:, n * 512:(n + 1) * 512], HS[:, n * 512:(n + 1) * 512],
                                     bank(SPREAD_BANKS[(n + 8 + half * 16) % 6]), ALU.mult)\
                        .then_inc(sem("l0a_bc_taken"), DV.sends("l0a_bc_taken"))
            nc.vector.wait_ge(sem("l0a_added"), DV.due("l0a_added", n=8))
            ve.scalar_tensor_tensor(out=Y0, in0=U, scalar=w("l0a_D"), in1=bank(1), op0=ALU.mult, op1=ALU.add)\
                .then_inc(sem("dve_step"), DV.sends("dve_step"))
            nc.vector.wait_ge(sem("dve_step"), DV.sent("dve_step"))
            ve.scalar_tensor_tensor(out=OT[:, :], in0=Y0, scalar=0.5, in1=VG, op0=ALU.mult, op1=ALU.mult)\
                .then_inc(sem("l0a_y"), DV.sends("l0a_y"))
            nc.vector.wait_ge(sem("l0a_y"), DV.sent("l0a_y"))
            tail_dve()

            norm_dve(X)
            nc.vector.wait_ge(sem("logits"), DV.due("logits"))
            ve.tensor_copy(LG[:, 0:32], PSUM[:, 5, 0:32]).then_inc(sem("dve_step"), DV.sends("dve_step"))
            nc.vector.wait_ge(sem("dve_step"), DV.sent("dve_step"))
            lg = LG[:, 0:32].rearrange("p (b e) -> p b e", b=B)
            gx = GX[:, 0:32].rearrange("p (b e) -> p b e", b=B)
            for b in range(B):
                last = ve.max(M8[:, b, :], lg[:, b, :])
            last.then_inc(sem("dve_step"), DV.sends("dve_step"))
            nc.vector.wait_ge(sem("dve_step"), DV.sent("dve_step"))
            ve.tensor_tensor(gx, lg, M8[:, :, 0:1].broadcast_to([P, B, 8]), ALU.subtract)\
                .then_inc(sem("gate_shifted"), DV.sends("gate_shifted"))
            nc.vector.wait_ge(sem("gate_shifted"), DV.sent("gate_shifted"))
            ve.tensor_tensor(lg, lg, M8[:, :, 1:2].broadcast_to([P, B, 8]), ALU.is_ge)\
                .then_inc(sem("dve_step"), DV.sends("dve_step"))
            nc.vector.wait_ge(sem("dve_step"), DV.sent("dve_step"))
            nc.vector.wait_ge(sem("gate_exp"), DV.due("gate_exp"))
            ve.tensor_tensor(gx, gx, lg, ALU.mult).then_inc(sem("dve_step"), DV.sends("dve_step"))
            nc.vector.wait_ge(sem("dve_step"), DV.sent("dve_step"))
            ve.tensor_reduce(GS, gx, AX.X, ALU.add).then_inc(sem("dve_step"), DV.sends("dve_step"))
            nc.vector.wait_ge(sem("dve_step"), DV.sent("dve_step"))
            ve.reciprocal(GS, GS).then_inc(sem("dve_step"), DV.sends("dve_step"))
            nc.vector.wait_ge(sem("dve_step"), DV.sent("dve_step"))
            ve.tensor_tensor(GATE[:, 0:32].rearrange("p (b e) -> p b e", b=B), gx, each(GS, 8), ALU.mult)\
                .then_inc(sem("gates_ready"), DV.sends("gates_ready"))
            nc.vector.wait_ge(sem("gates_ready"), DV.sent("gates_ready"))
            ve.memset(EACC[:, :, :], 0.0).then_inc(sem("dve_step"), DV.sends("dve_step"))
            nc.vector.wait_ge(sem("dve_step"), DV.sent("dve_step"))
            for e in range(N2):
                if e == 1:
                    nc.vector.wait_ge(sem("block_out"), DV.due("block_out"))
                    ve.tensor_tensor(X[:, :, :], X[:, :, :], bank4(7), ALU.add).then_inc(sem("dve_step"), DV.sends("dve_step"))
                    nc.vector.wait_ge(sem("dve_step"), DV.sent("dve_step"))
                nc.vector.wait_ge(sem("expert_out"), DV.due("expert_out"))
                for b in range(B):
                    last = ve.scalar_tensor_tensor(out=EACC[:, b, :], in0=PSUM[:, 3 + e % 2, b * P:(b + 1) * P],
                                                   scalar=GATE[:, b * N2 + e:b * N2 + e + 1], in1=EACC[:, b, :],
                                                   op0=ALU.mult, op1=ALU.add)
                last.then_inc(sem("expert_added"), DV.sends("expert_added"))
                nc.vector.wait_ge(sem("expert_added"), DV.sent("expert_added"))
            ve.tensor_tensor(X[:, :, :], X[:, :, :], EACC[:, :, :], ALU.add).then_inc(sem("x_ready"), DV.sends("x_ready"))
            nc.vector.wait_ge(sem("x_ready"), DV.sent("x_ready"))

            nc.vector.wait_ge(sem("dma_mask"), DV.due("dma_mask"))
            ve.tensor_copy(NEG, MASK8[:, :]).then_inc(sem("dve_step"), DV.sends("dve_step"))
            nc.vector.wait_ge(sem("dve_step"), DV.sent("dve_step"))
            ve.tensor_scalar(KEEP, NEG, -1.0, 1.0, ALU.mult, ALU.add).then_inc(sem("dve_step"), DV.sends("dve_step"))
            nc.vector.wait_ge(sem("dve_step"), DV.sent("dve_step"))
            ve.tensor_scalar(NEG, NEG, MASKED, None, ALU.mult).then_inc(sem("dve_step"), DV.sends("dve_step"))
            nc.vector.wait_ge(sem("dve_step"), DV.sent("dve_step"))
            norm_dve(X)
            nc.vector.wait_ge(sem("l1x_product"), DV.due("l1x_product"))
            ve.tensor_scalar(QT[0:HD, :], bank(6, HD), w("l1x_bqh", HD), HD ** -0.5, ALU.add, ALU.mult)\
                .then_inc(sem("l1x_product_kept"), DV.sends("l1x_product_kept"))
            nc.vector.wait_ge(sem("l1x_product_kept"), DV.sent("l1x_product_kept"))
            for b in range(B):
                nc.vector.wait_ge(sem("long_scores"), DV.due("long_scores"))
                s = SL[:, b % 2, :]
                ve.tensor_tensor(s, PSUM[:, 0:4, :].rearrange("p c n -> p (c n)"), KEEP, ALU.mult)\
                    .then_inc(sem("dve_step"), DV.sends("dve_step"))
                nc.vector.wait_ge(sem("dve_step"), DV.sent("dve_step"))
                ve.tensor_tensor(s, s, NEG, ALU.add).then_inc(sem("dve_step"), DV.sends("dve_step"))
                nc.vector.wait_ge(sem("dve_step"), DV.sent("dve_step"))
                ve.tensor_reduce(LMX[:, b:b + 1], s, AX.X, ALU.max).then_inc(sem("dve_step"), DV.sends("dve_step"))
                nc.vector.wait_ge(sem("dve_step"), DV.sent("dve_step"))
                ve.tensor_scalar(LNM[:, b:b + 1], LMX[:, b:b + 1], -1.0, None, ALU.mult)\
                    .then_inc(sem("long_shift"), DV.sends("long_shift"))
                nc.vector.wait_ge(sem("long_shift"), DV.sent("long_shift"))
            nc.vector.wait_ge(sem("l1x_product"), DV.due("l1x_product"))
            ve.reciprocal(LINV, LSUM).then_inc(sem("dve_step"), DV.sends("dve_step"))
            nc.vector.wait_ge(sem("dve_step"), DV.sent("dve_step"))
            ve.tensor_tensor(OH8, PSUM[:, 5, 0:B * HD].rearrange("p (b e) -> p b e", b=B), each(LINV, HD), ALU.mult)\
                .then_inc(sem("dve_step"), DV.sends("dve_step"))
            nc.vector.wait_ge(sem("dve_step"), DV.sent("dve_step"))
            ve.tensor_tensor(OH8, OH8, over(row("l1x_bvh"), B), ALU.add).then_inc(sem("dve_step"), DV.sends("dve_step"))
            nc.vector.wait_ge(sem("dve_step"), DV.sent("dve_step"))
            for b in range(B):
                last = ve.tensor_copy(ACC[:, b, :].rearrange("p (h e) -> p h e", h=H), over(OH8[:, b, :], H))
            last.then_inc(sem("tokens_ready"), DV.sends("tokens_ready"))
            nc.vector.wait_ge(sem("tokens_ready"), DV.sent("tokens_ready"))
            tail_dve()

            def pieces_dve(dst):
                for j in range(1, H, 2):
                    nc.vector.wait_ge(sem("pieces_odd"), DV.due("pieces_odd"))
                    ve.tensor_copy(dst[0:HD, :].rearrange("p (t j) -> p t j", j=H)[:, :, j], bank(3 + j % 4, HD))\
                        .then_inc(sem("pieces_kept_dve"), DV.sends("pieces_kept_dve"))

            norm_dve(X)
            lift_dve(row("l1a_bproj"))
            for b in range(B):
                nc.vector.wait_ge(sem("l1a_rows"), DV.due("l1a_rows"))
                ve.tensor_tensor(QKV[:, b, :], PSUM[:, 1 + b, 0:3 * P], row("l1a_bqkv"), ALU.add)\
                    .then_inc(sem("l1a_rows_kept"), DV.sends("l1a_rows_kept"))
            pieces_dve(KS)
            pieces_dve(QS)
            nc.vector.wait_ge(sem("l1a_v"), DV.due("l1a_v"))
            ve.tensor_copy(VS, bank(1)).then_inc(sem("v_kept"), DV.sends("v_kept"))
            nc.vector.wait_ge(sem("v_kept"), DV.sent("v_kept"))
            pieces_dve(KS)
            core_dve(16, w("causal"), norms_from=64)
            nc.vector.wait_ge(sem("values_summed"), DV.due("values_summed", n=16))
            o = ACC[:, :, :].rearrange("p b (h e) -> p (b h) e", h=H)
            ve.tensor_tensor(o, PSUM[:, 6, :].rearrange("p (a e) -> p a e", e=HD), each(L_INV, HD), ALU.mult)\
                .then_inc(sem("tokens_ready"), DV.sends("tokens_ready"))
            nc.vector.wait_ge(sem("tokens_ready"), DV.sent("tokens_ready"))
            tail_dve()

            norm_dve(X)
            lift_dve(row("l1f_bbase"))
            nc.vector.wait_ge(sem("key_norm"), DV.sent("key_norm"))
            ve.tensor_scalar(RK[:, :], RK[:, :], 1e-24, None, ALU.max)\
                .then_inc(sem("key_squares_all"), DV.sends("key_squares_all"))
            nc.vector.wait_ge(sem("dma_idx"), DV.due("dma_idx"))
            ve.tensor_copy(IDXF, IDX[:, :]).then_inc(sem("dve_step"), DV.sends("dve_step"))
            nc.vector.wait_ge(sem("dve_step"), DV.sent("dve_step"))
            iota = row("iota")[:, 0:NA]
            ve.tensor_tensor(EQ, each(iota, NA), over(IDXF, NA), ALU.is_equal).then_inc(sem("dve_step"), DV.sends("dve_step"))
            nc.vector.wait_ge(sem("dve_step"), DV.sent("dve_step"))
            for n in range(NA):
                nc.vector.wait_ge(sem("l1f_recon"), DV.due("l1f_recon"))
                ve.scalar_tensor_tensor(out=DIFF[:, n % 2, :], in0=bank(3 + n % 2), scalar=w("l1f_bdec")[:, n:n + 1],
                                        in1=HT[:, :], op0=ALU.add, op1=ALU.subtract)\
                    .then_inc(sem("l1f_recon_taken"), DV.sends("l1f_recon_taken"))
                nc.vector.wait_ge(sem("l1f_recon_taken"), DV.sent("l1f_recon_taken"))
                ve.tensor_tensor(DIFF[:, n % 2, :], DIFF[:, n % 2, :], DIFF[:, n % 2, :], ALU.mult)\
                    .then_inc(sem("dve_step"), DV.sends("dve_step"))
                nc.vector.wait_ge(sem("dve_step"), DV.sent("dve_step"))
                last = ve.tensor_reduce(LOSS[:, :, n], DIFF[:, n % 2, :].rearrange("p (b t) -> p b t", b=B), AX.X, ALU.add)
            last.then_inc(sem("l1f_losses"), DV.sends("l1f_losses"))
            nc.vector.wait_ge(sem("l1f_losses"), DV.sent("l1f_losses"))
            nc.vector.wait_ge(sem("l1f_loss"), DV.due("l1f_loss"))
            loss = PSUM[:, 5, 0:32].rearrange("p (b n) -> p b n", b=B)
            ve.tensor_reduce(LMIN, loss, AX.X, ALU.min).then_inc(sem("dve_step"), DV.sends("dve_step"))
            nc.vector.wait_ge(sem("dve_step"), DV.sent("dve_step"))
            ve.tensor_tensor(SEL, loss, each(LMIN, NA), ALU.is_equal).then_inc(sem("dve_step"), DV.sends("dve_step"))
            nc.vector.wait_ge(sem("dve_step"), DV.sent("dve_step"))
            for b in range(B):
                last = ve.tensor_tensor(PICK[:, b, :, :], EQ, over(SEL[:, b, :], NA), ALU.mult)
            last.then_inc(sem("dve_step"), DV.sends("dve_step"))
            nc.vector.wait_ge(sem("dve_step"), DV.sent("dve_step"))
            ve.tensor_reduce(OH, PICK, AX.X, ALU.add).then_inc(sem("dve_step"), DV.sends("dve_step"))
            nc.vector.wait_ge(sem("dve_step"), DV.sent("dve_step"))
            oh2 = OH.rearrange("p b (j i) -> p b j i", i=2)
            ve.tensor_copy(SHALF[0:NR, :, :], oh2[0:NR, :, :, 0])
            ve.tensor_copy(SHALF[NR:P, :, :], oh2[NR:P, :, :, 1]).then_inc(sem("dve_step"), DV.sends("dve_step"))
            nc.vector.wait_ge(sem("dve_step"), DV.sent("dve_step"))
            ohd = PICK[:, :, :, 0]
            ve.tensor_tensor(ohd[0:NA, :, :], OH[0:NA, :, :], over(ident[0:NA, 0:NA], B), ALU.mult)\
                .then_inc(sem("dve_step"), DV.sends("dve_step"))
            nc.vector.wait_ge(sem("dve_step"), DV.sent("dve_step"))
            ve.tensor_reduce(BUP[0:NA, :], ohd[0:NA, :, :], AX.X, ALU.add).then_inc(sem("dve_step"), DV.sends("dve_step"))
            nc.vector.wait_ge(sem("dve_step"), DV.sent("dve_step"))
            ve.tensor_copy(OHT[0:NA, :].rearrange("p (b t) -> p b t", b=B), each(BUP[0:NA, :], P))\
                .then_inc(sem("dve_step"), DV.sends("dve_step"))
            nc.vector.wait_ge(sem("dve_step"), DV.sent("dve_step"))
            nc.vector.wait_ge(sem("l1f_hidden_kept"), DV.due("l1f_hidden_kept", n=6))
            for k in range(4):
                m = MID[:, k, :].rearrange("p (b t) -> p b t", b=B)
                last = ve.tensor_tensor(m, m, each(SHALF[:, :, k], P), ALU.mult)
            last.then_inc(sem("l1f_masked"), DV.sends("l1f_masked"))
            nc.vector.wait_ge(sem("l1f_masked"), DV.sent("l1f_masked"))
            nc.vector.wait_ge(sem("block_out"), DV.due("block_out"))
            ve.tensor_tensor(X[:, :, :], X[:, :, :], bank4(6), ALU.add).then_inc(sem("x_ready"), DV.sends("x_ready"))
            nc.vector.wait_ge(sem("x_ready"), DV.sent("x_ready"))

            norm_dve(X)
            lift_dve(row("l2x_bv"))
            for b in range(B):
                nc.vector.wait_ge(sem("long_scores"), DV.due("long_scores"))
                ve.tensor_reduce(LMX[:, b:b + 1], PSUM[:, 0:4, :].rearrange("p c n -> p (c n)"), AX.X, ALU.max)\
                    .then_inc(sem("dve_step"), DV.sends("dve_step"))
                nc.vector.wait_ge(sem("dve_step"), DV.sent("dve_step"))
                ve.tensor_scalar(LNM[:, b:b + 1], LMX[:, b:b + 1], -(P ** -0.5), None, ALU.mult)\
                    .then_inc(sem("long_shift"), DV.sends("long_shift"))
                nc.vector.wait_ge(sem("long_shift"), DV.sent("long_shift"))
            nc.vector.wait_ge(sem("block_out"), DV.due("block_out"))
            ve.reciprocal(LINV, LSUM).then_inc(sem("dve_step"), DV.sends("dve_step"))
            nc.vector.wait_ge(sem("dve_step"), DV.sent("dve_step"))
            ve.tensor_tensor(ACC[:, :, :], bank4(7), each(LINV, P), ALU.mult).then_inc(sem("dve_step"), DV.sends("dve_step"))
            nc.vector.wait_ge(sem("dve_step"), DV.sent("dve_step"))
            ve.tensor_tensor(X[:, :, :], X[:, :, :], ACC[:, :, :], ALU.add).then_inc(sem("x_ready"), DV.sends("x_ready"))
            nc.vector.wait_ge(sem("x_ready"), DV.sent("x_ready"))

            ve.tensor_scalar(SM[0:16, 0:1], w("l2a_big", 16), 0.5, None, ALU.mult).then_inc(sem("dve_step"), DV.sends("dve_step"))
            nc.vector.wait_ge(sem("dve_step"), DV.sent("dve_step"))
            ve.tensor_scalar(SM[0:16, 1:2], w("l2a_bfg", 16), 0.5, None, ALU.mult)\
                .then_inc(sem("l2a_halves"), DV.sends("l2a_halves"))
            nc.vector.wait_ge(sem("l2a_halves"), DV.sent("l2a_halves"))
            norm_dve(X)
            lift_dve(row("l2a_beta"))
            nc.vector.wait_ge(sem("l2a_gates"), DV.due("l2a_gates"))
            ve.tensor_scalar(IG[0:16, :], IG[0:16, :], 0.5, 0.5, ALU.mult, ALU.add)\
                .then_inc(sem("dve_step"), DV.sends("dve_step"))
            nc.vector.wait_ge(sem("dve_step"), DV.sent("dve_step"))
            ve.tensor_scalar(FG[0:16, :], FG[0:16, :], 0.5, 0.5, ALU.mult, ALU.add)\
                .then_inc(sem("dve_step"), DV.sends("dve_step"))
            nc.vector.wait_ge(sem("dve_step"), DV.sent("dve_step"))
            ve.memset(FG[0:16, :].rearrange("p (b t) -> p b t", b=B)[:, :, 0:1], 0.0)\
                .then_inc(sem("dve_step"), DV.sends("dve_step"))
            nc.vector.wait_ge(sem("dve_step"), DV.sent("dve_step"))
            nc.vector.wait_ge(sem("l2a_mm"), DV.due("l2a_mm", n=5))
            ve.tensor_tensor(BX[0:16, :], bank(5, 16), IG[0:16, :], ALU.mult).then_inc(sem("dve_step"), DV.sends("dve_step"))
            nc.vector.wait_ge(sem("dve_step"), DV.sent("dve_step"))
            ve.tensor_tensor_scan(HR[0:16, :], FG[0:16, :], BX[0:16, :], 0.0, ALU.mult, ALU.add)\
                .then_inc(sem("l2a_h"), DV.sends("l2a_h"))
            nc.vector.wait_ge(sem("l2a_h"), DV.sent("l2a_h"))
            nc.vector.wait_ge(sem("l2a_out"), DV.due("l2a_out"))
            ve.tensor_tensor(ACC[:, :, :], bank4(7), over(row("l2a_bout"), B), ALU.add)\
                .then_inc(sem("dve_step"), DV.sends("dve_step"))
            nc.vector.wait_ge(sem("dve_step"), DV.sent("dve_step"))
            norm_dve(ACC, turned=False)
            ve.tensor_tensor(ACC[:, :, :], HN[:, :, :], over(row("l2a_gamma"), B), ALU.mult)\
                .then_inc(sem("dve_step"), DV.sends("dve_step"))
            nc.vector.wait_ge(sem("dve_step"), DV.sent("dve_step"))
            ve.tensor_tensor(X[:, :, :], X[:, :, :], ACC[:, :, :], ALU.add).then_inc(sem("x_ready"), DV.sends("x_ready"))
            nc.vector.wait_ge(sem("x_ready"), DV.sent("x_ready"))

            def block9_scales_dve():
                ve.tensor_tensor(SCR, row("l3x_qs"), row("l3x_ks"), ALU.mult).then_inc(sem("dve_step"), DV.sends("dve_step"))
                nc.vector.wait_ge(sem("dve_step"), DV.sent("dve_step"))
                ve.tensor_scalar(SCR, SCR, 8.0, None, ALU.mult).then_inc(sem("dve_step"), DV.sends("dve_step"))
                nc.vector.wait_ge(sem("dve_step"), DV.sent("dve_step"))
                ve.tensor_tensor(SCRC, w("l3x_qsc"), w("l3x_ksc"), ALU.mult).then_inc(sem("dve_step"), DV.sends("dve_step"))
                nc.vector.wait_ge(sem("dve_step"), DV.sent("dve_step"))
                ve.tensor_scalar(SCRC, SCRC, 8.0, None, ALU.mult).then_inc(sem("dve_step"), DV.sends("dve_step"))
                nc.vector.wait_ge(sem("dve_step"), DV.sent("dve_step"))
                ve.tensor_reduce(TOP, SCR, AX.X, ALU.max).then_inc(sem("dve_step"), DV.sends("dve_step"))
                nc.vector.wait_ge(sem("dve_step"), DV.sent("dve_step"))
                ve.tensor_reduce(LOW, SCR, AX.X, ALU.min).then_inc(sem("dve_step"), DV.sends("dve_step"))
                nc.vector.wait_ge(sem("dve_step"), DV.sent("dve_step"))
                ve.scalar_tensor_tensor(out=TOP, in0=LOW, scalar=-1.0, in1=TOP, op0=ALU.mult, op1=ALU.max)\
                    .then_inc(sem("dve_step"), DV.sends("dve_step"))
                nc.vector.wait_ge(sem("dve_step"), DV.sent("dve_step"))
                ve.tensor_scalar(SHIFT, TOP, -1.0, SAFE_EXPONENT, ALU.mult, ALU.add).then_inc(sem("dve_step"), DV.sends("dve_step"))
                nc.vector.wait_ge(sem("dve_step"), DV.sent("dve_step"))
                ve.tensor_scalar(SHIFT, SHIFT, 0.0, None, ALU.min).then_inc(sem("l3x_scales"), DV.sends("l3x_scales"))
                nc.vector.wait_ge(sem("l3x_scales"), DV.sent("l3x_scales"))
                ve.tensor_tensor(NKH, row("l3x_nk"), row("l3x_nk"), ALU.mult).then_inc(sem("dve_step"), DV.sends("dve_step"))
                nc.vector.wait_ge(sem("dve_step"), DV.sent("dve_step"))
                ve.tensor_reduce(NSS, NKH, AX.X, ALU.add).then_inc(sem("dve_step"), DV.sends("dve_step"))
                nc.vector.wait_ge(sem("dve_step"), DV.sent("dve_step"))
                ve.tensor_scalar(NSS, NSS, 1e-24, None, ALU.max).then_inc(sem("l3x_null_square"), DV.sends("l3x_null_square"))
                nc.vector.wait_ge(sem("l3x_null_square"), DV.sent("l3x_null_square"))
                nc.vector.wait_ge(sem("key_norms"), DV.due("key_norms"))
                ve.reciprocal(RK[:, :], RK[:, :]).then_inc(sem("dve_step"), DV.sends("dve_step"))
                nc.vector.wait_ge(sem("dve_step"), DV.sent("dve_step"))
                nc.vector.wait_ge(sem("l3x_null_rnorm"), DV.due("l3x_null_rnorm"))
                ve.tensor_scalar(NKH, row("l3x_nk"), NSS, None, ALU.mult).then_inc(sem("dve_step"), DV.sends("dve_step"))
                nc.vector.wait_ge(sem("dve_step"), DV.sent("dve_step"))
                ve.tensor_tensor(SNK, NKH, SCR, ALU.mult).then_inc(sem("dve_step"), DV.sends("dve_step"))
                nc.vector.wait_ge(sem("dve_step"), DV.sent("dve_step"))

            norm_dve(X)
            nc.vector.wait_ge(sem("logits"), DV.due("logits"))
            lp = PSUM[:, 5, 0:B * 16].rearrange("p (b e) -> p b e", b=B)
            lg = LG.rearrange("p (b e) -> p b e", b=B)
            gx = GX.rearrange("p (b e) -> p b e", b=B)
            ve.tensor_reduce(GS, lp, AX.X, ALU.max).then_inc(sem("dve_step"), DV.sends("dve_step"))
            nc.vector.wait_ge(sem("dve_step"), DV.sent("dve_step"))
            ve.tensor_tensor(lg, lp, each(GS, 16), ALU.is_equal).then_inc(sem("l2f_onehot"), DV.sends("l2f_onehot"))
            nc.vector.wait_ge(sem("l2f_onehot"), DV.sent("l2f_onehot"))
            ve.tensor_tensor(gx, lp, each(GS, 16), ALU.subtract).then_inc(sem("gate_shifted"), DV.sends("gate_shifted"))
            nc.vector.wait_ge(sem("gate_shifted"), DV.sent("gate_shifted"))
            nc.vector.wait_ge(sem("l2f_places"), DV.due("l2f_places"))
            ve.tensor_tensor(GATE, PSUM[:, 6, 0:B * 16], LG, ALU.mult).then_inc(sem("dve_step"), DV.sends("dve_step"))
            nc.vector.wait_ge(sem("dve_step"), DV.sent("dve_step"))
            slots = row("iota")[:, 1:CAPACITY + 1]
            ve.tensor_tensor(PLACED.rearrange("p (a c) -> p a c", c=CAPACITY), each(GATE, CAPACITY),
                             over(slots, B * 16), ALU.is_equal)\
                .then_inc(sem("l2f_onehot"), DV.sends("l2f_onehot"))
            nc.vector.wait_ge(sem("l2f_onehot"), DV.sent("l2f_onehot"))
            nc.vector.wait_ge(sem("gate_exp"), DV.due("gate_exp"))
            ve.tensor_reduce(GS, gx, AX.X, ALU.add).then_inc(sem("dve_step"), DV.sends("dve_step"))
            nc.vector.wait_ge(sem("dve_step"), DV.sent("dve_step"))
            ve.reciprocal(GS, GS).then_inc(sem("dve_step"), DV.sends("dve_step"))
            nc.vector.wait_ge(sem("dve_step"), DV.sent("dve_step"))
            block9_scales_dve()
            nc.vector.wait_ge(sem("l2f_part_kept"), DV.due("l2f_part_kept", n=2))
            for g in range(PAIRS8):
                due = DV.due("l2f_combined", lag=2)
                if due is not None:
                    nc.vector.wait_ge(sem("l2f_combined"), due)
                for i in range(2):
                    nc.vector.wait_ge(sem("l2f_turned"), DV.due("l2f_turned"))
                    ve.tensor_copy(PLACED_T[:, 2 * (g % 2) + i, :], bank(1 + i, CAPACITY))\
                        .then_inc(sem("l2f_turned_kept"), DV.sends("l2f_turned_kept"))
            nc.vector.wait_ge(sem("l2f_combined"), DV.due("l2f_combined", n=0))
            for b in range(B):
                last = ve.scalar_tensor_tensor(out=X[:, b, :], in0=PSUM[:, 7, b * P:(b + 1) * P], scalar=GS[:, b:b + 1],
                                               in1=X[:, b, :], op0=ALU.mult, op1=ALU.add)
            last.then_inc(sem("x_ready"), DV.sends("x_ready"))
            nc.vector.wait_ge(sem("x_ready"), DV.sent("x_ready"))

            norm_dve(X, turned=False)
            norm_dve(HN)
            q4 = QN.rearrange("p b (h e) -> p b h e", h=H)
            t1 = T1.rearrange("p (h e) -> p h e", h=H)
            for b in range(B):
                nc.vector.wait_ge(sem("l3x_squares"), DV.due("l3x_squares"))
                ve.tensor_reduce(QSS[:, b * H:(b + 1) * H], Q2[:, b % 2, :].rearrange("p (h e) -> p h e", h=H),
                                 AX.X, ALU.add)\
                    .then_inc(sem("l3x_squares_summed"), DV.sends("l3x_squares_summed"))
            nc.vector.wait_ge(sem("l3x_squares_summed"), DV.sent("l3x_squares_summed"))
            ve.tensor_scalar(QSS, QSS, 1e-24, None, ALU.max).then_inc(sem("l3x_squares_ready"), DV.sends("l3x_squares_ready"))
            nc.vector.wait_ge(sem("l3x_squares_ready"), DV.sent("l3x_squares_ready"))
            nc.vector.wait_ge(sem("l3x_norms"), DV.due("l3x_norms"))
            ve.reciprocal(QSS, QSS).then_inc(sem("dve_step"), DV.sends("dve_step"))
            nc.vector.wait_ge(sem("dve_step"), DV.sent("dve_step"))
            for b in range(B):
                q = PSUM[:, 2 * b:2 * b + 2, :].rearrange("p c (h e) -> p (c h) e", e=DH)
                ve.tensor_tensor(q4[:, b, :, :], q, each(QSS[:, b * H:(b + 1) * H], DH), ALU.mult)\
                    .then_inc(sem("l3x_q_rows"), DV.sends("l3x_q_rows"))

            def scale(b, k, t):
                for c in range(4):
                    nc.vector.wait_ge(sem("l3x_scores"), DV.due("l3x_scores"))
                    if c == 0:
                        due = DV.due("l3x_gathered", lag=2)
                        if due is not None:
                            nc.vector.wait_ge(sem("l3x_gathered"), due)
                        due = DV.due("l3x_summed", lag=2)
                        if due is not None:
                            nc.vector.wait_ge(sem("l3x_summed"), due)
                    at = t * H + (b * KEY_TILES * H + 4 * c)
                    rk = RK[:, at:at + 4] if isinstance(t, int) else RK[:, bass.ds(at, 4)]
                    ve.tensor_tensor(PR[:, k % 2, c * 512:(c + 1) * 512].rearrange("p (j n) -> p j n", j=4),
                                     PSUM[:, c % 2, :].rearrange("p (j n) -> p j n", j=4), each(rk, P), ALU.mult)\
                        .then_inc(sem("l3x_scores_taken"), DV.sends("l3x_scores_taken"))

            ln = LT[:, 0:H]
            o = OTK.rearrange("p (h e) -> p h e", h=H)

            def null_scores(b):
                nc.vector.wait_ge(sem("l3x_q_rows"), DV.sent("l3x_q_rows"))
                ve.tensor_tensor(t1, q4[:, b, :, :], over(SNK, H), ALU.mult).then_inc(sem("dve_step"), DV.sends("dve_step"))
                nc.vector.wait_ge(sem("dve_step"), DV.sent("dve_step"))
                ve.tensor_reduce(PN[:, b * H:(b + 1) * H], t1, AX.X, ALU.add)\
                    .then_inc(sem("l3x_null_scores"), DV.sends("l3x_null_scores"))
                nc.vector.wait_ge(sem("l3x_null_scores"), DV.sent("l3x_null_scores"))

            def finish_sums(b):
                nc.vector.wait_ge(sem("l3x_null"), DV.due("l3x_null"))
                nc.vector.wait_ge(sem("l3x_l"), DV.due("l3x_l"))
                ve.tensor_tensor(ln, PSUM[:, 2, 0:H], PN[:, b * H:(b + 1) * H], ALU.add)\
                    .then_inc(sem("l3x_l_kept"), DV.sends("l3x_l_kept"))
                nc.vector.wait_ge(sem("l3x_l_kept"), DV.sent("l3x_l_kept"))
                ve.reciprocal(ln, ln).then_inc(sem("dve_step"), DV.sends("dve_step"))
                nc.vector.wait_ge(sem("dve_step"), DV.sent("dve_step"))
                ve.tensor_tensor(t1, over(row("l3x_nv"), H), each(PN[:, b * H:(b + 1) * H], DH), ALU.mult)\
                    .then_inc(sem("dve_step"), DV.sends("dve_step"))
                nc.vector.wait_ge(sem("dve_step"), DV.sent("dve_step"))

            def finish_values():
                nc.vector.wait_ge(sem("l3x_o"), DV.due("l3x_o"))
                ve.tensor_tensor(o, PSUM[:, 2:4, :].rearrange("p c (h e) -> p (c h) e", h=8), t1, ALU.add)\
                    .then_inc(sem("dve_step"), DV.sends("dve_step"))
                nc.vector.wait_ge(sem("dve_step"), DV.sent("dve_step"))
                ve.tensor_tensor(o, o, each(ln, DH), ALU.mult).then_inc(sem("l3x_o_kept"), DV.sends("l3x_o_kept"))
                nc.vector.wait_ge(sem("l3x_o_kept"), DV.sent("l3x_o_kept"))

            def finish_out(b):
                nc.vector.wait_ge(sem("l3x_out"), DV.due("l3x_out"))
                ve.tensor_copy(OAT[:, b, :], PSUM[:, 2, 0:P]).then_inc(sem("l3x_out_kept"), DV.sends("l3x_out_kept"))
                nc.vector.wait_ge(sem("l3x_out_kept"), DV.sent("l3x_out_kept"))

            for b in range(B):
                for k in range(DEEP):
                    scale(b, k, k)
                    if b and k == 1:
                        finish_sums(b - 1)
                    if b and k == 2:
                        finish_values()
                    if k == 3:
                        null_scores(b)
                with DV.loop(TILE_GROUPS - 1, made=[("l3x_scores_taken", 16)],
                             seen=[("l3x_scores", 16), ("l3x_gathered", 4), ("l3x_summed", 4)]) as i:
                    for k in range(DEEP):
                        scale(b, k, DEEP * i + (DEEP + k))
                if b:
                    finish_out(b - 1)
            finish_sums(B - 1)
            finish_values()
            finish_out(B - 1)
            norm_dve(OAT, turned=False)
            ve.tensor_tensor(ACC[:, :, :], HN[:, :, :], over(row("l3x_go"), B), ALU.mult)\
                .then_inc(sem("dve_step"), DV.sends("dve_step"))
            nc.vector.wait_ge(sem("dve_step"), DV.sent("dve_step"))
            ve.tensor_tensor(X[:, :, :], X[:, :, :], ACC[:, :, :], ALU.add).then_inc(sem("x_ready"), DV.sends("x_ready"))
            nc.vector.wait_ge(sem("x_ready"), DV.sent("x_ready"))

            norm_dve(X)
            lift_dve(row("l3a_bfc"))
            nc.vector.wait_ge(sem("l3a_v"), DV.due("l3a_v"))
            ve.tensor_copy(V3, bank4(7)).then_inc(sem("v_kept"), DV.sends("v_kept"))
            nc.vector.wait_ge(sem("v_kept"), DV.sent("v_kept"))
            core_dve(1, w("causal"))
            nc.vector.wait_ge(sem("values_summed"), DV.due("values_summed"))
            ve.tensor_tensor(ACC[:, :, :], bank4(6), each(L_INV[:, 0:B], P), ALU.mult)\
                .then_inc(sem("dve_step"), DV.sends("dve_step"))
            nc.vector.wait_ge(sem("dve_step"), DV.sent("dve_step"))
            ve.tensor_tensor(ACC[:, :, :], ACC[:, :, :], V3, ALU.add).then_inc(sem("dve_step"), DV.sends("dve_step"))
            nc.vector.wait_ge(sem("dve_step"), DV.sent("dve_step"))
            norm_dve(ACC)
            tail_dve()

            norm_dve(X)
            nc.vector.wait_ge(sem("l3f_scores"), DV.due("l3f_scores"))
            lg = LG.rearrange("p (b e) -> p b e", b=B)
            gx = GX.rearrange("p (b e) -> p b e", b=B)
            ve.tensor_scalar(LG, LG, 0.5, 0.5, ALU.mult, ALU.add).then_inc(sem("dve_step"), DV.sends("dve_step"))
            nc.vector.wait_ge(sem("dve_step"), DV.sent("dve_step"))
            ve.tensor_tensor(gx, lg, over(row("l3f_gb"), B), ALU.add).then_inc(sem("dve_step"), DV.sends("dve_step"))
            nc.vector.wait_ge(sem("dve_step"), DV.sent("dve_step"))
            for b in range(B):
                last = ve.max(M8[:, b, :], gx[:, b, :])
            last.then_inc(sem("dve_step"), DV.sends("dve_step"))
            nc.vector.wait_ge(sem("dve_step"), DV.sent("dve_step"))
            ve.tensor_tensor(gx, gx, M8[:, :, 3:4].broadcast_to([P, B, 16]), ALU.is_ge)\
                .then_inc(sem("dve_step"), DV.sends("dve_step"))
            nc.vector.wait_ge(sem("dve_step"), DV.sent("dve_step"))
            ve.tensor_tensor(lg, lg, gx, ALU.mult).then_inc(sem("dve_step"), DV.sends("dve_step"))
            nc.vector.wait_ge(sem("dve_step"), DV.sent("dve_step"))
            ve.tensor_reduce(GS, lg, AX.X, ALU.add).then_inc(sem("dve_step"), DV.sends("dve_step"))
            nc.vector.wait_ge(sem("dve_step"), DV.sent("dve_step"))
            ve.reciprocal(GS, GS).then_inc(sem("dve_step"), DV.sends("dve_step"))
            nc.vector.wait_ge(sem("dve_step"), DV.sent("dve_step"))
            ve.tensor_scalar(GS, GS, 2.5 * 0.5, None, ALU.mult).then_inc(sem("dve_step"), DV.sends("dve_step"))
            nc.vector.wait_ge(sem("dve_step"), DV.sent("dve_step"))
            ve.tensor_tensor(GATE.rearrange("p (b e) -> p b e", b=B), lg, each(GS, 16), ALU.mult)\
                .then_inc(sem("gates_ready"), DV.sends("gates_ready"))
            nc.vector.wait_ge(sem("gates_ready"), DV.sent("gates_ready"))
            for p in range(PAIRS):
                k = p % 2
                nc.vector.wait_ge(sem("l3f_tanh"), DV.due("l3f_tanh"))
                due = DV.due("l3f_down", lag=2)
                if due is not None:
                    nc.vector.wait_ge(sem("l3f_down"), due)
                ve.scalar_tensor_tensor(out=HP[:, k, :], in0=TG[:, k, :], scalar=1.0, in1=bank(1 + 2 * k),
                                        op0=ALU.add, op1=ALU.mult)\
                    .then_inc(sem("dve_step"), DV.sends("dve_step"))
                nc.vector.wait_ge(sem("dve_step"), DV.sent("dve_step"))
                if p < PAIRS - 1:
                    ve.tensor_tensor(HP[:, k, :], HP[:, k, :], bank(2 + 2 * k), ALU.mult).then_inc(sem("dve_step"), DV.sends("dve_step"))
                    nc.vector.wait_ge(sem("dve_step"), DV.sent("dve_step"))
                    nc.vector.wait_ge(sem("l3f_gate"), DV.due("l3f_gate"))
                    ve.tensor_tensor(HP[:, k, :], HP[:, k, :], bank(5 + k), ALU.mult).then_inc(sem("l3f_h"), DV.sends("l3f_h"))
                    nc.vector.wait_ge(sem("l3f_h"), DV.sent("l3f_h"))
                else:
                    ve.scalar_tensor_tensor(out=HP[:, k, :], in0=HP[:, k, :], scalar=0.5, in1=bank(2 + 2 * k),
                                            op0=ALU.mult, op1=ALU.mult)\
                        .then_inc(sem("l3f_h"), DV.sends("l3f_h"))
                    nc.vector.wait_ge(sem("l3f_h"), DV.sent("l3f_h"))
            nc.vector.wait_ge(sem("l3f_down"), DV.due("l3f_down", n=0))
            ve.tensor_tensor(X[:, :, :], X[:, :, :], bank4(7), ALU.add).then_inc(sem("x_ready"), DV.sends("x_ready"))
            nc.vector.wait_ge(sem("x_ready"), DV.sent("x_ready"))

        @block.tensor
        def _(tensor):
            def turn_pe(src=HN):
                nc.tensor.wait_ge(sem("tokens_ready"), PE.due("tokens_ready"))
                for b in range(B):
                    last = tp(PSUM[:, 0, b * P:(b + 1) * P], src[:, b, :], ident)
                last.then_inc(sem("turned"), PE.sends("turned"))

            def tail_pe(weight, src=OT):
                for b in range(B):
                    last = mm(PSUM[:, 7, b * P:(b + 1) * P], src[:, b * P:(b + 1) * P], weight, start=True, stop=True)
                last.then_inc(sem("block_out"), PE.sends("block_out"))

            def key_norms_pe(n0, n):
                for m in range(n0, n0 + n):
                    t, c = m // 2, m % 2
                    due = PE.due("key_squares", lag=2)
                    if due is not None:
                        nc.tensor.wait_ge(sem("key_squares"), due)
                    mm(bank(5 + 2 * c), CT[:, t * P:(t + 1) * P], WK[:, c * 512:(c + 1) * 512],
                        start=True, stop=True).then_inc(sem("key_rows"), PE.sends("key_rows"))

            def core_pe(groups, q_of, k_of, v_of, out_of, norms_from=None):
                def scores(g):
                    due = PE.due("scores_shifted", lag=2)
                    if due is not None:
                        nc.tensor.wait_ge(sem("scores_shifted"), due)
                    for j in range(4):
                        last = mm(PSUM[:, 1 + g % 2, j * P:(j + 1) * P], q_of(g, j), k_of(g, j), start=True, stop=True)
                    last.then_inc(sem("scores"), PE.sends("scores"))

                scores(0)
                for g in range(groups):
                    if g + 1 < groups:
                        scores(g + 1)
                    if norms_from is not None:
                        key_norms_pe(norms_from + 4 * g, 2)
                    nc.tensor.wait_ge(sem("probs"), PE.due("probs"))
                    for j in range(4):
                        last = tp(PSUM[:, 3 + g % 2, j * P:(j + 1) * P], SX[:, g % 2, j * P:(j + 1) * P], ident)
                    last.then_inc(sem("probs_turned"), PE.sends("probs_turned"))
                    if norms_from is not None:
                        key_norms_pe(norms_from + 4 * g + 2, 2)
                    nc.tensor.wait_ge(sem("pt_ready"), PE.due("pt_ready"))
                    for j in range(4):
                        last = mm(out_of(g, j), PT[:, g % 2, j * P:(j + 1) * P], v_of(g, j), start=True, stop=True)
                    last.then_inc(sem("values_summed"), PE.sends("values_summed"))

            def long_pe(rows_, masked):
                def scores(b):
                    for c in range(4):
                        last = mm(PSUM[:, c, :], QT[0:rows_, b * P:(b + 1) * P],
                                  KT[0:rows_, b * S + c * 512:b * S + (c + 1) * 512], start=True, stop=True)
                    last.then_inc(sem("long_scores"), PE.sends("long_scores"))

                scores(0)
                for b in range(B):
                    if masked:
                        nc.tensor.wait_ge(sem("long_shift"), PE.due("long_shift"))
                    else:
                        nc.tensor.wait_ge(sem("long_probs"), PE.due("long_probs"))
                    if b + 1 < B:
                        scores(b + 1)
                    if masked:
                        nc.tensor.wait_ge(sem("long_probs"), PE.due("long_probs"))
                    for c in range(4):
                        due = PE.due("long_pt", lag=2)
                        if due is not None:
                            nc.tensor.wait_ge(sem("long_pt"), due)
                        for j in range(4):
                            t = 4 * c + j
                            last = tp(PSUM[:, 4 + c % 2, j * P:(j + 1) * P], SL[:, b % 2, t * P:(t + 1) * P], ident)
                        last.then_inc(sem("long_turned"), PE.sends("long_turned"))
                    nc.tensor.wait_ge(sem("long_pt"), PE.seen["long_pt"])
                    if masked and b == 0:
                        nc.tensor.wait_ge(sem("dma_ck"), PE.due("dma_ck"))
                    due = PE.due("long_z_kept", lag=1)
                    if due is not None:
                        nc.tensor.wait_ge(sem("long_z_kept"), due)
                    for t in range(KEY_TILES):
                        last = mm(PSUM[:, 6, 0:P], CK[:, b * KEY_TILES + t, :], PTL[:, t, :],
                                  start=t == 0, stop=t == KEY_TILES - 1)
                    last.then_inc(sem("long_z"), PE.sends("long_z"))

            def context_keys_pe(weight, m=P, c0=0, c1=CHUNKS):
                for c in range(c0, c1):
                    due = PE.due("context_keys_kept", lag=2)
                    if due is not None:
                        nc.tensor.wait_ge(sem("context_keys_kept"), due)
                    mm(bank(1 + c % 2, m), weight, CT[:, c * 512:(c + 1) * 512], start=True, stop=True)\
                        .then_inc(sem("context_keys"), PE.sends("context_keys"))

            nc.tensor.wait_ge(sem("dma_wa"), PE.due("dma_wa"))
            turn_pe()
            nc.tensor.wait_ge(sem("turned_kept"), PE.due("turned_kept"))
            mm(bank(5), w("l0x_WqT"), HT[:, :], start=True, stop=True).then_inc(sem("q_rows"), PE.sends("q_rows"))
            for b in range(B):
                nc.tensor.wait_ge(sem("dma_ctx%d" % b), PE.due("dma_ctx%d" % b))
                context_keys_pe(w("l0x_WkT"), c0=4 * b, c1=4 * b + 4)
                for h in range(H):
                    at = (b * H + h) * HD
                    last = mm(PSUM[:, 3, at:at + HD], CTB[:, b, h, :], w("l0x_WvT")[:, h * HD:(h + 1) * HD],
                              start=True, stop=True)
            last.then_inc(sem("l0x_v"), PE.sends("l0x_v"))
            nc.tensor.wait_ge(sem("dma_wk"), PE.due("dma_wk"))
            nc.tensor.wait_ge(sem("v_kept"), PE.due("v_kept"))
            nc.tensor.wait_ge(sem("l0x_q_heads"), PE.due("l0x_q_heads"))
            nc.tensor.wait_ge(sem("context_keys_kept"), 16)
            core_pe(16, lambda g, j: QM[:, 4 * (g % 4) + j, (g // 4) * P:(g // 4 + 1) * P],
                    lambda g, j: KSB[:, g // 4, 4 * (g % 4) + j, :],
                    lambda g, j: VS[:, (4 * g + j) * HD:(4 * g + j + 1) * HD],
                    lambda g, j: PSUM[:, 6, (4 * g + j) * HD:(4 * g + j + 1) * HD], norms_from=0)
            turn_pe(ACC)
            nc.tensor.wait_ge(sem("turned_kept"), PE.due("turned_kept"))
            tail_pe(w("l0x_WoT"))

            nc.tensor.wait_ge(sem("dma_wb"), PE.due("dma_wb"))
            turn_pe()
            nc.tensor.wait_ge(sem("turned_kept"), PE.due("turned_kept"))
            mm(bank(1), w("l0a_w1"), HT[:, :], start=True, stop=True).then_inc(sem("l0a_x1"), PE.sends("l0a_x1"))
            mm(bank(2), w("l0a_v1"), HT[:, :], start=True, stop=True).then_inc(sem("l0a_product"), PE.sends("l0a_product"))
            mm(PSUM[:, 7, 0:HD], w("l1x_WkT"), w("l1x_wkh"), start=True, stop=True)\
                .then_inc(sem("l1x_product"), PE.sends("l1x_product"))
            mm(PSUM[:, 7, HD:2 * HD], w("l1x_WvT"), w("l1x_wvh"), start=True, stop=True)\
                .then_inc(sem("l1x_product"), PE.sends("l1x_product"))
            nc.tensor.wait_ge(sem("l0a_u"), PE.due("l0a_u"))
            mm(bank(3), w("l0a_Wdt"), U, start=True, stop=True).then_inc(sem("l0a_product"), PE.sends("l0a_product"))
            def spread(k):
                name, n = ("l0a_WB", "l0a_WC")[k // 8 % 2], k // 16 * 8 + k % 8
                due = PE.due("l0a_bc_taken", lag=6)
                if due is not None:
                    nc.tensor.wait_ge(sem("l0a_bc_taken"), due)
                mm(bank(SPREAD_BANKS[k % 6]), w(name)[:, n:n + 1].broadcast_to([P, P]), U, start=True, stop=True)\
                    .then_inc(sem("l0a_bc"), PE.sends("l0a_bc"))

            def add_state(half, n):
                nc.tensor.wait_ge(sem("l0a_bc_taken"), 16 * half + 8 + n + 1)
                mm(bank(1), ident, DBU[:, n * 512:(n + 1) * 512], start=half == 0 and n == 0,
                    stop=half == 1 and n == 7, skip_group_check=True)\
                    .then_inc(sem("l0a_added"), PE.sends("l0a_added"))

            for half in range(2):
                for k in range(22 * half, 16 * half + 14):
                    spread(k)
                for n in range(8):
                    add_state(half, n)
                    if 16 * half + 14 + n < 32:
                        spread(16 * half + 14 + n)
            nc.tensor.wait_ge(sem("l0a_y"), PE.due("l0a_y"))
            tail_pe(w("l0a_w2"))

            def logits_pe(weight, e):
                for b in range(B):
                    last = mm(PSUM[:, 5, b * e:(b + 1) * e], hT(b), weight, start=True, stop=True)
                last.then_inc(sem("logits"), PE.sends("logits"))

            nc.tensor.wait_ge(sem("x_ready"), PE.due("x_ready", n=2))
            nc.tensor.wait_ge(sem("l1x_product_kept"), PE.due("l1x_product_kept"))
            context_keys_pe(WKK, HD, 0, CHUNKS // 2)
            turn_pe()
            nc.tensor.wait_ge(sem("turned_kept"), PE.due("turned_kept"))
            logits_pe(w("l0f_Wg"), 8)
            nc.tensor.wait_ge(sem("dma_moe2"), PE.due("dma_moe2"))

            def first(e):
                for c in range(FC):
                    due = PE.due("hidden_kept", lag=2)
                    if due is not None:
                        nc.tensor.wait_ge(sem("hidden_kept"), due)
                    mm(bank(1 + c % 2), E2[:, e * NW + c * P:e * NW + (c + 1) * P], HT[:, :], start=True, stop=True)\
                        .then_inc(sem("hidden"), PE.sends("hidden"))

            def second(e):
                nc.tensor.wait_ge(sem("hidden_kept"), (e + 1) * FC)
                due = PE.due("expert_added", lag=2)
                if due is not None:
                    nc.tensor.wait_ge(sem("expert_added"), due)
                for b in range(B):
                    for c in range(FC):
                        at = e * NW + FF + c * P
                        last = mm(PSUM[:, 3 + e % 2, b * P:(b + 1) * P], HB[:, e % 2, c, b * P:(b + 1) * P],
                                  E2[:, at:at + P], start=c == 0, stop=c == FC - 1)
                last.then_inc(sem("expert_out"), PE.sends("expert_out"))

            first(0)
            for e in range(N2):
                if e == 1:
                    nc.tensor.wait_ge(sem("gates_ready"), PE.due("gates_ready"))
                    for b in range(B):
                        last = tp(PSUM[0:8, 6, b * P:(b + 1) * P], GATE[:, b * 8:(b + 1) * 8], ident)
                    last.then_inc(sem("gates_turned"), PE.sends("gates_turned"))
                    nc.tensor.wait_ge(sem("gates_kept"), PE.due("gates_kept"))
                    for b in range(B):
                        last = mm(PSUM[:, 7, b * P:(b + 1) * P], GT[0:8, b * P:(b + 1) * P], w("l0f_b2", 8), start=True, stop=True)
                    last.then_inc(sem("block_out"), PE.sends("block_out"))
                if e + 1 < N2:
                    first(e + 1)
                second(e)

            context_keys_pe(WKK, HD, CHUNKS // 2)
            turn_pe()
            nc.tensor.wait_ge(sem("turned_kept"), PE.due("turned_kept"))
            mm(bank(5), w("l1x_Wq"), HT[:, :], start=True, stop=True).then_inc(sem("q_rows"), PE.sends("q_rows"))
            nc.tensor.wait_ge(sem("q_rows_kept"), PE.due("q_rows_kept", n=2))
            mm(bank(6, HD), w("l1x_wqh"), TMP[:, :], start=True, stop=True).then_inc(sem("l1x_product"), PE.sends("l1x_product"))
            nc.tensor.wait_ge(sem("l1x_product_kept"), PE.due("l1x_product_kept"))
            nc.tensor.wait_ge(sem("context_keys_kept"), 32)
            long_pe(HD, True)
            nc.tensor.wait_ge(sem("long_z_kept"), 4)
            for b in range(B):
                last = mm(PSUM[:, 5, b * HD:(b + 1) * HD], ZT[:, b * P:(b + 1) * P], WVV, start=True, stop=True)
            last.then_inc(sem("l1x_product"), PE.sends("l1x_product"))
            turn_pe(ACC)
            nc.tensor.wait_ge(sem("turned_kept"), PE.due("turned_kept"))
            tail_pe(w("l1x_Wo"))

            def pieces_pe(part):
                for j in range(H):
                    at = part * P + j * HD
                    due = PE.due(PIECES_KEPT[j % 2], lag=2)
                    if due is not None:
                        nc.tensor.wait_ge(sem(PIECES_KEPT[j % 2]), due)
                    for b in range(B):
                        last = tp(PSUM[0:HD, 3 + j % 4, b * P:(b + 1) * P], QKV[:, b, at:at + HD], ident)
                    last.then_inc(sem(PIECES[j % 2]), PE.sends(PIECES[j % 2]))

            turn_pe()
            nc.tensor.wait_ge(sem("turned_kept"), PE.due("turned_kept"))
            for b in range(B):
                mm(PSUM[:, 1 + b, 0:3 * P], hT(b), w("l1a_Wqkv"), start=True, stop=True)\
                    .then_inc(sem("l1a_rows"), PE.sends("l1a_rows"))
            nc.tensor.wait_ge(sem("l1a_rows_kept"), PE.due("l1a_rows_kept", n=B))
            pieces_pe(2)
            nc.tensor.wait_ge(sem("pieces_kept_act"), 8)
            nc.tensor.wait_ge(sem("pieces_kept_dve"), 8)
            for a in range(B * H):
                last = tp(PSUM[:, 1, a * HD:(a + 1) * HD], piece(KS, a), ident[0:HD, 0:HD])
            last.then_inc(sem("l1a_v"), PE.sends("l1a_v"))
            pieces_pe(0)
            pieces_pe(1)
            nc.tensor.wait_ge(sem("pieces_kept_act"), 24)
            nc.tensor.wait_ge(sem("pieces_kept_dve"), 24)
            nc.tensor.wait_ge(sem("v_kept"), PE.due("v_kept"))
            core_pe(16, lambda g, j: piece(QS, 4 * g + j), lambda g, j: piece(KS, 4 * g + j),
                    lambda g, j: VS[:, (4 * g + j) * HD:(4 * g + j + 1) * HD],
                    lambda g, j: PSUM[:, 6, (4 * g + j) * HD:(4 * g + j + 1) * HD], norms_from=64)
            turn_pe(ACC)
            nc.tensor.wait_ge(sem("turned_kept"), PE.due("turned_kept"))
            tail_pe(w("l1a_Wproj"))

            nc.tensor.wait_ge(sem("x_ready"), PE.due("x_ready", n=3))
            context_keys_pe(w("l2x_WkT"), c1=CHUNKS // 2)
            turn_pe()
            nc.tensor.wait_ge(sem("turned_kept"), PE.due("turned_kept"))
            for k in range(2):
                mm(bank(1 + k), w("l1f_Wenc")[:, k * P:(k + 1) * P], HT[:, :], start=True, stop=True)\
                    .then_inc(sem("l1f_hidden"), PE.sends("l1f_hidden"))
            nc.tensor.wait_ge(sem("l1f_hidden_kept"), PE.due("l1f_hidden_kept", n=2))
            for n in range(NA):
                r = NH * (n % 4)
                due = PE.due("l1f_recon_taken", lag=2)
                if due is not None:
                    nc.tensor.wait_ge(sem("l1f_recon_taken"), due)
                mm(bank(3 + n % 2), w("l1f_Wdec")[r:r + NH, (n // 4) * P:(n // 4 + 1) * P],
                    ENC[r:r + NH, n // 4, :], start=True, stop=True)\
                    .then_inc(sem("l1f_recon"), PE.sends("l1f_recon"))
            for k in range(4):
                if k >= 2:
                    nc.tensor.wait_ge(sem("l1f_hidden_kept"), PE.due("l1f_hidden_kept"))
                mm(bank(1 + k % 2), w("l1f_Wdown")[:, k * P:(k + 1) * P], HT[:, :], start=True, stop=True)\
                    .then_inc(sem("l1f_hidden"), PE.sends("l1f_hidden"))
            nc.tensor.wait_ge(sem("l1f_losses"), PE.due("l1f_losses"))
            mm(PSUM[:, 5, 0:32], w("ones"), SM[:, 0:32], start=True, stop=True).then_inc(sem("l1f_loss"), PE.sends("l1f_loss"))
            nc.tensor.wait_ge(sem("l1f_masked"), PE.due("l1f_masked"))
            for b in range(B):
                sl = slice(b * P, (b + 1) * P)
                mm(PSUM[:, 6, sl], HT[:, sl], w("l1f_Wbase"), start=True, stop=False)
                for k in range(4):
                    last = mm(PSUM[:, 6, sl], MID[:, k, sl], w("l1f_Wup")[:, k * P:(k + 1) * P],
                              start=False, stop=False)
                last = mm(PSUM[:, 6, sl], PICKT_(b), w("l1f_bup", NA), start=False, stop=True)
            last.then_inc(sem("block_out"), PE.sends("block_out"))

            context_keys_pe(w("l2x_WkT"), c0=CHUNKS // 2)
            turn_pe()
            nc.tensor.wait_ge(sem("turned_kept"), PE.due("turned_kept"))
            mm(bank(5), w("l2x_WqT"), HT[:, :], start=True, stop=True).then_inc(sem("q_rows"), PE.sends("q_rows"))
            nc.tensor.wait_ge(sem("q_rows_kept"), PE.due("q_rows_kept"))
            nc.tensor.wait_ge(sem("context_keys_kept"), 48)
            long_pe(P, False)
            nc.tensor.wait_ge(sem("long_z_kept"), 8)
            tail_pe(w("l2x_WvT"))

            turn_pe()
            nc.tensor.wait_ge(sem("turned_kept"), PE.due("turned_kept"))
            mm(bank(1), w("l2a_Win"), HT[:, :], start=True, stop=True).then_inc(sem("l2a_mm"), PE.sends("l2a_mm"))
            nc.tensor.wait_ge(sem("l2a_kept"), PE.due("l2a_kept"))
            mm(bank(2), w("l2a_WB"), XP, start=True, stop=True).then_inc(sem("l2a_mm"), PE.sends("l2a_mm"))
            mm(bank(3, 16), w("l2a_Wig"), XP, start=True, stop=True).then_inc(sem("l2a_mm"), PE.sends("l2a_mm"))
            mm(bank(4, 16), w("l2a_Wfg"), XP, start=True, stop=True).then_inc(sem("l2a_mm"), PE.sends("l2a_mm"))
            nc.tensor.wait_ge(sem("l2a_kept"), PE.due("l2a_kept"))
            mm(bank(5, 16), w("l2a_Bmat"), XB, start=True, stop=True).then_inc(sem("l2a_mm"), PE.sends("l2a_mm"))
            nc.tensor.wait_ge(sem("l2a_h"), PE.due("l2a_h"))
            mm(bank(6), w("l2a_WD"), XP, start=True, stop=False)
            mm(bank(6), w("l2a_Cmat", 16), HR[0:16, :], start=False, stop=True).then_inc(sem("l2a_mm"), PE.sends("l2a_mm"))
            nc.tensor.wait_ge(sem("l2a_kept"), PE.due("l2a_kept"))
            for b in range(B):
                sl = slice(b * P, (b + 1) * P)
                mm(PSUM[:, 7, sl], YT[:, sl], w("l2a_Wout"), start=True, stop=False)
                last = mm(PSUM[:, 7, sl], XP[:, sl], ident, start=False, stop=True)
            last.then_inc(sem("l2a_out"), PE.sends("l2a_out"))

            turn_pe()
            nc.tensor.wait_ge(sem("turned_kept"), PE.due("turned_kept"))
            logits_pe(w("l2f_WgT"), 16)
            nc.tensor.wait_ge(sem("l2f_onehot"), PE.due("l2f_onehot"))
            for b in range(B):
                for c in range(b + 1):
                    last = mm(PSUM[:, 6, b * 16:(b + 1) * 16], w("upto") if c == b else w("ones"),
                              LG[:, c * 16:(c + 1) * 16], start=c == 0, stop=c == b)
            last.then_inc(sem("l2f_places"), PE.sends("l2f_places"))
            nc.tensor.wait_ge(sem("l2f_onehot"), PE.due("l2f_onehot"))
            for s in range(2):
                for b in range(B):
                    at = b * SLOTS + s * HALF
                    last = mm(PSUM[:, 1 + s, 0:HALF], HN[:, b, :], PLACED[:, at:at + HALF], start=b == 0, stop=b == B - 1)
                last.then_inc(sem("l2f_part"), PE.sends("l2f_part"))

            def first(g):
                due = PE.due("hidden_kept", lag=2)
                if due is not None:
                    nc.tensor.wait_ge(sem("hidden_kept"), due)
                for i in range(2):
                    e = 2 * g + i
                    for c in range(FC):
                        at = (i * FC + c) * CAPACITY
                        last = mm(PSUM[:, 3 + g % 2, at:at + CAPACITY], E8[e][:, c * P:(c + 1) * P],
                                  XD[:, e * CAPACITY:(e + 1) * CAPACITY], start=True, stop=True)
                last.then_inc(sem("hidden"), PE.sends("hidden"))

            def turn_placed(g):
                if g:
                    nc.tensor.wait_ge(sem("l2f_turned_kept"), 2 * g)
                for i in range(2):
                    for b in range(B):
                        at = b * SLOTS + (2 * g + i) * CAPACITY
                        last = tp(PSUM[0:CAPACITY, 1 + i, b * P:(b + 1) * P], PLACED[:, at:at + CAPACITY], ident)
                    last.then_inc(sem("l2f_turned"), PE.sends("l2f_turned"))

            def second(g):
                nc.tensor.wait_ge(sem("hidden_kept"), N2 * FC + g + 1)
                for i in range(2):
                    for c in range(FC):
                        h = g * PW + (i * FC + c) * CAPACITY
                        last = mm(PSUM[0:CAPACITY, 5 + g % 2, i * P:(i + 1) * P], HID8[:, h:h + CAPACITY],
                                  E8[2 * g + i][:, FF + c * P:FF + (c + 1) * P], start=c == 0, stop=c == FC - 1)
                last.then_inc(sem("l2f_part"), PE.sends("l2f_part"))

            def combine(g):
                nc.tensor.wait_ge(sem("l2f_turned_kept"), 2 * g + 2)
                nc.tensor.wait_ge(sem("l2f_part_kept"), 2 + g + 1)
                for i in range(2):
                    for b in range(B):
                        last = mm(PSUM[:, 7, b * P:(b + 1) * P], PLACED_T[:, 2 * (g % 2) + i, b * P:(b + 1) * P],
                                  OS[:, g % 2, i * P:(i + 1) * P], start=g == 0 and i == 0 and b == 0,
                                  stop=g == PAIRS8 - 1 and i == 1, skip_group_check=True)
                last.then_inc(sem("l2f_combined"), PE.sends("l2f_combined"))

            nc.tensor.wait_ge(sem("dma_moe8_early"), PE.due("dma_moe8_early", n=2))
            nc.tensor.wait_ge(sem("l2f_part_kept"), PE.due("l2f_part_kept"))
            first(0)
            nc.tensor.wait_ge(sem("l2f_part_kept"), PE.due("l2f_part_kept"))
            first(1)
            for g in range(PAIRS8):
                turn_placed(g)
                if g == 0:
                    nc.tensor.wait_ge(sem("dma_moe8"), PE.due("dma_moe8"))
                if g == 2:
                    nc.tensor.wait_ge(sem("dma_moe8_late"), PE.due("dma_moe8_late"))
                second(g)
                if g + 2 < PAIRS8:
                    first(g + 2)
                if g:
                    combine(g - 1)
            combine(PAIRS8 - 1)

            nc.tensor.wait_ge(sem("dma_wc"), PE.due("dma_wc"))
            turn_pe()
            nc.tensor.wait_ge(sem("turned_kept"), PE.due("turned_kept"))
            for b in range(B):
                for c in range(2):
                    last = mm(bank(2 * b + c), hT(b), w("l3x_Wq")[:, c * 512:(c + 1) * 512], start=True, stop=True)
                last.then_inc(sem("l3x_q"), PE.sends("l3x_q"))
            for b in range(B):
                nc.tensor.wait_ge(sem("l3x_q_rows"), PE.due("l3x_q_rows"))
                for c in range(8):
                    last = tp(PSUM[:, 2 * b + c // 4, (c % 4) * P:(c % 4 + 1) * P], QN[:, b, c * P:(c + 1) * P], ident)
                last.then_inc(sem("l3x_q_turned"), PE.sends("l3x_q_turned"))
            for b in range(B):
                nc.tensor.wait_ge(sem("l3x_q_scaled"), PE.due("l3x_q_scaled"))
                for j in range(4):
                    due = PE.due("l3x_qp_kept", lag=2)
                    if due is not None:
                        nc.tensor.wait_ge(sem("l3x_qp_kept"), due)
                    for i in range(4):
                        r = DH * (j % 2)
                        h = 8 * (j // 2) + 2 * i + j % 2
                        last = mm(PSUM[:, j % 2, i * P:(i + 1) * P],
                                  w("l3x_WkT")[r:r + DH, (h // 2) * P:(h // 2 + 1) * P],
                                  QSC[r:r + DH, h // 2, b * P:(b + 1) * P], start=True, stop=True)
                    last.then_inc(sem("l3x_qp"), PE.sends("l3x_qp"))
            nc.tensor.wait_ge(sem("l3x_qp_kept"), 4 * B)
            qpb = QP.rearrange("p (b n) -> p b n", b=B)

            def score(b, k, c):
                due = PE.due("l3x_scores_taken", lag=2)
                if due is not None:
                    nc.tensor.wait_ge(sem("l3x_scores_taken"), due)
                mm(bank(c % 2), CTT[:, k, :], qpb[:, b, c * 512:(c + 1) * 512], start=True, stop=True)\
                    .then_inc(sem("l3x_scores"), PE.sends("l3x_scores"))

            def gather(k, c, first=False, final=False):
                return mm(bank(4 + c), CKT[:, k, :], PR[:, k % 2, c * 512:(c + 1) * 512], start=first, stop=final,
                          skip_group_check=True)

            def tile(b, k, first=False, final=False):
                b_next = b + 1 if final else b
                if b_next < B:
                    nc.tensor.wait_ge(sem("dma_ktile%d" % ((k + 1) % DEEP)), PE.due("dma_ktile%d" % ((k + 1) % DEEP), n=2))
                    score(b_next, (k + 1) % DEEP, 0)
                    score(b_next, (k + 1) % DEEP, 1)
                nc.tensor.wait_ge(sem("l3x_probs"), PE.due("l3x_probs"))
                if first and b:
                    nc.tensor.wait_ge(sem("l3x_z_kept"), PE.due("l3x_z_kept"))
                for c in range(4):
                    last = gather(k, c, first, final)
                    if c < 2 and b_next < B:
                        score(b_next, (k + 1) % DEEP, c + 2)
                last.then_inc(sem("l3x_gathered"), PE.sends("l3x_gathered"))

            def finish_sums(b):
                nc.tensor.wait_ge(sem("l3x_summed"), PE.due("l3x_summed", n=KEY_TILES))
                due = PE.due("l3x_out_kept", lag=1)
                if due is not None:
                    nc.tensor.wait_ge(sem("l3x_out_kept"), due)
                for h in range(H):
                    last = mm(PSUM[:, 2, h:h + 1], LS[b % 2][:, h * P:(h + 1) * P], w("ones")[:, 0:1], start=True, stop=True)
                last.then_inc(sem("l3x_l"), PE.sends("l3x_l"))

            def finish_values():
                nc.tensor.wait_ge(sem("l3x_l_kept"), PE.due("l3x_l_kept"))
                for h in range(H):
                    last = mm(PSUM[:, 2 + h // 8, (h % 8) * DH:(h % 8 + 1) * DH], ZS[:, h * P:(h + 1) * P],
                              w("l3x_Wv")[:, h * DH:(h + 1) * DH], start=True, stop=True)
                last.then_inc(sem("l3x_o"), PE.sends("l3x_o"))

            def finish_turn():
                nc.tensor.wait_ge(sem("l3x_o_kept"), PE.due("l3x_o_kept"))
                for c in range(8):
                    last = tp(PSUM[:, 2 + c // 4, (c % 4) * P:(c % 4 + 1) * P], OTK[:, c * P:(c + 1) * P], ident)
                last.then_inc(sem("l3x_oT"), PE.sends("l3x_oT"))

            def finish_out():
                nc.tensor.wait_ge(sem("l3x_oT_kept"), PE.due("l3x_oT_kept"))
                for c in range(8):
                    last = mm(PSUM[:, 2, 0:P], OT8[:, c * P:(c + 1) * P], w("l3x_Wout")[:, c * P:(c + 1) * P],
                              start=c == 0, stop=c == 7)
                last.then_inc(sem("l3x_out"), PE.sends("l3x_out"))

            nc.tensor.wait_ge(sem("dma_ktile0"), PE.due("dma_ktile0", n=2))
            for c in range(4):
                score(0, 0, c)
            for b in range(B):
                tile(b, 0, first=True)
                if b:
                    finish_sums(b - 1)
                tile(b, 1)
                if b:
                    finish_values()
                tile(b, 2)
                if b:
                    finish_turn()
                tile(b, 3)
                if b:
                    finish_out()
                with PE.loop(TILE_GROUPS - 2, made=[("l3x_scores", 16), ("l3x_gathered", 4)],
                             seen=[("dma_ktile%d" % k, 2) for k in range(DEEP)] + [("l3x_scores_taken", 16), ("l3x_probs", 4)]):
                    for k in range(DEEP):
                        tile(b, k)
                for k in range(DEEP - 1):
                    tile(b, k)
                tile(b, DEEP - 1, final=True)
            nc.tensor.wait_ge(sem("l3x_z_kept"), PE.due("l3x_z_kept"))
            finish_sums(B - 1)
            finish_values()
            finish_turn()
            finish_out()

            turn_pe()
            nc.tensor.wait_ge(sem("turned_kept"), PE.due("turned_kept"))
            mm(bank(5), w("l3a_Wq"), HT[:, :], start=True, stop=True).then_inc(sem("l3a_qk"), PE.sends("l3a_qk"))
            mm(bank(6), w("l3a_Wk"), HT[:, :], start=True, stop=True).then_inc(sem("l3a_qk"), PE.sends("l3a_qk"))
            for b in range(B):
                last = mm(PSUM[:, 7, b * P:(b + 1) * P], hT(b), w("l3a_Wv"), start=True, stop=True)
            last.then_inc(sem("l3a_v"), PE.sends("l3a_v"))
            nc.tensor.wait_ge(sem("l3a_qk_kept"), PE.due("l3a_qk_kept", n=2))
            nc.tensor.wait_ge(sem("v_kept"), PE.due("v_kept"))
            core_pe(1, lambda g, j: QT[:, j * P:(j + 1) * P], lambda g, j: KT3[:, j * P:(j + 1) * P],
                    lambda g, j: V3[:, j, :], lambda g, j: PSUM[:, 6, j * P:(j + 1) * P])
            turn_pe()
            nc.tensor.wait_ge(sem("turned_kept"), PE.due("turned_kept"))
            tail_pe(w("l3a_Wfc"))

            turn_pe()
            nc.tensor.wait_ge(sem("turned_kept"), PE.due("turned_kept"))
            logits_pe(w("l3f_WgT"), 16)
            nc.tensor.wait_ge(sem("dma_moe11"), PE.due("dma_moe11"))

            def up(p):
                k = p % 2
                due = PE.due("l3f_h", lag=2)
                if due is not None:
                    nc.tensor.wait_ge(sem("l3f_h"), due)
                for c in range(2):
                    last = mm(bank(1 + 2 * k + c), E11[:, p, c * P:(c + 1) * P], HT[:, :], start=True, stop=True)
                last.then_inc(sem("l3f_up"), PE.sends("l3f_up"))

            def gate(p):
                if p < PAIRS - 1:
                    mm(bank(5 + p % 2), PICK2[:, p * P:(p + 1) * P], GT[0:16, :], start=True, stop=True)\
                        .then_inc(sem("l3f_gate"), PE.sends("l3f_gate"))

            def down(p):
                nc.tensor.wait_ge(sem("l3f_h"), p + 1)
                rows_ = P if p < PAIRS - 1 else DH
                for b in range(B):
                    last = mm(PSUM[:, 7, b * P:(b + 1) * P], HP[0:rows_, p % 2, b * P:(b + 1) * P],
                              E11[0:rows_, p, 2 * P:3 * P], start=p == 0 and b == 0, stop=p == PAIRS - 1, skip_group_check=True)
                last.then_inc(sem("l3f_down"), PE.sends("l3f_down"))

            up(0)
            up(1)
            nc.tensor.wait_ge(sem("gates_ready"), PE.due("gates_ready"))
            for b in range(B):
                last = tp(PSUM[0:16, 6, b * P:(b + 1) * P], GATE[:, b * 16:(b + 1) * 16], ident)
            last.then_inc(sem("gates_turned"), PE.sends("gates_turned"))
            nc.tensor.wait_ge(sem("gates_kept"), PE.due("gates_kept"))
            gate(0)
            gate(1)
            for p in range(PAIRS):
                down(p)
                if p + 2 < PAIRS:
                    up(p + 2)
                    gate(p + 2)


def pack(parts):
    where, out, at = {}, [], 0
    for name, a in parts:
        full = np.zeros((P, a.shape[1]), a.dtype)
        full[:a.shape[0]] = a
        where[name] = (at, a.shape[1])
        out.append(full)
        at += a.shape[1]
    return where, np.concatenate(out, axis=1)


def lay_out(i):
    c = lambda v: np.ascontiguousarray(v)
    col = lambda v: v.reshape(-1, 1)
    eye = np.eye(P, dtype=np.float32)
    k = np.arange(P)
    a = [("ident", eye), ("ones", np.ones((P, P), np.float32)),
         ("headmask", (k[:, None] // HD == np.arange(H)[None]).astype(np.float32)),
         ("l0x_WqT", i["L0_xattn_Wq"].T), ("l0x_WkT", i["L0_xattn_Wk"].T), ("l0x_WvT", i["L0_xattn_Wv"].T),
         ("l0x_WoT", i["L0_xattn_Wo"].T), ("l0x_bq", col(i["L0_xattn_bq"])), ("l0x_bk", col(i["L0_xattn_bk"])),
         ("l0x_bv", col(i["L0_xattn_bv"]))]
    enc, dec = i["L1_ffn_W_enc"], i["L1_ffn_W_dec"]
    down, up = i["L1_ffn_W_down"], i["L1_ffn_W_up"]
    b = [("causal", np.where(k[:, None] >= k[None], 0.0, FAR).astype(np.float32)),
         ("upto", (k[:, None] <= k[None]).astype(np.float32)),
         ("l0a_w1", i["L0_attn_w1_w"]), ("l0a_v1", i["L0_attn_v1_w"]), ("l0a_w2", i["L0_attn_w2_w"]),
         ("l0a_Wdt", i["L0_attn_W_dt"]), ("l0a_WB", i["L0_attn_W_B"]), ("l0a_WC", i["L0_attn_W_C"]),
         ("l0a_Alog", i["L0_attn_A_log"]), ("l0a_conv", i["L0_attn_conv_w"].reshape(P, 3)),
         ("l0a_g", col(i["L0_attn_ln_g"])), ("l0a_b", col(i["L0_attn_ln_b"])), ("l0a_w1b", col(i["L0_attn_w1_b"])),
         ("l0a_v1b", col(i["L0_attn_v1_b"])), ("l0a_bdt", col(i["L0_attn_b_dt"])), ("l0a_D", col(i["L0_attn_D_skip"])),
         ("l0f_Wg", i["L0_ffn_Wg"]), ("l0f_b2", i["L0_ffn_b2"]),
         ("l0f_b1", i["L0_ffn_b1"].reshape(-1, P).T),
         ("l1x_WkT", i["L1_xattn_Wk"].T), ("l1x_WvT", i["L1_xattn_Wv"].T), ("l1x_wkh", i["L1_xattn_wk_h"]),
         ("l1x_wvh", i["L1_xattn_wv_h"]), ("l1x_Wq", i["L1_xattn_Wq"]), ("l1x_wqh", i["L1_xattn_wq_h"]),
         ("l1x_bqh", col(i["L1_xattn_bq_h"])), ("l1x_bkh", col(i["L1_xattn_bk_h"])), ("l1x_Wo", i["L1_xattn_Wo"]),
         ("l1a_Wqkv", i["L1_attn_Wqkv"]), ("l1a_Wproj", i["L1_attn_Wproj"]),
         ("l1f_Wenc", enc.transpose(1, 0, 2).reshape(P, 256)),
         ("l1f_benc", i["L1_ffn_b_enc"].reshape(2, P).T),
         ("l1f_Wdec", dec.reshape(2, P, P).transpose(1, 0, 2).reshape(P, 256)),
         ("l1f_bdec", i["L1_ffn_b_dec"].T),
         ("l1f_Wdown", down.transpose(1, 0, 2).reshape(P, 512)),
         ("l1f_bdown", i["L1_ffn_b_down"].reshape(4, P).T),
         ("l1f_Wup", up.reshape(4, P, P).transpose(1, 0, 2).reshape(P, 512)),
         ("l1f_bup", i["L1_ffn_b_up"]), ("l1f_Wbase", i["L1_ffn_W_base"]),
         ("l2x_WqT", i["L2_xattn_Wq"].T), ("l2x_WkT", i["L2_xattn_Wk"].T), ("l2x_WvT", i["L2_xattn_Wv"].T),
         ("l2x_bq", col(i["L2_xattn_bq"])), ("l2x_bk", col(i["L2_xattn_bk"])),
         ("l2a_Win", i["L2_attn_W_in"]), ("l2a_bin", col(i["L2_attn_b_in"])), ("l2a_WB", i["L2_attn_W_B"]),
         ("l2a_bB", col(i["L2_attn_b_B"])), ("l2a_Bmat", i["L2_attn_B_mat"]), ("l2a_Cmat", i["L2_attn_C_mat"]),
         ("l2a_Wig", i["L2_attn_W_ig"]), ("l2a_Wfg", i["L2_attn_W_fg"]), ("l2a_big", col(i["L2_attn_b_ig"])),
         ("l2a_bfg", col(i["L2_attn_b_fg"])), ("l2a_WD", i["L2_attn_W_D"]), ("l2a_bD", col(i["L2_attn_b_D"])),
         ("l2a_Wout", i["L2_attn_W_out"]), ("l2f_WgT", i["L2_ffn_gate_w"].T),
         ("l3a_Wq", i["L3_attn_Wq"]), ("l3a_Wk", i["L3_attn_Wk"]), ("l3a_Wv", i["L3_attn_Wv"]),
         ("l3a_Wfc", i["L3_attn_Wfc"]), ("l3a_gamma", col(i["L3_attn_gamma"])), ("l3a_beta", col(i["L3_attn_beta"])),
         ("l3f_WgT", i["L3_ffn_gate_w"].T), ("l3x_gn", col(i["L3_xattn_g_norm"])),
         ("l3x_qsc", col(np.tile(i["L3_xattn_q_scale"], 2))), ("l3x_ksc", col(np.tile(i["L3_xattn_k_scale"], 2)))]
    wkv = i["L3_xattn_Wkv"]
    cc = [("l3x_Wq", i["L3_xattn_Wq"]),
          ("l3x_WkT", wkv[:, :H * DH].T.reshape(8, P, P).transpose(1, 0, 2).reshape(P, 1024)),
          ("l3x_Wv", wkv[:, H * DH:]),
          ("l3x_Wout", i["L3_xattn_Wout"].reshape(8, P, P).transpose(1, 0, 2).reshape(P, 1024))]
    r = [("iota", np.arange(CAPACITY + 1, dtype=np.float32)), ("l0x_bo", i["L0_xattn_bo"]),
         ("l0a_w2b", i["L0_attn_w2_b"]), ("l1x_bvh", i["L1_xattn_bv_h"]), ("l1a_bproj", i["L1_attn_bproj"]),
         ("l1a_bqkv", i["L1_attn_bqkv"]),
         ("l1f_bbase", i["L1_ffn_b_base"]), ("l2x_bv", i["L2_xattn_bv"]), ("l2a_bout", i["L2_attn_b_out"]),
         ("l2a_gamma", i["L2_attn_gamma"]), ("l2a_beta", i["L2_attn_beta"]), ("l3x_qs", i["L3_xattn_q_scale"]),
         ("l3x_ks", i["L3_xattn_k_scale"]), ("l3x_nk", i["L3_xattn_null_kv"][0]), ("l3x_nv", i["L3_xattn_null_kv"][1]),
         ("l3x_go", i["L3_xattn_g_out"]), ("l3a_bfc", i["L3_attn_bfc"]), ("l3f_gb", i["L3_ffn_gate_b"])]
    cols, arrays = {}, {}
    for part, parts in (("a", a), ("b", b), ("c", cc)):
        where, arrays["w" + part] = pack(parts)
        cols.update({n: (part, *v) for n, v in where.items()})
    rows, at = {}, 0
    for name, v in r:
        rows[name] = (at, v.shape[0])
        at += v.shape[0]
    arrays["rows"] = np.concatenate([v for _, v in r])[None]
    ctx = i["ctx_1024"].reshape(NK, P)
    arrays["wk"] = c(wkv[:, :H * DH])
    arrays["x"] = c(i["x"].transpose(1, 0, 2))
    arrays["ctxT"] = c(ctx.T)
    arrays["ctxr"] = c(ctx)
    arrays["ctxk"] = c(ctx.reshape(NK // P, P, P).transpose(1, 0, 2))
    arrays["mask"] = c(i["mask_SxS2_bk1"])
    arrays["idx"] = c(i["L1_ffn_connected_idx"])[None]

    def side_by_side(w1, w2):
        e = w1.shape[0]
        parts = [w1, w2.reshape(e, FC, P, P).transpose(0, 2, 1, 3).reshape(e, P, FF)]
        return c(np.concatenate(parts, axis=2).transpose(1, 0, 2).reshape(P, -1))

    arrays["l0f_experts"] = side_by_side(i["L0_ffn_W1"], i["L0_ffn_W2"])
    arrays["l2f_experts"] = side_by_side(i["L2_ffn_w1"], i["L2_ffn_w2"])
    w13, w2 = i["L3_ffn_w13"], i["L3_ffn_w2"]
    pairs = np.zeros((9, P, 3 * P), np.float32)
    for p in range(9):
        for q in range(2):
            if p == 8 and q == 1:
                continue
            w13e, w2e = (w13[2 * p + q], w2[2 * p + q]) if p < 8 else (i["L3_ffn_w13_s"], i["L3_ffn_w2_s"])
            pairs[p, :, q * DH:(q + 1) * DH] = w13e[:DH].T
            pairs[p, :, P + q * DH:P + (q + 1) * DH] = w13e[DH:].T
            pairs[p, q * DH:(q + 1) * DH, 2 * P:] = w2e.T
    pick = np.repeat(np.eye(P, 16, dtype=np.float32), DH, axis=1)
    arrays["l3f_experts"] = c(np.concatenate([pairs.transpose(1, 0, 2).reshape(P, -1), pick], axis=1))
    return arrays, cols, rows



def kernel(**inputs):
    import concourse.bacc as bacc
    from concourse.bass_utils import run_bass_kernel_spmd

    arrays, cols, rows = lay_out({k: np.asarray(v) for k, v in inputs.items()})
    nc = bacc.Bacc("TRN2", target_bir_lowering=False, num_devices=1)
    d = {n: nc.dram_tensor("in_" + n, a.shape, mybir.dt.from_np(a.dtype), kind="ExternalInput").ap()
         for n, a in arrays.items()}
    d["out"] = nc.dram_tensor("out_x", (P, B, P), F32, kind="ExternalOutput").ap()
    build(nc, d, cols, rows)
    r = run_bass_kernel_spmd(nc, [{"in_" + n: a for n, a in arrays.items()}], core_ids=[0])
    return np.ascontiguousarray(r.results[0]["out_x"].transpose(1, 0, 2))
```
